# Optimizing a Trainium2 kernel written in Bass

```python
import numpy as np
import jax
import jax.numpy as jnp

def _softmax(x, axis=-1):
    return jax.nn.softmax(x, axis=axis)

def _gelu(x):
    return jax.nn.gelu(x, approximate=True)

def _silu(x):
    return jax.nn.silu(x)

def _sigmoid(x):
    return jax.nn.sigmoid(x)

def _layernorm(x, axis=-1, eps=1e-05):
    m = jnp.mean(x, axis=axis, keepdims=True)
    v = jnp.var(x, axis=axis, keepdims=True)
    return (x - m) / jnp.sqrt(v + eps)

def _scatter_add(tgt, idx, src, axis=0):
    return tgt.at[idx].add(src)

def _segment_sum(src, seg, n):
    return jax.ops.segment_sum(src, seg, n)
kernel_name = 'mk_gps_d2_gnn_r8_7d0531'

def setup_inputs(seed: int=0):
    np.random.seed(seed)
    _w = jnp.asarray

    def _rec_inputs():
        import jax
        import jax.numpy as jnp
        _gk = jax.random.key(seed)
        x = -0.0003713 + 1 * jax.random.normal(jax.random.fold_in(_gk, 1), (6250, 256), jnp.float32)
        src = jax.random.randint(jax.random.fold_in(_gk, 2), (100000,), 0, 6250, jnp.int32)
        dst = jax.random.randint(jax.random.fold_in(_gk, 3), (100000,), 0, 6250, jnp.int32)
        _o = jnp.argsort(dst, stable=True)
        src = src[_o]
        dst = dst[_o]
        edge_attr_128 = 9.41057e-06 + 1 * jax.random.normal(jax.random.fold_in(_gk, 11), (100000, 128), jnp.float32)
        edge_weight = jax.random.uniform(jax.random.fold_in(_gk, 13), (100000,), jnp.float32, 0.0, 0.999998)
        node_vec1 = jax.random.uniform(jax.random.fold_in(_gk, 14), (6250, 1), jnp.float32, 0.0, 0.999973)
        node_vec1_n2 = jax.random.uniform(jax.random.fold_in(_gk, 15), (6250, 1), jnp.float32, 0.0, 0.999973)
        return (x, src, dst, edge_attr_128, edge_weight, node_vec1, node_vec1_n2)
    x, src, dst, edge_attr_128, edge_weight, node_vec1, node_vec1_n2 = _rec_inputs()

    def _L0_gnn_setup():
        import jax, jax.numpy as jnp
        import numpy as np
        EPS = 1e-05

        def _bn(x, gamma, beta):
            m = jnp.mean(x, axis=0)
            v = jnp.mean((x - m) ** 2, axis=0)
            return gamma * (x - m) * jax.lax.rsqrt(v + EPS) + beta

        def _hconv(x, src, dst, ew, w1, b1, w2, b2, g, b):
            h = jax.nn.relu(x @ w1 + b1)
            msg = ew[:, None] * h[src]
            agg = jax.ops.segment_sum(msg, dst, num_segments=x.shape[0])
            h = agg @ w2 + b2
            return jax.nn.relu(_bn(h, g, b))
        N, C, E = (6250, 256, 37500)
        key = jax.random.key(seed)
        ks = jax.random.split(key, 16)
        s = 1.0 / np.sqrt(C)
        inp = {'x': jax.random.normal(ks[0], (N, C), dtype=jnp.float32), 'hyperedge_index': jax.random.randint(ks[1], (2, E), 0, N, dtype=jnp.int32), 'hyperedge_weight': jax.random.uniform(ks[2], (E,), dtype=jnp.float32), 'c1_w1': jax.random.normal(ks[3], (C, C), dtype=jnp.float32) * s, 'c1_b1': jnp.zeros((C,), jnp.float32), 'c1_w2': jax.random.normal(ks[4], (C, C), dtype=jnp.float32) * s, 'c1_b2': jnp.zeros((C,), jnp.float32), 'c1_g': jnp.ones((C,), jnp.float32), 'c1_b': jnp.zeros((C,), jnp.float32), 'bn1_g': jnp.ones((C,), jnp.float32), 'bn1_b': jnp.zeros((C,), jnp.float32), 'c2_w1': jax.random.normal(ks[5], (C, C), dtype=jnp.float32) * s, 'c2_b1': jnp.zeros((C,), jnp.float32), 'c2_w2': jax.random.normal(ks[6], (C, C), dtype=jnp.float32) * s, 'c2_b2': jnp.zeros((C,), jnp.float32), 'c2_g': jnp.ones((C,), jnp.float32), 'c2_b': jnp.zeros((C,), jnp.float32), 'bn2_g': jnp.ones((C,), jnp.float32), 'bn2_b': jnp.zeros((C,), jnp.float32)}
        return inp
    _L0_gnn_all = _L0_gnn_setup()
    _L0_gnn_in = {k: v for k, v in _L0_gnn_all.items() if k in ('c1_w1', 'c1_b1', 'c1_w2', 'c1_b2', 'c1_g', 'c1_b', 'bn1_g', 'bn1_b', 'c2_w1', 'c2_b1', 'c2_w2', 'c2_b2', 'c2_g', 'c2_b', 'bn2_g', 'bn2_b')}
    del _L0_gnn_all

    def _L0_mix_setup():
        import jax, jax.numpy as jnp
        import numpy as np
        HEADS = 8
        EPS = 1e-05

        def _ln(t, w, b, headc):
            m = jnp.mean(t, axis=-1, keepdims=True)
            d = t - m
            std = jnp.sqrt(jnp.sum(d * d, axis=-1, keepdims=True) / (headc - 1))
            return w * (d / (std + EPS)) + b
        key = jax.random.key(seed)
        B, N, C = (32, 512, 256)
        headc = C // HEADS
        x = jax.random.normal(key, (B, N, C), dtype=jnp.float32)
        return {'x': x, 'kln_weight': jnp.ones((HEADS, 1, headc), dtype=jnp.float32), 'kln_bias': jnp.zeros((HEADS, 1, headc), dtype=jnp.float32), 'vln_weight': jnp.ones((HEADS, 1, headc), dtype=jnp.float32), 'vln_bias': jnp.zeros((HEADS, 1, headc), dtype=jnp.float32)}
    _L0_mix_all = _L0_mix_setup()
    _L0_mix_in = {k: v for k, v in _L0_mix_all.items() if k in ('kln_weight', 'kln_bias', 'vln_weight', 'vln_bias')}
    del _L0_mix_all

    def _L0_ffn_setup():
        import jax, jax.numpy as jnp
        import numpy as np
        E = 8
        K = 2
        D = 256
        H = 512
        DOUT = 256
        EPS = 1e-05
        key = jax.random.key(seed)
        ks = jax.random.split(key, 9)
        s = 0.02
        return {'x': jax.random.normal(ks[0], (4, 1024, D), jnp.float32), 'gamma': 1.0 + 0.05 * jax.random.normal(ks[1], (D,), jnp.float32), 'beta': 0.05 * jax.random.normal(ks[2], (D,), jnp.float32), 'Wr': 0.01 * jax.random.normal(ks[3], (D, E), jnp.float32), 'br': jnp.zeros((E,), jnp.float32), 'W1': s * jax.random.normal(ks[4], (E, D, H), jnp.float32), 'b1': s * jax.random.normal(ks[5], (E, H), jnp.float32), 'W2': s * jax.random.normal(ks[6], (E, H, DOUT), jnp.float32), 'b2': s * jax.random.normal(ks[7], (E, DOUT), jnp.float32)}
    _L0_ffn_all = _L0_ffn_setup()
    _L0_ffn_in = {k: v for k, v in _L0_ffn_all.items() if k in ('gamma', 'beta', 'Wr', 'br', 'W1', 'b1', 'W2', 'b2')}
    del _L0_ffn_all

    def _L1_gnn_setup():
        import jax, jax.numpy as jnp
        import numpy as np
        NUM_NODES = 6250
        NUM_EDGES = 200000
        NODE_DIM = 256
        EDGE_DIM = 128
        MAX_IN_DEGREE = 512
        MAX_OUT_DEGREE = 512
        key = jax.random.key(seed)
        ks = jax.random.split(key, 12)
        x = jax.random.normal(ks[0], (NUM_NODES, NODE_DIM), dtype=jnp.float32)
        edge_index = jax.random.randint(ks[1], (2, NUM_EDGES), 0, NUM_NODES, dtype=jnp.int64 if jax.config.read('jax_enable_x64') else jnp.int32)
        edge_attr = jax.random.normal(ks[2], (NUM_EDGES, EDGE_DIM), dtype=jnp.float32)
        voronoi_values = jax.random.uniform(ks[3], (NUM_NODES, 1), dtype=jnp.float32)
        centralities = jax.random.uniform(ks[4], (NUM_NODES, 1), dtype=jnp.float32)
        z_in = jax.random.normal(ks[5], (MAX_IN_DEGREE, NODE_DIM), dtype=jnp.float32)
        z_out = jax.random.normal(ks[6], (MAX_OUT_DEGREE, NODE_DIM), dtype=jnp.float32)
        W_cent = jax.random.normal(ks[7], (1, NODE_DIM), dtype=jnp.float32) * 0.5
        b_cent = jnp.zeros((NODE_DIM,), dtype=jnp.float32)
        W_vor = jax.random.normal(ks[8], (1, NODE_DIM), dtype=jnp.float32) * 0.5
        b_vor = jnp.zeros((NODE_DIM,), dtype=jnp.float32)
        W_sum = jax.random.normal(ks[9], (EDGE_DIM, NODE_DIM), dtype=jnp.float32) * (1.0 / np.sqrt(EDGE_DIM))
        b_sum = jnp.zeros((NODE_DIM,), dtype=jnp.float32)
        return {'x': x, 'edge_index': edge_index, 'edge_attr': edge_attr, 'voronoi_values': voronoi_values, 'centralities': centralities, 'z_in': z_in, 'z_out': z_out, 'W_cent': W_cent, 'b_cent': b_cent, 'W_vor': W_vor, 'b_vor': b_vor, 'W_sum': W_sum, 'b_sum': b_sum}
    _L1_gnn_all = _L1_gnn_setup()
    _L1_gnn_in = {k: v for k, v in _L1_gnn_all.items() if k in ('z_in', 'z_out', 'W_cent', 'b_cent', 'W_vor', 'b_vor', 'W_sum', 'b_sum')}
    del _L1_gnn_all

    def _L1_mix_setup():
        import jax, jax.numpy as jnp
        import numpy as np
        HEADS = 4
        DIM_HEAD = 32
        key = jax.random.key(seed)
        k1, k2, k3 = jax.random.split(key, 3)
        B, L, D = (16, 1024, 256)
        hidden = HEADS * DIM_HEAD
        x = jax.random.normal(k1, (B, L, D), dtype=jnp.float32)
        W_qkv = jax.random.normal(k2, (D, 3 * hidden), dtype=jnp.float32) * D ** (-0.5)
        W_out = jax.random.normal(k3, (hidden, D), dtype=jnp.float32) * hidden ** (-0.5)
        b_out = jnp.zeros((D,), dtype=jnp.float32)
        return {'x': x, 'W_qkv': W_qkv, 'W_out': W_out, 'b_out': b_out}
    _L1_mix_all = _L1_mix_setup()
    _L1_mix_in = {k: v for k, v in _L1_mix_all.items() if k in ('W_qkv', 'W_out', 'b_out')}
    del _L1_mix_all

    def _L1_ffn_setup():
        import jax, jax.numpy as jnp
        import numpy as np
        B, N, D = (16, 512, 256)
        NUM_EXPERTS, TOP_K, HEADS = (4, 2, 4)
        N_EDGES = 131072
        LN_EPS = 1e-05

        def _layernorm(x, g, b):
            mu = x.mean(-1, keepdims=True)
            var = ((x - mu) ** 2).mean(-1, keepdims=True)
            return (x - mu) * jax.lax.rsqrt(var + LN_EPS) * g + b

        def _forward(x, edge_index, W_gat, att_src, att_dst, b_gat, ln_gamma, ln_beta, W1, b1, W2, b2):
            Bc, Nc, Dc = x.shape
            M = Bc * Nc
            x_flat = x.reshape(M, Dc)
            h = (x_flat @ W_gat).reshape(M, HEADS, NUM_EXPERTS)
            loops = jnp.arange(M, dtype=edge_index.dtype)
            src = jnp.concatenate([edge_index[0], loops])
            dst = jnp.concatenate([edge_index[1], loops])
            a_src = (h * att_src).sum(-1)
            a_dst = (h * att_dst).sum(-1)
            e = jax.nn.leaky_relu(a_src[src] + a_dst[dst], negative_slope=0.2)
            e_max = jax.ops.segment_max(e, dst, num_segments=M)
            ee = jnp.exp(e - e_max[dst])
            denom = jax.ops.segment_sum(ee, dst, num_segments=M)
            alpha = ee / (denom[dst] + 1e-16)
            msg = h[src] * alpha[:, :, None]
            agg = jax.ops.segment_sum(msg, dst, num_segments=M).reshape(M, HEADS * NUM_EXPERTS) + b_gat
            scores = _layernorm(agg, ln_gamma, ln_beta).reshape(M, HEADS, NUM_EXPERTS).mean(1)
            scores = scores.reshape(Bc, Nc, NUM_EXPERTS)
            topk_s, topk_i = jax.lax.top_k(scores, TOP_K)
            w = jax.nn.softmax(topk_s, axis=-1)
            out = jnp.zeros_like(x)
            for ei in range(NUM_EXPERTS):
                g = jnp.where(topk_i == ei, w, 0.0).sum(-1)
                hh = jax.nn.gelu(x @ W1[ei] + b1[ei], approximate=False)
                out = out + g[..., None] * (hh @ W2[ei] + b2[ei])
            return out
        key = jax.random.key(seed)
        ks = jax.random.split(key, 8)
        s = 0.05
        return {'x': jax.random.normal(ks[0], (B, N, D), jnp.float32), 'W_gat': jax.random.normal(ks[1], (D, HEADS * NUM_EXPERTS), jnp.float32) * s, 'att_src': jax.random.normal(ks[2], (HEADS, NUM_EXPERTS), jnp.float32) * s, 'att_dst': jax.random.normal(ks[3], (HEADS, NUM_EXPERTS), jnp.float32) * s, 'b_gat': jnp.zeros((HEADS * NUM_EXPERTS,), jnp.float32), 'ln_gamma': jnp.ones((HEADS * NUM_EXPERTS,), jnp.float32), 'ln_beta': jnp.zeros((HEADS * NUM_EXPERTS,), jnp.float32), 'W1': jax.random.normal(ks[4], (NUM_EXPERTS, D, 2 * D), jnp.float32) * s, 'b1': jnp.zeros((NUM_EXPERTS, 2 * D), jnp.float32), 'W2': jax.random.normal(ks[5], (NUM_EXPERTS, 2 * D, D), jnp.float32) * s, 'b2': jnp.zeros((NUM_EXPERTS, D), jnp.float32), 'edge_index': jax.random.randint(ks[6], (2, N_EDGES), 0, B * N, jnp.int32)}
    _L1_ffn_all = _L1_ffn_setup()
    _L1_ffn_in = {k: v for k, v in _L1_ffn_all.items() if k in ('W_gat', 'att_src', 'att_dst', 'b_gat', 'ln_gamma', 'ln_beta', 'W1', 'b1', 'W2', 'b2', 'edge_index')}
    del _L1_ffn_all
    return {'x': x, 'src': src, 'dst': dst, 'edge_attr_128': edge_attr_128, 'edge_weight': edge_weight, 'node_vec1': node_vec1, 'node_vec1_n2': node_vec1_n2, 'L0_gnn_c1_w1': _L0_gnn_in['c1_w1'], 'L0_gnn_c1_b1': _L0_gnn_in['c1_b1'], 'L0_gnn_c1_w2': _L0_gnn_in['c1_w2'], 'L0_gnn_c1_b2': _L0_gnn_in['c1_b2'], 'L0_gnn_c1_g': _L0_gnn_in['c1_g'], 'L0_gnn_c1_b': _L0_gnn_in['c1_b'], 'L0_gnn_bn1_g': _L0_gnn_in['bn1_g'], 'L0_gnn_bn1_b': _L0_gnn_in['bn1_b'], 'L0_gnn_c2_w1': _L0_gnn_in['c2_w1'], 'L0_gnn_c2_b1': _L0_gnn_in['c2_b1'], 'L0_gnn_c2_w2': _L0_gnn_in['c2_w2'], 'L0_gnn_c2_b2': _L0_gnn_in['c2_b2'], 'L0_gnn_c2_g': _L0_gnn_in['c2_g'], 'L0_gnn_c2_b': _L0_gnn_in['c2_b'], 'L0_gnn_bn2_g': _L0_gnn_in['bn2_g'], 'L0_gnn_bn2_b': _L0_gnn_in['bn2_b'], 'L0_mix_kln_weight': _L0_mix_in['kln_weight'], 'L0_mix_kln_bias': _L0_mix_in['kln_bias'], 'L0_mix_vln_weight': _L0_mix_in['vln_weight'], 'L0_mix_vln_bias': _L0_mix_in['vln_bias'], 'L0_ffn_gamma': _L0_ffn_in['gamma'], 'L0_ffn_beta': _L0_ffn_in['beta'], 'L0_ffn_Wr': _L0_ffn_in['Wr'], 'L0_ffn_br': _L0_ffn_in['br'], 'L0_ffn_W1': _L0_ffn_in['W1'], 'L0_ffn_b1': _L0_ffn_in['b1'], 'L0_ffn_W2': _L0_ffn_in['W2'], 'L0_ffn_b2': _L0_ffn_in['b2'], 'L1_gnn_z_in': _L1_gnn_in['z_in'], 'L1_gnn_z_out': _L1_gnn_in['z_out'], 'L1_gnn_W_cent': _L1_gnn_in['W_cent'], 'L1_gnn_b_cent': _L1_gnn_in['b_cent'], 'L1_gnn_W_vor': _L1_gnn_in['W_vor'], 'L1_gnn_b_vor': _L1_gnn_in['b_vor'], 'L1_gnn_W_sum': _L1_gnn_in['W_sum'], 'L1_gnn_b_sum': _L1_gnn_in['b_sum'], 'L1_mix_W_qkv': _L1_mix_in['W_qkv'], 'L1_mix_W_out': _L1_mix_in['W_out'], 'L1_mix_b_out': _L1_mix_in['b_out'], 'L1_ffn_W_gat': _L1_ffn_in['W_gat'], 'L1_ffn_att_src': _L1_ffn_in['att_src'], 'L1_ffn_att_dst': _L1_ffn_in['att_dst'], 'L1_ffn_b_gat': _L1_ffn_in['b_gat'], 'L1_ffn_ln_gamma': _L1_ffn_in['ln_gamma'], 'L1_ffn_ln_beta': _L1_ffn_in['ln_beta'], 'L1_ffn_W1': _L1_ffn_in['W1'], 'L1_ffn_b1': _L1_ffn_in['b1'], 'L1_ffn_W2': _L1_ffn_in['W2'], 'L1_ffn_b2': _L1_ffn_in['b2'], 'L1_ffn_edge_index': _L1_ffn_in['edge_index']}

def reference(x, src, dst, edge_attr_128, edge_weight, node_vec1, node_vec1_n2, L0_gnn_c1_w1, L0_gnn_c1_b1, L0_gnn_c1_w2, L0_gnn_c1_b2, L0_gnn_c1_g, L0_gnn_c1_b, L0_gnn_bn1_g, L0_gnn_bn1_b, L0_gnn_c2_w1, L0_gnn_c2_b1, L0_gnn_c2_w2, L0_gnn_c2_b2, L0_gnn_c2_g, L0_gnn_c2_b, L0_gnn_bn2_g, L0_gnn_bn2_b, L0_mix_kln_weight, L0_mix_kln_bias, L0_mix_vln_weight, L0_mix_vln_bias, L0_ffn_gamma, L0_ffn_beta, L0_ffn_Wr, L0_ffn_br, L0_ffn_W1, L0_ffn_b1, L0_ffn_W2, L0_ffn_b2, L1_gnn_z_in, L1_gnn_z_out, L1_gnn_W_cent, L1_gnn_b_cent, L1_gnn_W_vor, L1_gnn_b_vor, L1_gnn_W_sum, L1_gnn_b_sum, L1_mix_W_qkv, L1_mix_W_out, L1_mix_b_out, L1_ffn_W_gat, L1_ffn_att_src, L1_ffn_att_dst, L1_ffn_b_gat, L1_ffn_ln_gamma, L1_ffn_ln_beta, L1_ffn_W1, L1_ffn_b1, L1_ffn_W2, L1_ffn_b2, L1_ffn_edge_index):
    import jax
    import jax.numpy as jnp

    def _L0_gnn_ref(x, hyperedge_index, hyperedge_weight, c1_w1, c1_b1, c1_w2, c1_b2, c1_g, c1_b, bn1_g, bn1_b, c2_w1, c2_b1, c2_w2, c2_b2, c2_g, c2_b, bn2_g, bn2_b):
        import jax, jax.numpy as jnp
        import numpy as np
        EPS = 1e-05

        def _bn(x, gamma, beta):
            m = jnp.mean(x, axis=0)
            v = jnp.mean((x - m) ** 2, axis=0)
            return gamma * (x - m) * jax.lax.rsqrt(v + EPS) + beta

        def _hconv(x, src, dst, ew, w1, b1, w2, b2, g, b):
            h = jax.nn.relu(x @ w1 + b1)
            msg = ew[:, None] * h[src]
            agg = jax.ops.segment_sum(msg, dst, num_segments=x.shape[0])
            h = agg @ w2 + b2
            return jax.nn.relu(_bn(h, g, b))
        src, dst = (hyperedge_index[0], hyperedge_index[1])
        residual = x
        h = _hconv(x, src, dst, hyperedge_weight, c1_w1, c1_b1, c1_w2, c1_b2, c1_g, c1_b)
        h = jax.nn.relu(_bn(h, bn1_g, bn1_b))
        h = _hconv(h, src, dst, hyperedge_weight, c2_w1, c2_b1, c2_w2, c2_b2, c2_g, c2_b)
        h = _bn(h, bn2_g, bn2_b)
        return jax.nn.relu(h + residual)

    def _L0_mix_ref(x, kln_weight, kln_bias, vln_weight, vln_bias):
        import jax, jax.numpy as jnp
        import numpy as np
        HEADS = 8
        EPS = 1e-05

        def _ln(t, w, b, headc):
            m = jnp.mean(t, axis=-1, keepdims=True)
            d = t - m
            std = jnp.sqrt(jnp.sum(d * d, axis=-1, keepdims=True) / (headc - 1))
            return w * (d / (std + EPS)) + b
        B, N, C = x.shape
        headc = C // HEADS
        qkv = x.reshape(B, N, HEADS, headc).transpose(0, 2, 1, 3)
        k = _ln(qkv, kln_weight, kln_bias, headc)
        v = _ln(qkv, vln_weight, vln_bias, headc)
        kv = jnp.einsum('bhnd,bhne->bhde', k, v) / N
        out = jnp.einsum('bhnd,bhde->bhne', qkv, kv)
        out = out.transpose(0, 2, 1, 3).reshape(B, N, C)
        return out + x

    def _L0_ffn_ref(x, gamma, beta, Wr, br, W1, b1, W2, b2):
        import jax, jax.numpy as jnp
        import numpy as np
        E = 8
        K = 2
        D = 256
        H = 512
        DOUT = 256
        EPS = 1e-05
        mu = jnp.mean(x, axis=-1, keepdims=True)
        var = jnp.mean(jnp.square(x - mu), axis=-1, keepdims=True)
        xn = (x - mu) * jax.lax.rsqrt(var + EPS) * gamma + beta
        logits = jnp.einsum('bsd,de->bse', xn, Wr) + br
        top_vals, top_idx = jax.lax.top_k(logits, K)
        w = jax.nn.softmax(top_vals, axis=-1)
        w_full = jnp.einsum('bsk,bske->bse', w, jax.nn.one_hot(top_idx, E, dtype=w.dtype))
        y = jnp.zeros(x.shape[:-1] + (DOUT,), x.dtype)
        for e in range(E):
            h = jax.nn.gelu(jnp.einsum('bsd,dh->bsh', xn, W1[e]) + b1[e], approximate=False)
            y_e = jnp.einsum('bsh,hd->bsd', h, W2[e]) + b2[e]
            y = y + y_e * w_full[..., e, None]
        return y

    def _L1_gnn_ref(x, edge_index, edge_attr, voronoi_values, centralities, z_in, z_out, W_cent, b_cent, W_vor, b_vor, W_sum, b_sum):
        import jax, jax.numpy as jnp
        import numpy as np
        NUM_NODES = 6250
        NUM_EDGES = 200000
        NODE_DIM = 256
        EDGE_DIM = 128
        MAX_IN_DEGREE = 512
        MAX_OUT_DEGREE = 512
        num_nodes = x.shape[0]
        src = edge_index[0]
        dst = edge_index[1]
        ones = jnp.ones_like(src, dtype=jnp.int32)
        in_deg = jnp.minimum(jax.ops.segment_sum(ones, dst, num_segments=num_nodes), MAX_IN_DEGREE - 1)
        out_deg = jnp.minimum(jax.ops.segment_sum(ones, src, num_segments=num_nodes), MAX_OUT_DEGREE - 1)
        edge_proj = edge_attr @ W_sum + b_sum
        sum3d = jax.ops.segment_sum(edge_proj, src, num_segments=num_nodes)
        cent_term = jax.nn.sigmoid(centralities @ W_cent + b_cent)
        vor_term = jax.nn.sigmoid(voronoi_values @ W_vor + b_vor)
        return x + z_in[in_deg] + z_out[out_deg] + cent_term + vor_term + sum3d

    def _L1_mix_ref(x, W_qkv, W_out, b_out):
        import jax, jax.numpy as jnp
        import numpy as np
        HEADS = 4
        DIM_HEAD = 32
        B, L, D = x.shape
        scale = DIM_HEAD ** (-0.5)
        qkv = jnp.einsum('bld,df->blf', x, W_qkv)
        qkv = qkv.reshape(B, L, 3, HEADS, DIM_HEAD)
        q = jnp.transpose(qkv[:, :, 0], (0, 2, 1, 3)) * scale
        k = jax.nn.softmax(jnp.transpose(qkv[:, :, 1], (0, 2, 1, 3)), axis=2)
        v = jnp.transpose(qkv[:, :, 2], (0, 2, 1, 3))
        context = jnp.einsum('bhld,bhle->bhde', k, v)
        out = jnp.einsum('bhde,bhld->bhle', context, q)
        out = jnp.transpose(out, (0, 2, 1, 3)).reshape(B, L, HEADS * DIM_HEAD)
        return jnp.einsum('blf,fd->bld', out, W_out) + b_out

    def _L1_ffn_ref(x, W_gat, att_src, att_dst, b_gat, ln_gamma, ln_beta, W1, b1, W2, b2, edge_index):
        import jax, jax.numpy as jnp
        import numpy as np
        B, N, D = (16, 512, 256)
        NUM_EXPERTS, TOP_K, HEADS = (4, 2, 4)
        N_EDGES = 131072
        LN_EPS = 1e-05

        def _layernorm(x, g, b):
            mu = x.mean(-1, keepdims=True)
            var = ((x - mu) ** 2).mean(-1, keepdims=True)
            return (x - mu) * jax.lax.rsqrt(var + LN_EPS) * g + b

        def _forward(x, edge_index, W_gat, att_src, att_dst, b_gat, ln_gamma, ln_beta, W1, b1, W2, b2):
            Bc, Nc, Dc = x.shape
            M = Bc * Nc
            x_flat = x.reshape(M, Dc)
            h = (x_flat @ W_gat).reshape(M, HEADS, NUM_EXPERTS)
            loops = jnp.arange(M, dtype=edge_index.dtype)
            src = jnp.concatenate([edge_index[0], loops])
            dst = jnp.concatenate([edge_index[1], loops])
            a_src = (h * att_src).sum(-1)
            a_dst = (h * att_dst).sum(-1)
            e = jax.nn.leaky_relu(a_src[src] + a_dst[dst], negative_slope=0.2)
            e_max = jax.ops.segment_max(e, dst, num_segments=M)
            ee = jnp.exp(e - e_max[dst])
            denom = jax.ops.segment_sum(ee, dst, num_segments=M)
            alpha = ee / (denom[dst] + 1e-16)
            msg = h[src] * alpha[:, :, None]
            agg = jax.ops.segment_sum(msg, dst, num_segments=M).reshape(M, HEADS * NUM_EXPERTS) + b_gat
            scores = _layernorm(agg, ln_gamma, ln_beta).reshape(M, HEADS, NUM_EXPERTS).mean(1)
            scores = scores.reshape(Bc, Nc, NUM_EXPERTS)
            topk_s, topk_i = jax.lax.top_k(scores, TOP_K)
            w = jax.nn.softmax(topk_s, axis=-1)
            out = jnp.zeros_like(x)
            for ei in range(NUM_EXPERTS):
                g = jnp.where(topk_i == ei, w, 0.0).sum(-1)
                hh = jax.nn.gelu(x @ W1[ei] + b1[ei], approximate=False)
                out = out + g[..., None] * (hh @ W2[ei] + b2[ei])
            return out
        return _forward(x, edge_index, W_gat, att_src, att_dst, b_gat, ln_gamma, ln_beta, W1, b1, W2, b2)
    edge_index = jnp.stack([src, dst])
    xn = _layernorm(x, axis=-1)
    x = x + _L0_gnn_ref(xn, edge_index, edge_weight, L0_gnn_c1_w1, L0_gnn_c1_b1, L0_gnn_c1_w2, L0_gnn_c1_b2, L0_gnn_c1_g, L0_gnn_c1_b, L0_gnn_bn1_g, L0_gnn_bn1_b, L0_gnn_c2_w1, L0_gnn_c2_b1, L0_gnn_c2_w2, L0_gnn_c2_b2, L0_gnn_c2_g, L0_gnn_c2_b, L0_gnn_bn2_g, L0_gnn_bn2_b) + _L0_mix_ref(xn[None], L0_mix_kln_weight, L0_mix_kln_bias, L0_mix_vln_weight, L0_mix_vln_bias)[0]
    x = x + _L0_ffn_ref(_layernorm(x, axis=-1)[None], L0_ffn_gamma, L0_ffn_beta, L0_ffn_Wr, L0_ffn_br, L0_ffn_W1, L0_ffn_b1, L0_ffn_W2, L0_ffn_b2)[0]
    xn = _layernorm(x, axis=-1)
    x = x + _L1_gnn_ref(xn, edge_index, edge_attr_128, node_vec1, node_vec1_n2, L1_gnn_z_in, L1_gnn_z_out, L1_gnn_W_cent, L1_gnn_b_cent, L1_gnn_W_vor, L1_gnn_b_vor, L1_gnn_W_sum, L1_gnn_b_sum) + _L1_mix_ref(xn[None], L1_mix_W_qkv, L1_mix_W_out, L1_mix_b_out)[0]
    x = x + _L1_ffn_ref(_layernorm(x, axis=-1)[None], L1_ffn_W_gat, L1_ffn_att_src, L1_ffn_att_dst, L1_ffn_b_gat, L1_ffn_ln_gamma, L1_ffn_ln_beta, L1_ffn_W1, L1_ffn_b1, L1_ffn_W2, L1_ffn_b2, L1_ffn_edge_index)[0]
    return x

_drawn_inputs = setup_inputs


def setup_inputs(seed=0):
    import zlib

    import numpy as np

    out = dict(_drawn_inputs(seed))
    spreads = {'L0_gnn_c1_b1': (0.0, 0.332),
     'L0_gnn_c1_b2': (0.0, 2.0),
     'L0_gnn_c1_g': (1.0, 0.6),
     'L0_gnn_c1_b': (0.0, 0.8),
     'L0_gnn_bn1_g': (1.0, 0.2),
     'L0_gnn_bn1_b': (0.0, 0.573),
     'L0_gnn_c2_b1': (0.0, 0.359),
     'L0_gnn_c2_b2': (0.0, 2.0),
     'L0_gnn_c2_g': (1.0, 0.6),
     'L0_gnn_c2_b': (0.0, 0.8),
     'L0_gnn_bn2_g': (1.0, 0.2),
     'L0_gnn_bn2_b': (0.0, 0.609),
     'L0_mix_kln_weight': (1.0, 0.2),
     'L0_mix_kln_bias': (0.0, 0.768),
     'L0_mix_vln_weight': (1.0, 0.2),
     'L0_mix_vln_bias': (0.0, 0.767),
     'L0_ffn_br': (0.0, 0.709),
     'L1_gnn_b_cent': (0.0, 2.0),
     'L1_gnn_b_vor': (0.0, 2.0),
     'L1_gnn_b_sum': (0.0, 0.504),
     'L1_mix_b_out': (0.0, 2.0),
     'L1_ffn_b_gat': (0.0, 2.0),
     'L1_ffn_ln_gamma': (1.0, 0.6),
     'L1_ffn_ln_beta': (0.0, 2.0),
     'L1_ffn_b1': (0.0, 2.0),
     'L1_ffn_b2': (0.0, 2.0)}
    factors = {'node_vec1': 64.0,
     'node_vec1_n2': 64.0,
     'L0_ffn_gamma': 8.0,
     'L0_ffn_beta': 8.0,
     'L0_ffn_Wr': 7.474,
     'L0_ffn_W1': 5.397,
     'L0_ffn_b1': 8.0,
     'L0_ffn_W2': 5.244,
     'L0_ffn_b2': 28.365,
     'L1_gnn_W_cent': 40.56,
     'L1_gnn_W_vor': 41.64,
     'L1_mix_W_qkv': 5.3,
     'L1_mix_W_out': 5.25,
     'L1_ffn_att_src': 64.0,
     'L1_ffn_att_dst': 64.0,
     'L1_gnn_z_in': 5.719,
     'L1_gnn_z_out': 5.784,
     'L1_ffn_W_gat': 8.0,
     'L1_ffn_W1': 8.0,
     'L1_ffn_W2': 8.0}
    for name, (base, spread) in spreads.items():
        noise = np.random.default_rng([zlib.crc32(name.encode()), seed]).standard_normal(out[name].shape)
        drawn = base * np.exp(spread * noise) if base else spread * noise
        out[name] = jnp.asarray(drawn.astype(out[name].dtype))
    for name, factor in factors.items():
        out[name] = (out[name] * factor).astype(out[name].dtype)
    return out
```

```python
from contextlib import ExitStack, contextmanager

import numpy as np
import concourse.bass as bass
from concourse import mybir

F32 = mybir.dt.float32
BF16 = mybir.dt.bfloat16
I32 = mybir.dt.int32
ALU = mybir.AluOpType
ACT = mybir.ActivationFunctionType
AX_X = mybir.AxisListType.X

P = 128
N = 6250
C = 256
NT = 49
NP = NT * P
REAL_T = -(-N // P)
LAST = N - (REAL_T - 1) * P
E = 100000
CE = 784
EP = CE * P
G = 131072
CG = G // P
NHI = 64
PAD_KEY = NHI * P - 1
NS = 832
NSB = 7
NEG = -3.0e38
EPS = 1e-5


def ds(start, n):
    return bass.ds(start, n)


class Kernel:

    def __init__(self, nc, ins, out):
        self.nc, self.ins, self.out = nc, ins, out
        self.buffers = {}
        self.retired = []

    @contextmanager
    def semaphore(self, name):
        if len(self.retired) > 64:
            self.nc.clear_and_free_semaphores(self.retired)
            self.nc.all_engine_barrier()
            self.retired = []
        sem = self.nc.alloc_semaphore(name)
        yield sem
        self.retired.append(sem)

    @staticmethod
    def nth(t, b):
        return t // 2 + 1 if isinstance(t, int) else (t - b) // 2 + 1

    def dram(self, name, shape, dt=F32):
        t = self.nc.dram_tensor(name, shape, dt, kind="Internal").ap()
        self.buffers[name] = t
        return t


def constants(k, ctx):
    nc = k.nc

    def sb(name, shape, dt=F32):
        return ctx.enter_context(nc.sbuf_tensor(name, shape, dt))

    ident = sb("ident", [P, P])
    ones = sb("ones", [P, P])
    before = sb("before", [P, P])
    block_diag = sb("block_diag", [P, P])
    ramp = sb("ramp", [P, P])
    ramp_bf = sb("ramp_bf", [P, P], BF16)
    lane = sb("lane", [P, 1])
    eps = sb("eps", [P, 1])
    lane_i = sb("lane_i", [P, 1], I32)
    ramp_i = sb("ramp_i", [P, P], I32)
    k.ident, k.ones, k.before, k.block_diag, k.ramp, k.ramp_bf, k.lane, k.eps = (
        ident, ones, before, block_diag, ramp, ramp_bf, lane, eps)
    with k.semaphore("const_made") as made, nc.Block() as block:
        @block.gpsimd
        def _(pool):
            nc.gpsimd.memset(ones[:], 1.0).then_inc(made, 1)
            nc.gpsimd.iota(ramp_i[:], [[1, P]], base=0, channel_multiplier=0).then_inc(made, 1)
            nc.gpsimd.iota(lane_i[:], [[1, 1]], base=0, channel_multiplier=1).then_inc(made, 1)
            pool.wait_ge(made, 3)
            nc.gpsimd.affine_select(out=ident[:], in_=ones[:], pattern=[[-1, P]], compare_op=ALU.is_equal,
                                    fill=0.0, base=0, channel_multiplier=1)
            nc.gpsimd.affine_select(out=before[:], in_=ones[:], pattern=[[1, P]], compare_op=ALU.is_gt,
                                    fill=0.0, base=0, channel_multiplier=-1)
            for q in range(4):
                cols = slice(32 * q, 32 * q + 32)
                nc.gpsimd.affine_select(out=block_diag[:, cols], in_=ones[:, cols], pattern=[[0, 32]],
                                        compare_op=ALU.is_ge, fill=0.0, base=-32 * q,
                                        channel_multiplier=1)
            pool.drain()
            for q in range(4):
                cols = slice(32 * q, 32 * q + 32)
                nc.gpsimd.affine_select(out=block_diag[:, cols], in_=block_diag[:, cols],
                                        pattern=[[0, 32]], compare_op=ALU.is_gt, fill=0.0,
                                        base=32 * q + 32, channel_multiplier=-1)

        @block.vector
        def _(dve):
            nc.vector.memset(eps[:], EPS)
            dve.wait_ge(made, 3)
            nc.vector.tensor_copy(ramp[:], ramp_i[:])
            nc.vector.tensor_copy(ramp_bf[:], ramp_i[:])
            nc.vector.tensor_copy(lane[:], lane_i[:])


def edge_keys(k, ctx, tag, chunks, real, inputs, clamp, pad, sort_by):
    nc = k.nc
    per = 7 if chunks == CE else chunks // P
    parts = chunks // per
    width = per * P
    rows_d = k.dram(f"{tag}_rows", (chunks, len(inputs), P))
    low_d = k.dram(f"{tag}_low", (chunks * P,), BF16)
    cols = [ctx.enter_context(nc.sbuf_tensor(f"{tag}_{n}_cols", [P, chunks], F32)) for n, _ in inputs]
    with ExitStack() as c:
        raw = [c.enter_context(nc.sbuf_tensor(f"{tag}_{n}_raw", [P, width], a.dtype)) for n, a in inputs]
        rows = [c.enter_context(nc.sbuf_tensor(f"{tag}_{n}_f", [P, width], F32)) for n, _ in inputs]
        key_i = c.enter_context(nc.sbuf_tensor(f"{tag}_key_i", [P, width], I32))
        low_i = c.enter_context(nc.sbuf_tensor(f"{tag}_low_i", [P, width], I32))
        low = c.enter_context(nc.sbuf_tensor(f"{tag}_low_bf", [P, width], BF16))
        turned = c.enter_context(nc.psum_tensor(f"{tag}_turned", [P, 2, 512], F32))
        low_made = c.enter_context(k.semaphore(f"{tag}_low_made"))
        padded = c.enter_context(k.semaphore(f"{tag}_padded"))
        loaded = c.enter_context(k.semaphore(f"{tag}_loaded"))
        made = c.enter_context(k.semaphore(f"{tag}_made"))
        transposed = c.enter_context(k.semaphore(f"{tag}_transposed"))
        copied = c.enter_context(k.semaphore(f"{tag}_copied"))
        stored = c.enter_context(k.semaphore(f"{tag}_stored"))
        block = c.enter_context(nc.Block())
        full, rest = divmod(real, width)
        n_in = len(inputs)

        @block.sync
        def _(sp):
            n = 0
            sp.wait_ge(padded, n_in)
            for t, (_, a) in zip(raw, inputs):
                sp.dma_start(t[0:full, :], a[0:full * width].rearrange("(p w) -> p w", w=width)
                             ).then_inc(loaded, 16)
                n += 1
                if rest:
                    sp.dma_start(t[full:full + 1, 0:rest],
                                 a[full * width:real].rearrange("(p w) -> p w", p=1)).then_inc(loaded, 16)
                    n += 1
            sp.wait_ge(made, n_in)
            for j in range(n_in):
                sp.dma_start(rows_d[:, j, :].rearrange("(p b) e -> p b e", b=per),
                             rows[j][0:parts].rearrange("p (b e) -> p b e", e=P)).then_inc(stored, 16)
            sp.wait_ge(low_made, 1)
            sp.dma_start(low_d.rearrange("(p w) -> p w", w=width), low[0:parts, :]).then_inc(stored, 16)
            sp.wait_ge(stored, 16 * (n_in + 1))

        @block.vector
        def _(dve):
            for t, v in zip(raw, pad):
                nc.vector.memset(t[:], v).then_inc(padded, 1)
            dve.wait_ge(loaded, 16 * n_in * (2 if rest else 1))
            for j in range(n_in):
                if clamp[j] is None:
                    nc.vector.tensor_copy(rows[j][:], raw[j][:]).then_inc(made, 1)
                else:
                    nc.vector.tensor_scalar(rows[j][:], raw[j][:], float(clamp[j]), None,
                                            ALU.min).then_inc(made, 1)
            dve.drain()
            nc.vector.tensor_copy(key_i[:], rows[sort_by][:])
            dve.drain()
            nc.vector.tensor_scalar(low_i[:], key_i[:], 127, None, ALU.bitwise_and)
            dve.drain()
            nc.vector.tensor_copy(low[:], low_i[:]).then_inc(low_made, 1)
            for n in range(n_in * per):
                j, b = divmod(n, per)
                dve.wait_ge(transposed, n + 1)
                nc.vector.tensor_copy(cols[j][:].rearrange("e (p b) -> e b p", b=per)[:, b, :],
                                      turned[:, n % 2, 0:parts]).then_inc(copied, 1)

        @block.tensor
        def _(pe):
            pe.wait_ge(made, n_in)
            for n in range(n_in * per):
                j, b = divmod(n, per)
                if n >= 2:
                    pe.wait_ge(copied, n - 1)
                nc.tensor.transpose(turned[:, n % 2, 0:parts], rows[j][0:parts, b * P:(b + 1) * P],
                                    k.ident[0:parts, 0:parts]).then_inc(transposed, 1)
    return rows_d, low_d, cols


def digits(k, ctx, tag, key, chunks):
    nc = k.nc
    lo = ctx.enter_context(nc.sbuf_tensor(f"{tag}_lo", [P, chunks], BF16))
    hi = ctx.enter_context(nc.sbuf_tensor(f"{tag}_hi", [P, chunks], BF16))
    with (nc.sbuf_tensor(f"{tag}_ki", [P, chunks], I32) as ki,
          nc.sbuf_tensor(f"{tag}_di", [P, chunks], I32) as di,
          nc.Block() as block):
        @block.vector
        def _(dve):
            nc.vector.tensor_copy(ki[:], key[:])
            dve.drain()
            nc.vector.tensor_scalar(di[:], ki[:], 7, None, ALU.logical_shift_right)
            dve.drain()
            nc.vector.tensor_copy(hi[:], di[:])
            dve.drain()
            nc.vector.tensor_scalar(di[:], ki[:], 127, None, ALU.bitwise_and)
            dve.drain()
            nc.vector.tensor_copy(lo[:], di[:])
    return lo, hi


def histogram(k, tag, lo, hi, chunks, count):
    nc = k.nc
    B = 8
    batches = chunks // B
    with ExitStack() as c:
        one_lo = [c.enter_context(nc.sbuf_tensor(f"{tag}_one_lo{b}", [P, B, P], BF16)) for b in (0, 1)]
        one_hi = [c.enter_context(nc.sbuf_tensor(f"{tag}_one_hi{b}", [P, B, NHI], BF16)) for b in (0, 1)]
        zero = c.enter_context(nc.sbuf_tensor(f"{tag}_zero", [P, P], BF16))
        total = c.enter_context(nc.psum_tensor(f"{tag}_total", [P, NHI], F32))
        made = c.enter_context(k.semaphore(f"{tag}_h_made"))
        used = c.enter_context(k.semaphore(f"{tag}_h_used"))
        summed = c.enter_context(k.semaphore(f"{tag}_h_summed"))
        zeroed = c.enter_context(k.semaphore(f"{tag}_h_zeroed"))
        block = c.enter_context(nc.Block())

        @block.vector
        def _(dve):
            nc.vector.memset(zero[:], 0.0).then_inc(zeroed, 1)
            dve.sem_inc(used, 2)
            with dve.Fori(0, batches // 2) as i:
                for b in (0, 1):
                    dve.wait_ge(used, 2 * i + b + 1)
                    at = ds((2 * i + b) * B, B)
                    nc.vector.tensor_tensor(one_lo[b][:], k.ramp_bf[:].unsqueeze(1).broadcast_to([P, B, P]),
                                            lo[:, at].unsqueeze(2).broadcast_to([P, B, P]), ALU.is_equal)
                    nc.vector.tensor_tensor(one_hi[b][:], k.ramp_bf[:, 0:NHI].unsqueeze(1).broadcast_to([P, B, NHI]),
                                            hi[:, at].unsqueeze(2).broadcast_to([P, B, NHI]), ALU.is_equal)
                    dve.drain().then_inc(made, 1)
            dve.wait_ge(summed, 1)
            nc.vector.tensor_copy(count[:], total[:])

        @block.tensor
        def _(pe):
            pe.wait_ge(zeroed, 1)
            nc.tensor.matmul(total[:], zero[:], zero[:, 0:NHI], start=True, stop=False,
                             skip_group_check=True)
            with pe.Fori(0, batches // 2) as i:
                for b in (0, 1):
                    pe.wait_ge(made, 2 * i + b + 1)
                    for j in range(B):
                        mm = nc.tensor.matmul(total[:], one_lo[b][:, j, :], one_hi[b][:, j, :],
                                              start=False, stop=False, skip_group_check=True)
                    mm.then_inc(used, 1)
            nc.tensor.matmul(total[:], zero[:], zero[:, 0:NHI], start=False, stop=True,
                             skip_group_check=True).then_inc(summed, 1)


def prefix(k, tag, count, start, tile_start):
    nc = k.nc
    with ExitStack() as c:
        per_hi = c.enter_context(nc.psum_tensor(f"{tag}_per_hi", [P, NHI], F32))
        within = c.enter_context(nc.psum_tensor(f"{tag}_within", [P, NHI], F32))
        total = c.enter_context(nc.sbuf_tensor(f"{tag}_total_sb", [P, NHI], F32))
        upto = c.enter_context(nc.sbuf_tensor(f"{tag}_upto", [P, NHI], F32))
        summed = c.enter_context(k.semaphore(f"{tag}_p_summed"))
        block = c.enter_context(nc.Block())

        @block.tensor
        def _(pe):
            nc.tensor.matmul(per_hi[:], k.ones[:], count[:], start=True, stop=True)
            nc.tensor.matmul(within[:], k.before[:], count[:], start=True, stop=True).then_inc(summed, 1)

        @block.vector
        def _(dve):
            dve.wait_ge(summed, 1)
            nc.vector.tensor_copy(total[:], per_hi[:])
            dve.drain()
            nc.vector.tensor_tensor_scan(upto[:], k.ones[:, 0:NHI], total[:], 0.0, ALU.mult, ALU.add)
            dve.drain()
            nc.vector.tensor_tensor(tile_start[:], upto[:], total[:], ALU.subtract)
            dve.drain()
            nc.vector.tensor_tensor(start[:], tile_start[:], within[:], ALU.add)


def schedule(k, ctx, tag, tile_start):
    nc = k.nc
    step_tile = ctx.enter_context(nc.sbuf_tensor(f"{tag}_step_tile", [P, NSB], F32))
    step_chunk = ctx.enter_context(nc.sbuf_tensor(f"{tag}_step_chunk", [P, NSB], F32))
    T1 = REAL_T - 1
    with (nc.sbuf_tensor(f"{tag}_qi", [P, NHI], I32) as qi,
          nc.sbuf_tensor(f"{tag}_enter", [P, NHI], F32) as enter,
          nc.sbuf_tensor(f"{tag}_cmp", [P, NHI], F32) as cmp,
          nc.sbuf_tensor(f"{tag}_s", [P, NSB], F32) as s,
          nc.Block() as block):
        @block.vector
        def _(dve):
            nc.vector.tensor_copy(qi[:], tile_start[:])
            for b in range(NSB):
                nc.vector.tensor_scalar(s[:, b:b + 1], k.lane[:], float(b * P), None, ALU.add)
            dve.drain()
            nc.vector.tensor_scalar(qi[:], qi[:], 7, None, ALU.logical_shift_right)
            dve.drain()
            nc.vector.tensor_tensor(enter[:], qi[:], k.ramp[:, 0:NHI], ALU.add)
            dve.drain()
            for b in range(NSB):
                nc.vector.tensor_scalar(cmp[:, 0:T1], enter[:, 1:1 + T1], s[:, b:b + 1], 0.0, ALU.is_le,
                                        ALU.add, accum_out=step_tile[:, b:b + 1])
                dve.drain()
            nc.vector.tensor_tensor(step_chunk[:], s[:], step_tile[:], ALU.subtract)
            dve.drain()
            nc.vector.tensor_scalar(step_chunk[:], step_chunk[:], float(CE - 1), None, ALU.min)
    return step_tile, step_chunk


def step_columns(k, tag, rows_d, step_tile, step_chunk, src_i, rel, weight):
    nc = k.nc
    table = rows_d.rearrange("c j e -> c (j e)")
    with ExitStack() as c:
        got = [c.enter_context(nc.sbuf_tensor(f"{tag}_got{b}", [P, 3 * P], F32)) for b in range(NSB)]
        chunk_i = c.enter_context(nc.sbuf_tensor(f"{tag}_chunk_i", [P, NSB], I32))
        first = c.enter_context(nc.sbuf_tensor(f"{tag}_first", [P, NSB], F32))
        turned = c.enter_context(nc.psum_tensor(f"{tag}_turned2", [P, 2, 4, P], F32))
        index_made = c.enter_context(k.semaphore(f"{tag}_index_made"))
        gathered = [c.enter_context(k.semaphore(f"{tag}_gathered{b}")) for b in range(NSB)]
        made = c.enter_context(k.semaphore(f"{tag}_rel_made"))
        transposed = c.enter_context(k.semaphore(f"{tag}_transposed2"))
        copied = c.enter_context(k.semaphore(f"{tag}_copied2"))
        block = c.enter_context(nc.Block())

        @block.gpsimd
        def _(pool):
            pool.wait_ge(index_made, 1)
            for b in range(NSB):
                nc.gpsimd.indirect_dma_start(got[b][:], None, table, bass.IndirectOffsetOnAxis(
                    ap=chunk_i[:, b:b + 1], axis=0)).then_inc(gathered[b], 16)

        @block.vector
        def _(dve):
            nc.vector.tensor_copy(chunk_i[:], step_chunk[:]).then_inc(index_made, 1)
            nc.vector.tensor_scalar(first[:], step_tile[:], float(P), None, ALU.mult)
            dve.drain()
            for b in range(NSB):
                dve.wait_ge(gathered[b], 16)
                nc.vector.tensor_scalar(got[b][:, P:2 * P], got[b][:, P:2 * P], first[:, b:b + 1], None,
                                        ALU.subtract)
                nc.vector.tensor_scalar(got[b][:, 0:P], got[b][:, 0:P], float(N - 1), None, ALU.min)
                dve.drain().then_inc(made, 1)
            for b in range(NSB):
                dve.wait_ge(transposed, b + 1)
                at = slice(b * P, (b + 1) * P)
                nc.vector.tensor_copy(src_i[:, at], turned[:, b % 2, 0, :])
                nc.vector.tensor_copy(rel[:, at], turned[:, b % 2, 1, :])
                nc.vector.tensor_copy(weight[:, at], turned[:, b % 2, 2, :])
                dve.drain().then_inc(copied, 1)

        @block.tensor
        def _(pe):
            for b in range(NSB):
                pe.wait_ge(made, b + 1)
                if b >= 2:
                    pe.wait_ge(copied, b - 1)
                for j in range(3):
                    mm = nc.tensor.transpose(turned[:, b % 2, j, :], got[b][:, j * P:(j + 1) * P], k.ident[:])
                mm.then_inc(transposed, 1)


def step_registers(k, tag, values, row):
    nc = k.nc
    row_d = k.dram(f"{tag}_row_d", (NSB * P,), I32)
    with ExitStack() as c:
        as_int = c.enter_context(nc.sbuf_tensor(f"{tag}_as_int", [P, NSB], I32))
        made = c.enter_context(k.semaphore(f"{tag}_made"))
        moved = c.enter_context(k.semaphore(f"{tag}_moved"))
        block = c.enter_context(nc.Block())

        @block.vector
        def _(dve):
            nc.vector.tensor_copy(as_int[:], values[:]).then_inc(made, 1)

        @block.sync
        def _(sp):
            sp.wait_ge(made, 1)
            for b in range(NSB):
                sp.dma_start(row_d[b * P:(b + 1) * P].rearrange("(p b) -> p b", b=1),
                             as_int[:, b:b + 1]).then_inc(moved, 16)
            sp.wait_ge(moved, 16 * NSB)
            sp.dma_start(row[:], row_d.rearrange("(a s) -> a s", a=1)).then_inc(moved, 16)
            sp.wait_ge(moved, 16 * (NSB + 1))


def aggregate(k, tag, table, src_i, rel, weight, tile_row, acc):
    nc = k.nc
    R = 8
    with ExitStack() as c:
        def sb(name, shape, dt=F32):
            return c.enter_context(nc.sbuf_tensor(f"{tag}_{name}", shape, dt))

        def sem(name):
            return c.enter_context(k.semaphore(f"{tag}_{name}"))

        idx = [sb(f"idx{h}", [P, R], I32) for h in (0, 1)]
        msg = [sb(f"msg{b}", [P, C]) for b in range(2 * R)]
        pick = [sb(f"pick{b}", [P, P]) for b in range(4)]
        part = [c.enter_context(nc.psum_tensor(f"{tag}_part{b}", [P, 4, P], F32)) for b in range(4)]
        idx_ready, pick_ready = sem("idx_ready"), sem("pick_ready")
        zeroed = sem("zeroed")
        gathered = [sem(f"gathered{b}") for b in range(2 * R)]
        turn = sem("turn")
        summed, added = sem("summed"), sem("added")
        block = c.enter_context(nc.Block())

        @block.gpsimd
        def _(pool):
            pool.sem_inc(summed, 2 * R)
            with pool.Fori(0, NS // (2 * R)) as i:
                for h in (0, 1):
                    half = 2 * i + h
                    pool.wait_ge(summed, (half + 1) * R)
                    pool.sem_inc(turn, 1)
                    nc.gpsimd.tensor_copy(idx[h][:], src_i[:, ds(half * R, R)]).then_inc(idx_ready, 1)
                    pool.wait_ge(idx_ready, half + 1)
                    pool.sem_inc(turn, 1)
                    for b in range(R):
                        nc.gpsimd.indirect_dma_start(msg[h * R + b][:], None, table, bass.IndirectOffsetOnAxis(
                            ap=idx[h][:, b:b + 1], axis=0)).then_inc(gathered[h * R + b], 16)

        @block.vector
        def _(dve):
            nc.vector.memset(acc[:], 0.0)
            dve.drain()
            regs = [dve.alloc_register(f"{tag}_tile{b}") for b in range(4)]
            with dve.Fori(0, NS // (2 * R)) as i:
                for g in range(4):
                    dve.reg_load(regs, tile_row[0:1, ds(i * (2 * R) + 4 * g, 4)])
                    tiles = [dve.snap(r, min_val=0, max_val=REAL_T - 1) for r in regs]
                    for b in range(4):
                        s = i * (2 * R) + 4 * g + b
                        nc.vector.tensor_scalar(pick[b][:], k.ramp[:], rel[:, ds(s, 1)],
                                                weight[:, ds(s, 1)], ALU.is_equal, ALU.mult
                                                ).then_inc(pick_ready, 1)
                    for b in range(4):
                        s = i * (2 * R) + 4 * g + b
                        dve.wait_ge(summed, s + 1 + 2 * R)
                        at = ds(tiles[b] * P, P)
                        nc.vector.tensor_tensor(acc[:, :, at], acc[:, :, at], part[b][:, 0:2, :], ALU.add)
                        dve.drain().then_inc(added, 1)

        @block.tensor
        def _(pe):
            pe.sem_inc(added, 4)
            with pe.Fori(0, NS // (2 * R)) as i:
                for h in (0, 1):
                    for b in range(R):
                        s = (2 * i + h) * R + b
                        pe.wait_ge(gathered[h * R + b], i * 16 + 16)
                        pe.wait_ge(pick_ready, s + 1)
                        pe.wait_ge(added, s + 1)
                        for half in (0, 1):
                            mm = nc.tensor.matmul(part[b % 4][:, half, :], msg[h * R + b][:, half * P:(half + 1) * P],
                                                  pick[b % 4][:], start=True, stop=True)
                        mm.then_inc(summed, 1)


def sort_edges(k, ctx, tag, chunks, key, lo, hi, start, key_rows, low_d, payload, width, fill, out_d):
    nc = k.nc
    Q = 8
    n_iter = chunks // (2 * Q)
    with ExitStack() as c:
        def sb(name, shape, dt=F32):
            return c.enter_context(nc.sbuf_tensor(f"{tag}_{name}", shape, dt))

        def sem(name):
            return c.enter_context(k.semaphore(f"{tag}_{name}"))

        key_row = [sb(f"key_row{q}", [P, Q * P]) for q in (0, 1)]
        low_row = [sb(f"low_row{q}", [P, Q * P], BF16) for q in (0, 1)]
        pay = [sb(f"pay{q}", [P, Q, width]) for q in (0, 1)]
        pos = [sb(f"pos{q}", [P, Q], I32) for q in (0, 1)]
        base = [sb(f"base{q}", [P, Q]) for q in (0, 1)]
        same = [sb(f"same{q}", [P, Q]) for q in (0, 1)]
        hi_f = sb("hi_f", [P, chunks])
        lowT = [sb(f"lowT{b}", [P, 2 * P]) for b in (0, 1)]
        one_lo = [sb(f"s_one_lo{b}", [P, 2, P], BF16) for b in (0, 1)]
        one_hi = [sb(f"s_one_hi{b}", [P, 2, NHI], BF16) for b in (0, 1)]
        junk_hi = sb("junk_hi", [P, NHI])
        junk_row = sb("junk_row", [P, 2 * P])
        earlier = sb("earlier", [P, 2, 2 * P])
        counts_sb = [sb(f"counts_sb{b}", [P, NHI]) for b in (0, 1)]
        counts = c.enter_context(nc.psum_tensor(f"{tag}_counts", [P, 512], F32))
        found = [c.enter_context(nc.psum_tensor(f"{tag}_found{b}", [P, 8, NHI], F32)) for b in (0, 1)]
        rows_in = [sem(f"rows_in{q}") for q in (0, 1)]
        pay_in = [sem(f"pay_in{q}") for q in (0, 1)]
        hot_ready, hot_used = sem("hot_ready"), sem("hot_used")
        count_ready, count_copied, found_ready = sem("count_ready"), sem("count_copied"), sem("found_ready")
        found_read, pos_ready, rows_used = sem("found_read"), sem("pos_ready"), sem("rows_used")
        turn, pay_free = sem("turn"), sem("pay_free")
        scattered = [sem(f"scattered{q}") for q in (0, 1)]
        mask_made = sem("mask_made")
        block = c.enter_context(nc.Block())

        @block.sync
        def _(sp):
            def quad(i, q, last):
                n = 2 * i + q
                sp.dma_start(key_row[q][:].rearrange("p (b e) -> p b e", e=P),
                             key_rows[ds(n * Q, Q), :].unsqueeze(0).broadcast_to([P, Q, P])
                             ).then_inc(rows_in[q], 16)
                sp.dma_start(low_row[q][:], low_d[ds(n * Q * P, Q * P)].unsqueeze(0)
                             .broadcast_to([P, Q * P])).then_inc(rows_in[q], 16)
                if fill:
                    fill(sp, pay[q], n, last, pay_in[q], turn)

            def next_quad(i, q, last):
                sp.wait_ge(scattered[q], (i + 1) * 16 * Q)
                sp.sem_inc(pay_free, 1)
                sp.wait_ge(rows_used, 2 * i + q + 1)
                quad(i + 1, q, last)

            for q in (0, 1):
                quad(0, q, False)
            with sp.Fori(0, n_iter - 2) as i:
                for q in (0, 1):
                    next_quad(i, q, False)
            for q in (0, 1):
                next_quad(n_iter - 2, q, True)
            for q in (0, 1):
                sp.wait_ge(scattered[q], 16 * Q * n_iter)

        @block.gpsimd
        def _(pool):
            nc.gpsimd.memset(earlier[:], 1.0).then_inc(mask_made, 1)
            pool.wait_ge(mask_made, 1)
            nc.gpsimd.affine_select(out=earlier[:], in_=earlier[:], pattern=[[P, 2], [-1, 2 * P]],
                                    compare_op=ALU.is_gt, fill=0.0, base=0,
                                    channel_multiplier=1).then_inc(mask_made, 1)
            with pool.Fori(0, n_iter) as i:
                for q in (0, 1):
                    pool.wait_ge(pos_ready, 2 * i + q + 1)
                    pool.sem_inc(turn, 1)
                    if fill:
                        pool.wait_ge(pay_in[q], 16 * i + 16)
                        pool.sem_inc(turn, 1)
                    for b in range(Q):
                        nc.gpsimd.indirect_dma_start(out_d, bass.IndirectOffsetOnAxis(
                            ap=pos[q][:, b:b + 1], axis=0), pay[q][:, b, :], None).then_inc(scattered[q], 16)

        @block.vector
        def _(dve):
            nc.vector.tensor_copy(hi_f[:], hi[:])
            dve.wait_ge(mask_made, 2)
            dve.drain()
            dve.sem_inc(hot_used, 2)
            dve.sem_inc(pay_free, 2)
            with dve.Fori(0, n_iter) as i:
                def one_hots(q, g):
                    n = (2 * i + q) * 4 + g
                    at = ds(n * 2, 2)
                    b = g % 2
                    dve.wait_ge(hot_used, n + 1)
                    nc.vector.tensor_scalar(lowT[b][:], low_row[q][:, g * 2 * P:(g + 1) * 2 * P],
                                            k.lane[:, 0:1], None, ALU.is_equal)
                    nc.vector.tensor_tensor(one_lo[b][:], k.ramp_bf[:].unsqueeze(1).broadcast_to([P, 2, P]),
                                            lo[:, at].unsqueeze(2).broadcast_to([P, 2, P]), ALU.is_equal)
                    nc.vector.tensor_tensor(one_hi[b][:], k.ramp_bf[:, 0:NHI].unsqueeze(1).broadcast_to([P, 2, NHI]),
                                            hi[:, at].unsqueeze(2).broadcast_to([P, 2, NHI]), ALU.is_equal)
                    dve.drain().then_inc(hot_ready, 1)

                def ranks(q, g):
                    n = (2 * i + q) * 4 + g
                    dve.wait_ge(found_ready, n + 1)
                    for j in (0, 1):
                        ch = (2 * i + q) * Q + 2 * g + j
                        col = 2 * g + j
                        nc.vector.scalar_tensor_tensor(junk_hi[:], k.ramp[:, 0:NHI], hi_f[:, ds(ch, 1)],
                                                       found[g % 2][:, j, :], ALU.is_equal, ALU.mult,
                                                       accum_out=base[q][:, col:col + 1])
                        w = (j + 1) * P
                        nc.vector.scalar_tensor_tensor(junk_row[:, 0:w], key_row[q][:, g * 2 * P:g * 2 * P + w],
                                                       key[:, ds(ch, 1)], earlier[:, j, 0:w],
                                                       ALU.is_equal, ALU.mult,
                                                       accum_out=same[q][:, col:col + 1])
                        dve.drain()
                    dve.sem_inc(found_read, 1)

                for q in (0, 1):
                    dve.wait_ge(rows_in[q], 32 * i + 32)
                    one_hots(q, 0)
                    for g in range(4):
                        if g < 3:
                            one_hots(q, g + 1)
                        ranks(q, g)
                    dve.sem_inc(rows_used, 1)
                    dve.wait_ge(pay_free, 2 * i + q + 1)
                    nc.vector.tensor_tensor(pos[q][:], base[q][:], same[q][:], ALU.add)
                    for cols, tile in payload:
                        nc.vector.tensor_copy(pay[q][:, :, cols], tile[:, ds((2 * i + q) * Q, Q)])
                    dve.drain().then_inc(pos_ready, 1)

        @block.scalar
        def _(act):
            with act.Fori(0, n_iter) as i:
                for g in range(8):
                    n = 8 * i + g
                    act.wait_ge(count_ready, n + 1)
                    nc.scalar.copy(counts_sb[g % 2][:], counts[:, 0:NHI]).then_inc(count_copied, 1)

        @block.tensor
        def _(pe):
            pe.sem_inc(found_read, 2)
            nc.tensor.matmul(counts[:, 0:NHI], k.ident[:], start[:], start=True, stop=False,
                             skip_group_check=True).then_inc(count_ready, 1)
            with pe.Fori(0, n_iter) as i:
                for g in range(8):
                    n = 8 * i + g
                    b = g % 2
                    pe.wait_ge(hot_ready, n + 1)
                    pe.wait_ge(count_copied, n + 1)
                    pe.wait_ge(found_read, n + 1)
                    for j in (0, 1):
                        mm = nc.tensor.matmul(found[b][:, j, :], lowT[b][:, j * P:(j + 1) * P],
                                              counts_sb[b][:], start=True, stop=True)
                    mm.then_inc(found_ready, 1)
                    for j in (0, 1):
                        mm = nc.tensor.matmul(counts[:, 0:NHI], one_lo[b][:, j, :], one_hi[b][:, j, :],
                                              start=False, stop=False, skip_group_check=True)
                    mm.then_inc(count_ready, 1)
                    pe.drain().then_inc(hot_used, 1)
            nc.tensor.matmul(counts[:, 0:NHI], one_lo[0][:, 0, :], one_hi[0][:, 0, :], start=False,
                             stop=True, skip_group_check=True)
    return out_d


def segment_sum(k, tag, sorted_d, width, chunk_row, first_all, tile_row, acc):
    nc = k.nc
    R = 8
    with ExitStack() as c:
        def sb(name, shape, dt=F32):
            return c.enter_context(nc.sbuf_tensor(f"{tag}_{name}", shape, dt))

        def sem(name):
            return c.enter_context(k.semaphore(f"{tag}_{name}"))

        rows = [sb(f"rows{b}", [P, width + 1]) for b in range(R)]
        pick = [sb(f"pick{b}", [P, P]) for b in range(4)]
        part = [c.enter_context(nc.psum_tensor(f"{tag}_part{b}", [P, 512], F32)) for b in range(4)]
        loaded = [sem(f"loaded{b}") for b in range(R)]
        pick_ready, summed, added = sem("pick_ready"), sem("summed"), sem("added")
        block = c.enter_context(nc.Block())

        @block.sync
        def _(sp):
            sp.sem_inc(summed, R)
            regs = [sp.alloc_register(f"{tag}_chunk{b}") for b in range(R)]
            with sp.Fori(0, NS // R) as i:
                sp.reg_load(regs, chunk_row[0:1, ds(i * R, R)])
                for b in range(R):
                    chunk = sp.snap(regs[b], min_val=0, max_val=CE - 1)
                    sp.wait_ge(summed, i * R + b + 1)
                    sp.dma_start(rows[b][:], sorted_d[ds(chunk * P, P), :]).then_inc(loaded[b], 16)

        @block.vector
        def _(dve):
            nc.vector.memset(acc[:], 0.0)
            dve.drain()
            regs = [dve.alloc_register(f"{tag}_tile{b}") for b in range(4)]
            with dve.Fori(0, NS // R) as i:
                for g in (0, 1):
                    dve.reg_load(regs, tile_row[0:1, ds(i * R + 4 * g, 4)])
                    tiles = [dve.snap(r, min_val=0, max_val=REAL_T - 1) for r in regs]
                    for b in range(4):
                        s = i * R + 4 * g + b
                        dve.wait_ge(loaded[4 * g + b], i * 16 + 16)
                        nc.vector.tensor_scalar(pick[b][:], k.ramp[:], first_all[:, ds(s, 1)],
                                                rows[4 * g + b][:, width:width + 1], ALU.add,
                                                ALU.is_equal).then_inc(pick_ready, 1)
                    for b in range(4):
                        s = i * R + 4 * g + b
                        dve.wait_ge(summed, s + 1 + R)
                        at = ds(tiles[b] * P, P)
                        nc.vector.tensor_tensor(acc[:, at], acc[:, at], part[b][:, 0:P], ALU.add)
                        dve.drain().then_inc(added, 1)

        @block.tensor
        def _(pe):
            pe.sem_inc(added, 4)
            with pe.Fori(0, NS // R) as i:
                for b in range(R):
                    pe.wait_ge(pick_ready, i * R + b + 1)
                    pe.wait_ge(loaded[b], i * 16 + 16)
                    pe.wait_ge(added, i * R + b + 1)
                    nc.tensor.matmul(part[b % 4][:, 0:P], rows[b][:, 0:width], pick[b % 4][:],
                                     start=True, stop=True).then_inc(summed, 1)


def over_tiles(eng, body):
    with eng.Fori(0, (REAL_T - 1) // 2) as i:
        for b in (0, 1):
            body(2 * i + b, b, P)
    body(REAL_T - 1, 0, LAST)


def layer_norm(k, dve, x, out, st, rows, asked, answered, nth):
    nc = k.nc
    nc.vector.bn_stats(st[0:rows, 0:6], x)
    dve.drain()
    nc.vector.bn_aggr(st[0:rows, 6:8], st[0:rows, 0:6]).then_inc(asked, 1)
    dve.wait_ge(answered, nth)
    nc.vector.reciprocal(st[0:rows, 9:10], st[0:rows, 8:9])
    dve.drain()
    nc.vector.tensor_scalar(out, x, st[0:rows, 6:7], st[0:rows, 9:10], ALU.subtract, ALU.mult)
    dve.drain()


def root(k, act, st, rows, asked, answered, nth):
    act.wait_ge(asked, nth)
    k.nc.scalar.activation(st[0:rows, 8:9], st[0:rows, 7:8], ACT.Sqrt,
                           bias=k.eps[0:rows, 0:1]).then_inc(answered, 1)


def load_params(k, ctx, tag, loads):
    nc = k.nc
    tiles = [ctx.enter_context(nc.sbuf_tensor(f"{tag}_{name}", shape, F32)) for name, shape, _ in loads]
    with k.semaphore(f"{tag}_params_in") as loaded, nc.Block() as block:
        @block.sync
        def _(sp):
            for t, (_, _, source) in zip(tiles, loads):
                sp.dma_start(t[:], source, allow_slow_non_contiguous=True).then_inc(loaded, 16)
            sp.wait_ge(loaded, 16 * len(loads))
    return tiles


def row_on_all(v):
    return v.unsqueeze(0).broadcast_to([P, v.shape[0]])


def halves(w):
    return w.rearrange("(h p) m -> p h m", p=P)


def halves_col(v):
    return v.rearrange("(h p) -> p h", p=P)


def input_stage(k, ctx, tag, h_d, kv):
    nc, I = k.nc, k.ins
    with ExitStack() as c:
        def sb(name, shape, dt=F32):
            return c.enter_context(nc.sbuf_tensor(f"{tag}_{name}", shape, dt))

        def sem(name):
            return c.enter_context(k.semaphore(f"{tag}_{name}"))

        def flat(w):
            return row_on_all(w.rearrange("h a d -> (h a d)"))

        w1, b1, kw, kb, vw, vb = load_params(k, c, tag, [
            ("w1", [P, 2, C], halves(I["L0_gnn_c1_w1"])), ("b1", [1, C], I["L0_gnn_c1_b1"].unsqueeze(0)),
            ("kw", [P, C], flat(I["L0_mix_kln_weight"])), ("kb", [P, C], flat(I["L0_mix_kln_bias"])),
            ("vw", [P, C], flat(I["L0_mix_vln_weight"])), ("vb", [P, C], flat(I["L0_mix_vln_bias"]))])
        x = [sb(f"x{b}", [P, C]) for b in (0, 1)]
        xn = [sb(f"xn{b}", [P, C]) for b in (0, 1)]
        xnT = [sb(f"xnT{b}", [P, 2, P]) for b in (0, 1)]
        h = [sb(f"h{b}", [P, C]) for b in (0, 1)]
        z = [sb(f"z{b}", [P, C]) for b in (0, 1)]
        kk = [sb(f"kk{b}", [P, C]) for b in (0, 1)]
        vv = [sb(f"vv{b}", [P, C]) for b in (0, 1)]
        sq, st, hs = sb("sq", [P, C]), sb("st", [P, 16]), sb("hs", [P, 4, 8])
        zero = sb("zero", [P, P])
        turned = [c.enter_context(nc.psum_tensor(f"{tag}_turned{b}", [P, 4, P], F32)) for b in (0, 1)]
        hp = [c.enter_context(nc.psum_tensor(f"{tag}_hp{b}", [P, 512], F32)) for b in (0, 1)]
        kvp = c.enter_context(nc.psum_tensor(f"{tag}_kvp", [P, 4, P], F32))
        x_in = [sem("x_in0"), sem("x_in1")]
        x_used, xn_ready, xn_used, z_ready, kv_ready, kv_used = map(
            sem, ("x_used", "xn_ready", "xn_used", "z_ready", "kv_ready", "kv_used"))
        turned_ready, xnT_ready, hp_ready, h_ready, pool_step, zeroed, kv_summed = map(
            sem, ("turned_ready", "xnT_ready", "hp_ready", "h_ready", "pool_step", "zeroed", "kv_summed"))
        h_out = [sem("h_out0"), sem("h_out1")]
        h_free, asked, answered = sem("h_free"), sem("asked"), sem("answered")
        block = c.enter_context(nc.Block())

        @block.sync
        def _(sp):
            sp.sem_inc(x_used, 2)

            def load(t, b, rows):
                sp.wait_ge(x_used, t + 1)
                sp.dma_start(x[b][0:rows, :], I["x"][ds(t * P, rows), :]).then_inc(x_in[b], 16)
            over_tiles(sp, load)

        @block.vector
        def _(dve):
            nc.vector.memset(zero[:], 0.0).then_inc(zeroed, 1)
            dve.sem_inc(xn_used, 2)
            dve.sem_inc(kv_ready, 2)

            def tile(t, b, r):
                dve.wait_ge(x_in[b], k.nth(t, b) * 16)
                dve.wait_ge(xn_used, t + 1)
                layer_norm(k, dve, x[b][0:r, :], xn[b][0:r, :], st, r, asked, answered, 2 * t + 1)
                dve.sem_inc(x_used, 1)
                dve.drain().then_inc(xn_ready, 1)
                by_head = xn[b][0:r].rearrange("p (h d) -> p h d", d=32)
                sqh = sq[0:r].rearrange("p (h d) -> p h d", d=32)
                nc.vector.tensor_reduce(hs[0:r, 0, :], by_head, AX_X, ALU.add)
                dve.drain()
                nc.vector.tensor_scalar(hs[0:r, 0, :], hs[0:r, 0, :], 1.0 / 32, None, ALU.mult)
                dve.drain()
                dve.wait_ge(kv_ready, t + 1)
                zh = z[b][0:r].rearrange("p (h d) -> p h d", d=32)
                nc.vector.tensor_tensor(zh, by_head, hs[0:r, 0, :].unsqueeze(2).broadcast_to([r, 8, 32]),
                                        ALU.subtract)
                dve.drain()
                nc.vector.tensor_tensor(sqh, zh, zh, ALU.mult)
                dve.drain()
                nc.vector.tensor_reduce(hs[0:r, 1, :], sqh, AX_X, ALU.add).then_inc(asked, 1)
                dve.wait_ge(answered, 2 * t + 2)
                nc.vector.tensor_scalar(hs[0:r, 2, :], hs[0:r, 2, :], EPS, None, ALU.add)
                dve.drain()
                nc.vector.reciprocal(hs[0:r, 3, :], hs[0:r, 2, :])
                dve.drain()
                nc.vector.tensor_tensor(zh, zh, hs[0:r, 3, :].unsqueeze(2).broadcast_to([r, 8, 32]), ALU.mult)
                dve.drain().then_inc(z_ready, 1)
            over_tiles(dve, tile)
            dve.wait_ge(kv_summed, 1)
            for half in (0, 1):
                nc.vector.scalar_tensor_tensor(kv[:, half, :], kvp[:, half, :], 1.0 / N, k.block_diag[:],
                                               ALU.mult, ALU.mult)

        @block.gpsimd
        def _(pool):
            pool.sem_inc(kv_used, 2)

            def tile(t, b, r):
                pool.wait_ge(z_ready, t + 1)
                pool.sem_inc(pool_step, 1)
                pool.wait_ge(kv_used, t + 1)
                pool.sem_inc(pool_step, 1)
                nc.gpsimd.tensor_tensor(kk[b][0:r], z[b][0:r], kw[0:r], ALU.mult)
                nc.gpsimd.tensor_tensor(vv[b][0:r], z[b][0:r], vw[0:r], ALU.mult)
                pool.drain()
                nc.gpsimd.tensor_tensor(kk[b][0:r], kk[b][0:r], kb[0:r], ALU.add)
                nc.gpsimd.tensor_tensor(vv[b][0:r], vv[b][0:r], vb[0:r], ALU.add)
                pool.drain().then_inc(kv_ready, 1)
            over_tiles(pool, tile)

        @block.tensor
        def _(pe):
            pe.wait_ge(zeroed, 1)
            for half in (0, 1):
                nc.tensor.matmul(kvp[:, half, :], zero[:], zero[:], start=half == 0, stop=False, skip_group_check=True)

            def tile(t, b, r):
                pe.wait_ge(xn_ready, t + 1)
                for half in (0, 1):
                    mm = nc.tensor.transpose(turned[b][:, half, 0:r], xn[b][0:r, half * P:(half + 1) * P],
                                             k.ident[0:r, 0:r])
                mm.then_inc(turned_ready, 1)
                pe.wait_ge(xnT_ready, t + 1)
                nc.tensor.matmul(hp[b][0:r, 0:C], k.ones[0:1, 0:r], b1[:], start=True, stop=False)
                for half in (0, 1):
                    mm = nc.tensor.matmul(hp[b][0:r, 0:C], xnT[b][:, half, 0:r], w1[:, half, :],
                                          start=False, stop=half == 1)
                mm.then_inc(hp_ready, 1)
                pe.wait_ge(kv_ready, t + 3)
                for half in (0, 1):
                    at = slice(half * P, (half + 1) * P)
                    mm = nc.tensor.matmul(kvp[:, half, :], kk[b][0:r, at], vv[b][0:r, at], start=False,
                                          stop=False, skip_group_check=True)
                mm.then_inc(kv_used, 1)
                pe.sem_inc(xn_used, 1)
            over_tiles(pe, tile)
            nc.tensor.matmul(kvp[:, 0, :], zero[:], zero[:], start=False, stop=True,
                             skip_group_check=True).then_inc(kv_summed, 1)

        @block.scalar
        def _(act):
            act.sem_inc(h_free, 2)

            def tile(t, b, r):
                root(k, act, st, r, asked, answered, 2 * t + 1)
                act.wait_ge(turned_ready, t + 1)
                nc.scalar.copy(xnT[b][:, :, 0:r], turned[b][:, 0:2, 0:r]).then_inc(xnT_ready, 1)
                act.wait_ge(asked, 2 * t + 2)
                nc.scalar.activation(hs[0:r, 2, :], hs[0:r, 1, :], ACT.Sqrt,
                                     scale=1.0 / 31).then_inc(answered, 1)
                act.wait_ge(hp_ready, t + 1)
                act.wait_ge(h_free, t + 1)
                nc.scalar.activation(h[b][0:r, :], hp[b][0:r, 0:C], ACT.Relu).then_inc(h_ready, 1)
                act.wait_ge(h_ready, t + 1)
                act.dma_start(h_d[ds(t * P, r), :], h[b][0:r, :]).then_inc(h_out[b], 16)
                act.wait_ge(h_out[b], k.nth(t, b) * 16)
                act.sem_inc(h_free, 1)
            over_tiles(act, tile)


W = 448


def dense_and_norms(k, ctx, tag, acc, w_name, b_name, norms):
    nc, I = k.nc, k.ins
    blocks = NP // W
    NCK, CK = 25, N // 25
    with ExitStack() as c:
        def sb(name, shape, dt=F32):
            return c.enter_context(nc.sbuf_tensor(f"{tag}_{name}", shape, dt))

        def sem(name):
            return c.enter_context(k.semaphore(f"{tag}_{name}"))

        loads = [("w", [P, 2, C], halves(I[w_name])), ("b", [P, 2], halves_col(I[b_name]))]
        for n, (g, b, _) in enumerate(norms):
            loads += [(f"g{n}", [P, 2], halves_col(I[g])), (f"b{n}", [P, 2], halves_col(I[b]))]
        w, b, *gb = load_params(k, c, tag, loads)
        stats = sb("stats", [P, 2, NCK, 6])
        mv, sc = sb("mv", [P, 2, 2]), sb("sc", [P, 4, 2])
        out = [[c.enter_context(nc.psum_tensor(f"{tag}_out{s}{h}", [P, 512], F32)) for h in (0, 1)]
               for s in (0, 1)]
        made, moved = sem("made"), sem("moved")
        asked, answered, scaled, applied = sem("asked"), sem("answered"), sem("scaled"), sem("applied")
        block = c.enter_context(nc.Block())

        @block.tensor
        def _(pe):
            pe.sem_inc(moved, 2)
            with pe.Fori(0, blocks // 2) as i:
                for s in (0, 1):
                    n = 2 * i + s
                    pe.wait_ge(moved, n + 1)
                    for co in (0, 1):
                        for ci in (0, 1):
                            mm = nc.tensor.matmul(out[s][co][:, 0:W], w[:, ci, co * P:(co + 1) * P],
                                                  acc[:, ci, ds(n * W, W)], start=ci == 0, stop=ci == 1)
                    mm.then_inc(made, 1)

        @block.scalar
        def _(act):
            with act.Fori(0, blocks // 2) as i:
                for s in (0, 1):
                    n = 2 * i + s
                    act.wait_ge(made, n + 1)
                    for co in (0, 1):
                        nc.scalar.activation(acc[:, co, ds(n * W, W)], out[s][co][:, 0:W], ACT.Identity,
                                             bias=b[:, co:co + 1])
                    act.drain().then_inc(moved, 1)
            for n, (_, _, relu) in enumerate(norms):
                act.wait_ge(asked, n + 1)
                nc.scalar.activation(sc[:, 0, :], mv[:, :, 1], ACT.Sqrt, bias=k.eps[:, 0:1]
                                     ).then_inc(answered, 1)
                act.wait_ge(scaled, n + 1)
                for half in (0, 1):
                    nc.scalar.activation(acc[:, half, :], acc[:, half, :], ACT.Relu if relu else ACT.Identity,
                                         bias=sc[:, 3, half:half + 1], scale=sc[:, 2, half:half + 1])
                act.drain().then_inc(applied, 1)

        @block.vector
        def _(dve):
            dve.wait_ge(moved, 2 + blocks)
            for n in range(len(norms)):
                if n:
                    dve.wait_ge(applied, n)
                with dve.Fori(0, NCK) as i:
                    for half in (0, 1):
                        nc.vector.bn_stats(stats[:, half, ds(i, 1), :], acc[:, half, ds(i * CK, CK)])
                dve.drain()
                for half in (0, 1):
                    nc.vector.bn_aggr(mv[:, half, :], stats[:, half].rearrange("p a b -> p (a b)"))
                dve.drain().then_inc(asked, 1)
                dve.wait_ge(answered, n + 1)
                nc.vector.reciprocal(sc[:, 1, :], sc[:, 0, :])
                dve.drain()
                nc.vector.tensor_tensor(sc[:, 2, :], sc[:, 1, :], gb[2 * n][:], ALU.mult)
                dve.drain()
                nc.vector.tensor_tensor(sc[:, 1, :], mv[:, :, 0], sc[:, 2, :], ALU.mult)
                dve.drain()
                nc.vector.tensor_tensor(sc[:, 3, :], gb[2 * n + 1][:], sc[:, 1, :], ALU.subtract)
                dve.drain().then_inc(scaled, 1)
            dve.wait_ge(applied, len(norms))


def rows_from_channels(k, ctx, tag, acc, h_d, w_name, b_name):
    nc, I = k.nc, k.ins
    with ExitStack() as c:
        def sb(name, shape, dt=F32):
            return c.enter_context(nc.sbuf_tensor(f"{tag}_{name}", shape, dt))

        def sem(name):
            return c.enter_context(k.semaphore(f"{tag}_{name}"))

        w, b1 = load_params(k, c, tag, [("w", [P, 2, C], halves(I[w_name])),
                                        ("b", [1, C], I[b_name].unsqueeze(0))])
        aT = [sb(f"aT{b}", [P, 2, P]) for b in (0, 1)]
        h = [sb(f"h{b}", [P, C]) for b in (0, 1)]
        hp = [c.enter_context(nc.psum_tensor(f"{tag}_hp{b}", [P, 512], F32)) for b in (0, 1)]
        a_ready, hp_ready, h_ready, h_free = sem("a_ready"), sem("hp_ready"), sem("h_ready"), sem("h_free")
        h_out = [sem("h_out0"), sem("h_out1")]
        block = c.enter_context(nc.Block())

        @block.vector
        def _(dve):
            dve.sem_inc(hp_ready, 2)

            def tile(t, b, r):
                dve.wait_ge(hp_ready, t + 1)
                nc.vector.tensor_copy(aT[b][:, :, 0:r], acc[:, :, ds(t * P, r)]).then_inc(a_ready, 1)
            over_tiles(dve, tile)

        @block.tensor
        def _(pe):
            pe.sem_inc(h_ready, 2)

            def tile(t, b, r):
                pe.wait_ge(a_ready, t + 1)
                pe.wait_ge(h_ready, t + 1)
                nc.tensor.matmul(hp[b][0:r, 0:C], k.ones[0:1, 0:r], b1[:], start=True, stop=False)
                for half in (0, 1):
                    mm = nc.tensor.matmul(hp[b][0:r, 0:C], aT[b][:, half, 0:r], w[:, half, :],
                                          start=False, stop=half == 1)
                mm.then_inc(hp_ready, 1)
            over_tiles(pe, tile)

        @block.scalar
        def _(act):
            act.sem_inc(h_free, 2)

            def tile(t, b, r):
                act.wait_ge(hp_ready, t + 3)
                act.wait_ge(h_free, t + 1)
                nc.scalar.activation(h[b][0:r, :], hp[b][0:r, 0:C], ACT.Relu).then_inc(h_ready, 1)
            over_tiles(act, tile)

        @block.sync
        def _(sp):
            def tile(t, b, r):
                sp.wait_ge(h_ready, t + 3)
                sp.dma_start(h_d[ds(t * P, r), :], h[b][0:r, :]).then_inc(h_out[b], 16)
                sp.wait_ge(h_out[b], k.nth(t, b) * 16)
                sp.sem_inc(h_free, 1)
            over_tiles(sp, tile)


def mix_and_gate_stage(k, ctx, tag, z, kv, x1_d, yT_d, gates):
    nc, I = k.nc, k.ins
    NE = 8
    with ExitStack() as c:
        def sb(name, shape, dt=F32):
            return c.enter_context(nc.sbuf_tensor(f"{tag}_{name}", shape, dt))

        def sem(name):
            return c.enter_context(k.semaphore(f"{tag}_{name}"))

        gamma, beta, wr, br = load_params(k, c, tag, [
            ("gamma", [P, C], row_on_all(I["L0_ffn_gamma"])), ("beta", [P, C], row_on_all(I["L0_ffn_beta"])),
            ("wr", [P, 2, NE], halves(I["L0_ffn_Wr"])), ("br", [P, NE], row_on_all(I["L0_ffn_br"]))])
        x = [sb(f"x{b}", [P, C]) for b in (0, 1)]
        xn = [sb(f"xn{b}", [P, C]) for b in (0, 1)]
        xnT = [sb(f"xnT{b}", [P, 2, P]) for b in (0, 1)]
        zc = [sb(f"zc{b}", [P, 2, P]) for b in (0, 1)]
        x1 = [sb(f"x1{b}", [P, C]) for b in (0, 1)]
        y = [sb(f"y{b}", [P, C]) for b in (0, 1)]
        yT = [sb(f"yT{b}", [P, 2, P]) for b in (0, 1)]
        t1, st = sb("t1", [P, C]), sb("st", [P, 16])
        masks = gate_buffers(k, c, tag, NE)
        logits = sb("logits", [P, NT, NE])
        turned = [c.enter_context(nc.psum_tensor(f"{tag}_turned{b}", [P, 4, P], F32)) for b in (0, 1)]
        mixed = [c.enter_context(nc.psum_tensor(f"{tag}_mixed{b}", [P, 4, P], F32)) for b in (0, 1)]
        yturn = [c.enter_context(nc.psum_tensor(f"{tag}_yturn{b}", [P, 4, P], F32)) for b in (0, 1)]
        lg = [c.enter_context(nc.psum_tensor(f"{tag}_lg{b}", [P, 512], F32)) for b in (0, 1)]
        x_in = [sem("x_in0"), sem("x_in1")]
        x1_out, y_out = [sem("x1_out0"), sem("x1_out1")], [sem("y_out0"), sem("y_out1")]
        x_used, asked, answered, xn_ready, z_ready, turned_ready, xnT_ready, mixed_ready = map(sem, (
            "x_used", "asked", "answered", "xn_ready", "z_ready", "turned_ready", "xnT_ready", "mixed_ready"))
        x1_ready, x1_free, y_ready, yturn_ready, yT_ready, yT_free, lg_ready, tile_done = map(sem, (
            "x1_ready", "x1_free", "y_ready", "yturn_ready", "yT_ready", "yT_free", "lg_ready", "tile_done"))
        block = c.enter_context(nc.Block())

        @block.sync
        def _(sp):
            sp.sem_inc(x_used, 2)

            def load(t, b, rows):
                sp.wait_ge(x_used, t + 1)
                sp.dma_start(x[b][0:rows, :], I["x"][ds(t * P, rows), :]).then_inc(x_in[b], 16)
            over_tiles(sp, load)

        @block.gpsimd
        def _(pool):
            pool.sem_inc(x1_free, 2)
            pool.sem_inc(yT_free, 2)
            pool.wait_ge(x1_ready, 1)

            def store(t, b, r):
                pool.wait_ge(x1_ready, t + 1)
                pool.sem_inc(k.turn, 1)
                pool.dma_start(x1_d[ds(t * P, r), :], x1[b][0:r, :]).then_inc(x1_out[b], 16)
                pool.wait_ge(yT_ready, t + 1)
                pool.sem_inc(k.turn, 1)
                pool.dma_start(yT_d[:, :, ds(t * P, r)], yT[b][:, :, 0:r]).then_inc(y_out[b], 16)
                pool.wait_ge(x1_out[b], k.nth(t, b) * 16)
                pool.sem_inc(x1_free, 1)
                pool.wait_ge(y_out[b], k.nth(t, b) * 16)
                pool.sem_inc(yT_free, 1)
            over_tiles(pool, store)

        @block.vector
        def _(dve):
            dve.sem_inc(tile_done, 2)
            nc.vector.memset(logits[:], 0.0)
            nc.vector.memset(gates[:], 0.0)
            dve.drain()

            def tile(t, b, r):
                dve.wait_ge(x_in[b], k.nth(t, b) * 16)
                layer_norm(k, dve, x[b][0:r, :], xn[b][0:r, :], st, r, asked, answered, 3 * t + 1)
                dve.sem_inc(xn_ready, 1)
                dve.wait_ge(mixed_ready, t + 1)
                zt = turned[b][0:r, 2:4, :].rearrange("p h d -> p (h d)")
                nc.vector.tensor_tensor(t1[0:r], zt, xn[b][0:r], ALU.add)
                dve.drain()
                nc.vector.scalar_tensor_tensor(t1[0:r], t1[0:r], 0.0, xn[b][0:r], ALU.max, ALU.add)
                dve.drain()
                nc.vector.tensor_tensor(t1[0:r], t1[0:r], mixed[b][0:r, 0:2, :].rearrange("p h d -> p (h d)"),
                                        ALU.add)
                dve.drain()
                dve.wait_ge(x1_free, t + 1)
                nc.vector.tensor_tensor(x1[b][0:r], t1[0:r], x[b][0:r], ALU.add).then_inc(x1_ready, 1)
                dve.drain()
                dve.sem_inc(x_used, 1)
                layer_norm(k, dve, x1[b][0:r, :], t1[0:r, :], st, r, asked, answered, 3 * t + 2)
                layer_norm(k, dve, t1[0:r, :], y[b][0:r, :], st, r, asked, answered, 3 * t + 3)
                nc.vector.tensor_tensor(y[b][0:r], y[b][0:r], gamma[0:r], ALU.mult)
                dve.drain()
                nc.vector.tensor_tensor(y[b][0:r], y[b][0:r], beta[0:r], ALU.add).then_inc(y_ready, 1)
                dve.wait_ge(lg_ready, t + 1)
                nc.vector.tensor_tensor(logits[0:r, ds(t, 1), :], lg[b][0:r, 0:NE], br[0:r, :], ALU.add)
                dve.drain().then_inc(tile_done, 1)
            over_tiles(dve, tile)
            top_two(k, dve, logits, gates, NE, asked, answered, 3 * REAL_T + 1, masks)

        @block.scalar
        def _(act):
            def tile(t, b, r):
                root(k, act, st, r, asked, answered, 3 * t + 1)
                nc.scalar.copy(zc[b][:, :, 0:r], z[:, :, ds(t * P, r)]).then_inc(z_ready, 1)
                act.wait_ge(turned_ready, t + 1)
                nc.scalar.copy(xnT[b][:, :, 0:r], turned[b][:, 0:2, 0:r]).then_inc(xnT_ready, 1)
                root(k, act, st, r, asked, answered, 3 * t + 2)
                root(k, act, st, r, asked, answered, 3 * t + 3)
                act.wait_ge(yturn_ready, t + 1)
                act.wait_ge(yT_free, t + 1)
                nc.scalar.copy(yT[b][:, :, 0:r], yturn[b][:, 0:2, 0:r]).then_inc(yT_ready, 1)
            over_tiles(act, tile)
            act.wait_ge(asked, 3 * REAL_T + 1)
            nc.scalar.activation(masks[5][:], masks[5][:], ACT.Exp).then_inc(answered, 1)

        @block.tensor
        def _(pe):
            def tile(t, b, r):
                pe.wait_ge(xn_ready, t + 1)
                pe.wait_ge(tile_done, t + 1)
                for half in (0, 1):
                    mm = nc.tensor.transpose(turned[b][:, half, 0:r], xn[b][0:r, half * P:(half + 1) * P],
                                             k.ident[0:r, 0:r])
                mm.then_inc(turned_ready, 1)
                pe.wait_ge(z_ready, t + 1)
                pe.wait_ge(xnT_ready, t + 1)
                for half in (0, 1):
                    nc.tensor.transpose(turned[b][0:r, 2 + half, :], zc[b][:, half, 0:r], k.ident[:])
                for half in (0, 1):
                    mm = nc.tensor.matmul(mixed[b][0:r, half, :], xnT[b][:, half, 0:r], kv[:, half, :],
                                          start=True, stop=True)
                mm.then_inc(mixed_ready, 1)
                pe.wait_ge(y_ready, t + 1)
                for half in (0, 1):
                    mm = nc.tensor.transpose(yturn[b][:, half, 0:r], y[b][0:r, half * P:(half + 1) * P],
                                             k.ident[0:r, 0:r])
                mm.then_inc(yturn_ready, 1)
                pe.wait_ge(yT_ready, t + 1)
                for half in (0, 1):
                    mm = nc.tensor.matmul(lg[b][0:r, 0:NE], yT[b][:, half, 0:r], wr[:, half, :],
                                          start=half == 0, stop=half == 1)
                mm.then_inc(lg_ready, 1)
            over_tiles(pe, tile)


def gate_buffers(k, c, tag, NE):
    nc = k.nc
    big = [c.enter_context(nc.sbuf_tensor(f"{tag}_gm{n}", [P, NT, NE], F32)) for n in range(4)]
    small = [c.enter_context(nc.sbuf_tensor(f"{tag}_gs{n}", [P, NT], F32)) for n in range(4)]
    return big + small


def top_two(k, dve, score, gates, NE, asked, answered, nth, bufs):
    nc = k.nc
    masked, number, hot1, hot2, best, gap, w1, w2 = bufs
    shape = [P, NT, NE]

    def wide(a):
        return a[:].unsqueeze(2).broadcast_to(shape)

    ramp = k.ramp[:, 0:NE].unsqueeze(1).broadcast_to(shape)
    nc.vector.tensor_copy(masked[:], score[:])
    dve.drain()
    for hot, value in ((hot1, best), (hot2, gap)):
        nc.vector.tensor_reduce(value[:], masked[:], AX_X, ALU.max)
        dve.drain()
        nc.vector.tensor_tensor(number[:], masked[:], wide(value), ALU.is_lt)
        dve.drain()
        nc.vector.scalar_tensor_tensor(number[:], number[:], float(NE), ramp, ALU.mult, ALU.add)
        dve.drain()
        nc.vector.tensor_reduce(w1[:], number[:], AX_X, ALU.min)
        dve.drain()
        nc.vector.tensor_tensor(hot[:], ramp, wide(w1), ALU.is_equal)
        dve.drain()
        nc.vector.scalar_tensor_tensor(masked[:], hot[:], NEG, masked[:], ALU.mult, ALU.add)
        dve.drain()
    nc.vector.tensor_tensor(gap[:], gap[:], best[:], ALU.subtract).then_inc(asked, 1)
    dve.wait_ge(answered, nth)
    nc.vector.tensor_scalar(w1[:], gap[:], 1.0, None, ALU.add)
    dve.drain()
    nc.vector.reciprocal(w2[:], w1[:])
    dve.drain()
    nc.vector.tensor_tensor(w1[:], gap[:], w2[:], ALU.mult)
    nc.vector.tensor_tensor(hot1[:], hot1[:], wide(w2), ALU.mult)
    dve.drain()
    nc.vector.tensor_tensor(hot2[:], hot2[:], wide(w1), ALU.mult)
    dve.drain()
    nc.vector.tensor_tensor(gates[:], hot1[:], hot2[:], ALU.add)
    dve.drain()


def expert_stage(k, ctx, tag, NE, xT_d, x_d, out_d, gates, w1_name, b1_name, w2_name, b2_name):
    nc, I = k.nc, k.ins
    GN = 2 * P
    H = 4
    with ExitStack() as c:
        def sb(name, shape, dt=F32):
            return c.enter_context(nc.sbuf_tensor(f"{tag}_{name}", shape, dt))

        def sem(name):
            return c.enter_context(k.semaphore(f"{tag}_{name}"))

        w1, w2, b2, b1_rows = load_params(k, c, tag, [
            ("w1", [P, NE, 2, H * P], I[w1_name].rearrange("e (h p) m -> p e h m", p=P)),
            ("w2", [P, NE, H, C], I[w2_name].rearrange("e (h p) m -> p e h m", p=P)),
            ("b2", [NE, C], I[b2_name]),
            ("b1", [NE * H, P], I[b1_name].rearrange("e (h p) -> (e h) p", p=P))])
        b1 = sb("b1c", [P, NE * H])
        xT = [sb(f"xT{u}", [P, 2, GN]) for u in (0, 1)]
        x = [sb(f"x{u}", [P, 2, C]) for u in (0, 1)]
        gs = [sb(f"gs{u}", [P, 2, NE]) for u in (0, 1)]
        gT = [sb(f"gT{u}", [NE, 2, P]) for u in (0, 1)]
        hid = [sb(f"hid{v}", [P, H, GN]) for v in (0, 1)]
        hp = [c.enter_context(nc.psum_tensor(f"{tag}_hp{v}", [P, H, GN], F32)) for v in (0, 1)]
        yp = [c.enter_context(nc.psum_tensor(f"{tag}_yp{v}", [P, 2, C], F32)) for v in (0, 1)]
        gp = c.enter_context(nc.psum_tensor(f"{tag}_gp", [P, 4, P], F32))
        bp = c.enter_context(nc.psum_tensor(f"{tag}_bp", [P, 2, C], F32))
        xT_in, x_in = [sem("xT_in0"), sem("xT_in1")], [sem("x_in0"), sem("x_in1")]
        x_out = [sem("x_out0"), sem("x_out1")]
        xT_used, x_free, g_ready, gp_ready, gT_ready, bp_ready = map(
            sem, ("xT_used", "x_free", "g_ready", "gp_ready", "gT_ready", "bp_ready"))
        hp_ready, hid_ready, yp_ready, yp_read, x_ready = map(
            sem, ("hp_ready", "hid_ready", "yp_ready", "yp_read", "x_ready"))
        b1_turned, b1_ready, hp_read, hid_used, gp_read = map(
            sem, ("b1_turned", "b1_ready", "hp_read", "hid_used", "gp_read"))
        block = c.enter_context(nc.Block())

        def over_groups(eng, body):
            with eng.Fori(0, N // GN // 2) as i:
                for u in (0, 1):
                    body(2 * i + u, u, (P, P))
            body(N // GN, 0, (LAST,))

        @block.sync
        def _(sp):
            sp.sem_inc(xT_used, 2)
            sp.sem_inc(x_free, 2)

            def load(n, u, tiles):
                w = sum(tiles)
                sp.wait_ge(xT_used, n + 1)
                sp.dma_start(xT[u][:, :, 0:w], xT_d[:, :, ds(n * GN, w)]).then_inc(xT_in[u], 16)
                sp.wait_ge(x_free, n + 1)
                r = tiles[0]
                sp.dma_start(x[u][0:r, 0:len(tiles), :], x_d[ds(n * GN, w), :].rearrange(
                    "(a p) m -> p a m", p=r)).then_inc(x_in[u], 16)
            over_groups(sp, load)

        @block.gpsimd
        def _(pool):
            def store(n, u, tiles):
                w, r = sum(tiles), tiles[0]
                pool.wait_ge(x_ready, n + 1)
                pool.sem_inc(k.turn, 1)
                pool.dma_start(out_d[ds(n * GN, w), :].rearrange("(a p) m -> p a m", p=r),
                               x[u][0:r, 0:len(tiles), :]).then_inc(x_out[u], 16)
                pool.wait_ge(x_out[u], k.nth(n, u) * 16)
                pool.sem_inc(x_free, 1)
            over_groups(pool, store)

        @block.vector
        def _(dve):
            dve.sem_inc(gp_read, 1)

            def group(n, u, tiles):
                r, nt = tiles[0], len(tiles)
                nc.vector.tensor_copy(gs[u][:, 0:nt, :], gates[:, ds(n * 2, nt), :]).then_inc(g_ready, 1)
                dve.wait_ge(gp_ready, n + 1)
                nc.vector.tensor_copy(gT[u][:, 0:nt, :], gp[0:NE, 0:nt, :]).then_inc(gT_ready, 1)
                dve.wait_ge(x_in[u], k.nth(n, u) * 16)
                dve.wait_ge(bp_ready, n + 1)
                nc.vector.tensor_tensor(x[u][0:r, 0:nt, :], x[u][0:r, 0:nt, :], bp[0:r, 0:nt, :], ALU.add)
                dve.drain()
                dve.sem_inc(gp_read, 1)
                for e in range(NE):
                    m = n * NE + e
                    dve.wait_ge(yp_ready, m + 1)
                    for a in range(nt):
                        nc.vector.scalar_tensor_tensor(x[u][0:r, a, :], yp[e % 2][0:r, a, :],
                                                       gs[u][0:r, a, e:e + 1], x[u][0:r, a, :],
                                                       ALU.mult, ALU.add)
                    dve.drain().then_inc(yp_read, 1)
                dve.sem_inc(x_ready, 1)
            over_groups(dve, group)

        @block.scalar
        def _(act):
            act.wait_ge(b1_turned, 1)
            nc.scalar.copy(b1[:], gp[:, 0, 0:NE * H]).then_inc(b1_ready, 1)
            act.wait_ge(b1_ready, 1)

            def group(n, u, tiles):
                w = sum(tiles)
                for e in range(NE):
                    m = n * NE + e
                    act.wait_ge(hp_ready, m + 1)
                    act.wait_ge(hid_used, m + 1)
                    for j in range(H):
                        nc.scalar.activation(hid[e % 2][:, j, 0:w], hp[e % 2][:, j, 0:w], ACT.Gelu,
                                             bias=b1[:, e * H + j:e * H + j + 1])
                    act.drain().then_inc(hid_ready, 1)
            over_groups(act, group)

        @block.tensor
        def _(pe):
            nc.tensor.transpose(gp[:, 0, 0:NE * H], b1_rows[:], k.ident[0:NE * H, 0:NE * H]
                                ).then_inc(b1_turned, 1)
            pe.wait_ge(b1_ready, 1)
            pe.sem_inc(hid_used, 2)
            pe.sem_inc(yp_read, 2)

            def group(n, u, tiles):
                w, r, nt = sum(tiles), tiles[0], len(tiles)

                def up(e):
                    m = n * NE + e
                    if e >= 2:
                        pe.wait_ge(hid_ready, m - 1)
                    for j in range(H):
                        for ci in (0, 1):
                            mm = nc.tensor.matmul(hp[e % 2][:, j, 0:w], w1[:, e, ci, j * P:(j + 1) * P],
                                                  xT[u][:, ci, 0:w], start=ci == 0, stop=ci == 1)
                    mm.then_inc(hp_ready, 1)

                def down(e):
                    m = n * NE + e
                    pe.wait_ge(hid_ready, m + 1)
                    pe.wait_ge(yp_read, m + 1)
                    for a in range(nt):
                        for j in range(H):
                            mm = nc.tensor.matmul(yp[e % 2][0:r, a, :], hid[e % 2][:, j, a * P:a * P + r],
                                                  w2[:, e, j, :], start=j == 0, stop=j == H - 1)
                    mm.then_inc(yp_ready, 1)
                    pe.sem_inc(hid_used, 1)

                pe.wait_ge(xT_in[u], k.nth(n, u) * 16)
                up(0)
                pe.wait_ge(g_ready, n + 1)
                pe.wait_ge(gp_read, n + 1)
                for a in range(nt):
                    mm = nc.tensor.transpose(gp[0:NE, a, :], gs[u][:, a, :], k.ident[:])
                mm.then_inc(gp_ready, 1)
                up(1)
                pe.wait_ge(gT_ready, n + 1)
                for a in range(nt):
                    mm = nc.tensor.matmul(bp[0:r, a, :], gT[u][:, a, 0:r], b2[:], start=True, stop=True)
                mm.then_inc(bp_ready, 1)
                for e in range(NE):
                    down(e)
                    if e + 2 < NE:
                        up(e + 2)
                pe.sem_inc(xT_used, 1)
            over_groups(pe, group)


SCALE = 32 ** -0.5
HG = 16
ROW = HG + 4


def channels_stage(k, ctx, tag, x2_d, xn_d, xT, kmax):
    nc, I = k.nc, k.ins
    blocks = NP // W
    with ExitStack() as c:
        def sb(name, shape, dt=F32):
            return c.enter_context(nc.sbuf_tensor(f"{tag}_{name}", shape, dt))

        def sem(name):
            return c.enter_context(k.semaphore(f"{tag}_{name}"))

        wk, = load_params(k, c, tag, [("wk", [P, 2, P], halves(I["L1_mix_W_qkv"])[:, :, P:2 * P])])
        x = [sb(f"x{b}", [P, C]) for b in (0, 1)]
        xn = [sb(f"xn{b}", [P, C]) for b in (0, 1)]
        st, kpart = sb("st", [P, 16]), sb("kpart", [P, blocks])
        turned = [c.enter_context(nc.psum_tensor(f"{tag}_turned{b}", [P, 4, P], F32)) for b in (0, 1)]
        kp = [c.enter_context(nc.psum_tensor(f"{tag}_kp{b}", [P, 512], F32)) for b in (0, 1)]
        x_in, xn_out = [sem("x_in0"), sem("x_in1")], [sem("xn_out0"), sem("xn_out1")]
        x_used, xn_ready, xn_free, turned_ready, turned_read, asked, answered, kp_ready, kp_read = map(sem, (
            "x_used", "xn_ready", "xn_free", "turned_ready", "turned_read", "asked", "answered", "kp_ready",
            "kp_read"))
        block = c.enter_context(nc.Block())

        @block.sync
        def _(sp):
            sp.sem_inc(x_used, 2)

            def load(t, b, r):
                sp.wait_ge(x_used, t + 1)
                sp.dma_start(x[b][0:r, :], x2_d[ds(t * P, r), :]).then_inc(x_in[b], 16)
            over_tiles(sp, load)

        @block.gpsimd
        def _(pool):
            pool.sem_inc(xn_free, 2)

            def store(t, b, r):
                pool.wait_ge(xn_ready, t + 1)
                pool.sem_inc(k.turn, 1)
                pool.dma_start(xn_d[ds(t * P, r), :], xn[b][0:r, :]).then_inc(xn_out[b], 16)
                pool.wait_ge(xn_out[b], k.nth(t, b) * 16)
                pool.sem_inc(xn_free, 1)
            over_tiles(pool, store)

        @block.vector
        def _(dve):
            def tile(t, b, r):
                dve.wait_ge(x_in[b], k.nth(t, b) * 16)
                dve.wait_ge(xn_free, t + 1)
                dve.wait_ge(turned_ready, t + 1)
                layer_norm(k, dve, x[b][0:r, :], xn[b][0:r, :], st, r, asked, answered, t + 1)
                dve.sem_inc(x_used, 1)
                dve.drain().then_inc(xn_ready, 1)
            dve.sem_inc(turned_ready, 2)
            over_tiles(dve, tile)
            with dve.Fori(0, blocks // 2 - 1) as i:
                for s in (0, 1):
                    dve.wait_ge(kp_ready, 2 * i + s + 1)
                    nc.vector.tensor_reduce(kpart[:, ds(2 * i + s, 1)], kp[s][:, 0:W], AX_X, ALU.max
                                            ).then_inc(kp_read, 1)
            for n in (blocks - 2, blocks - 1):
                dve.wait_ge(kp_ready, n + 1)
                w = min(W, N - n * W)
                nc.vector.tensor_reduce(kpart[:, n:n + 1], kp[n % 2][:, 0:w], AX_X, ALU.max).then_inc(kp_read, 1)
            dve.drain()
            nc.vector.tensor_reduce(kmax[:], kpart[:], AX_X, ALU.max)

        @block.scalar
        def _(act):
            nc.scalar.activation(xT[:, :, N:NP], k.ones[:, 0:2 * (NP - N)].rearrange("p (a b) -> p a b", a=2),
                                 ACT.Copy, scale=0.0)

            def tile(t, b, r):
                root(k, act, st, r, asked, answered, t + 1)
                act.wait_ge(turned_ready, t + 3)
                nc.scalar.copy(xT[:, :, ds(t * P, r)], turned[b][:, 0:2, 0:r]).then_inc(turned_read, 1)
            over_tiles(act, tile)

        @block.tensor
        def _(pe):
            pe.sem_inc(turned_read, 2)
            pe.sem_inc(kp_read, 2)

            def tile(t, b, r):
                pe.wait_ge(xn_ready, t + 1)
                pe.wait_ge(turned_read, t + 1)
                for half in (0, 1):
                    mm = nc.tensor.transpose(turned[b][:, half, 0:r], xn[b][0:r, half * P:(half + 1) * P],
                                             k.ident[0:r, 0:r])
                mm.then_inc(turned_ready, 1)
            over_tiles(pe, tile)
            pe.wait_ge(turned_read, 2 + REAL_T)
            with pe.Fori(0, blocks // 2) as i:
                for s in (0, 1):
                    pe.wait_ge(kp_read, 2 * i + s + 1)
                    for ci in (0, 1):
                        mm = nc.tensor.matmul(kp[s][:, 0:W], wk[:, ci, :], xT[:, ci, ds((2 * i + s) * W, W)],
                                              start=ci == 0, stop=ci == 1)
                    mm.then_inc(kp_ready, 1)


def context_stage(k, ctx, tag, xT, kmax, ctx_out):
    nc, I = k.nc, k.ins
    with ExitStack() as c:
        def sb(name, shape, dt=F32):
            return c.enter_context(nc.sbuf_tensor(f"{tag}_{name}", shape, dt))

        def sem(name):
            return c.enter_context(k.semaphore(f"{tag}_{name}"))

        wkv, wo = load_params(k, c, tag, [("wkv", [P, 2, 2 * P], halves(I["L1_mix_W_qkv"])[:, :, P:3 * P]),
                                          ("wo", [P, C], I["L1_mix_W_out"])])
        xs = [sb(f"xs{b}", [P, 2, P]) for b in (0, 1)]
        ek = [sb(f"ek{b}", [P, P]) for b in (0, 1)]
        v1 = [sb(f"v1{b}", [P, P + 1]) for b in (0, 1)]
        maxrow, kmax_wide = sb("maxrow", [P, P]), sb("kmax_wide", [P, P])
        zero = sb("zero", [P, P + 1])
        cs, csT, inv = sb("cs", [P, P]), sb("csT", [P, P]), sb("inv", [P, 1])
        kvp = [c.enter_context(nc.psum_tensor(f"{tag}_kvp{b}", [P, 512], F32)) for b in (0, 1)]
        cp = c.enter_context(nc.psum_tensor(f"{tag}_cp", [P, 512], F32))
        mp = c.enter_context(nc.psum_tensor(f"{tag}_mp", [P, 512], F32))
        xs_ready, kvp_ready, shifted, v_ready, ek_ready, summed = map(
            sem, ("xs_ready", "kvp_ready", "shifted", "v_ready", "ek_ready", "summed"))
        begun, row_ready, one, turned, copied, outed = map(
            sem, ("begun", "row_ready", "one", "turned", "copied", "outed"))
        block = c.enter_context(nc.Block())

        @block.gpsimd
        def _(pool):
            pool.sem_inc(kvp_ready, 2)

            def tile(t, b, r):
                pool.wait_ge(kvp_ready, t + 1)
                pool.sem_inc(k.turn, 1)
                nc.gpsimd.tensor_copy(xs[b][:, :, 0:r], xT[:, :, ds(t * P, r)]).then_inc(xs_ready, 1)
            over_tiles(pool, tile)

        @block.vector
        def _(dve):
            nc.vector.memset(zero[:], 0.0)
            for b in (0, 1):
                nc.vector.memset(v1[b][:, P:P + 1], 1.0)
            nc.vector.tensor_scalar(kmax_wide[:], k.ones[:], kmax[:, 0:1], None, ALU.mult)
            dve.drain().then_inc(begun, 1)
            dve.wait_ge(row_ready, 1)
            nc.vector.tensor_copy(maxrow[:], mp[:, 0:P])
            dve.drain()
            dve.sem_inc(summed, 2)

            def tile(t, b, r):
                dve.wait_ge(kvp_ready, t + 3)
                dve.wait_ge(summed, t + 1)
                nc.vector.tensor_tensor(ek[b][0:r], kvp[b][0:r, 0:P], maxrow[0:r], ALU.subtract
                                        ).then_inc(shifted, 1)
                nc.vector.tensor_copy(v1[b][0:r, 0:P], kvp[b][0:r, P:2 * P]).then_inc(v_ready, 1)
            over_tiles(dve, tile)
            dve.wait_ge(summed, 3 + REAL_T)
            nc.vector.reciprocal(inv[:], cp[:, P:P + 1])
            dve.drain()
            nc.vector.tensor_scalar(cs[:], cp[:, 0:P], inv[:, 0:1], SCALE, ALU.mult, ALU.mult)
            dve.drain()
            nc.vector.tensor_tensor(cs[:], cs[:], k.block_diag[:], ALU.mult)
            dve.drain().then_inc(one, 1)
            dve.wait_ge(turned, 1)
            nc.vector.tensor_copy(csT[:], mp[:, 0:P]).then_inc(copied, 1)
            dve.wait_ge(outed, 1)
            nc.vector.tensor_copy(ctx_out[:], kvp[0][:, 0:C])

        @block.scalar
        def _(act):
            def tile(t, b, r):
                act.wait_ge(shifted, t + 1)
                nc.scalar.activation(ek[b][0:r], ek[b][0:r], ACT.Exp).then_inc(ek_ready, 1)
            over_tiles(act, tile)

        @block.tensor
        def _(pe):
            pe.wait_ge(begun, 1)
            nc.tensor.matmul(mp[:, 0:P], kmax_wide[:], k.ident[:], start=True, stop=True).then_inc(row_ready, 1)
            nc.tensor.matmul(cp[:, 0:P + 1], zero[:, 0:P], zero[:], start=True, stop=False,
                             skip_group_check=True)

            def tile(t, b, r):
                pe.wait_ge(xs_ready, t + 1)
                for half in (0, 1):
                    mm = nc.tensor.matmul(kvp[b][0:r, 0:2 * P], xs[b][:, half, 0:r], wkv[:, half, :],
                                          start=half == 0, stop=half == 1)
                mm.then_inc(kvp_ready, 1)
                pe.wait_ge(v_ready, t + 1)
                pe.wait_ge(ek_ready, t + 1)
                nc.tensor.matmul(cp[:, 0:P + 1], ek[b][0:r, :], v1[b][0:r, :], start=False, stop=False,
                                 skip_group_check=True).then_inc(summed, 1)
            over_tiles(pe, tile)
            nc.tensor.matmul(cp[:, 0:P + 1], zero[:, 0:P], zero[:], start=False, stop=True,
                             skip_group_check=True).then_inc(summed, 1)
            pe.wait_ge(one, 1)
            nc.tensor.transpose(mp[:, 0:P], cs[:], k.ident[:]).then_inc(turned, 1)
            pe.wait_ge(copied, 1)
            nc.tensor.matmul(kvp[0][:, 0:C], csT[:], wo[:], start=True, stop=True).then_inc(outed, 1)


def degree_rows(k, tag, z_d, count, out_d):
    nc = k.nc
    with ExitStack() as c:
        idx = c.enter_context(nc.sbuf_tensor(f"{tag}_idx", [P, NT], I32))
        rows = [c.enter_context(nc.sbuf_tensor(f"{tag}_rows{b}", [P, C], F32)) for b in range(4)]
        made = c.enter_context(k.semaphore(f"{tag}_made"))
        got = [c.enter_context(k.semaphore(f"{tag}_got{b}")) for b in range(4)]
        out = [c.enter_context(k.semaphore(f"{tag}_out{b}")) for b in range(4)]
        block = c.enter_context(nc.Block())

        @block.vector
        def _(dve):
            nc.vector.tensor_scalar(idx[:], count[:, 0:NT], float(z_d.shape[0] - 1), None, ALU.min
                                    ).then_inc(made, 1)

        @block.gpsimd
        def _(pool):
            pool.wait_ge(made, 1)
            for t in range(NT):
                b = t % 4
                if t >= 4:
                    pool.wait_ge(out[b], 16 * (t // 4))
                nc.gpsimd.indirect_dma_start(rows[b][:], None, z_d, bass.IndirectOffsetOnAxis(
                    ap=idx[:, t:t + 1], axis=0)).then_inc(got[b], 16)

        @block.sync
        def _(sp):
            for t in range(NT):
                b = t % 4
                sp.wait_ge(got[b], 16 * (t // 4 + 1))
                sp.dma_start(out_d[t * P:(t + 1) * P, :], rows[b][:]).then_inc(out[b], 16)
            for b in range(4):
                sp.wait_ge(out[b], 16 * ((NT - b + 3) // 4))


def graph_and_mix_stage(k, ctx, tag, x2_d, xn_d, xT, cw, edge_sum, out_deg, zin_d, zout_d, x3_d, yT_d,
                        h_d, node_h):
    nc, I = k.nc, k.ins
    with ExitStack() as c:
        def sb(name, shape, dt=F32):
            return c.enter_context(nc.sbuf_tensor(f"{tag}_{name}", shape, dt))

        def sem(name):
            return c.enter_context(k.semaphore(f"{tag}_{name}"))

        def col(v):
            return v.rearrange("n a -> (n a)")

        wq, ws, wc, bc, wv, bv, bs, bo, wg, a_src, a_dst = load_params(k, c, tag, [
            ("wq", [P, 2, P], halves(I["L1_mix_W_qkv"])[:, :, 0:P]),
            ("ws", [P, C], I["L1_gnn_W_sum"]),
            ("wc", [P, C], row_on_all(I["L1_gnn_W_cent"].rearrange("a c -> (a c)"))),
            ("bc", [P, C], row_on_all(I["L1_gnn_b_cent"])),
            ("wv", [P, C], row_on_all(I["L1_gnn_W_vor"].rearrange("a c -> (a c)"))),
            ("bv", [P, C], row_on_all(I["L1_gnn_b_vor"])),
            ("bs", [P, C], row_on_all(I["L1_gnn_b_sum"])),
            ("bo", [1, C], I["L1_mix_b_out"].unsqueeze(0)),
            ("wg", [P, 2, HG], halves(I["L1_ffn_W_gat"])),
            ("as", [P, HG], row_on_all(I["L1_ffn_att_src"].rearrange("a b -> (a b)"))),
            ("ad", [P, HG], row_on_all(I["L1_ffn_att_dst"].rearrange("a b -> (a b)")))])
        x2 = [sb(f"x2{b}", [P, C]) for b in (0, 1)]
        xn = [sb(f"xn{b}", [P, C]) for b in (0, 1)]
        zi = [sb(f"zi{b}", [P, C]) for b in (0, 1)]
        zo = [sb(f"zo{b}", [P, C]) for b in (0, 1)]
        cv = [sb(f"cv{b}", [P, 2]) for b in (0, 1)]
        es = [sb(f"es{b}", [P, P]) for b in (0, 1)]
        qT = [sb(f"qT{b}", [P, P]) for b in (0, 1)]
        cent = [sb(f"cent{b}", [P, 2, C]) for b in (0, 1)]
        x3 = [sb(f"x3{b}", [P, C]) for b in (0, 1)]
        y = [sb(f"y{b}", [P, C]) for b in (0, 1)]
        yT = [sb(f"yT{b}", [P, 2, P]) for b in (0, 1)]
        hrow = [sb(f"hrow{b}", [P, ROW + 4]) for b in (0, 1)]
        t1, st, prod = sb("t1", [P, C]), sb("st", [P, 16]), sb("prod", [P, 2, HG])
        qp = [c.enter_context(nc.psum_tensor(f"{tag}_qp{b}", [P, 512], F32)) for b in (0, 1)]
        sp_ = [c.enter_context(nc.psum_tensor(f"{tag}_sp{b}", [P, 512], F32)) for b in (0, 1)]
        yp = [c.enter_context(nc.psum_tensor(f"{tag}_yp{b}", [P, 4, P], F32)) for b in (0, 1)]
        hp = [c.enter_context(nc.psum_tensor(f"{tag}_hp{b}", [P, 512], F32)) for b in (0, 1)]
        loaded = [sem("loaded0"), sem("loaded1")]
        out = [sem("out0"), sem("out1")]
        used, asked, answered, es_ready, qp_ready, qT_ready, sum_ready, cent_ready, sig_ready = map(sem, (
            "used", "asked", "answered", "es_ready", "qp_ready", "qT_ready", "sum_ready", "cent_ready",
            "sig_ready"))
        x3_ready, y_ready, yp_ready, yT_ready, hp_ready, hrow_ready, free = map(sem, (
            "x3_ready", "y_ready", "yp_ready", "yT_ready", "hp_ready", "hrow_ready", "free"))
        block = c.enter_context(nc.Block())

        @block.sync
        def _(sp):
            sp.sem_inc(used, 2)

            def load(t, b, r):
                at = ds(t * P, r)
                sp.wait_ge(used, t + 1)
                for dst, src in ((x2, x2_d), (xn, xn_d), (zi, zin_d), (zo, zout_d)):
                    sp.dma_start(dst[b][0:r, :], src[at, :]).then_inc(loaded[b], 16)
                sp.dma_start(cv[b][0:r, 0:1], I["node_vec1_n2"][at, :]).then_inc(loaded[b], 16)
                sp.dma_start(cv[b][0:r, 1:2], I["node_vec1"][at, :]).then_inc(loaded[b], 16)
            over_tiles(sp, load)

        @block.gpsimd
        def _(pool):
            pool.sem_inc(free, 2)

            def store(t, b, r):
                at = ds(t * P, r)
                pool.wait_ge(qp_ready, t + 1)
                pool.sem_inc(k.turn, 1)
                nc.gpsimd.tensor_copy(es[b][:, 0:r], edge_sum[:, at]).then_inc(es_ready, 1)
                pool.wait_ge(hrow_ready, t + 1)
                pool.sem_inc(k.turn, 1)
                pool.dma_start(x3_d[at, :], x3[b][0:r, :]).then_inc(out[b], 16)
                pool.dma_start(yT_d[:, :, at], yT[b][:, :, 0:r]).then_inc(out[b], 16)
                pool.dma_start(h_d[at, :], hrow[b][0:r, 0:ROW]).then_inc(out[b], 16)
                pool.wait_ge(out[b], k.nth(t, b) * 48)
                pool.sem_inc(free, 1)
            over_tiles(pool, store)

        @block.vector
        def _(dve):
            dve.sem_inc(sig_ready, 2)
            nc.vector.memset(node_h[:], 0.0)
            dve.drain()

            def tile(t, b, r):
                dve.wait_ge(loaded[b], k.nth(t, b) * 96)
                for j, (w_, b_) in enumerate(((wc, bc), (wv, bv))):
                    nc.vector.scalar_tensor_tensor(cent[b][0:r, j, :], w_[0:r], cv[b][0:r, j:j + 1], b_[0:r],
                                                   ALU.mult, ALU.add)
                dve.drain().then_inc(cent_ready, 1)
                nc.vector.tensor_tensor(t1[0:r], x2[b][0:r], xn[b][0:r], ALU.add)
                dve.drain()
                nc.vector.tensor_tensor(t1[0:r], t1[0:r], zi[b][0:r], ALU.add)
                dve.drain()
                nc.vector.tensor_tensor(t1[0:r], t1[0:r], zo[b][0:r], ALU.add)
                dve.drain()
                nc.vector.scalar_tensor_tensor(t1[0:r], bs[0:r], out_deg[0:r, ds(t, 1)], t1[0:r], ALU.mult,
                                               ALU.add)
                dve.drain()
                dve.wait_ge(sig_ready, t + 3)
                nc.vector.tensor_tensor(t1[0:r], t1[0:r], cent[b][0:r, 0, :], ALU.add)
                dve.drain()
                nc.vector.tensor_tensor(t1[0:r], t1[0:r], cent[b][0:r, 1, :], ALU.add)
                dve.drain()
                dve.wait_ge(sum_ready, t + 1)
                dve.wait_ge(free, t + 1)
                nc.vector.tensor_tensor(x3[b][0:r], t1[0:r], sp_[b][0:r, 0:C], ALU.add).then_inc(x3_ready, 1)
                dve.sem_inc(used, 1)
                dve.drain()
                layer_norm(k, dve, x3[b][0:r], y[b][0:r], st, r, asked, answered, t + 1)
                dve.sem_inc(y_ready, 1)
                dve.wait_ge(hp_ready, t + 1)
                nc.vector.tensor_copy(hrow[b][0:r, 0:HG], hp[b][0:r, 0:HG])
                nc.vector.tensor_tensor(prod[0:r, 0, :], hp[b][0:r, 0:HG], a_src[0:r], ALU.mult)
                nc.vector.tensor_tensor(prod[0:r, 1, :], hp[b][0:r, 0:HG], a_dst[0:r], ALU.mult)
                dve.drain()
                nc.vector.tensor_reduce(hrow[b][0:r, HG:HG + 8].rearrange("p (a h) -> p a h", a=2),
                                        prod[0:r].rearrange("p a (h e) -> p a h e", e=4), AX_X, ALU.add)
                dve.drain()
                nc.vector.tensor_copy(node_h[0:r, ds(t, 1), :], hrow[b][0:r, :])
                dve.drain().then_inc(hrow_ready, 1)
            over_tiles(dve, tile)

        @block.scalar
        def _(act):
            def tile(t, b, r):
                act.wait_ge(cent_ready, t + 1)
                nc.scalar.activation(cent[b][0:r], cent[b][0:r], ACT.Sigmoid).then_inc(sig_ready, 1)
                act.wait_ge(qp_ready, t + 3)
                nc.scalar.copy(qT[b][:, 0:r], qp[b][:, 0:r]).then_inc(qT_ready, 1)
                root(k, act, st, r, asked, answered, t + 1)
                act.wait_ge(yp_ready, t + 1)
                nc.scalar.copy(yT[b][:, :, 0:r], yp[b][:, 0:2, 0:r]).then_inc(yT_ready, 1)
            over_tiles(act, tile)

        @block.tensor
        def _(pe):
            pe.sem_inc(qp_ready, 2)

            def tile(t, b, r):
                for half in (0, 1):
                    mm = nc.tensor.matmul(qp[b][:, 0:r], wq[:, half, :], xT[:, half, ds(t * P, r)],
                                          start=half == 0, stop=half == 1)
                mm.then_inc(qp_ready, 1)
                pe.wait_ge(es_ready, t + 1)
                pe.wait_ge(qT_ready, t + 1)
                nc.tensor.matmul(sp_[b][0:r, 0:C], k.ones[0:1, 0:r], bo[:], start=True, stop=False)
                nc.tensor.matmul(sp_[b][0:r, 0:C], es[b][:, 0:r], ws[:], start=False, stop=False)
                nc.tensor.matmul(sp_[b][0:r, 0:C], qT[b][:, 0:r], cw[:], start=False, stop=True
                                 ).then_inc(sum_ready, 1)
                pe.wait_ge(y_ready, t + 1)
                for half in (0, 1):
                    mm = nc.tensor.transpose(yp[b][:, half, 0:r], y[b][0:r, half * P:(half + 1) * P],
                                             k.ident[0:r, 0:r])
                mm.then_inc(yp_ready, 1)
                pe.wait_ge(yT_ready, t + 1)
                for half in (0, 1):
                    mm = nc.tensor.matmul(hp[b][0:r, 0:HG], yT[b][:, half, 0:r], wg[:, half, :],
                                          start=half == 0, stop=half == 1)
                mm.then_inc(hp_ready, 1)
            over_tiles(pe, tile)


J = G // P
LOW = -1.0e38


def carry_in(k, ctx, tag, last, factor, K, op0, op1, init):
    nc = k.nc
    cin = ctx.enter_context(nc.sbuf_tensor(f"{tag}_cin", [P, K], F32))
    with ExitStack() as c:
        rows = [c.enter_context(nc.sbuf_tensor(f"{tag}_row{n}", [K, P], F32)) for n in (0, 1)]
        state = c.enter_context(nc.sbuf_tensor(f"{tag}_state", [K, P + 1], F32))
        turned = [c.enter_context(nc.psum_tensor(f"{tag}_turn{n}", [P, 512], F32)) for n in range(3)]
        there, scanned, back = [c.enter_context(k.semaphore(f"{tag}_{n}")) for n in ("there", "scanned", "back")]
        block = c.enter_context(nc.Block())

        @block.tensor
        def _(pe):
            nc.tensor.transpose(turned[0][0:K, 0:P], last[:], k.ident[:])
            nc.tensor.transpose(turned[1][0:K, 0:P], factor[:], k.ident[:]).then_inc(there, 1)
            pe.wait_ge(scanned, 1)
            nc.tensor.transpose(turned[2][:, 0:K], state[:, 0:P], k.ident[0:K, 0:K]).then_inc(back, 1)

        @block.vector
        def _(dve):
            nc.vector.memset(state[:, 0:1], init)
            dve.wait_ge(there, 1)
            for n in (0, 1):
                nc.vector.tensor_copy(rows[n][:], turned[n][0:K, 0:P])
            dve.drain()
            nc.vector.tensor_tensor_scan(state[:, 1:P + 1], rows[1][:], rows[0][:], init, op0, op1)
            dve.drain().then_inc(scanned, 1)
            dve.wait_ge(back, 1)
            nc.vector.tensor_copy(cin[:], turned[2][:, 0:K])
    return cin


def node_targets(k, ctx, tag, start, count):
    nc = k.nc
    first = ctx.enter_context(nc.sbuf_tensor(f"{tag}_first_i", [P, NT], I32))
    last = ctx.enter_context(nc.sbuf_tensor(f"{tag}_last_i", [P, NT], I32))
    some = ctx.enter_context(nc.sbuf_tensor(f"{tag}_some", [P, NT], F32))
    with (nc.sbuf_tensor(f"{tag}_spare", [P, 1], F32) as spare,
          nc.sbuf_tensor(f"{tag}_a", [P, NT], F32) as a,
          nc.sbuf_tensor(f"{tag}_b", [P, NT], F32) as b,
          nc.Block() as block):
        @block.vector
        def _(dve):
            s, n = start[:, 0:NT], count[:, 0:NT]
            nc.vector.tensor_scalar(some[:], n, 0.0, None, ALU.is_gt)
            nc.vector.tensor_scalar(spare[:], k.lane[:], float(G), None, ALU.add)
            nc.vector.tensor_tensor(b[:], s, n, ALU.add)
            dve.drain()
            nc.vector.tensor_scalar(last[:], b[:], -1.0, 0.0, ALU.add, ALU.max)
            nc.vector.tensor_scalar(a[:], s, spare[:, 0:1], None, ALU.subtract)
            dve.drain()
            nc.vector.tensor_tensor(a[:], a[:], some[:], ALU.mult)
            dve.drain()
            nc.vector.tensor_scalar(first[:], a[:], spare[:, 0:1], None, ALU.add)
    return first, last, some


def spread_to_starts(k, tag, node_h, first_i, adst_d):
    nc = k.nc
    with ExitStack() as c:
        zero = c.enter_context(nc.sbuf_tensor(f"{tag}_zero", [P, J * 4], F32))
        rows = c.enter_context(nc.sbuf_tensor(f"{tag}_rows", [P, NT, 4], F32))
        made, cleared, done = [c.enter_context(k.semaphore(f"{tag}_{n}")) for n in ("made", "cleared", "done")]
        block = c.enter_context(nc.Block())

        @block.vector
        def _(dve):
            nc.vector.memset(zero[:], 0.0)
            nc.vector.tensor_copy(rows[:], node_h[:, :, ROW:ROW + 4])
            dve.drain().then_inc(made, 1)

        @block.sync
        def _(sp):
            sp.wait_ge(made, 1)
            sp.dma_start(adst_d[0:G, :].rearrange("(p j) h -> p (j h)", p=P), zero[:]).then_inc(cleared, 16)

        @block.gpsimd
        def _(pool):
            pool.wait_ge(cleared, 16)
            for t in range(NT):
                nc.gpsimd.indirect_dma_start(adst_d, bass.IndirectOffsetOnAxis(ap=first_i[:, t:t + 1], axis=0),
                                             rows[:, t, :], None).then_inc(done, 16)
            pool.wait_ge(done, 16 * NT)


def gather_edges(k, tag, sorted_d, table, edge, same):
    nc = k.nc
    R = 8
    with ExitStack() as c:
        idx_all = c.enter_context(nc.sbuf_tensor(f"{tag}_idx_all", [P, J], I32))
        with (nc.sbuf_tensor(f"{tag}_cur", [P, J, 2], F32) as cur,
              nc.sbuf_tensor(f"{tag}_prev", [P, J, 2], F32) as prev,
              k.semaphore(f"{tag}_lists_in") as lists_in, nc.Block() as block):
            @block.sync
            def _(sp):
                for tile, at in ((cur, 1), (prev, 0)):
                    sp.dma_start(tile[:], sorted_d[at:at + G, :].rearrange("(p j) w -> p j w", p=P)
                                 ).then_inc(lists_in, 16)

            @block.vector
            def _(dve):
                dve.wait_ge(lists_in, 32)
                nc.vector.tensor_copy(idx_all[:], cur[:, :, 0])
                nc.vector.tensor_tensor(same[:], cur[:, :, 1], prev[:, :, 1], ALU.is_equal)

        idx = [c.enter_context(nc.sbuf_tensor(f"{tag}_idx{h}", [P, R], I32)) for h in (0, 1)]
        got = [c.enter_context(nc.sbuf_tensor(f"{tag}_got{h}", [P, R, ROW], F32)) for h in (0, 1)]
        gathered = [c.enter_context(k.semaphore(f"{tag}_gathered{h}")) for h in (0, 1)]
        moved = c.enter_context(k.semaphore(f"{tag}_moved"))
        idx_ready = c.enter_context(k.semaphore(f"{tag}_idx_ready"))
        block = c.enter_context(nc.Block())

        @block.gpsimd
        def _(pool):
            pool.sem_inc(moved, 2)
            with pool.Fori(0, J // (2 * R)) as i:
                for h in (0, 1):
                    pool.wait_ge(moved, 2 * i + h + 1)
                    pool.sem_inc(k.turn, 1)
                    nc.gpsimd.tensor_copy(idx[h][:], idx_all[:, ds((2 * i + h) * R, R)]).then_inc(idx_ready, 1)
                    pool.wait_ge(idx_ready, 2 * i + h + 1)
                    pool.sem_inc(k.turn, 1)
                    for b in range(R):
                        nc.gpsimd.indirect_dma_start(got[h][:, b, :], None, table, bass.IndirectOffsetOnAxis(
                            ap=idx[h][:, b:b + 1], axis=0)).then_inc(gathered[h], 16)

        @block.scalar
        def _(act):
            with act.Fori(0, J // (2 * R)) as i:
                for h in (0, 1):
                    act.wait_ge(gathered[h], 16 * R * i + 16 * R)
                    nc.scalar.copy(edge[:, ds((2 * i + h) * R, R), :], got[h][:]).then_inc(moved, 1)


def leaky(nc, out, x):
    nc.vector.scalar_tensor_tensor(out, x, 0.2, x, ALU.mult, ALU.max)


def edge_softmax(k, tag, edge, same, adst_d, seg_d, segm_d):
    nc = k.nc
    with ExitStack() as c:
        def sb(name, shape, dt=F32):
            return c.enter_context(nc.sbuf_tensor(f"{tag}_{name}", shape, dt))

        a_dst, top = sb("a_dst", [P, J, 4]), sb("top", [P, J, 4])
        pen, junk = sb("pen", [P, J]), sb("junk", [P, J])
        all_same, all_pen = sb("all_same", [P, 4]), sb("all_pen", [P, 4])
        last4, last20 = sb("last4", [P, 4]), sb("last20", [P, ROW])
        a_src = edge[:, :, HG:ROW]
        same4 = same[:].unsqueeze(2).broadcast_to([P, J, 4])

        with k.semaphore(f"{tag}_a_in") as a_in, nc.Block() as block:
            @block.sync
            def _(sp):
                sp.dma_start(a_dst[:], adst_d[0:G, :].rearrange("(p j) h -> p j h", p=P)).then_inc(a_in, 16)

            @block.vector
            def _(dve):
                nc.vector.tensor_reduce(all_same[:, 0:1], same[:], AX_X, ALU.min)
                nc.vector.tensor_scalar(pen[:], same[:], -1.0, -LOW, ALU.add, ALU.mult)
                dve.drain()
                for h in (1, 2, 3):
                    nc.vector.tensor_copy(all_same[:, h:h + 1], all_same[:, 0:1])
                dve.drain()
                nc.vector.tensor_scalar(all_pen[:], all_same[:], -1.0, -LOW, ALU.add, ALU.mult)
                dve.wait_ge(a_in, 16)
                for h in range(4):
                    nc.vector.tensor_tensor_scan(junk[:], same[:], a_dst[:, :, h], 0.0, ALU.mult, ALU.add)
                    dve.drain()
                    nc.vector.tensor_copy(last4[:, h:h + 1], junk[:, J - 1:J])
                    dve.drain()
        fill_in = carry_in(k, c, f"{tag}_c1", last4, all_same, 4, ALU.mult, ALU.add, 0.0)

        with nc.Block() as block:
            @block.vector
            def _(dve):
                for h in range(4):
                    nc.vector.tensor_tensor_scan(a_dst[:, :, h], same[:], a_dst[:, :, h],
                                                 fill_in[:, h:h + 1], ALU.mult, ALU.add)
                    nc.vector.tensor_tensor_scan(junk[:], pen[:], a_src[:, :, h], LOW, ALU.add, ALU.max)
                    dve.drain()
                    nc.vector.tensor_copy(last4[:, h:h + 1], junk[:, J - 1:J])
                    dve.drain()
        top_in = carry_in(k, c, f"{tag}_c2", last4, all_pen, 4, ALU.add, ALU.max, LOW)

        decay = a_dst
        before0, factor = sb("before0", [P, 4]), sb("factor", [P, ROW])
        with k.semaphore(f"{tag}_asked") as asked, k.semaphore(f"{tag}_answered") as answered, \
                nc.Block() as block:
            @block.vector
            def _(dve):
                for h in range(4):
                    nc.vector.tensor_tensor_scan(top[:, :, h], pen[:], a_src[:, :, h], top_in[:, h:h + 1],
                                                 ALU.add, ALU.max)
                dve.drain()
                nc.vector.tensor_tensor(top[:], top[:], a_dst[:], ALU.add)
                nc.vector.tensor_tensor(a_src, a_src, a_dst[:], ALU.add)
                nc.vector.tensor_tensor(before0[:], top_in[:], a_dst[:, 0, :], ALU.add)
                dve.drain()
                leaky(nc, top[:], top[:])
                leaky(nc, a_src, a_src)
                leaky(nc, before0[:], before0[:])
                dve.drain()
                nc.vector.tensor_tensor(a_src, a_src, top[:], ALU.subtract).then_inc(asked, 1)
                nc.vector.tensor_tensor(decay[:, 1:J, :], top[:, 0:J - 1, :], top[:, 1:J, :], ALU.subtract)
                nc.vector.tensor_tensor(decay[:, 0, :], before0[:], top[:, 0, :], ALU.subtract)
                nc.vector.tensor_tensor(factor[:, 0:4], before0[:], top[:, J - 1, :], ALU.subtract)
                dve.drain()
                nc.vector.tensor_scalar(decay[:], decay[:], 0.0, None, ALU.min).then_inc(asked, 1)
                nc.vector.tensor_scalar(factor[:, 0:4], factor[:, 0:4], 0.0, None, ALU.min).then_inc(asked, 1)
                dve.wait_ge(answered, 3)
                nc.vector.tensor_tensor(decay[:], decay[:], same4, ALU.mult)
                nc.vector.tensor_tensor(factor[:, HG:ROW], factor[:, 0:4], all_same[:], ALU.mult)
                h16 = edge[:, :, 0:HG].rearrange("p j (h e) -> p j h e", e=4)
                for h in range(4):
                    nc.vector.tensor_tensor(h16[:, :, h, :], h16[:, :, h, :],
                                            a_src[:, :, h].unsqueeze(2).broadcast_to([P, J, 4]), ALU.mult)
                dve.drain()
                for h in range(4):
                    nc.vector.tensor_scalar(factor[:, 4 * h:4 * h + 4], k.ones[:, 0:4],
                                            factor[:, HG + h:HG + h + 1], None, ALU.mult)
                for f in range(ROW):
                    h = f // 4 if f < HG else f - HG
                    nc.vector.tensor_tensor_scan(junk[:], decay[:, :, h], edge[:, :, f], 0.0, ALU.mult, ALU.add)
                    dve.drain()
                    nc.vector.tensor_copy(last20[:, f:f + 1], junk[:, J - 1:J])
                    dve.drain()

            @block.scalar
            def _(act):
                for n, x in enumerate((a_src, decay[:], factor[:, 0:4])):
                    act.wait_ge(asked, n + 1)
                    nc.scalar.activation(x, x, ACT.Exp).then_inc(answered, 1)
        sum_in = carry_in(k, c, f"{tag}_c3", last20, factor, ROW, ALU.mult, ALU.add, 0.0)

        with k.semaphore(f"{tag}_ran") as ran, k.semaphore(f"{tag}_stored") as stored, nc.Block() as block:
            @block.vector
            def _(dve):
                for f in range(ROW):
                    h = f // 4 if f < HG else f - HG
                    nc.vector.tensor_tensor_scan(edge[:, :, f], decay[:, :, h], edge[:, :, f],
                                                 sum_in[:, f:f + 1], ALU.mult, ALU.add)
                dve.drain().then_inc(ran, 1)

            @block.sync
            def _(sp):
                sp.dma_start(segm_d.rearrange("(p j) w -> p j w", p=P), top[:]).then_inc(stored, 16)
                sp.wait_ge(ran, 1)
                sp.dma_start(seg_d.rearrange("(p j) w -> p j w", p=P), edge[:]).then_inc(stored, 16)
                sp.wait_ge(stored, 32)


def node_gates(k, tag, node_h, last_i, some, seg_d, segm_d, gates):
    nc, I = k.nc, k.ins
    with ExitStack() as c:
        def sb(name, shape, dt=F32):
            return c.enter_context(nc.sbuf_tensor(f"{tag}_{name}", shape, dt))

        b_gat, gamma, beta = load_params(k, c, tag, [
            ("bg", [P, HG], row_on_all(I["L1_ffn_b_gat"])), ("gamma", [P, HG], row_on_all(I["L1_ffn_ln_gamma"])),
            ("beta", [P, HG], row_on_all(I["L1_ffn_ln_beta"]))])
        sums, top = sb("sums", [P, NT, ROW]), sb("top", [P, NT, 4])
        loop, best, c1, c2 = (sb(n, [P, NT, 4]) for n in ("loop", "best", "c1", "c2"))
        agg, tmp = sb("agg", [P, NT, HG]), sb("tmp", [P, NT, HG])
        den, mean, var, gone = sb("den", [P, NT, 4]), sb("mean", [P, NT]), sb("var", [P, NT]), sb("gone", [P, NT])
        score = sb("score", [P, NT, 4])
        bufs = gate_buffers(k, c, tag, 4)
        got = c.enter_context(k.semaphore(f"{tag}_got"))
        asked = c.enter_context(k.semaphore(f"{tag}_asked"))
        answered = c.enter_context(k.semaphore(f"{tag}_answered"))
        block = c.enter_context(nc.Block())

        def wide(a, n):
            return a.unsqueeze(2).broadcast_to([P, NT, n])

        def by_head(a):
            return a.unsqueeze(3).broadcast_to([P, NT, 4, 4])

        def h4(a):
            return a.rearrange("p t (h e) -> p t h e", e=4)

        def param(v):
            return v[:].unsqueeze(1).broadcast_to([P, NT, HG])

        @block.gpsimd
        def _(pool):
            for t in range(NT):
                at = bass.IndirectOffsetOnAxis(ap=last_i[:, t:t + 1], axis=0)
                nc.gpsimd.indirect_dma_start(sums[:, t, :], None, seg_d, at).then_inc(got, 16)
                at = bass.IndirectOffsetOnAxis(ap=last_i[:, t:t + 1], axis=0)
                nc.gpsimd.indirect_dma_start(top[:, t, :], None, segm_d, at).then_inc(got, 16)

        @block.scalar
        def _(act):
            act.wait_ge(asked, 1)
            nc.scalar.activation(c1[:], c1[:], ACT.Exp)
            nc.scalar.activation(c2[:], c2[:], ACT.Exp)
            act.drain().then_inc(answered, 1)
            act.wait_ge(asked, 2)
            nc.scalar.activation(var[:], var[:], ACT.Sqrt, bias=k.eps[:, 0:1], scale=1.0 / HG).then_inc(answered, 1)
            act.wait_ge(asked, 3)
            nc.scalar.activation(bufs[5][:], bufs[5][:], ACT.Exp).then_inc(answered, 1)

        @block.vector
        def _(dve):
            def then(ins):
                dve.drain()

            h = node_h[:, :, 0:HG]
            then(nc.vector.tensor_tensor(loop[:], node_h[:, :, HG:ROW], node_h[:, :, ROW:ROW + 4], ALU.add))
            then(leaky(nc, loop[:], loop[:]))
            then(nc.vector.tensor_scalar(gone[:], some[:], -1.0, -LOW, ALU.add, ALU.mult))
            dve.wait_ge(got, 32 * NT)
            then(nc.vector.tensor_tensor(top[:], top[:], wide(some[:], 4), ALU.mult))
            then(nc.vector.tensor_tensor(top[:], top[:], wide(gone[:], 4), ALU.add))
            then(nc.vector.tensor_tensor(best[:], top[:], loop[:], ALU.max))
            nc.vector.tensor_tensor(c1[:], top[:], best[:], ALU.subtract)
            nc.vector.tensor_tensor(c2[:], loop[:], best[:], ALU.subtract)
            dve.drain().then_inc(asked, 1)
            dve.wait_ge(answered, 1)
            then(nc.vector.tensor_tensor(den[:], sums[:, :, HG:ROW], c1[:], ALU.mult))
            then(nc.vector.tensor_tensor(den[:], den[:], c2[:], ALU.add))
            then(nc.vector.tensor_scalar(den[:], den[:], 1e-16, None, ALU.add))
            then(nc.vector.reciprocal(best[:], den[:]))
            nc.vector.tensor_tensor(c1[:], c1[:], best[:], ALU.mult)
            then(nc.vector.tensor_tensor(c2[:], c2[:], best[:], ALU.mult))
            nc.vector.tensor_tensor(h4(agg[:]), h4(sums[:, :, 0:HG]), by_head(c1[:]), ALU.mult)
            then(nc.vector.tensor_tensor(h4(tmp[:]), h4(h), by_head(c2[:]), ALU.mult))
            then(nc.vector.tensor_tensor(agg[:], agg[:], tmp[:], ALU.add))
            then(nc.vector.tensor_tensor(agg[:], agg[:], param(b_gat), ALU.add))
            then(nc.vector.tensor_reduce(mean[:], agg[:], AX_X, ALU.add))
            then(nc.vector.tensor_scalar(mean[:], mean[:], 1.0 / HG, None, ALU.mult))
            then(nc.vector.tensor_tensor(agg[:], agg[:], wide(mean[:], HG), ALU.subtract))
            then(nc.vector.tensor_tensor(tmp[:], agg[:], agg[:], ALU.mult))
            nc.vector.tensor_reduce(var[:], tmp[:], AX_X, ALU.add).then_inc(asked, 1)
            dve.wait_ge(answered, 2)
            then(nc.vector.reciprocal(mean[:], var[:]))
            then(nc.vector.tensor_tensor(agg[:], agg[:], wide(mean[:], HG), ALU.mult))
            then(nc.vector.tensor_tensor(agg[:], agg[:], param(gamma), ALU.mult))
            then(nc.vector.tensor_tensor(agg[:], agg[:], param(beta), ALU.add))
            then(nc.vector.tensor_reduce(score[:], agg[:].rearrange("p t (h e) -> p t e h", e=4), AX_X, ALU.add))
            then(nc.vector.tensor_scalar(score[:], score[:], 0.25, None, ALU.mult))
            top_two(k, dve, score, gates, 4, asked, answered, 3, bufs)


NAMES = ['x', 'src', 'dst', 'edge_attr_128', 'edge_weight', 'node_vec1', 'node_vec1_n2', 'L0_gnn_c1_w1',
         'L0_gnn_c1_b1', 'L0_gnn_c1_w2', 'L0_gnn_c1_b2', 'L0_gnn_c1_g', 'L0_gnn_c1_b', 'L0_gnn_bn1_g',
         'L0_gnn_bn1_b', 'L0_gnn_c2_w1', 'L0_gnn_c2_b1', 'L0_gnn_c2_w2', 'L0_gnn_c2_b2', 'L0_gnn_c2_g',
         'L0_gnn_c2_b', 'L0_gnn_bn2_g', 'L0_gnn_bn2_b', 'L0_mix_kln_weight', 'L0_mix_kln_bias',
         'L0_mix_vln_weight', 'L0_mix_vln_bias', 'L0_ffn_gamma', 'L0_ffn_beta', 'L0_ffn_Wr', 'L0_ffn_br',
         'L0_ffn_W1', 'L0_ffn_b1', 'L0_ffn_W2', 'L0_ffn_b2', 'L1_gnn_z_in', 'L1_gnn_z_out', 'L1_gnn_W_cent',
         'L1_gnn_b_cent', 'L1_gnn_W_vor', 'L1_gnn_b_vor', 'L1_gnn_W_sum', 'L1_gnn_b_sum', 'L1_mix_W_qkv',
         'L1_mix_W_out', 'L1_mix_b_out', 'L1_ffn_W_gat', 'L1_ffn_att_src', 'L1_ffn_att_dst', 'L1_ffn_b_gat',
         'L1_ffn_ln_gamma', 'L1_ffn_ln_beta', 'L1_ffn_W1', 'L1_ffn_b1', 'L1_ffn_W2', 'L1_ffn_b2',
         'L1_ffn_edge_index']


def load_attributes(k, rest_in):
    attr = k.ins["edge_attr_128"]
    Q = 8

    def fill(sp, pay, n, last, sem, turn):
        full, rest = Q, 0
        if last:
            full, rest = divmod(E - n * Q * P, P)
            if full >= Q:
                full, rest = Q, 0
            if rest:
                sp.dma_start(pay[0:rest, full, 0:P], attr[E - rest:E, :]).then_inc(rest_in, 16)
                sp.wait_ge(rest_in, 16)
        sp.dma_start(pay[:, 0:full, 0:P], attr[ds(n * Q * P, full * P), :].rearrange("(b p) f -> p b f", p=P)
                     ).then_inc(sem, 16)
    return fill


def first_node_columns(k, tag, tile_row_d, out):
    nc = k.nc
    with (nc.sbuf_tensor(f"{tag}_fi", [P, NSB * P], I32) as raw,
          k.semaphore(f"{tag}_fin") as landed, nc.Block() as block):
        @block.sync
        def _(sp):
            sp.dma_start(raw[:], row_on_all(tile_row_d)).then_inc(landed, 16)

        @block.vector
        def _(dve):
            dve.wait_ge(landed, 16)
            nc.vector.tensor_scalar(out[:], raw[:], float(P), None, ALU.mult)


def build(nc, ins, out):
    k = Kernel(nc, ins, out)
    I = ins
    h_d = k.dram("h_d", (N, C))
    x1_d, x2_d, x3_d, xn_d = (k.dram(n, (N, C)) for n in ("x1_d", "x2_d", "x3_d", "xn_d"))
    yT_d, y2T_d = k.dram("yT_d", (P, 2, NP)), k.dram("y2T_d", (P, 2, NP))
    zin_d, zout_d = k.dram("zin_d", (NP, C)), k.dram("zout_d", (NP, C))
    attr_sorted_d = k.dram("attr_sorted_d", (EP, P + 1))
    gat_sorted_d = k.dram("gat_sorted_d", (G + 1, 2))
    gat_rows_d = k.dram("gat_rows_d", (N, ROW))
    adst_d, seg_d, segm_d = k.dram("adst_d", (G + P, 4)), k.dram("seg_d", (G, ROW)), k.dram("segm_d", (G, 4))

    with ExitStack() as top:
        def keep(name, shape, dt=F32):
            return top.enter_context(nc.sbuf_tensor(name, shape, dt))

        k.turn = top.enter_context(k.semaphore("turn"))
        rest_in = top.enter_context(k.semaphore("rest_in"))
        constants(k, top)
        in_deg, in_start, in_tiles = (keep(f"dst_{n}", [P, NHI]) for n in ("count", "start", "tiles"))
        out_deg, out_start, out_tiles = (keep(f"src_{n}", [P, NHI]) for n in ("count", "start", "tiles"))
        gat_count, gat_start, gat_tiles = (keep(f"gat_{n}", [P, NHI]) for n in ("count", "start", "tiles"))
        gates8, gates4 = keep("gates8", [P, NT, 8]), keep("gates4", [P, NT, 4])

        with ExitStack() as c:
            rows, low, (gsrc, gdst) = edge_keys(k, c, "g", CG, G, [
                ("src", I["L1_ffn_edge_index"][0]), ("dst", I["L1_ffn_edge_index"][1])],
                [N - 1, N], [0, 0], 1)
            lo, hi = digits(k, c, "gd", gdst, CG)
            histogram(k, "gd", lo, hi, CG, gat_count)
            prefix(k, "gd", gat_count, gat_start, gat_tiles)
            shifted = c.enter_context(nc.sbuf_tensor("gat_shifted", [P, NHI], F32))
            first = c.enter_context(nc.sbuf_tensor("gat_first_row", [1, 2], F32))
            with k.semaphore("gat_minus") as made, k.semaphore("gat_zeroth") as stored, nc.Block() as block:
                @block.vector
                def _(dve):
                    nc.vector.tensor_scalar(shifted[:], gat_start[:], 1.0, None, ALU.add)
                    nc.vector.memset(first[:], -1.0).then_inc(made, 1)

                @block.sync
                def _(sp):
                    sp.wait_ge(made, 1)
                    sp.dma_start(gat_sorted_d[0:1, :], first[:]).then_inc(stored, 16)
                    sp.wait_ge(stored, 16)
            sort_edges(k, c, "gs", CG, gdst, lo, hi, shifted, rows[:, 1, :], low,
                       [(0, gsrc), (1, gdst)], 2, None, gat_sorted_d)

        with ExitStack() as c:
            conv_tile_row = c.enter_context(nc.sbuf_tensor("conv_tile_row", [1, NSB * P], I32))
            sum_tile_row = c.enter_context(nc.sbuf_tensor("sum_tile_row", [1, NSB * P], I32))
            sum_chunk_row = c.enter_context(nc.sbuf_tensor("sum_chunk_row", [1, NSB * P], I32))
            src_i = c.enter_context(nc.sbuf_tensor("conv_src", [P, NSB * P], I32))
            rel = c.enter_context(nc.sbuf_tensor("conv_rel", [P, NSB * P], F32))
            weight = c.enter_context(nc.sbuf_tensor("conv_weight", [P, NSB * P], F32))
            with ExitStack() as c2:
                rows, low, (esrc, edst, _) = edge_keys(k, c2, "e", CE, E, [
                    ("src", I["src"]), ("dst", I["dst"]), ("weight", I["edge_weight"])],
                    [None] * 3, [PAD_KEY, PAD_KEY, 0.0], 0)
                dlo, dhi = digits(k, c2, "ed", edst, CE)
                histogram(k, "ed", dlo, dhi, CE, in_deg)
                slo, shi = digits(k, c2, "es", esrc, CE)
                histogram(k, "es", slo, shi, CE, out_deg)
                prefix(k, "ed", in_deg, in_start, in_tiles)
                prefix(k, "es", out_deg, out_start, out_tiles)
                tile, chunk = schedule(k, c2, "ed", in_tiles)
                step_columns(k, "ed", rows, tile, chunk, src_i, rel, weight)
                step_registers(k, "ed_tile", tile, conv_tile_row)
                tile, chunk = schedule(k, c2, "es", out_tiles)
                step_registers(k, "es_tile", tile, sum_tile_row)
                step_registers(k, "es_chunk", chunk, sum_chunk_row)
                sort_edges(k, c2, "ss", CE, esrc, slo, shi, out_start, rows[:, 0, :], low, [(P, esrc)],
                           P + 1, load_attributes(k, rest_in), attr_sorted_d)

            with ExitStack() as c2:
                kv = c2.enter_context(nc.sbuf_tensor("kv", [P, 2, P], F32))
                acc = c2.enter_context(nc.sbuf_tensor("acc", [P, 2, NP], F32))
                input_stage(k, c2, "in", h_d, kv)
                aggregate(k, "a1", h_d, src_i, rel, weight, conv_tile_row, acc)
                dense_and_norms(k, c2, "n1", acc, "L0_gnn_c1_w2", "L0_gnn_c1_b2", [
                    ("L0_gnn_c1_g", "L0_gnn_c1_b", True), ("L0_gnn_bn1_g", "L0_gnn_bn1_b", True)])
                rows_from_channels(k, c2, "rc", acc, h_d, "L0_gnn_c2_w1", "L0_gnn_c2_b1")
                aggregate(k, "a2", h_d, src_i, rel, weight, conv_tile_row, acc)
                dense_and_norms(k, c2, "n2", acc, "L0_gnn_c2_w2", "L0_gnn_c2_b2", [
                    ("L0_gnn_c2_g", "L0_gnn_c2_b", True), ("L0_gnn_bn2_g", "L0_gnn_bn2_b", False)])
                mix_and_gate_stage(k, c2, "mg", acc, kv, x1_d, yT_d, gates8)
            expert_stage(k, c, "e0", 8, yT_d, x1_d, x2_d, gates8, "L0_ffn_W1", "L0_ffn_b1", "L0_ffn_W2",
                         "L0_ffn_b2")

            edge_sum = c.enter_context(nc.sbuf_tensor("edge_sum", [P, NP], F32))
            with ExitStack() as c2:
                first_all = c2.enter_context(nc.sbuf_tensor("first_all", [P, NSB * P], F32))
                first_node_columns(k, "fa", k.buffers["es_tile_row_d"], first_all)
                segment_sum(k, "sm", attr_sorted_d, P, sum_chunk_row, first_all, sum_tile_row, edge_sum)
            degree_rows(k, "di", I["L1_gnn_z_in"], in_deg, zin_d)
            degree_rows(k, "do", I["L1_gnn_z_out"], out_deg, zout_d)
            node_h = c.enter_context(nc.sbuf_tensor("node_h", [P, NT, ROW + 4], F32))
            with ExitStack() as c2:
                xT = c2.enter_context(nc.sbuf_tensor("xT", [P, 2, NP], F32))
                kmax = c2.enter_context(nc.sbuf_tensor("kmax", [P, 1], F32))
                cw = c2.enter_context(nc.sbuf_tensor("cw", [P, C], F32))
                channels_stage(k, c2, "cs", x2_d, xn_d, xT, kmax)
                context_stage(k, c2, "cx", xT, kmax, cw)
                graph_and_mix_stage(k, c2, "gm", x2_d, xn_d, xT, cw, edge_sum, out_deg, zin_d, zout_d,
                                    x3_d, y2T_d, gat_rows_d, node_h)

            first_i, last_i, some = node_targets(k, c, "nt", gat_start, gat_count)
            spread_to_starts(k, "sp", node_h, first_i, adst_d)
            node_gates_in = (node_h, last_i, some, seg_d, segm_d, gates4)
            with ExitStack() as c2:
                edge = c2.enter_context(nc.sbuf_tensor("edge", [P, J, ROW], F32))
                same = c2.enter_context(nc.sbuf_tensor("same", [P, J], F32))
                gather_edges(k, "ge", gat_sorted_d, gat_rows_d, edge, same)
                edge_softmax(k, "ex", edge, same, adst_d, seg_d, segm_d)
            node_gates(k, "ng", *node_gates_in)
        expert_stage(k, top, "e1", 4, y2T_d, x3_d, out, gates4, "L1_ffn_W1", "L1_ffn_b1", "L1_ffn_W2",
                     "L1_ffn_b2")


def kernel(**inputs):
    import concourse.bacc as bacc
    from concourse.bass_utils import run_bass_kernel_spmd

    nc = bacc.Bacc("TRN2", target_bir_lowering=False, num_devices=1)
    arrays, ins = {}, {}
    for name in NAMES:
        a = np.ascontiguousarray(inputs[name])
        arrays[f"in_{name}"] = a
        ins[name] = nc.dram_tensor(f"in_{name}", a.shape, mybir.dt.from_np(a.dtype), kind="ExternalInput").ap()
    out = nc.dram_tensor("out_0", (N, C), F32, kind="ExternalOutput").ap()
    build(nc, ins, out)
    r = run_bass_kernel_spmd(nc, [arrays], core_ids=[0])
    return r.results[0]["out_0"]
```

```python
from contextlib import ExitStack, contextmanager

import numpy as np
import concourse.bass as bass
from concourse import mybir

F32 = mybir.dt.float32
BF16 = mybir.dt.bfloat16
I32 = mybir.dt.int32
ALU = mybir.AluOpType
ACT = mybir.ActivationFunctionType
AX_X = mybir.AxisListType.X

P = 128
N = 6250
C = 256
NT = 49
NP = NT * P
REAL_T = -(-N // P)
LAST = N - (REAL_T - 1) * P
E = 100000
CE = 784
EP = CE * P
G = 131072
CG = G // P
NHI = 64
PAD_KEY = NHI * P - 1
NS = 832
NSB = 7
NEG = -3.0e38
EPS = 1e-5


def ds(start, n):
    return bass.ds(start, n)


class Kernel:

    def __init__(self, nc, ins, out):
        self.nc, self.ins, self.out = nc, ins, out
        self.buffers = {}
        self.retired = []

    @contextmanager
    def semaphore(self, name):
        if len(self.retired) > 64:
            self.nc.clear_and_free_semaphores(self.retired)
            self.nc.all_engine_barrier()
            self.retired = []
        sem = self.nc.alloc_semaphore(name)
        yield sem
        self.retired.append(sem)

    @staticmethod
    def nth(t, b):
        return t // 2 + 1 if isinstance(t, int) else (t - b) // 2 + 1

    def dram(self, name, shape, dt=F32):
        t = self.nc.dram_tensor(name, shape, dt, kind="Internal").ap()
        self.buffers[name] = t
        return t


def constants(k, ctx):
    nc = k.nc

    def sb(name, shape, dt=F32):
        return ctx.enter_context(nc.sbuf_tensor(name, shape, dt))

    ident = sb("ident", [P, P])
    ones = sb("ones", [P, P])
    before = sb("before", [P, P])
    block_diag = sb("block_diag", [P, P])
    ramp = sb("ramp", [P, P])
    ramp_bf = sb("ramp_bf", [P, P], BF16)
    lane = sb("lane", [P, 1])
    eps = sb("eps", [P, 1])
    minus_lane = sb("minus_lane", [P, 1])
    ramp_8 = sb("ramp_8", [P, P, 8], BF16)
    lane_i = sb("lane_i", [P, 1], I32)
    ramp_i = sb("ramp_i", [P, P], I32)
    k.ident, k.ones, k.before, k.block_diag, k.ramp, k.ramp_bf, k.lane, k.eps = (
        ident, ones, before, block_diag, ramp, ramp_bf, lane, eps)
    k.minus_lane, k.ramp_8 = minus_lane, ramp_8
    with k.semaphore("const_made") as made, nc.Block() as block:
        @block.gpsimd
        def _(pool):
            nc.gpsimd.memset(ones[:], 1.0).then_inc(made, 1)
            nc.gpsimd.iota(ramp_i[:], [[1, P]], base=0, channel_multiplier=0).then_inc(made, 1)
            nc.gpsimd.iota(lane_i[:], [[1, 1]], base=0, channel_multiplier=1).then_inc(made, 1)
            pool.wait_ge(made, 3)
            nc.gpsimd.affine_select(out=ident[:], in_=ones[:], pattern=[[-1, P]], compare_op=ALU.is_equal,
                                    fill=0.0, base=0, channel_multiplier=1)
            nc.gpsimd.affine_select(out=before[:], in_=ones[:], pattern=[[1, P]], compare_op=ALU.is_gt,
                                    fill=0.0, base=0, channel_multiplier=-1)
            for q in range(4):
                cols = slice(32 * q, 32 * q + 32)
                nc.gpsimd.affine_select(out=block_diag[:, cols], in_=ones[:, cols], pattern=[[0, 32]],
                                        compare_op=ALU.is_ge, fill=0.0, base=-32 * q,
                                        channel_multiplier=1)
            pool.drain()
            for q in range(4):
                cols = slice(32 * q, 32 * q + 32)
                nc.gpsimd.affine_select(out=block_diag[:, cols], in_=block_diag[:, cols],
                                        pattern=[[0, 32]], compare_op=ALU.is_gt, fill=0.0,
                                        base=32 * q + 32, channel_multiplier=-1)

        @block.vector
        def _(dve):
            nc.vector.memset(eps[:], EPS)
            dve.wait_ge(made, 3)
            nc.vector.tensor_copy(ramp[:], ramp_i[:])
            nc.vector.tensor_copy(ramp_bf[:], ramp_i[:])
            nc.vector.tensor_copy(lane[:], lane_i[:])
            nc.vector.tensor_scalar(minus_lane[:], lane_i[:], -1.0, None, ALU.mult)
            nc.vector.tensor_copy(ramp_8[:], ramp_i[:].unsqueeze(2).broadcast_to([P, P, 8]))


def edge_keys(k, ctx, tag, chunks, real, inputs, clamp, pad, sort_by):
    nc = k.nc
    per = 7 if chunks == CE else chunks // P
    parts = chunks // per
    width = per * P
    rows_d = k.dram(f"{tag}_rows", (chunks, len(inputs), P))
    low_d = k.dram(f"{tag}_low", (chunks * P,), BF16)
    cols = [ctx.enter_context(nc.sbuf_tensor(f"{tag}_{n}_cols", [P, chunks], F32)) for n, _ in inputs]
    with ExitStack() as c:
        raw = [c.enter_context(nc.sbuf_tensor(f"{tag}_{n}_raw", [P, width], a.dtype)) for n, a in inputs]
        rows = [c.enter_context(nc.sbuf_tensor(f"{tag}_{n}_f", [P, width], F32)) for n, _ in inputs]
        key_i = c.enter_context(nc.sbuf_tensor(f"{tag}_key_i", [P, width], I32))
        low_i = c.enter_context(nc.sbuf_tensor(f"{tag}_low_i", [P, width], I32))
        low = c.enter_context(nc.sbuf_tensor(f"{tag}_low_bf", [P, width], BF16))
        turned = c.enter_context(nc.psum_tensor(f"{tag}_turned", [P, 2, 512], F32))
        low_made = c.enter_context(k.semaphore(f"{tag}_low_made"))
        padded = c.enter_context(k.semaphore(f"{tag}_padded"))
        loaded = c.enter_context(k.semaphore(f"{tag}_loaded"))
        made = c.enter_context(k.semaphore(f"{tag}_made"))
        transposed = c.enter_context(k.semaphore(f"{tag}_transposed"))
        copied = c.enter_context(k.semaphore(f"{tag}_copied"))
        stored = c.enter_context(k.semaphore(f"{tag}_stored"))
        block = c.enter_context(nc.Block())
        full, rest = divmod(real, width)
        n_in = len(inputs)

        @block.sync
        def _(sp):
            n = 0
            sp.wait_ge(padded, n_in)
            for t, (_, a) in zip(raw, inputs):
                sp.dma_start(t[0:full, :], a[0:full * width].rearrange("(p w) -> p w", w=width)
                             ).then_inc(loaded, 16)
                n += 1
                if rest:
                    sp.dma_start(t[full:full + 1, 0:rest],
                                 a[full * width:real].rearrange("(p w) -> p w", p=1)).then_inc(loaded, 16)
                    n += 1
            sp.wait_ge(made, n_in)
            for j in range(n_in):
                sp.dma_start(rows_d[:, j, :].rearrange("(p b) e -> p b e", b=per),
                             rows[j][0:parts].rearrange("p (b e) -> p b e", e=P)).then_inc(stored, 16)
            sp.wait_ge(low_made, 1)
            sp.dma_start(low_d.rearrange("(p w) -> p w", w=width), low[0:parts, :]).then_inc(stored, 16)
            sp.wait_ge(stored, 16 * (n_in + 1))

        @block.vector
        def _(dve):
            for t, v in zip(raw, pad):
                nc.vector.memset(t[:], v).then_inc(padded, 1)
            dve.wait_ge(loaded, 16 * n_in * (2 if rest else 1))
            for j in range(n_in):
                if clamp[j] is None:
                    nc.vector.tensor_copy(rows[j][:], raw[j][:]).then_inc(made, 1)
                else:
                    nc.vector.tensor_scalar(rows[j][:], raw[j][:], float(clamp[j]), None,
                                            ALU.min).then_inc(made, 1)
            dve.drain()
            nc.vector.tensor_copy(key_i[:], rows[sort_by][:])
            dve.drain()
            nc.vector.tensor_scalar(low_i[:], key_i[:], 127, None, ALU.bitwise_and)
            dve.drain()
            nc.vector.tensor_copy(low[:], low_i[:]).then_inc(low_made, 1)
            for n in range(n_in * per):
                j, b = divmod(n, per)
                dve.wait_ge(transposed, n + 1)
                nc.vector.tensor_copy(cols[j][:].rearrange("e (p b) -> e b p", b=per)[:, b, :],
                                      turned[:, n % 2, 0:parts]).then_inc(copied, 1)

        @block.tensor
        def _(pe):
            pe.wait_ge(made, n_in)
            for n in range(n_in * per):
                j, b = divmod(n, per)
                if n >= 2:
                    pe.wait_ge(copied, n - 1)
                nc.tensor.transpose(turned[:, n % 2, 0:parts], rows[j][0:parts, b * P:(b + 1) * P],
                                    k.ident[0:parts, 0:parts]).then_inc(transposed, 1)
    return rows_d, low_d, cols


def digits(k, ctx, tag, key, chunks):
    nc = k.nc
    lo = ctx.enter_context(nc.sbuf_tensor(f"{tag}_lo", [P, chunks], BF16))
    hi = ctx.enter_context(nc.sbuf_tensor(f"{tag}_hi", [P, chunks], BF16))
    with (nc.sbuf_tensor(f"{tag}_ki", [P, chunks], I32) as ki,
          nc.sbuf_tensor(f"{tag}_di", [P, chunks], I32) as di,
          nc.Block() as block):
        @block.vector
        def _(dve):
            nc.vector.tensor_copy(ki[:], key[:])
            dve.drain()
            nc.vector.tensor_scalar(di[:], ki[:], 7, None, ALU.logical_shift_right)
            dve.drain()
            nc.vector.tensor_copy(hi[:], di[:])
            dve.drain()
            nc.vector.tensor_scalar(di[:], ki[:], 127, None, ALU.bitwise_and)
            dve.drain()
            nc.vector.tensor_copy(lo[:], di[:])
    return lo, hi


def histogram(k, tag, lo, hi, chunks, count):
    nc = k.nc
    B = 8
    batches = chunks // B
    with ExitStack() as c:
        one_lo = [c.enter_context(nc.sbuf_tensor(f"{tag}_one_lo{b}", [P, P, B], BF16)) for b in (0, 1)]
        one_hi = [c.enter_context(nc.sbuf_tensor(f"{tag}_one_hi{b}", [P, NHI, B], BF16)) for b in (0, 1)]
        zero = c.enter_context(nc.sbuf_tensor(f"{tag}_zero", [P, P], BF16))
        total = c.enter_context(nc.psum_tensor(f"{tag}_total", [P, NHI], F32))
        made = c.enter_context(k.semaphore(f"{tag}_h_made"))
        used = c.enter_context(k.semaphore(f"{tag}_h_used"))
        summed = c.enter_context(k.semaphore(f"{tag}_h_summed"))
        zeroed = c.enter_context(k.semaphore(f"{tag}_h_zeroed"))
        block = c.enter_context(nc.Block())

        @block.vector
        def _(dve):
            nc.vector.memset(zero[:], 0.0).then_inc(zeroed, 1)
            dve.sem_inc(used, 2)
            with dve.Fori(0, batches // 2) as i:
                for b in (0, 1):
                    dve.wait_ge(used, 2 * i + b + 1)
                    at = ds((2 * i + b) * B, B)
                    nc.vector.tensor_tensor(one_lo[b][:], k.ramp_8[:], lo[:, at].unsqueeze(1).broadcast_to(
                        [P, P, B]), ALU.is_equal)
                    nc.vector.tensor_tensor(one_hi[b][:], k.ramp_8[:, 0:NHI, :], hi[:, at].unsqueeze(1).broadcast_to(
                        [P, NHI, B]), ALU.is_equal)
                    dve.drain().then_inc(made, 1)
            dve.wait_ge(summed, 1)
            nc.vector.tensor_copy(count[:], total[:])

        @block.tensor
        def _(pe):
            pe.wait_ge(zeroed, 1)
            nc.tensor.matmul(total[:], zero[:], zero[:, 0:NHI], start=True, stop=False,
                             skip_group_check=True)
            with pe.Fori(0, batches // 2) as i:
                for b in (0, 1):
                    pe.wait_ge(made, 2 * i + b + 1)
                    for j in range(B):
                        mm = nc.tensor.matmul(total[:], one_lo[b][:, :, j], one_hi[b][:, :, j],
                                              start=False, stop=False, skip_group_check=True)
                    mm.then_inc(used, 1)
            nc.tensor.matmul(total[:], zero[:], zero[:, 0:NHI], start=False, stop=True,
                             skip_group_check=True).then_inc(summed, 1)


def prefix(k, tag, count, start, tile_start):
    nc = k.nc
    with ExitStack() as c:
        per_hi = c.enter_context(nc.psum_tensor(f"{tag}_per_hi", [P, NHI], F32))
        within = c.enter_context(nc.psum_tensor(f"{tag}_within", [P, NHI], F32))
        total = c.enter_context(nc.sbuf_tensor(f"{tag}_total_sb", [P, NHI], F32))
        upto = c.enter_context(nc.sbuf_tensor(f"{tag}_upto", [P, NHI], F32))
        summed = c.enter_context(k.semaphore(f"{tag}_p_summed"))
        block = c.enter_context(nc.Block())

        @block.tensor
        def _(pe):
            nc.tensor.matmul(per_hi[:], k.ones[:], count[:], start=True, stop=True)
            nc.tensor.matmul(within[:], k.before[:], count[:], start=True, stop=True).then_inc(summed, 1)

        @block.vector
        def _(dve):
            dve.wait_ge(summed, 1)
            nc.vector.tensor_copy(total[:], per_hi[:])
            dve.drain()
            nc.vector.tensor_tensor_scan(upto[:], k.ones[:, 0:NHI], total[:], 0.0, ALU.mult, ALU.add)
            dve.drain()
            nc.vector.tensor_tensor(tile_start[:], upto[:], total[:], ALU.subtract)
            dve.drain()
            nc.vector.tensor_tensor(start[:], tile_start[:], within[:], ALU.add)


def schedule(k, ctx, tag, tile_start):
    nc = k.nc
    step_tile = ctx.enter_context(nc.sbuf_tensor(f"{tag}_step_tile", [P, NSB], F32))
    step_chunk = ctx.enter_context(nc.sbuf_tensor(f"{tag}_step_chunk", [P, NSB], F32))
    T1 = REAL_T - 1
    with (nc.sbuf_tensor(f"{tag}_qi", [P, NHI], I32) as qi,
          nc.sbuf_tensor(f"{tag}_enter", [P, NHI], F32) as enter,
          nc.sbuf_tensor(f"{tag}_cmp", [P, NHI], F32) as cmp,
          nc.sbuf_tensor(f"{tag}_s", [P, NSB], F32) as s,
          nc.Block() as block):
        @block.vector
        def _(dve):
            nc.vector.tensor_copy(qi[:], tile_start[:])
            for b in range(NSB):
                nc.vector.tensor_scalar(s[:, b:b + 1], k.lane[:], float(b * P), None, ALU.add)
            dve.drain()
            nc.vector.tensor_scalar(qi[:], qi[:], 7, None, ALU.logical_shift_right)
            dve.drain()
            nc.vector.tensor_tensor(enter[:], qi[:], k.ramp[:, 0:NHI], ALU.add)
            dve.drain()
            for b in range(NSB):
                nc.vector.tensor_scalar(cmp[:, 0:T1], enter[:, 1:1 + T1], s[:, b:b + 1], 0.0, ALU.is_le,
                                        ALU.add, accum_out=step_tile[:, b:b + 1])
                dve.drain()
            nc.vector.tensor_tensor(step_chunk[:], s[:], step_tile[:], ALU.subtract)
            dve.drain()
            nc.vector.tensor_scalar(step_chunk[:], step_chunk[:], float(CE - 1), None, ALU.min)
    return step_tile, step_chunk


def step_columns(k, tag, rows_d, step_tile, step_chunk, src_i, rel, weight):
    nc = k.nc
    table = rows_d.rearrange("c j e -> c (j e)")
    with ExitStack() as c:
        got = [c.enter_context(nc.sbuf_tensor(f"{tag}_got{b}", [P, 3 * P], F32)) for b in range(NSB)]
        chunk_i = c.enter_context(nc.sbuf_tensor(f"{tag}_chunk_i", [P, NSB], I32))
        first = c.enter_context(nc.sbuf_tensor(f"{tag}_first", [P, NSB], F32))
        turned = c.enter_context(nc.psum_tensor(f"{tag}_turned2", [P, 2, 4, P], F32))
        index_made = c.enter_context(k.semaphore(f"{tag}_index_made"))
        gathered = [c.enter_context(k.semaphore(f"{tag}_gathered{b}")) for b in range(NSB)]
        made = c.enter_context(k.semaphore(f"{tag}_rel_made"))
        transposed = c.enter_context(k.semaphore(f"{tag}_transposed2"))
        copied = c.enter_context(k.semaphore(f"{tag}_copied2"))
        block = c.enter_context(nc.Block())

        @block.gpsimd
        def _(pool):
            pool.wait_ge(index_made, 1)
            for b in range(NSB):
                nc.gpsimd.indirect_dma_start(got[b][:], None, table, bass.IndirectOffsetOnAxis(
                    ap=chunk_i[:, b:b + 1], axis=0)).then_inc(gathered[b], 16)

        @block.vector
        def _(dve):
            nc.vector.tensor_copy(chunk_i[:], step_chunk[:]).then_inc(index_made, 1)
            nc.vector.tensor_scalar(first[:], step_tile[:], float(P), None, ALU.mult)
            dve.drain()
            for b in range(NSB):
                dve.wait_ge(gathered[b], 16)
                nc.vector.tensor_scalar(got[b][:, P:2 * P], got[b][:, P:2 * P], first[:, b:b + 1], None,
                                        ALU.subtract)
                nc.vector.tensor_scalar(got[b][:, 0:P], got[b][:, 0:P], float(N - 1), None, ALU.min)
                dve.drain().then_inc(made, 1)
            for b in range(NSB):
                dve.wait_ge(transposed, b + 1)
                at = slice(b * P, (b + 1) * P)
                nc.vector.tensor_copy(src_i[:, at], turned[:, b % 2, 0, :])
                nc.vector.tensor_copy(rel[:, at], turned[:, b % 2, 1, :])
                nc.vector.tensor_copy(weight[:, at], turned[:, b % 2, 2, :])
                dve.drain().then_inc(copied, 1)

        @block.tensor
        def _(pe):
            for b in range(NSB):
                pe.wait_ge(made, b + 1)
                if b >= 2:
                    pe.wait_ge(copied, b - 1)
                for j in range(3):
                    mm = nc.tensor.transpose(turned[:, b % 2, j, :], got[b][:, j * P:(j + 1) * P], k.ident[:])
                mm.then_inc(transposed, 1)


def step_registers(k, tag, values, row):
    nc = k.nc
    row_d = k.dram(f"{tag}_row_d", (NSB * P,), I32)
    with ExitStack() as c:
        as_int = c.enter_context(nc.sbuf_tensor(f"{tag}_as_int", [P, NSB], I32))
        made = c.enter_context(k.semaphore(f"{tag}_made"))
        moved = c.enter_context(k.semaphore(f"{tag}_moved"))
        block = c.enter_context(nc.Block())

        @block.vector
        def _(dve):
            nc.vector.tensor_copy(as_int[:], values[:]).then_inc(made, 1)

        @block.sync
        def _(sp):
            sp.wait_ge(made, 1)
            for b in range(NSB):
                sp.dma_start(row_d[b * P:(b + 1) * P].rearrange("(p b) -> p b", b=1),
                             as_int[:, b:b + 1]).then_inc(moved, 16)
            sp.wait_ge(moved, 16 * NSB)
            sp.dma_start(row[:], row_d.rearrange("(a s) -> a s", a=1)).then_inc(moved, 16)
            sp.wait_ge(moved, 16 * (NSB + 1))


def aggregate(k, tag, table, src_i, rel, weight, tile_row, acc):
    nc = k.nc
    R = 8
    with ExitStack() as c:
        def sb(name, shape, dt=F32):
            return c.enter_context(nc.sbuf_tensor(f"{tag}_{name}", shape, dt))

        def sem(name):
            return c.enter_context(k.semaphore(f"{tag}_{name}"))

        idx = [sb(f"idx{h}", [P, R], I32) for h in (0, 1)]
        msg = [sb(f"msg{b}", [P, C]) for b in range(2 * R)]
        pick = [sb(f"pick{b}", [P, P]) for b in range(R)]
        part = [c.enter_context(nc.psum_tensor(f"{tag}_part{b}", [P, 4, P], F32)) for b in range(R)]
        idx_ready, pick_ready = sem("idx_ready"), sem("pick_ready")
        zeroed = sem("zeroed")
        gathered = [sem(f"gathered{b}") for b in range(2 * R)]
        turn = sem("turn")
        summed, added = sem("summed"), sem("added")
        block = c.enter_context(nc.Block())

        @block.gpsimd
        def _(pool):
            pool.sem_inc(summed, 2 * R)
            with pool.Fori(0, NS // (2 * R)) as i:
                for h in (0, 1):
                    half = 2 * i + h
                    pool.wait_ge(summed, (half + 1) * R)
                    pool.sem_inc(turn, 1)
                    nc.gpsimd.tensor_copy(idx[h][:], src_i[:, ds(half * R, R)]).then_inc(idx_ready, 1)
                    pool.wait_ge(idx_ready, half + 1)
                    pool.sem_inc(turn, 1)
                    for b in range(R):
                        nc.gpsimd.indirect_dma_start(msg[h * R + b][:], None, table, bass.IndirectOffsetOnAxis(
                            ap=idx[h][:, b:b + 1], axis=0)).then_inc(gathered[h * R + b], 16)

        @block.vector
        def _(dve):
            nc.vector.memset(acc[:], 0.0)
            dve.drain()
            regs = [dve.alloc_register(f"{tag}_tile{b}") for b in range(R)]

            def picks(first, slot):
                for b in range(4):
                    s = first + b
                    nc.vector.tensor_scalar(pick[slot + b][:], k.ramp[:], rel[:, ds(s, 1)],
                                            weight[:, ds(s, 1)], ALU.is_equal, ALU.mult
                                            ).then_inc(pick_ready, 1)

            picks(0, 0)
            with dve.Fori(0, NS // R) as i:
                dve.reg_load(regs, tile_row[0:1, ds(i * R, R)])
                tiles = [dve.snap(r, min_val=0, max_val=REAL_T - 1) for r in regs]
                for g in (0, 1):
                    picks(i * R + 4 * g + 4, 4 - 4 * g)
                    for b in range(4 * g, 4 * g + 4):
                        dve.wait_ge(summed, i * R + b + 1 + 2 * R)
                        at = ds(tiles[b] * P, P)
                        nc.vector.tensor_tensor(acc[:, :, at], acc[:, :, at], part[b][:, 0:2, :], ALU.add)
                        dve.drain().then_inc(added, 1)

        @block.tensor
        def _(pe):
            pe.sem_inc(added, R)
            with pe.Fori(0, NS // (2 * R)) as i:
                for h in (0, 1):
                    for b in range(R):
                        s = (2 * i + h) * R + b
                        pe.wait_ge(gathered[h * R + b], i * 16 + 16)
                        pe.wait_ge(pick_ready, s + 1)
                        pe.wait_ge(added, s + 1)
                        for half in (0, 1):
                            mm = nc.tensor.matmul(part[b][:, half, :], msg[h * R + b][:, half * P:(half + 1) * P],
                                                  pick[b][:], start=True, stop=True)
                        mm.then_inc(summed, 1)


def sort_edges(k, ctx, tag, chunks, key, lo, hi, start, key_rows, low_d, payload, width, fill, out_d,
               pos_all=None):
    nc = k.nc
    Q = 8
    S = 4
    quads = chunks // Q
    with ExitStack() as c:
        def sb(name, shape, dt=F32):
            return c.enter_context(nc.sbuf_tensor(f"{tag}_{name}", shape, dt))

        def sem(name):
            return c.enter_context(k.semaphore(f"{tag}_{name}"))

        key_row = [sb(f"key_row{s}", [P, Q * P]) for s in range(S)]
        low_row = [sb(f"low_row{s}", [P, Q * P], BF16) for s in range(S)]
        pay = [sb(f"pay{q}", [P, Q, width]) for q in (0, 1)] if pos_all is None else [None, None]
        pos = [sb(f"pos{q}", [P, Q], I32) for q in (0, 1)]
        base = [sb(f"base{q}", [P, Q]) for q in (0, 1)]
        same = [sb(f"same{q}", [P, Q]) for q in (0, 1)]
        hi_f = sb("hi_f", [P, chunks])
        lowT = [sb(f"lowT{q}", [P, Q * P]) for q in (0, 1)]
        one_lo = [sb(f"s_one_lo{q}", [P, P, Q], BF16) for q in (0, 1)]
        one_hi = [sb(f"s_one_hi{q}", [P, NHI, Q], BF16) for q in (0, 1)]
        junk_hi = [sb(f"junk_hi{j}", [P, NHI]) for j in (0, 1)]
        junk_row = [sb(f"junk_row{j}", [P, 2 * P]) for j in (0, 1)]
        earlier = sb("earlier", [P, 2, 2 * P])
        counts_sb = [sb(f"counts_sb{b}", [P, NHI]) for b in (0, 1)]
        counts = c.enter_context(nc.psum_tensor(f"{tag}_counts", [P, 512], F32))
        found = [c.enter_context(nc.psum_tensor(f"{tag}_found{g}", [P, 8, NHI], F32)) for g in range(4)]
        key_in = [sem(f"key_in{s}") for s in range(S)]
        low_in = [sem(f"low_in{s}") for s in range(S)]
        pay_in = [sem(f"pay_in{q}") for q in (0, 1)]
        hot_ready, quad_used, lowT_ready = sem("hot_ready"), sem("quad_used"), sem("lowT_ready")
        count_ready, count_copied, found_ready = sem("count_ready"), sem("count_copied"), sem("found_ready")
        found_read, pos_ready, key_used = sem("found_read"), sem("pos_ready"), sem("key_used")
        turn, pay_free = sem("turn"), sem("pay_free")
        scattered = [sem(f"scattered{q}") for q in (0, 1)]
        mask_made = sem("mask_made")
        block = c.enter_context(nc.Block())

        def over_quads(eng, first, count, body):
            whole = count // S
            with eng.Fori(0, whole) as i:
                for s in range(S):
                    body(i * S + (first + s), (first + s) % S, i + ((first + s) // S + 1))
            for n in range(first + whole * S, first + count):
                body(n, n % S, n // S + 1)

        @block.sync
        def _(sp):
            def rows(n, s):
                sp.dma_start(key_row[s][:].rearrange("p (b e) -> p b e", e=P),
                             key_rows[ds(n * Q, Q), :].unsqueeze(0).broadcast_to([P, Q, P])
                             ).then_inc(key_in[s], 16)
                sp.dma_start(low_row[s][:], low_d[ds(n * Q * P, Q * P)].unsqueeze(0)
                             .broadcast_to([P, Q * P])).then_inc(low_in[s], 16)

            for s in range(S - 1):
                rows(s, s)
            if fill:
                fill(sp, pay[0], 0, False, pay_in[0], turn)
                fill(sp, pay[1], 1, False, pay_in[1], turn)
            rows(S - 1, S - 1)

            def step(n, s, nth):
                if fill:
                    sp.wait_ge(scattered[s % 2], nth_two(n, s) * (16 * Q))
                    sp.sem_inc(pay_free, 1)
                    fill(sp, pay[s % 2], n + 2, isinstance(n, int) and n + 2 == quads - 1, pay_in[s % 2], turn)
                sp.wait_ge(key_used, n + 1)
                sp.wait_ge(lowT_ready, n + 1)
                if not isinstance(n, int) or n + S < quads:
                    rows(n + S, s)

            def nth_two(n, s):
                return n // 2 + 1 if isinstance(n, int) else (n - s % 2) // 2 + 1
            over_quads(sp, 0, quads - S, step)
            for n in range(quads - S, quads - 2):
                step(n, n % S, None)
            if pos_all is None:
                for q in (0, 1):
                    sp.wait_ge(scattered[q], 8 * Q * quads)

        @block.gpsimd
        def _(pool):
            nc.gpsimd.memset(earlier[:], 1.0).then_inc(mask_made, 1)
            pool.wait_ge(mask_made, 1)
            nc.gpsimd.affine_select(out=earlier[:], in_=earlier[:], pattern=[[P, 2], [-1, 2 * P]],
                                    compare_op=ALU.is_gt, fill=0.0, base=0,
                                    channel_multiplier=1).then_inc(mask_made, 1)
            if pos_all is not None:
                return
            with pool.Fori(0, quads // 2) as i:
                for q in (0, 1):
                    pool.wait_ge(pos_ready, 2 * i + q + 1)
                    pool.sem_inc(turn, 1)
                    if fill:
                        pool.wait_ge(pay_in[q], 16 * i + 16)
                        pool.sem_inc(turn, 1)
                    for b in range(Q):
                        nc.gpsimd.indirect_dma_start(out_d, bass.IndirectOffsetOnAxis(
                            ap=pos[q][:, b:b + 1], axis=0), pay[q][:, b, :], None).then_inc(scattered[q], 16)

        @block.vector
        def _(dve):
            nc.vector.tensor_copy(hi_f[:], hi[:])
            dve.wait_ge(mask_made, 2)
            dve.drain()
            dve.sem_inc(quad_used, 2)
            dve.sem_inc(pay_free, 2)

            def one_hots(n, s, nth):
                q = s % 2
                at = ds(n * Q, Q)
                dve.wait_ge(quad_used, n + 1)
                nc.vector.tensor_tensor(one_lo[q][:], k.ramp_8[:], lo[:, at].unsqueeze(1).broadcast_to(
                    [P, P, Q]), ALU.is_equal)
                nc.vector.tensor_tensor(one_hi[q][:], k.ramp_8[:, 0:NHI, :], hi[:, at].unsqueeze(1).broadcast_to(
                    [P, NHI, Q]), ALU.is_equal)
                dve.drain().then_inc(hot_ready, 1)

            def ranks(n, s, nth):
                q = s % 2
                dve.wait_ge(key_in[s], nth * 16)
                for g in range(4):
                    dve.wait_ge(found_ready, n * 4 + g + 1)
                    for j in (0, 1):
                        ch = n * Q + 2 * g + j
                        col = 2 * g + j
                        w = (j + 1) * P
                        nc.vector.scalar_tensor_tensor(junk_hi[j][:], k.ramp[:, 0:NHI], hi_f[:, ds(ch, 1)],
                                                       found[g][:, j, :], ALU.is_equal, ALU.mult,
                                                       accum_out=base[q][:, col:col + 1])
                        nc.vector.scalar_tensor_tensor(junk_row[j][:, 0:w],
                                                       key_row[s][:, g * 2 * P:g * 2 * P + w],
                                                       key[:, ds(ch, 1)], earlier[:, j, 0:w],
                                                       ALU.is_equal, ALU.mult,
                                                       accum_out=same[q][:, col:col + 1])
                    dve.drain().then_inc(found_read, 1)
                dve.sem_inc(key_used, 1)
                if pos_all is not None:
                    nc.vector.tensor_tensor(pos_all[:, ds(n * Q, Q)], base[q][:], same[q][:], ALU.add)
                    return
                dve.wait_ge(pay_free, n + 1)
                nc.vector.tensor_tensor(pos[q][:], base[q][:], same[q][:], ALU.add)
                for cols, tile in payload:
                    nc.vector.tensor_copy(pay[q][:, :, cols], tile[:, ds(n * Q, Q)])
                dve.drain().then_inc(pos_ready, 1)

            def quad(n, s, nth):
                one_hots(n + 1, (s + 1) % S, None)
                ranks(n, s, nth)
            one_hots(0, 0, None)
            over_quads(dve, 0, quads - 1, quad)
            ranks(quads - 1, (quads - 1) % S, (quads - 1) // S + 1)

        @block.scalar
        def _(act):
            def low_hots(n, s, nth, g):
                q = s % 2
                if g == 0:
                    act.wait_ge(low_in[s], nth * 16)
                    act.wait_ge(quad_used, n + 1)
                at = slice(2 * g * P, 2 * (g + 1) * P)
                nc.scalar.activation(lowT[q][:, at], low_row[s][:, at], ACT.Square, bias=k.minus_lane[:, 0:1])
                act.drain()
                nc.scalar.activation(lowT[q][:, at], lowT[q][:, at], ACT.Relu, bias=k.ones[:, 0:1], scale=-1.0)
                if g == 3:
                    act.drain().then_inc(lowT_ready, 1)

            def copy(n, g):
                act.wait_ge(count_ready, n * 4 + g + 1)
                nc.scalar.copy(counts_sb[g % 2][:], counts[:, 0:NHI]).then_inc(count_copied, 1)

            def quad(n, s, nth):
                for g in range(4):
                    copy(n - 1, g)
                    low_hots(n, s, nth, g)
            for g in range(4):
                low_hots(0, 0, 1, g)
            over_quads(act, 1, quads - 1, quad)
            for g in range(4):
                copy(quads - 1, g)

        @block.tensor
        def _(pe):
            pe.sem_inc(found_read, 4)
            nc.tensor.matmul(counts[:, 0:NHI], k.ident[:], start[:], start=True, stop=False,
                             skip_group_check=True).then_inc(count_ready, 1)
            with pe.Fori(0, quads // 2) as i:
                for q in (0, 1):
                    n = 2 * i + q
                    pe.wait_ge(hot_ready, n + 1)
                    pe.wait_ge(lowT_ready, n + 1)
                    for g in range(4):
                        pe.wait_ge(count_copied, n * 4 + g + 1)
                        for j in (0, 1):
                            mm = nc.tensor.matmul(counts[:, 0:NHI], one_lo[q][:, :, 2 * g + j],
                                                  one_hi[q][:, :, 2 * g + j],
                                                  start=False, stop=False, skip_group_check=True)
                        mm.then_inc(count_ready, 1)
                        pe.wait_ge(found_read, n * 4 + g + 1)
                        for j in (0, 1):
                            at = slice((2 * g + j) * P, (2 * g + j + 1) * P)
                            mm = nc.tensor.matmul(found[g][:, j, :], lowT[q][:, at], counts_sb[g % 2][:],
                                                  start=True, stop=True)
                        mm.then_inc(found_ready, 1)
                    pe.drain().then_inc(quad_used, 1)
            nc.tensor.matmul(counts[:, 0:NHI], one_lo[0][:, :, 0], one_hi[0][:, :, 0], start=False,
                             stop=True, skip_group_check=True)
    return out_d


def scatter_beside(k, c, tag, chunks, pos_all, payload, out_d):
    nc = k.nc
    R = 16
    pos = [c.enter_context(nc.sbuf_tensor(f"{tag}_pos{h}", [P, R], I32)) for h in (0, 1)]
    pay = [c.enter_context(nc.sbuf_tensor(f"{tag}_pay{h}", [P, R, 2], F32)) for h in (0, 1)]
    scattered = [c.enter_context(k.semaphore(f"{tag}_scattered{h}")) for h in (0, 1)]
    copied = c.enter_context(k.semaphore(f"{tag}_copied"))

    def program(pool):
        def slot(n, h, before):
            if before is not None:
                pool.wait_ge(scattered[h], before)
                pool.sem_inc(k.turn, 1)
            at = slice(h * R, h * R + R) if n is None else ds((2 * n + h) * R, R)
            nc.gpsimd.tensor_copy(pos[h][:], pos_all[:, at]).then_inc(copied, 1)
            for f in (0, 1):
                nc.gpsimd.tensor_copy(pay[h][:, :, f], payload[f][:, at]).then_inc(copied, 1)
            pool.wait_ge(copied, 3 * h + 3 if n is None else 6 * n + 3 * h + 3)
            pool.sem_inc(k.turn, 1)
            for b in range(R):
                nc.gpsimd.indirect_dma_start(out_d, bass.IndirectOffsetOnAxis(ap=pos[h][:, b:b + 1], axis=0),
                                             pay[h][:, b, :], None).then_inc(scattered[h], 16)
        for h in (0, 1):
            slot(None, h, None)
        with pool.Fori(1, chunks // (2 * R)) as i:
            for h in (0, 1):
                slot(i, h, i * (16 * R))
        for h in (0, 1):
            pool.wait_ge(scattered[h], chunks // 2 * 16)
    return program


def segment_sum(k, tag, sorted_d, width, chunk_row, first_all, tile_row, acc):
    nc = k.nc
    R = 8
    S = 16
    with ExitStack() as c:
        def sb(name, shape, dt=F32):
            return c.enter_context(nc.sbuf_tensor(f"{tag}_{name}", shape, dt))

        def sem(name):
            return c.enter_context(k.semaphore(f"{tag}_{name}"))

        rows = [sb(f"rows{b}", [P, width + 1]) for b in range(S)]
        pick = [sb(f"pick{b}", [P, P]) for b in range(R)]
        part = [c.enter_context(nc.psum_tensor(f"{tag}_part{b}", [P, 512], F32)) for b in range(R)]
        loaded = [sem(f"loaded{b}") for b in range(S)]
        pick_ready, summed, added = sem("pick_ready"), sem("summed"), sem("added")
        block = c.enter_context(nc.Block())

        def loads(eng, odd):
            regs = [eng.alloc_register(f"{tag}_chunk{odd}_{b}") for b in range(R)]
            with eng.Fori(0, NS // S) as i:
                for h in (0, R):
                    eng.reg_load(regs, chunk_row[0:1, ds(i * S + h, R)])
                    for b in range(odd, R, 2):
                        chunk = eng.snap(regs[b], min_val=0, max_val=CE - 1)
                        eng.wait_ge(summed, i * S + h + b + 1)
                        eng.dma_start(rows[h + b][:], sorted_d[ds(chunk * P, P), :]).then_inc(loaded[h + b], 16)

        @block.sync
        def _(sp):
            sp.sem_inc(summed, S)
            loads(sp, 0)

        @block.scalar
        def _(act):
            loads(act, 1)

        @block.vector
        def _(dve):
            nc.vector.memset(acc[:], 0.0)
            dve.drain()
            regs = [dve.alloc_register(f"{tag}_tile{b}") for b in range(R)]

            def pick_one(i, b):
                dve.wait_ge(loaded[b], i * 16 + 16)
                nc.vector.tensor_scalar(pick[b % R][:], k.ramp[:], first_all[:, ds(i * S + b, 1)],
                                        rows[b][:, width:width + 1], ALU.add,
                                        ALU.is_equal).then_inc(pick_ready, 1)

            def body(i, last):
                for h in (0, R):
                    dve.reg_load(regs, tile_row[0:1, ds(i * S + h, R)])
                    tiles = [dve.snap(r, min_val=0, max_val=REAL_T - 1) for r in regs]
                    for b in range(h, h + R):
                        if b % 4 == 0 and b + 4 < S:
                            for a in range(b + 4, b + 8):
                                pick_one(i, a)
                        elif b % 4 == 0 and not last:
                            for a in range(4):
                                pick_one(i + 1, a)
                        dve.wait_ge(summed, i * S + b + 1 + S)
                        at = ds(tiles[b - h] * P, P)
                        nc.vector.tensor_tensor(acc[:, at], acc[:, at], part[b % R][:, 0:P], ALU.add)
                        dve.drain().then_inc(added, 1)

            for b in range(4):
                pick_one(0, b)
            with dve.Fori(0, NS // S - 1) as i:
                body(i, False)
            body(NS // S - 1, True)

        @block.tensor
        def _(pe):
            pe.sem_inc(added, R)
            with pe.Fori(0, NS // S) as i:
                for b in range(S):
                    pe.wait_ge(pick_ready, i * S + b + 1)
                    pe.wait_ge(loaded[b], i * 16 + 16)
                    pe.wait_ge(added, i * S + b + 1)
                    nc.tensor.matmul(part[b % R][:, 0:P], rows[b][:, 0:width], pick[b % R][:],
                                     start=True, stop=True).then_inc(summed, 1)


def over_tiles(eng, body):
    with eng.Fori(0, (REAL_T - 1) // 2) as i:
        for b in (0, 1):
            body(2 * i + b, b, P)
    body(REAL_T - 1, 0, LAST)


def root(k, act, st, rows, asked, answered, nth):
    act.wait_ge(asked, nth)
    k.nc.scalar.activation(st[0:rows, 8:9], st[0:rows, 7:8], ACT.Sqrt,
                           bias=k.eps[0:rows, 0:1]).then_inc(answered, 1)


S4 = 4


def over_fours(eng, *phases):
    with eng.Fori(0, REAL_T // S4) as i:
        for phase in phases:
            for b in range(S4):
                phase(i * S4 + b, b, P)
    for phase in phases:
        phase(REAL_T - 1, 0, LAST)


def over_fours_io(sp, load, *stores):
    for b in range(S4):
        load(b, b, P)
    with sp.Fori(0, REAL_T // S4 - 1) as i:
        for b in range(S4):
            load(i * S4 + b + S4, b, P)
        for store in stores:
            for b in range(S4):
                store(i * S4 + b, b, P)
    load(REAL_T - 1, 0, LAST)
    for store in stores:
        for b in range(S4):
            store(REAL_T - 1 - S4 + b, b, P)
    for store in stores:
        store(REAL_T - 1, 0, LAST)


def times(t, b):
    return (t - b) // S4 + 1


def all_stored(sp, sems):
    for b, sem in enumerate(sems):
        sp.wait_ge(sem, 16 * (times(REAL_T - 1 if b == 0 else REAL_T - 1 - S4 + b, b) + 1))


def request(t, b, part, parts):
    if isinstance(t, int):
        return parts * t + part + 1
    return (t - b) * parts + (part * S4 + b + 1)


def norm_stats(k, dve, x, st, rows, asked):
    k.nc.vector.bn_stats(st[0:rows, 0:6], x)
    dve.drain()
    k.nc.vector.bn_aggr(st[0:rows, 6:8], st[0:rows, 0:6]).then_inc(asked, 1)


def norm_apply(k, dve, x, out, st, rows, answered, nth):
    dve.wait_ge(answered, nth)
    k.nc.vector.reciprocal(st[0:rows, 9:10], st[0:rows, 8:9])
    dve.drain()
    k.nc.vector.tensor_scalar(out, x, st[0:rows, 6:7], st[0:rows, 9:10], ALU.subtract, ALU.mult)
    dve.drain()


def load_params(k, ctx, tag, loads):
    nc = k.nc
    tiles = [ctx.enter_context(nc.sbuf_tensor(f"{tag}_{name}", shape, F32)) for name, shape, _ in loads]
    with k.semaphore(f"{tag}_params_in") as loaded, nc.Block() as block:
        @block.sync
        def _(sp):
            for t, (_, _, source) in zip(tiles, loads):
                sp.dma_start(t[:], source, allow_slow_non_contiguous=True).then_inc(loaded, 16)
            sp.wait_ge(loaded, 16 * len(loads))
    return tiles


def row_on_all(v):
    return v.unsqueeze(0).broadcast_to([P, v.shape[0]])


def halves(w):
    return w.rearrange("(h p) m -> p h m", p=P)


def halves_col(v):
    return v.rearrange("(h p) -> p h", p=P)


def input_stage(k, ctx, tag, h_d, kv):
    nc, I = k.nc, k.ins
    with ExitStack() as c:
        def sb(name, shape, dt=F32):
            return c.enter_context(nc.sbuf_tensor(f"{tag}_{name}", shape, dt))

        def sem(name):
            return c.enter_context(k.semaphore(f"{tag}_{name}"))

        def flat(w):
            return row_on_all(w.rearrange("h a d -> (h a d)"))

        w1, b1, kw, kb, vw, vb = load_params(k, c, tag, [
            ("w1", [P, 2, C], halves(I["L0_gnn_c1_w1"])), ("b1", [1, C], I["L0_gnn_c1_b1"].unsqueeze(0)),
            ("kw", [P, C], flat(I["L0_mix_kln_weight"])), ("kb", [P, C], flat(I["L0_mix_kln_bias"])),
            ("vw", [P, C], flat(I["L0_mix_vln_weight"])), ("vb", [P, C], flat(I["L0_mix_vln_bias"]))])
        def slots(name, shape):
            return [sb(f"{name}{b}", shape) for b in range(S4)]

        x, xn, h, z, kk, vv, sq = (slots(n, [P, C]) for n in ("x", "xn", "h", "z", "kk", "vv", "sq"))
        xnT, st, hs = slots("xnT", [P, 2, P]), slots("st", [P, 16]), slots("hs", [P, 4, 8])
        zero = sb("zero", [P, P])
        turned = [c.enter_context(nc.psum_tensor(f"{tag}_turned{b}", [P, 4, P], F32)) for b in range(S4)]
        hp = [c.enter_context(nc.psum_tensor(f"{tag}_hp{b}", [P, 512], F32)) for b in (0, 1)]
        kvp = c.enter_context(nc.psum_tensor(f"{tag}_kvp", [P, 4, P], F32))
        x_in, h_out = [sem(f"x_in{b}") for b in range(S4)], [sem(f"h_out{b}") for b in range(S4)]
        x_used, xn_ready, xn_used, z_ready, kv_ready, kv_used = map(
            sem, ("x_used", "xn_ready", "xn_used", "z_ready", "kv_ready", "kv_used"))
        turned_ready, xnT_ready, hp_ready, h_ready, pool_step, zeroed, kv_summed = map(
            sem, ("turned_ready", "xnT_ready", "hp_ready", "h_ready", "pool_step", "zeroed", "kv_summed"))
        asked, answered, bank_free = sem("asked"), sem("answered"), sem("bank_free")
        block = c.enter_context(nc.Block())

        @block.sync
        def _(sp):
            sp.sem_inc(x_used, S4)
            for b in range(S4):
                sp.sem_inc(h_out[b], 16)

            def load(t, b, rows):
                sp.wait_ge(x_used, t + 1)
                sp.dma_start(x[b][0:rows, :], I["x"][ds(t * P, rows), :]).then_inc(x_in[b], 16)

            def store(t, b, r):
                sp.wait_ge(h_ready, t + 1)
                sp.dma_start(h_d[ds(t * P, r), :], h[b][0:r, :]).then_inc(h_out[b], 16)
            over_fours_io(sp, load, store)
            all_stored(sp, h_out)

        @block.vector
        def _(dve):
            nc.vector.memset(zero[:], 0.0).then_inc(zeroed, 1)
            dve.sem_inc(xn_used, S4)
            dve.sem_inc(kv_ready, S4)

            def by_head(a, r):
                return a[0:r].rearrange("p (h d) -> p h d", d=32)

            def wide(a, r):
                return a.unsqueeze(2).broadcast_to([r, 8, 32])

            def stats(t, b, r):
                dve.wait_ge(x_in[b], times(t, b) * 16)
                norm_stats(k, dve, x[b][0:r, :], st[b], r, asked)

            def apply(t, b, r):
                dve.wait_ge(xn_used, t + 1)
                norm_apply(k, dve, x[b][0:r, :], xn[b][0:r, :], st[b], r, answered, request(t, b, 0, 2))
                dve.sem_inc(x_used, 1)
                dve.sem_inc(xn_ready, 1)

            def head_stats(t, b, r):
                nc.vector.tensor_reduce(hs[b][0:r, 0, :], by_head(xn[b], r), AX_X, ALU.add)
                dve.drain()
                nc.vector.tensor_scalar(hs[b][0:r, 0, :], hs[b][0:r, 0, :], 1.0 / 32, None, ALU.mult)
                dve.drain()
                dve.wait_ge(kv_ready, t + 1)
                nc.vector.tensor_tensor(by_head(z[b], r), by_head(xn[b], r), wide(hs[b][0:r, 0, :], r),
                                        ALU.subtract)
                dve.drain()
                nc.vector.tensor_tensor(sq[b][0:r], z[b][0:r], z[b][0:r], ALU.mult)
                dve.drain()
                nc.vector.tensor_reduce(hs[b][0:r, 1, :], by_head(sq[b], r), AX_X, ALU.add).then_inc(asked, 1)

            def head_apply(t, b, r):
                dve.wait_ge(answered, request(t, b, 1, 2))
                nc.vector.tensor_scalar(hs[b][0:r, 2, :], hs[b][0:r, 2, :], EPS, None, ALU.add)
                dve.drain()
                nc.vector.reciprocal(hs[b][0:r, 3, :], hs[b][0:r, 2, :])
                dve.drain()
                nc.vector.tensor_tensor(by_head(z[b], r), by_head(z[b], r), wide(hs[b][0:r, 3, :], r), ALU.mult)
                dve.drain().then_inc(z_ready, 1)
            over_fours(dve, stats, apply, head_stats, head_apply)
            dve.wait_ge(kv_summed, 1)
            for half in (0, 1):
                nc.vector.scalar_tensor_tensor(kv[:, half, :], kvp[:, half, :], 1.0 / N, k.block_diag[:],
                                               ALU.mult, ALU.mult)

        @block.gpsimd
        def _(pool):
            pool.sem_inc(kv_used, S4)

            def tile(t, b, r):
                pool.wait_ge(z_ready, t + 1)
                pool.sem_inc(pool_step, 1)
                pool.wait_ge(kv_used, t + 1)
                pool.sem_inc(pool_step, 1)
                nc.gpsimd.tensor_tensor(kk[b][0:r], z[b][0:r], kw[0:r], ALU.mult)
                nc.gpsimd.tensor_tensor(vv[b][0:r], z[b][0:r], vw[0:r], ALU.mult)
                pool.drain()
                nc.gpsimd.tensor_tensor(kk[b][0:r], kk[b][0:r], kb[0:r], ALU.add)
                nc.gpsimd.tensor_tensor(vv[b][0:r], vv[b][0:r], vb[0:r], ALU.add)
                pool.drain().then_inc(kv_ready, 1)
            over_fours(pool, tile)

        @block.tensor
        def _(pe):
            pe.wait_ge(zeroed, 1)
            pe.sem_inc(bank_free, 2)
            for half in (0, 1):
                nc.tensor.matmul(kvp[:, half, :], zero[:], zero[:], start=half == 0, stop=False, skip_group_check=True)

            def turn(t, b, r):
                pe.wait_ge(xn_ready, t + 1)
                for half in (0, 1):
                    mm = nc.tensor.transpose(turned[b][:, half, 0:r], xn[b][0:r, half * P:(half + 1) * P],
                                             k.ident[0:r, 0:r])
                mm.then_inc(turned_ready, 1)

            def dense(t, b, r):
                bank = hp[b % 2]
                pe.wait_ge(xnT_ready, t + 1)
                pe.sem_inc(xn_used, 1)
                pe.wait_ge(bank_free, t + 1)
                nc.tensor.matmul(bank[0:r, 0:C], k.ones[0:1, 0:r], b1[:], start=True, stop=False)
                for half in (0, 1):
                    mm = nc.tensor.matmul(bank[0:r, 0:C], xnT[b][:, half, 0:r], w1[:, half, :],
                                          start=False, stop=half == 1)
                mm.then_inc(hp_ready, 1)

            def outer(t, b, r):
                pe.wait_ge(kv_ready, t + 1 + S4)
                for half in (0, 1):
                    at = slice(half * P, (half + 1) * P)
                    mm = nc.tensor.matmul(kvp[:, half, :], kk[b][0:r, at], vv[b][0:r, at], start=False,
                                          stop=False, skip_group_check=True)
                mm.then_inc(kv_used, 1)
            over_fours(pe, turn, dense, outer)
            nc.tensor.matmul(kvp[:, 0, :], zero[:], zero[:], start=False, stop=True,
                             skip_group_check=True).then_inc(kv_summed, 1)

        @block.scalar
        def _(act):
            def first_root(t, b, r):
                root(k, act, st[b], r, asked, answered, request(t, b, 0, 2))

            def copy(t, b, r):
                act.wait_ge(turned_ready, t + 1)
                nc.scalar.copy(xnT[b][:, :, 0:r], turned[b][:, 0:2, 0:r]).then_inc(xnT_ready, 1)

            def head_root(t, b, r):
                act.wait_ge(asked, request(t, b, 1, 2))
                nc.scalar.activation(hs[b][0:r, 2, :], hs[b][0:r, 1, :], ACT.Sqrt,
                                     scale=1.0 / 31).then_inc(answered, 1)

            def relu(t, b, r):
                act.wait_ge(hp_ready, t + 1)
                act.wait_ge(h_out[b], times(t, b) * 16)
                nc.scalar.activation(h[b][0:r, :], hp[b % 2][0:r, 0:C], ACT.Relu).then_inc(h_ready, 1)
                act.wait_ge(h_ready, t + 1)
                act.sem_inc(bank_free, 1)
            over_fours(act, first_root, copy, relu, head_root)


W = 448


def dense_and_norms(k, ctx, tag, acc, w_name, b_name, norms):
    nc, I = k.nc, k.ins
    blocks = NP // W
    NCK, CK = 25, N // 25
    with ExitStack() as c:
        def sb(name, shape, dt=F32):
            return c.enter_context(nc.sbuf_tensor(f"{tag}_{name}", shape, dt))

        def sem(name):
            return c.enter_context(k.semaphore(f"{tag}_{name}"))

        loads = [("w", [P, 2, C], halves(I[w_name])), ("b", [P, 2], halves_col(I[b_name]))]
        for n, (g, b, _) in enumerate(norms):
            loads += [(f"g{n}", [P, 2], halves_col(I[g])), (f"b{n}", [P, 2], halves_col(I[b]))]
        w, b, *gb = load_params(k, c, tag, loads)
        stats = sb("stats", [P, 2, NCK, 6])
        mv, sc = sb("mv", [P, 2, 2]), sb("sc", [P, 4, 2])
        out = [[c.enter_context(nc.psum_tensor(f"{tag}_out{s}{h}", [P, 512], F32)) for h in (0, 1)]
               for s in (0, 1)]
        made, moved = sem("made"), sem("moved")
        asked, answered, scaled, applied = sem("asked"), sem("answered"), sem("scaled"), sem("applied")
        block = c.enter_context(nc.Block())

        @block.tensor
        def _(pe):
            pe.sem_inc(moved, 2)
            with pe.Fori(0, blocks // 2) as i:
                for s in (0, 1):
                    n = 2 * i + s
                    pe.wait_ge(moved, n + 1)
                    for co in (0, 1):
                        for ci in (0, 1):
                            mm = nc.tensor.matmul(out[s][co][:, 0:W], w[:, ci, co * P:(co + 1) * P],
                                                  acc[:, ci, ds(n * W, W)], start=ci == 0, stop=ci == 1)
                    mm.then_inc(made, 1)

        @block.scalar
        def _(act):
            with act.Fori(0, blocks // 2) as i:
                for s in (0, 1):
                    n = 2 * i + s
                    act.wait_ge(made, n + 1)
                    for co in (0, 1):
                        nc.scalar.activation(acc[:, co, ds(n * W, W)], out[s][co][:, 0:W], ACT.Identity,
                                             bias=b[:, co:co + 1])
                    act.drain().then_inc(moved, 1)
            for n, (_, _, relu) in enumerate(norms):
                act.wait_ge(asked, n + 1)
                nc.scalar.activation(sc[:, 0, :], mv[:, :, 1], ACT.Sqrt, bias=k.eps[:, 0:1]
                                     ).then_inc(answered, 1)
                act.wait_ge(scaled, n + 1)
                for half in (0, 1):
                    nc.scalar.activation(acc[:, half, :], acc[:, half, :], ACT.Relu if relu else ACT.Identity,
                                         bias=sc[:, 3, half:half + 1], scale=sc[:, 2, half:half + 1])
                act.drain().then_inc(applied, 1)

        @block.vector
        def _(dve):
            dve.wait_ge(moved, 2 + blocks)
            for n in range(len(norms)):
                if n:
                    dve.wait_ge(applied, n)
                with dve.Fori(0, NCK) as i:
                    for half in (0, 1):
                        nc.vector.bn_stats(stats[:, half, ds(i, 1), :], acc[:, half, ds(i * CK, CK)])
                dve.drain()
                for half in (0, 1):
                    nc.vector.bn_aggr(mv[:, half, :], stats[:, half].rearrange("p a b -> p (a b)"))
                dve.drain().then_inc(asked, 1)
                dve.wait_ge(answered, n + 1)
                nc.vector.reciprocal(sc[:, 1, :], sc[:, 0, :])
                dve.drain()
                nc.vector.tensor_tensor(sc[:, 2, :], sc[:, 1, :], gb[2 * n][:], ALU.mult)
                dve.drain()
                nc.vector.tensor_tensor(sc[:, 1, :], mv[:, :, 0], sc[:, 2, :], ALU.mult)
                dve.drain()
                nc.vector.tensor_tensor(sc[:, 3, :], gb[2 * n + 1][:], sc[:, 1, :], ALU.subtract)
                dve.drain().then_inc(scaled, 1)
            dve.wait_ge(applied, len(norms))


def rows_from_channels(k, ctx, tag, acc, h_d, w_name, b_name):
    nc, I = k.nc, k.ins
    with ExitStack() as c:
        def sb(name, shape, dt=F32):
            return c.enter_context(nc.sbuf_tensor(f"{tag}_{name}", shape, dt))

        def sem(name):
            return c.enter_context(k.semaphore(f"{tag}_{name}"))

        w, b1 = load_params(k, c, tag, [("w", [P, 2, C], halves(I[w_name])),
                                        ("b", [1, C], I[b_name].unsqueeze(0))])
        aT = [sb(f"aT{b}", [P, 2, P]) for b in (0, 1)]
        h = [sb(f"h{b}", [P, C]) for b in (0, 1)]
        hp = [c.enter_context(nc.psum_tensor(f"{tag}_hp{b}", [P, 512], F32)) for b in (0, 1)]
        a_ready, hp_ready, h_ready, h_free = sem("a_ready"), sem("hp_ready"), sem("h_ready"), sem("h_free")
        h_out = [sem("h_out0"), sem("h_out1")]
        block = c.enter_context(nc.Block())

        @block.vector
        def _(dve):
            dve.sem_inc(hp_ready, 2)

            def tile(t, b, r):
                dve.wait_ge(hp_ready, t + 1)
                nc.vector.tensor_copy(aT[b][:, :, 0:r], acc[:, :, ds(t * P, r)]).then_inc(a_ready, 1)
            over_tiles(dve, tile)

        @block.tensor
        def _(pe):
            pe.sem_inc(h_ready, 2)

            def tile(t, b, r):
                pe.wait_ge(a_ready, t + 1)
                pe.wait_ge(h_ready, t + 1)
                nc.tensor.matmul(hp[b][0:r, 0:C], k.ones[0:1, 0:r], b1[:], start=True, stop=False)
                for half in (0, 1):
                    mm = nc.tensor.matmul(hp[b][0:r, 0:C], aT[b][:, half, 0:r], w[:, half, :],
                                          start=False, stop=half == 1)
                mm.then_inc(hp_ready, 1)
            over_tiles(pe, tile)

        @block.scalar
        def _(act):
            act.sem_inc(h_free, 2)

            def tile(t, b, r):
                act.wait_ge(hp_ready, t + 3)
                act.wait_ge(h_free, t + 1)
                nc.scalar.activation(h[b][0:r, :], hp[b][0:r, 0:C], ACT.Relu).then_inc(h_ready, 1)
            over_tiles(act, tile)

        @block.sync
        def _(sp):
            def tile(t, b, r):
                sp.wait_ge(h_ready, t + 3)
                sp.dma_start(h_d[ds(t * P, r), :], h[b][0:r, :]).then_inc(h_out[b], 16)
                sp.wait_ge(h_out[b], k.nth(t, b) * 16)
                sp.sem_inc(h_free, 1)
            over_tiles(sp, tile)


def mix_and_gate_stage(k, ctx, tag, z, kv, x1_d, yT_d, gates):
    nc, I = k.nc, k.ins
    NE = 8
    with ExitStack() as c:
        def sb(name, shape, dt=F32):
            return c.enter_context(nc.sbuf_tensor(f"{tag}_{name}", shape, dt))

        def sem(name):
            return c.enter_context(k.semaphore(f"{tag}_{name}"))

        gamma, beta, wr, br = load_params(k, c, tag, [
            ("gamma", [P, C], row_on_all(I["L0_ffn_gamma"])), ("beta", [P, C], row_on_all(I["L0_ffn_beta"])),
            ("wr", [P, 2, NE], halves(I["L0_ffn_Wr"])), ("br", [P, NE], row_on_all(I["L0_ffn_br"]))])

        def slots(name, shape):
            return [sb(f"{name}{b}", shape) for b in range(S4)]

        x, xn, x1, y, t1 = (slots(n, [P, C]) for n in ("x", "xn", "x1", "y", "t1"))
        xnT, zc, yT = (slots(n, [P, 2, P]) for n in ("xnT", "zc", "yT"))
        st = slots("st", [P, 16])
        masks = gate_buffers(k, c, tag, NE)
        logits = sb("logits", [P, NT, NE])
        turned = [c.enter_context(nc.psum_tensor(f"{tag}_turned{b}", [P, 4, P], F32)) for b in range(S4)]
        mixed = [c.enter_context(nc.psum_tensor(f"{tag}_mixed{b}", [P, 4, P], F32)) for b in range(S4)]
        x_in, x1_out, y_out = ([sem(f"{n}{b}") for b in range(S4)] for n in ("x_in", "x1_out", "y_out"))
        x_used, asked, answered, xn_ready, z_ready, turned_ready, xnT_ready, mixed_ready = map(sem, (
            "x_used", "asked", "answered", "xn_ready", "z_ready", "turned_ready", "xnT_ready", "mixed_ready"))
        x1_ready, y_ready, yturn_ready, yT_ready, lg_ready, tile_done = map(sem, (
            "x1_ready", "y_ready", "yturn_ready", "yT_ready", "lg_ready", "tile_done"))
        block = c.enter_context(nc.Block())

        @block.sync
        def _(sp):
            sp.sem_inc(x_used, S4)
            for b in range(S4):
                sp.sem_inc(x1_out[b], 16)
                sp.sem_inc(y_out[b], 16)

            def load(t, b, rows):
                sp.wait_ge(x_used, t + 1)
                sp.dma_start(x[b][0:rows, :], I["x"][ds(t * P, rows), :]).then_inc(x_in[b], 16)

            def store_x1(t, b, r):
                sp.wait_ge(x1_ready, t + 1)
                sp.dma_start(x1_d[ds(t * P, r), :], x1[b][0:r, :]).then_inc(x1_out[b], 16)

            def store_y(t, b, r):
                sp.wait_ge(yT_ready, t + 1)
                sp.sem_inc(k.turn, 1)
                sp.dma_start(yT_d[:, :, ds(t * P, r)], yT[b][:, :, 0:r]).then_inc(y_out[b], 16)
            over_fours_io(sp, load, store_x1, store_y)
            all_stored(sp, x1_out)
            all_stored(sp, y_out)

        @block.gpsimd
        def _(pool):
            def copy(t, b, r):
                pool.wait_ge(tile_done, t + 1)
                pool.sem_inc(k.turn, 1)
                nc.gpsimd.tensor_copy(zc[b][:, :, 0:r], z[:, :, ds(t * P, r)]).then_inc(z_ready, 1)
            over_fours(pool, copy)

        @block.vector
        def _(dve):
            dve.sem_inc(tile_done, S4)
            nc.vector.memset(logits[:], 0.0)
            nc.vector.memset(gates[:], 0.0)
            dve.drain()

            def stats(t, b, r):
                dve.wait_ge(x_in[b], times(t, b) * 16)
                norm_stats(k, dve, x[b][0:r, :], st[b], r, asked)

            def apply(t, b, r):
                norm_apply(k, dve, x[b][0:r, :], xn[b][0:r, :], st[b], r, answered, request(t, b, 0, 3))
                dve.sem_inc(xn_ready, 1)

            def mix(t, b, r):
                dve.wait_ge(mixed_ready, t + 1)
                zt = turned[b][0:r, 2:4, :].rearrange("p h d -> p (h d)")
                nc.vector.tensor_tensor(t1[b][0:r], zt, xn[b][0:r], ALU.add)
                dve.drain()
                nc.vector.scalar_tensor_tensor(t1[b][0:r], t1[b][0:r], 0.0, xn[b][0:r], ALU.max, ALU.add)
                dve.drain()
                nc.vector.tensor_tensor(t1[b][0:r], t1[b][0:r], mixed[b][0:r, 0:2, :].rearrange(
                    "p h d -> p (h d)"), ALU.add)
                dve.drain()
                dve.wait_ge(x1_out[b], times(t, b) * 16)
                nc.vector.tensor_tensor(x1[b][0:r], t1[b][0:r], x[b][0:r], ALU.add)
                dve.drain().then_inc(x1_ready, 1)
                dve.sem_inc(x_used, 1)
                norm_stats(k, dve, x1[b][0:r, :], st[b], r, asked)

            def second_norm(t, b, r):
                norm_apply(k, dve, x1[b][0:r, :], t1[b][0:r, :], st[b], r, answered, request(t, b, 1, 3))
                norm_stats(k, dve, t1[b][0:r, :], st[b], r, asked)

            def third_norm(t, b, r):
                norm_apply(k, dve, t1[b][0:r, :], y[b][0:r, :], st[b], r, answered, request(t, b, 2, 3))
                nc.vector.tensor_tensor(y[b][0:r], y[b][0:r], gamma[0:r], ALU.mult)
                dve.drain()
                nc.vector.tensor_tensor(y[b][0:r], y[b][0:r], beta[0:r], ALU.add)
                dve.drain().then_inc(y_ready, 1)

            def take_logits(t, b, r):
                dve.wait_ge(lg_ready, t + 1)
                nc.vector.tensor_tensor(logits[0:r, ds(t, 1), :], turned[b][0:r, 0, 0:NE], br[0:r, :], ALU.add)
                dve.drain().then_inc(tile_done, 1)
            over_fours(dve, stats, apply, mix, second_norm, third_norm, take_logits)
            top_two(k, dve, logits, gates, NE, asked, answered, 3 * REAL_T + 1, masks)

        @block.scalar
        def _(act):
            def root_of(part):
                return lambda t, b, r: root(k, act, st[b], r, asked, answered, request(t, b, part, 3))

            def copy_xn(t, b, r):
                act.wait_ge(turned_ready, t + 1)
                nc.scalar.copy(xnT[b][:, :, 0:r], turned[b][:, 0:2, 0:r]).then_inc(xnT_ready, 1)

            def copy_y(t, b, r):
                act.wait_ge(yturn_ready, t + 1)
                act.wait_ge(y_out[b], times(t, b) * 16)
                nc.scalar.copy(yT[b][:, :, 0:r], mixed[b][:, 2:4, 0:r]).then_inc(yT_ready, 1)
            over_fours(act, root_of(0), copy_xn, root_of(1), root_of(2), copy_y)
            act.wait_ge(asked, 3 * REAL_T + 1)
            nc.scalar.activation(masks[5][:], masks[5][:], ACT.Exp).then_inc(answered, 1)

        @block.tensor
        def _(pe):
            def turn_xn(t, b, r):
                pe.wait_ge(xn_ready, t + 1)
                pe.wait_ge(tile_done, t + 1)
                for half in (0, 1):
                    mm = nc.tensor.transpose(turned[b][:, half, 0:r], xn[b][0:r, half * P:(half + 1) * P],
                                             k.ident[0:r, 0:r])
                mm.then_inc(turned_ready, 1)

            def mix(t, b, r):
                pe.wait_ge(z_ready, t + 1)
                pe.wait_ge(xnT_ready, t + 1)
                for half in (0, 1):
                    nc.tensor.transpose(turned[b][0:r, 2 + half, :], zc[b][:, half, 0:r], k.ident[:])
                for half in (0, 1):
                    mm = nc.tensor.matmul(mixed[b][0:r, half, :], xnT[b][:, half, 0:r], kv[:, half, :],
                                          start=True, stop=True)
                mm.then_inc(mixed_ready, 1)

            def turn_y(t, b, r):
                pe.wait_ge(y_ready, t + 1)
                for half in (0, 1):
                    mm = nc.tensor.transpose(mixed[b][:, 2 + half, 0:r], y[b][0:r, half * P:(half + 1) * P],
                                             k.ident[0:r, 0:r])
                mm.then_inc(yturn_ready, 1)

            def score(t, b, r):
                pe.wait_ge(yT_ready, t + 1)
                for half in (0, 1):
                    mm = nc.tensor.matmul(turned[b][0:r, 0, 0:NE], yT[b][:, half, 0:r], wr[:, half, :],
                                          start=half == 0, stop=half == 1)
                mm.then_inc(lg_ready, 1)
            over_fours(pe, turn_xn, mix, turn_y, score)


def gate_buffers(k, c, tag, NE):
    nc = k.nc
    big = [c.enter_context(nc.sbuf_tensor(f"{tag}_gm{n}", [P, NT, NE], F32)) for n in range(4)]
    small = [c.enter_context(nc.sbuf_tensor(f"{tag}_gs{n}", [P, NT], F32)) for n in range(4)]
    return big + small


def top_two(k, dve, score, gates, NE, asked, answered, nth, bufs):
    nc = k.nc
    masked, number, hot1, hot2, best, gap, w1, w2 = bufs
    shape = [P, NT, NE]

    def wide(a):
        return a[:].unsqueeze(2).broadcast_to(shape)

    ramp = k.ramp[:, 0:NE].unsqueeze(1).broadcast_to(shape)
    nc.vector.tensor_copy(masked[:], score[:])
    dve.drain()
    for hot, value in ((hot1, best), (hot2, gap)):
        nc.vector.tensor_reduce(value[:], masked[:], AX_X, ALU.max)
        dve.drain()
        nc.vector.tensor_tensor(number[:], masked[:], wide(value), ALU.is_lt)
        dve.drain()
        nc.vector.scalar_tensor_tensor(number[:], number[:], float(NE), ramp, ALU.mult, ALU.add)
        dve.drain()
        nc.vector.tensor_reduce(w1[:], number[:], AX_X, ALU.min)
        dve.drain()
        nc.vector.tensor_tensor(hot[:], ramp, wide(w1), ALU.is_equal)
        dve.drain()
        nc.vector.scalar_tensor_tensor(masked[:], hot[:], NEG, masked[:], ALU.mult, ALU.add)
        dve.drain()
    nc.vector.tensor_tensor(gap[:], gap[:], best[:], ALU.subtract).then_inc(asked, 1)
    dve.wait_ge(answered, nth)
    nc.vector.tensor_scalar(w1[:], gap[:], 1.0, None, ALU.add)
    dve.drain()
    nc.vector.reciprocal(w2[:], w1[:])
    dve.drain()
    nc.vector.tensor_tensor(w1[:], gap[:], w2[:], ALU.mult)
    nc.vector.tensor_tensor(hot1[:], hot1[:], wide(w2), ALU.mult)
    dve.drain()
    nc.vector.tensor_tensor(hot2[:], hot2[:], wide(w1), ALU.mult)
    dve.drain()
    nc.vector.tensor_tensor(gates[:], hot1[:], hot2[:], ALU.add)
    dve.drain()


def expert_stage(k, ctx, tag, NE, xT_d, x_d, out_d, gates, w1_name, b1_name, w2_name, b2_name, beside):
    nc, I = k.nc, k.ins
    GN = 2 * P
    H = 4
    with ExitStack() as c:
        def sb(name, shape, dt=F32):
            return c.enter_context(nc.sbuf_tensor(f"{tag}_{name}", shape, dt))

        def sem(name):
            return c.enter_context(k.semaphore(f"{tag}_{name}"))

        w1, w2, b2, b1_rows = load_params(k, c, tag, [
            ("w1", [P, NE, 2, H * P], I[w1_name].rearrange("e (h p) m -> p e h m", p=P)),
            ("w2", [P, NE, H, C], I[w2_name].rearrange("e (h p) m -> p e h m", p=P)),
            ("b2", [NE, C], I[b2_name]),
            ("b1", [NE * H, P], I[b1_name].rearrange("e (h p) -> (e h) p", p=P))])
        b1 = sb("b1c", [P, NE * H])
        xT = [sb(f"xT{u}", [P, 2, GN]) for u in (0, 1)]
        x = [sb(f"x{u}", [P, 2, C]) for u in (0, 1)]
        gs = [sb(f"gs{u}", [P, 2, NE]) for u in (0, 1)]
        gT = [sb(f"gT{u}", [NE, 2, P]) for u in (0, 1)]
        hid = [sb(f"hid{v}", [P, H, GN]) for v in (0, 1)]
        hp = [c.enter_context(nc.psum_tensor(f"{tag}_hp{v}", [P, H, GN], F32)) for v in (0, 1)]
        yp = [c.enter_context(nc.psum_tensor(f"{tag}_yp{v}", [P, 2, C], F32)) for v in (0, 1)]
        gp = c.enter_context(nc.psum_tensor(f"{tag}_gp", [P, 4, P], F32))
        bp = c.enter_context(nc.psum_tensor(f"{tag}_bp", [P, 2, C], F32))
        xT_in, x_in = [sem("xT_in0"), sem("xT_in1")], [sem("x_in0"), sem("x_in1")]
        x_out = [sem("x_out0"), sem("x_out1")]
        xT_used, g_ready, gp_ready, gT_ready, bp_ready = map(
            sem, ("xT_used", "g_ready", "gp_ready", "gT_ready", "bp_ready"))
        hp_ready, hid_ready, yp_ready, yp_read, x_ready = map(
            sem, ("hp_ready", "hid_ready", "yp_ready", "yp_read", "x_ready"))
        b1_turned, b1_ready, hp_read, hid_used, gp_read = map(
            sem, ("b1_turned", "b1_ready", "hp_read", "hid_used", "gp_read"))
        block = c.enter_context(nc.Block())

        pairs = N // GN // 2

        def over_groups(eng, body):
            with eng.Fori(0, pairs) as i:
                for u in (0, 1):
                    body(2 * i + u, u, (P, P))
            body(N // GN, 0, (LAST,))

        @block.sync
        def _(sp):
            sp.sem_inc(xT_used, 2)
            for u in (0, 1):
                sp.sem_inc(x_out[u], 16)

            def load(n, u, tiles):
                w = sum(tiles)
                sp.wait_ge(xT_used, n + 1)
                sp.dma_start(xT[u][:, :, 0:w], xT_d[:, :, ds(n * GN, w)]).then_inc(xT_in[u], 16)
                sp.wait_ge(x_out[u], k.nth(n, u) * 16)
                r = tiles[0]
                sp.dma_start(x[u][0:r, 0:len(tiles), :], x_d[ds(n * GN, w), :].rearrange(
                    "(a p) m -> p a m", p=r)).then_inc(x_in[u], 16)

            def store(n, u, tiles):
                w, r = sum(tiles), tiles[0]
                sp.wait_ge(x_ready, n + 1)
                sp.dma_start(out_d[ds(n * GN, w), :].rearrange("(a p) m -> p a m", p=r),
                             x[u][0:r, 0:len(tiles), :]).then_inc(x_out[u], 16)

            both = (P, P)
            load(0, 0, both)
            with sp.Fori(0, pairs - 1) as i:
                for u in (0, 1):
                    load(2 * i + u + 1, 1 - u, both)
                    store(2 * i + u, u, both)
            last = 2 * pairs
            load(last - 1, 1, both)
            store(last - 2, 0, both)
            load(last, 0, (LAST,))
            store(last - 1, 1, both)
            store(last, 0, (LAST,))
            for u in (0, 1):
                sp.wait_ge(x_out[u], 16 * (pairs + 2 - u))

        @block.gpsimd
        def _(pool):
            beside(pool)

        @block.vector
        def _(dve):
            dve.sem_inc(gp_read, 1)

            def group(n, u, tiles):
                r, nt = tiles[0], len(tiles)
                nc.vector.tensor_copy(gs[u][:, 0:nt, :], gates[:, ds(n * 2, nt), :]).then_inc(g_ready, 1)
                dve.wait_ge(gp_ready, n + 1)
                nc.vector.tensor_copy(gT[u][:, 0:nt, :], gp[0:NE, 0:nt, :]).then_inc(gT_ready, 1)
                dve.wait_ge(x_in[u], k.nth(n, u) * 16)
                dve.wait_ge(bp_ready, n + 1)
                nc.vector.tensor_tensor(x[u][0:r, 0:nt, :], x[u][0:r, 0:nt, :], bp[0:r, 0:nt, :], ALU.add)
                dve.drain()
                dve.sem_inc(gp_read, 1)
                for e in range(NE):
                    m = n * NE + e
                    dve.wait_ge(yp_ready, m + 1)
                    for a in range(nt):
                        nc.vector.scalar_tensor_tensor(x[u][0:r, a, :], yp[e % 2][0:r, a, :],
                                                       gs[u][0:r, a, e:e + 1], x[u][0:r, a, :],
                                                       ALU.mult, ALU.add)
                    dve.drain().then_inc(yp_read, 1)
                dve.sem_inc(x_ready, 1)
            over_groups(dve, group)

        @block.scalar
        def _(act):
            act.wait_ge(b1_turned, 1)
            nc.scalar.copy(b1[:], gp[:, 0, 0:NE * H]).then_inc(b1_ready, 1)
            act.wait_ge(b1_ready, 1)

            def group(n, u, tiles):
                w = sum(tiles)
                for e in range(NE):
                    m = n * NE + e
                    act.wait_ge(hp_ready, m + 1)
                    act.wait_ge(hid_used, m + 1)
                    for j in range(H):
                        nc.scalar.activation(hid[e % 2][:, j, 0:w], hp[e % 2][:, j, 0:w], ACT.Gelu,
                                             bias=b1[:, e * H + j:e * H + j + 1])
                    act.drain().then_inc(hid_ready, 1)
            over_groups(act, group)

        @block.tensor
        def _(pe):
            nc.tensor.transpose(gp[:, 0, 0:NE * H], b1_rows[:], k.ident[0:NE * H, 0:NE * H]
                                ).then_inc(b1_turned, 1)
            pe.wait_ge(b1_ready, 1)
            pe.sem_inc(hid_used, 2)
            pe.sem_inc(yp_read, 2)

            def group(n, u, tiles):
                w, r, nt = sum(tiles), tiles[0], len(tiles)

                def up(e):
                    m = n * NE + e
                    if e >= 2:
                        pe.wait_ge(hid_ready, m - 1)
                    for j in range(H):
                        for ci in (0, 1):
                            mm = nc.tensor.matmul(hp[e % 2][:, j, 0:w], w1[:, e, ci, j * P:(j + 1) * P],
                                                  xT[u][:, ci, 0:w], start=ci == 0, stop=ci == 1)
                    mm.then_inc(hp_ready, 1)

                def down(e):
                    m = n * NE + e
                    pe.wait_ge(hid_ready, m + 1)
                    pe.wait_ge(yp_read, m + 1)
                    for a in range(nt):
                        for j in range(H):
                            mm = nc.tensor.matmul(yp[e % 2][0:r, a, :], hid[e % 2][:, j, a * P:a * P + r],
                                                  w2[:, e, j, :], start=j == 0, stop=j == H - 1)
                    mm.then_inc(yp_ready, 1)
                    pe.sem_inc(hid_used, 1)

                pe.wait_ge(xT_in[u], k.nth(n, u) * 16)
                up(0)
                pe.wait_ge(g_ready, n + 1)
                pe.wait_ge(gp_read, n + 1)
                for a in range(nt):
                    mm = nc.tensor.transpose(gp[0:NE, a, :], gs[u][:, a, :], k.ident[:])
                mm.then_inc(gp_ready, 1)
                up(1)
                pe.wait_ge(gT_ready, n + 1)
                for a in range(nt):
                    mm = nc.tensor.matmul(bp[0:r, a, :], gT[u][:, a, 0:r], b2[:], start=True, stop=True)
                mm.then_inc(bp_ready, 1)
                for e in range(NE):
                    down(e)
                    if e + 2 < NE:
                        up(e + 2)
                pe.sem_inc(xT_used, 1)
            over_groups(pe, group)


def expert_outputs(k, ctx, tag, NE, xT_d, y_d, w1_name, b1_name, w2_name, b2_name, beside):
    nc, I = k.nc, k.ins
    GN = 2 * P
    H = 4
    with ExitStack() as c:
        def sb(name, shape, dt=F32):
            return c.enter_context(nc.sbuf_tensor(f"{tag}_{name}", shape, dt))

        def sem(name):
            return c.enter_context(k.semaphore(f"{tag}_{name}"))

        w1, w2, b2, b1_rows = load_params(k, c, tag, [
            ("w1", [P, NE, 2, H * P], I[w1_name].rearrange("e (h p) m -> p e h m", p=P)),
            ("w2", [P, NE, H, C], I[w2_name].rearrange("e (h p) m -> p e h m", p=P)),
            ("b2", [P, NE * C], row_on_all(I[b2_name].rearrange("e m -> (e m)"))),
            ("b1", [NE * H, P], I[b1_name].rearrange("e (h p) -> (e h) p", p=P))])
        b1 = sb("b1c", [P, NE * H])
        xT = [sb(f"xT{u}", [P, 2, GN]) for u in (0, 1)]
        y = [sb(f"y{e}", [P, 2, C]) for e in range(NE)]
        hid = [sb(f"hid{v}", [P, H, GN]) for v in (0, 1)]
        hp = [c.enter_context(nc.psum_tensor(f"{tag}_hp{v}", [P, H, GN], F32)) for v in (0, 1)]
        yp = [c.enter_context(nc.psum_tensor(f"{tag}_yp{v}", [P, 2, C], F32)) for v in (0, 1)]
        gp = c.enter_context(nc.psum_tensor(f"{tag}_gp", [P, 4, P], F32))
        xT_in = [sem("xT_in0"), sem("xT_in1")]
        y_out = [sem(f"y_out{e}") for e in range(NE)]
        xT_used, b1_turned, b1_ready, hid_used = map(sem, ("xT_used", "b1_turned", "b1_ready", "hid_used"))
        hp_ready, hid_ready, yp_ready, y_ready, yp_read = map(
            sem, ("hp_ready", "hid_ready", "yp_ready", "y_ready", "yp_read"))
        block = c.enter_context(nc.Block())

        pairs = N // GN // 2

        def over_groups(eng, body):
            with eng.Fori(0, pairs) as i:
                for u in (0, 1):
                    body(2 * i + u, u, (P, P))
            body(N // GN, 0, (LAST,))

        @block.sync
        def _(sp):
            sp.sem_inc(xT_used, 2)

            def load(n, u, w):
                sp.wait_ge(xT_used, n + 1)
                sp.dma_start(xT[u][:, :, 0:w], xT_d[:, :, ds(n * GN, w)]).then_inc(xT_in[u], 16)

            def store(n, tiles):
                w, r = sum(tiles), tiles[0]
                for e in range(NE):
                    sp.wait_ge(y_ready, n * NE + e + 1)
                    sp.dma_start(y_d[ds(n * GN, w), e, :].rearrange("(a p) m -> p a m", p=r),
                                 y[e][0:r, 0:len(tiles), :]).then_inc(y_out[e], 16)

            load(0, 0, GN)
            with sp.Fori(0, pairs - 1) as i:
                for u in (0, 1):
                    load(2 * i + u + 1, 1 - u, GN)
                    store(2 * i + u, (P, P))
            last = 2 * pairs
            load(last - 1, 1, GN)
            store(last - 2, (P, P))
            load(last, 0, LAST)
            store(last - 1, (P, P))
            store(last, (LAST,))
            for e in range(NE):
                sp.wait_ge(y_out[e], 16 * (last + 2))

        @block.gpsimd
        def _(pool):
            beside(pool)

        @block.vector
        def _(dve):
            for e in range(NE):
                dve.sem_inc(y_out[e], 16)

            def group(n, u, tiles):
                r, nt = tiles[0], len(tiles)
                for e in range(NE):
                    m = n * NE + e
                    dve.wait_ge(y_out[e], n * 16 + 16)
                    dve.wait_ge(yp_ready, m + 1)
                    nc.vector.tensor_tensor(y[e][0:r, 0:nt, :], yp[e % 2][0:r, 0:nt, :],
                                            b2[0:r, e * C:(e + 1) * C].unsqueeze(1).broadcast_to([r, nt, C]),
                                            ALU.add)
                    dve.drain().then_inc(y_ready, 1)
                    dve.sem_inc(yp_read, 1)
            over_groups(dve, group)

        @block.scalar
        def _(act):
            act.wait_ge(b1_turned, 1)
            nc.scalar.copy(b1[:], gp[:, 0, 0:NE * H]).then_inc(b1_ready, 1)
            act.wait_ge(b1_ready, 1)

            def group(n, u, tiles):
                w = sum(tiles)
                for e in range(NE):
                    m = n * NE + e
                    act.wait_ge(hp_ready, m + 1)
                    act.wait_ge(hid_used, m + 1)
                    for j in range(H):
                        nc.scalar.activation(hid[e % 2][:, j, 0:w], hp[e % 2][:, j, 0:w], ACT.Gelu,
                                             bias=b1[:, e * H + j:e * H + j + 1])
                    act.drain().then_inc(hid_ready, 1)
            over_groups(act, group)

        @block.tensor
        def _(pe):
            nc.tensor.transpose(gp[:, 0, 0:NE * H], b1_rows[:], k.ident[0:NE * H, 0:NE * H]
                                ).then_inc(b1_turned, 1)
            pe.wait_ge(b1_ready, 1)
            pe.sem_inc(hid_used, 2)
            pe.sem_inc(yp_read, 2)

            def group(n, u, tiles):
                w, r, nt = sum(tiles), tiles[0], len(tiles)

                def up(e):
                    m = n * NE + e
                    if e >= 2:
                        pe.wait_ge(hid_ready, m - 1)
                    for j in range(H):
                        for ci in (0, 1):
                            mm = nc.tensor.matmul(hp[e % 2][:, j, 0:w], w1[:, e, ci, j * P:(j + 1) * P],
                                                  xT[u][:, ci, 0:w], start=ci == 0, stop=ci == 1)
                    mm.then_inc(hp_ready, 1)

                def down(e):
                    m = n * NE + e
                    pe.wait_ge(hid_ready, m + 1)
                    pe.wait_ge(yp_read, m + 1)
                    for a in range(nt):
                        for j in range(H):
                            mm = nc.tensor.matmul(yp[e % 2][0:r, a, :], hid[e % 2][:, j, a * P:a * P + r],
                                                  w2[:, e, j, :], start=j == 0, stop=j == H - 1)
                    mm.then_inc(yp_ready, 1)
                    pe.sem_inc(hid_used, 1)

                pe.wait_ge(xT_in[u], k.nth(n, u) * 16)
                up(0)
                up(1)
                for e in range(NE):
                    down(e)
                    if e + 2 < NE:
                        up(e + 2)
                pe.sem_inc(xT_used, 1)
            over_groups(pe, group)


def combine_stage(k, ctx, tag, NE, y_d, x_d, out_d, gates):
    nc = k.nc
    S = 4
    with ExitStack() as c:
        x = [c.enter_context(nc.sbuf_tensor(f"{tag}_x{b}", [P, C], F32)) for b in range(S)]
        y = [c.enter_context(nc.sbuf_tensor(f"{tag}_y{b}", [P, NE, C], F32)) for b in range(S)]
        landed = [c.enter_context(k.semaphore(f"{tag}_landed{b}")) for b in range(S)]
        out = [c.enter_context(k.semaphore(f"{tag}_out{b}")) for b in range(S)]
        done = c.enter_context(k.semaphore(f"{tag}_done"))
        block = c.enter_context(nc.Block())

        def over(eng, body):
            with eng.Fori(0, REAL_T // S) as i:
                for b in range(S):
                    body(i * S + b, b, i * 16 + 16, P)
            body(REAL_T - 1, 0, REAL_T // S * 16 + 16, LAST)

        @block.sync
        def _(sp):
            def load(t, b, nth, r):
                sp.wait_ge(out[b], nth)
                sp.dma_start(y[b][0:r], y_d[ds(t * P, r), :, :]).then_inc(landed[b], 16)
                sp.dma_start(x[b][0:r, :], x_d[ds(t * P, r), :]).then_inc(landed[b], 16)
            over(sp, load)

        @block.vector
        def _(dve):
            def tile(t, b, nth, r):
                dve.wait_ge(landed[b], 2 * nth)
                for e in range(NE):
                    nc.vector.scalar_tensor_tensor(x[b][0:r, :], y[b][0:r, e, :], gates[0:r, ds(t, 1), e],
                                                   x[b][0:r, :], ALU.mult, ALU.add)
                    dve.drain()
                dve.sem_inc(done, 1)
            over(dve, tile)

        @block.scalar
        def _(act):
            for b in range(S):
                act.sem_inc(out[b], 16)

            def store(t, b, nth, r):
                act.wait_ge(done, t + 1)
                act.dma_start(out_d[ds(t * P, r), :], x[b][0:r, :]).then_inc(out[b], 16)
            over(act, store)
            for b in range(S):
                act.wait_ge(out[b], 16 * (REAL_T // S + 1 + (b == 0)))


SCALE = 32 ** -0.5
HG = 16
ROW = HG + 4


def channels_stage(k, ctx, tag, x2_d, xn_d, xT, kmax):
    nc, I = k.nc, k.ins
    blocks = NP // W
    with ExitStack() as c:
        def sb(name, shape, dt=F32):
            return c.enter_context(nc.sbuf_tensor(f"{tag}_{name}", shape, dt))

        def sem(name):
            return c.enter_context(k.semaphore(f"{tag}_{name}"))

        wk, = load_params(k, c, tag, [("wk", [P, 2, P], halves(I["L1_mix_W_qkv"])[:, :, P:2 * P])])
        x, xn = ([sb(f"{n}{b}", [P, C]) for b in range(S4)] for n in ("x", "xn"))
        st, kpart = [sb(f"st{b}", [P, 16]) for b in range(S4)], sb("kpart", [P, blocks])
        turned = [c.enter_context(nc.psum_tensor(f"{tag}_turned{b}", [P, 4, P], F32)) for b in range(S4)]
        kp = [c.enter_context(nc.psum_tensor(f"{tag}_kp{b}", [P, 512], F32)) for b in (0, 1)]
        x_in, xn_out = ([sem(f"{n}{b}") for b in range(S4)] for n in ("x_in", "xn_out"))
        x_used, xn_ready, turned_ready, turned_read, asked, answered, kp_ready, kp_read = map(sem, (
            "x_used", "xn_ready", "turned_ready", "turned_read", "asked", "answered", "kp_ready",
            "kp_read"))
        block = c.enter_context(nc.Block())

        @block.sync
        def _(sp):
            sp.sem_inc(x_used, S4)
            for b in range(S4):
                sp.sem_inc(xn_out[b], 16)

            def load(t, b, r):
                sp.wait_ge(x_used, t + 1)
                sp.dma_start(x[b][0:r, :], x2_d[ds(t * P, r), :]).then_inc(x_in[b], 16)

            def store(t, b, r):
                sp.wait_ge(xn_ready, t + 1)
                sp.dma_start(xn_d[ds(t * P, r), :], xn[b][0:r, :]).then_inc(xn_out[b], 16)
            over_fours_io(sp, load, store)
            all_stored(sp, xn_out)

        @block.vector
        def _(dve):
            def stats(t, b, r):
                dve.wait_ge(x_in[b], times(t, b) * 16)
                norm_stats(k, dve, x[b][0:r, :], st[b], r, asked)

            def apply(t, b, r):
                dve.wait_ge(xn_out[b], times(t, b) * 16)
                dve.wait_ge(turned_ready, t + 1)
                norm_apply(k, dve, x[b][0:r, :], xn[b][0:r, :], st[b], r, answered, t + 1)
                dve.sem_inc(x_used, 1)
                dve.sem_inc(xn_ready, 1)
            dve.sem_inc(turned_ready, S4)
            over_fours(dve, stats, apply)
            with dve.Fori(0, blocks // 2 - 1) as i:
                for s in (0, 1):
                    dve.wait_ge(kp_ready, 2 * i + s + 1)
                    nc.vector.tensor_reduce(kpart[:, ds(2 * i + s, 1)], kp[s][:, 0:W], AX_X, ALU.max
                                            ).then_inc(kp_read, 1)
            for n in (blocks - 2, blocks - 1):
                dve.wait_ge(kp_ready, n + 1)
                w = min(W, N - n * W)
                nc.vector.tensor_reduce(kpart[:, n:n + 1], kp[n % 2][:, 0:w], AX_X, ALU.max).then_inc(kp_read, 1)
            dve.drain()
            nc.vector.tensor_reduce(kmax[:], kpart[:], AX_X, ALU.max)

        @block.scalar
        def _(act):
            nc.scalar.activation(xT[:, :, N:NP], k.ones[:, 0:2 * (NP - N)].rearrange("p (a b) -> p a b", a=2),
                                 ACT.Copy, scale=0.0)

            def roots(t, b, r):
                root(k, act, st[b], r, asked, answered, t + 1)

            def copy(t, b, r):
                act.wait_ge(turned_ready, t + 1 + S4)
                nc.scalar.copy(xT[:, :, ds(t * P, r)], turned[b][:, 0:2, 0:r]).then_inc(turned_read, 1)
            over_fours(act, roots, copy)

        @block.tensor
        def _(pe):
            pe.sem_inc(turned_read, S4)
            pe.sem_inc(kp_read, 2)

            def tile(t, b, r):
                pe.wait_ge(xn_ready, t + 1)
                pe.wait_ge(turned_read, t + 1)
                for half in (0, 1):
                    mm = nc.tensor.transpose(turned[b][:, half, 0:r], xn[b][0:r, half * P:(half + 1) * P],
                                             k.ident[0:r, 0:r])
                mm.then_inc(turned_ready, 1)
            over_fours(pe, tile)
            pe.wait_ge(turned_read, S4 + REAL_T)
            with pe.Fori(0, blocks // 2) as i:
                for s in (0, 1):
                    pe.wait_ge(kp_read, 2 * i + s + 1)
                    for ci in (0, 1):
                        mm = nc.tensor.matmul(kp[s][:, 0:W], wk[:, ci, :], xT[:, ci, ds((2 * i + s) * W, W)],
                                              start=ci == 0, stop=ci == 1)
                    mm.then_inc(kp_ready, 1)


def context_stage(k, ctx, tag, xT, kmax, ctx_out):
    nc, I = k.nc, k.ins
    with ExitStack() as c:
        def sb(name, shape, dt=F32):
            return c.enter_context(nc.sbuf_tensor(f"{tag}_{name}", shape, dt))

        def sem(name):
            return c.enter_context(k.semaphore(f"{tag}_{name}"))

        wkv, wo = load_params(k, c, tag, [("wkv", [P, 2, 2 * P], halves(I["L1_mix_W_qkv"])[:, :, P:3 * P]),
                                          ("wo", [P, C], I["L1_mix_W_out"])])
        xs = [sb(f"xs{b}", [P, 2, P]) for b in range(S4)]
        ek = [sb(f"ek{b}", [P, P]) for b in range(S4)]
        v1 = [sb(f"v1{b}", [P, P + 1]) for b in range(S4)]
        maxrow, kmax_wide = sb("maxrow", [P, P]), sb("kmax_wide", [P, P])
        zero = sb("zero", [P, P + 1])
        cs, csT, inv = sb("cs", [P, P]), sb("csT", [P, P]), sb("inv", [P, 1])
        kvp = [c.enter_context(nc.psum_tensor(f"{tag}_kvp{b}", [P, 512], F32)) for b in range(S4)]
        cp = c.enter_context(nc.psum_tensor(f"{tag}_cp", [P, 512], F32))
        mp = c.enter_context(nc.psum_tensor(f"{tag}_mp", [P, 512], F32))
        xs_ready, kvp_ready, shifted, v_ready, ek_ready, summed = map(
            sem, ("xs_ready", "kvp_ready", "shifted", "v_ready", "ek_ready", "summed"))
        begun, row_ready, one, turned, copied, outed = map(
            sem, ("begun", "row_ready", "one", "turned", "copied", "outed"))
        block = c.enter_context(nc.Block())

        @block.gpsimd
        def _(pool):
            pool.sem_inc(kvp_ready, S4)

            def tile(t, b, r):
                pool.wait_ge(kvp_ready, t + 1)
                pool.sem_inc(k.turn, 1)
                nc.gpsimd.tensor_copy(xs[b][:, :, 0:r], xT[:, :, ds(t * P, r)]).then_inc(xs_ready, 1)
            over_fours(pool, tile)

        @block.vector
        def _(dve):
            nc.vector.memset(zero[:], 0.0)
            for b in range(S4):
                nc.vector.memset(v1[b][:, P:P + 1], 1.0)
            nc.vector.tensor_scalar(kmax_wide[:], k.ones[:], kmax[:, 0:1], None, ALU.mult)
            dve.drain().then_inc(begun, 1)
            dve.wait_ge(row_ready, 1)
            nc.vector.tensor_copy(maxrow[:], mp[:, 0:P])
            dve.drain()
            dve.sem_inc(summed, S4)

            def tile(t, b, r):
                dve.wait_ge(kvp_ready, t + 1 + S4)
                dve.wait_ge(summed, t + 1)
                nc.vector.tensor_tensor(ek[b][0:r], kvp[b][0:r, 0:P], maxrow[0:r], ALU.subtract
                                        ).then_inc(shifted, 1)
                nc.vector.tensor_copy(v1[b][0:r, 0:P], kvp[b][0:r, P:2 * P]).then_inc(v_ready, 1)
            over_fours(dve, tile)
            dve.wait_ge(summed, 1 + S4 + REAL_T)
            nc.vector.reciprocal(inv[:], cp[:, P:P + 1])
            dve.drain()
            nc.vector.tensor_scalar(cs[:], cp[:, 0:P], inv[:, 0:1], SCALE, ALU.mult, ALU.mult)
            dve.drain()
            nc.vector.tensor_tensor(cs[:], cs[:], k.block_diag[:], ALU.mult)
            dve.drain().then_inc(one, 1)
            dve.wait_ge(turned, 1)
            nc.vector.tensor_copy(csT[:], mp[:, 0:P]).then_inc(copied, 1)
            dve.wait_ge(outed, 1)
            nc.vector.tensor_copy(ctx_out[:], kvp[0][:, 0:C])

        @block.scalar
        def _(act):
            def tile(t, b, r):
                act.wait_ge(shifted, t + 1)
                nc.scalar.activation(ek[b][0:r], ek[b][0:r], ACT.Exp).then_inc(ek_ready, 1)
            over_fours(act, tile)

        @block.tensor
        def _(pe):
            pe.wait_ge(begun, 1)
            nc.tensor.matmul(mp[:, 0:P], kmax_wide[:], k.ident[:], start=True, stop=True).then_inc(row_ready, 1)
            nc.tensor.matmul(cp[:, 0:P + 1], zero[:, 0:P], zero[:], start=True, stop=False,
                             skip_group_check=True)

            def dense(t, b, r):
                pe.wait_ge(xs_ready, t + 1)
                for half in (0, 1):
                    mm = nc.tensor.matmul(kvp[b][0:r, 0:2 * P], xs[b][:, half, 0:r], wkv[:, half, :],
                                          start=half == 0, stop=half == 1)
                mm.then_inc(kvp_ready, 1)

            def outer(t, b, r):
                pe.wait_ge(v_ready, t + 1)
                pe.wait_ge(ek_ready, t + 1)
                nc.tensor.matmul(cp[:, 0:P + 1], ek[b][0:r, :], v1[b][0:r, :], start=False, stop=False,
                                 skip_group_check=True).then_inc(summed, 1)
            over_fours(pe, dense, outer)
            nc.tensor.matmul(cp[:, 0:P + 1], zero[:, 0:P], zero[:], start=False, stop=True,
                             skip_group_check=True).then_inc(summed, 1)
            pe.wait_ge(one, 1)
            nc.tensor.transpose(mp[:, 0:P], cs[:], k.ident[:]).then_inc(turned, 1)
            pe.wait_ge(copied, 1)
            nc.tensor.matmul(kvp[0][:, 0:C], csT[:], wo[:], start=True, stop=True).then_inc(outed, 1)


def degree_rows(k, tag, z_d, count, out_d):
    nc = k.nc
    with ExitStack() as c:
        idx = c.enter_context(nc.sbuf_tensor(f"{tag}_idx", [P, NT], I32))
        rows = [c.enter_context(nc.sbuf_tensor(f"{tag}_rows{b}", [P, C], F32)) for b in range(4)]
        made = c.enter_context(k.semaphore(f"{tag}_made"))
        got = [c.enter_context(k.semaphore(f"{tag}_got{b}")) for b in range(4)]
        out = [c.enter_context(k.semaphore(f"{tag}_out{b}")) for b in range(4)]
        block = c.enter_context(nc.Block())

        @block.vector
        def _(dve):
            nc.vector.tensor_scalar(idx[:], count[:, 0:NT], float(z_d.shape[0] - 1), None, ALU.min
                                    ).then_inc(made, 1)

        @block.gpsimd
        def _(pool):
            pool.wait_ge(made, 1)
            for t in range(NT):
                b = t % 4
                if t >= 4:
                    pool.wait_ge(out[b], 16 * (t // 4))
                nc.gpsimd.indirect_dma_start(rows[b][:], None, z_d, bass.IndirectOffsetOnAxis(
                    ap=idx[:, t:t + 1], axis=0)).then_inc(got[b], 16)

        @block.sync
        def _(sp):
            for t in range(NT):
                b = t % 4
                sp.wait_ge(got[b], 16 * (t // 4 + 1))
                sp.dma_start(out_d[t * P:(t + 1) * P, :], rows[b][:]).then_inc(out[b], 16)
            for b in range(4):
                sp.wait_ge(out[b], 16 * ((NT - b + 3) // 4))


def graph_and_mix_stage(k, ctx, tag, x2_d, xn_d, xT, cw, edge_sum, out_deg, zin_d, zout_d, x3_d, yT_d,
                        h_d, node_h):
    nc, I = k.nc, k.ins
    with ExitStack() as c:
        def sb(name, shape, dt=F32):
            return c.enter_context(nc.sbuf_tensor(f"{tag}_{name}", shape, dt))

        def sem(name):
            return c.enter_context(k.semaphore(f"{tag}_{name}"))

        def col(v):
            return v.rearrange("n a -> (n a)")

        wq, ws, wc, bc, wv, bv, bs, bo, wg, a_src, a_dst = load_params(k, c, tag, [
            ("wq", [P, 2, P], halves(I["L1_mix_W_qkv"])[:, :, 0:P]),
            ("ws", [P, C], I["L1_gnn_W_sum"]),
            ("wc", [P, C], row_on_all(I["L1_gnn_W_cent"].rearrange("a c -> (a c)"))),
            ("bc", [P, C], row_on_all(I["L1_gnn_b_cent"])),
            ("wv", [P, C], row_on_all(I["L1_gnn_W_vor"].rearrange("a c -> (a c)"))),
            ("bv", [P, C], row_on_all(I["L1_gnn_b_vor"])),
            ("bs", [P, C], row_on_all(I["L1_gnn_b_sum"])),
            ("bo", [1, C], I["L1_mix_b_out"].unsqueeze(0)),
            ("wg", [P, 2, HG], halves(I["L1_ffn_W_gat"])),
            ("as", [P, HG], row_on_all(I["L1_ffn_att_src"].rearrange("a b -> (a b)"))),
            ("ad", [P, HG], row_on_all(I["L1_ffn_att_dst"].rearrange("a b -> (a b)")))])

        def slots(name, shape):
            return [sb(f"{name}{b}", shape) for b in range(S4)]

        x2, xn, zi, zo, x3, y, t1 = (slots(n, [P, C]) for n in ("x2", "xn", "zi", "zo", "x3", "y", "t1"))
        cv, cent, prod = slots("cv", [P, 2]), slots("cent", [P, 2, C]), slots("prod", [P, 2, HG])
        es, qT, yT = slots("es", [P, P]), slots("qT", [P, P]), slots("yT", [P, 2, P])
        hrow, st = slots("hrow", [P, ROW + 4]), slots("st", [P, 16])
        qp = [c.enter_context(nc.psum_tensor(f"{tag}_qp{b}", [P, 4, P], F32)) for b in range(S4)]
        sp_ = [c.enter_context(nc.psum_tensor(f"{tag}_sp{b}", [P, 512], F32)) for b in range(S4)]
        loaded, out = ([sem(f"{n}{b}") for b in range(S4)] for n in ("loaded", "out"))
        used, asked, answered, es_ready, qp_ready, qT_ready, sum_ready, cent_ready, sig_ready = map(sem, (
            "used", "asked", "answered", "es_ready", "qp_ready", "qT_ready", "sum_ready", "cent_ready",
            "sig_ready"))
        y_ready, yp_ready, yT_ready, hp_ready, hrow_ready, hrow_used = map(sem, (
            "y_ready", "yp_ready", "yT_ready", "hp_ready", "hrow_ready", "hrow_used"))
        block = c.enter_context(nc.Block())

        @block.sync
        def _(sp):
            sp.sem_inc(used, S4)
            for b in range(S4):
                sp.sem_inc(out[b], 48)

            def load(t, b, r):
                at = ds(t * P, r)
                sp.wait_ge(used, t + 1)
                for dst, src in ((x2, x2_d), (xn, xn_d), (zi, zin_d), (zo, zout_d)):
                    sp.dma_start(dst[b][0:r, :], src[at, :]).then_inc(loaded[b], 16)
                sp.dma_start(cv[b][0:r, 0:1], I["node_vec1_n2"][at, :]).then_inc(loaded[b], 16)
                sp.dma_start(cv[b][0:r, 1:2], I["node_vec1"][at, :]).then_inc(loaded[b], 16)

            def store(t, b, r):
                at = ds(t * P, r)
                sp.wait_ge(hrow_ready, t + 1)
                sp.dma_start(x3_d[at, :], x3[b][0:r, :]).then_inc(out[b], 16)
                sp.dma_start(yT_d[:, :, at], yT[b][:, :, 0:r]).then_inc(out[b], 16)
                sp.dma_start(h_d[at, :], hrow[b][0:r, 0:ROW]).then_inc(out[b], 16)
            over_fours_io(sp, load, store)
            for b in range(S4):
                sp.wait_ge(out[b], 48 * (REAL_T // S4 + 1 + (b == 0)))

        @block.gpsimd
        def _(pool):
            pool.sem_inc(hp_ready, S4)

            def copy(t, b, r):
                pool.wait_ge(hp_ready, t + 1)
                pool.sem_inc(k.turn, 1)
                nc.gpsimd.tensor_copy(es[b][:, 0:r], edge_sum[:, ds(t * P, r)]).then_inc(es_ready, 1)
            over_fours(pool, copy)

        @block.vector
        def _(dve):
            dve.sem_inc(sig_ready, S4)
            nc.vector.memset(node_h[:], 0.0)
            dve.drain()

            def parts(t, b, r):
                dve.wait_ge(loaded[b], times(t, b) * 96)
                for j, (w_, b_) in enumerate(((wc, bc), (wv, bv))):
                    nc.vector.scalar_tensor_tensor(cent[b][0:r, j, :], w_[0:r], cv[b][0:r, j:j + 1], b_[0:r],
                                                   ALU.mult, ALU.add)
                dve.drain().then_inc(cent_ready, 1)
                nc.vector.tensor_tensor(t1[b][0:r], x2[b][0:r], xn[b][0:r], ALU.add)
                dve.drain()
                nc.vector.tensor_tensor(t1[b][0:r], t1[b][0:r], zi[b][0:r], ALU.add)
                dve.drain()
                nc.vector.tensor_tensor(t1[b][0:r], t1[b][0:r], zo[b][0:r], ALU.add)
                dve.drain()
                nc.vector.scalar_tensor_tensor(t1[b][0:r], bs[0:r], out_deg[0:r, ds(t, 1)], t1[b][0:r],
                                               ALU.mult, ALU.add)
                dve.drain().then_inc(used, 1)

            def whole(t, b, r):
                dve.wait_ge(sig_ready, t + 1 + S4)
                nc.vector.tensor_tensor(t1[b][0:r], t1[b][0:r], cent[b][0:r, 0, :], ALU.add)
                dve.drain()
                nc.vector.tensor_tensor(t1[b][0:r], t1[b][0:r], cent[b][0:r, 1, :], ALU.add)
                dve.drain()
                dve.wait_ge(sum_ready, t + 1)
                dve.wait_ge(out[b], times(t, b) * 48)
                nc.vector.tensor_tensor(x3[b][0:r], t1[b][0:r], sp_[b][0:r, 0:C], ALU.add)
                dve.drain()
                norm_stats(k, dve, x3[b][0:r], st[b], r, asked)

            def norm(t, b, r):
                norm_apply(k, dve, x3[b][0:r], y[b][0:r], st[b], r, answered, t + 1)
                dve.sem_inc(y_ready, 1)

            def attention(t, b, r):
                dve.wait_ge(hp_ready, t + 1 + S4)
                h = sp_[b][0:r, 0:HG]
                nc.vector.tensor_copy(hrow[b][0:r, 0:HG], h)
                nc.vector.tensor_tensor(prod[b][0:r, 0, :], h, a_src[0:r], ALU.mult)
                nc.vector.tensor_tensor(prod[b][0:r, 1, :], h, a_dst[0:r], ALU.mult)
                dve.drain()
                nc.vector.tensor_reduce(hrow[b][0:r, HG:HG + 8].rearrange("p (a h) -> p a h", a=2),
                                        prod[b][0:r].rearrange("p a (h e) -> p a h e", e=4), AX_X, ALU.add)
                dve.drain()
                nc.vector.tensor_copy(node_h[0:r, ds(t, 1), :], hrow[b][0:r, :])
                dve.drain().then_inc(hrow_ready, 1)
                dve.sem_inc(hrow_used, 1)
            over_fours(dve, parts, whole, norm, attention)

        @block.scalar
        def _(act):
            def sigmoid(t, b, r):
                act.wait_ge(cent_ready, t + 1)
                nc.scalar.activation(cent[b][0:r], cent[b][0:r], ACT.Sigmoid).then_inc(sig_ready, 1)

            def copy_q(t, b, r):
                act.wait_ge(qp_ready, t + 1)
                nc.scalar.copy(qT[b][:, 0:r], qp[b][:, 0, 0:r]).then_inc(qT_ready, 1)

            def roots(t, b, r):
                root(k, act, st[b], r, asked, answered, t + 1)

            def copy_y(t, b, r):
                act.wait_ge(yp_ready, t + 1)
                nc.scalar.copy(yT[b][:, :, 0:r], qp[b][:, 2:4, 0:r]).then_inc(yT_ready, 1)
            over_fours(act, copy_q, sigmoid, roots, copy_y)

        @block.tensor
        def _(pe):
            pe.sem_inc(hrow_used, S4)

            def query(t, b, r):
                for half in (0, 1):
                    mm = nc.tensor.matmul(qp[b][:, 0, 0:r], wq[:, half, :], xT[:, half, ds(t * P, r)],
                                          start=half == 0, stop=half == 1)
                mm.then_inc(qp_ready, 1)

            def total(t, b, r):
                pe.wait_ge(es_ready, t + 1)
                pe.wait_ge(qT_ready, t + 1)
                pe.wait_ge(hrow_used, t + 1)
                nc.tensor.matmul(sp_[b][0:r, 0:C], k.ones[0:1, 0:r], bo[:], start=True, stop=False)
                nc.tensor.matmul(sp_[b][0:r, 0:C], es[b][:, 0:r], ws[:], start=False, stop=False)
                nc.tensor.matmul(sp_[b][0:r, 0:C], qT[b][:, 0:r], cw[:], start=False, stop=True
                                 ).then_inc(sum_ready, 1)

            def turn(t, b, r):
                pe.wait_ge(y_ready, t + 1)
                for half in (0, 1):
                    mm = nc.tensor.transpose(qp[b][:, 2 + half, 0:r], y[b][0:r, half * P:(half + 1) * P],
                                             k.ident[0:r, 0:r])
                mm.then_inc(yp_ready, 1)

            def project(t, b, r):
                pe.wait_ge(yT_ready, t + 1)
                for half in (0, 1):
                    mm = nc.tensor.matmul(sp_[b][0:r, 0:HG], yT[b][:, half, 0:r], wg[:, half, :],
                                          start=half == 0, stop=half == 1)
                mm.then_inc(hp_ready, 1)
            over_fours(pe, query, total, turn, project)


J = G // P
LOW = -1.0e38


def carry_in(k, ctx, tag, last, factor, K, op0, op1, init):
    nc = k.nc
    cin = ctx.enter_context(nc.sbuf_tensor(f"{tag}_cin", [P, K], F32))
    with ExitStack() as c:
        rows = [c.enter_context(nc.sbuf_tensor(f"{tag}_row{n}", [K, P], F32)) for n in (0, 1)]
        state = c.enter_context(nc.sbuf_tensor(f"{tag}_state", [K, P + 1], F32))
        turned = [c.enter_context(nc.psum_tensor(f"{tag}_turn{n}", [P, 512], F32)) for n in range(3)]
        there, scanned, back = [c.enter_context(k.semaphore(f"{tag}_{n}")) for n in ("there", "scanned", "back")]
        block = c.enter_context(nc.Block())

        @block.tensor
        def _(pe):
            nc.tensor.transpose(turned[0][0:K, 0:P], last[:], k.ident[:])
            nc.tensor.transpose(turned[1][0:K, 0:P], factor[:], k.ident[:]).then_inc(there, 1)
            pe.wait_ge(scanned, 1)
            nc.tensor.transpose(turned[2][:, 0:K], state[:, 0:P], k.ident[0:K, 0:K]).then_inc(back, 1)

        @block.vector
        def _(dve):
            nc.vector.memset(state[:, 0:1], init)
            dve.wait_ge(there, 1)
            for n in (0, 1):
                nc.vector.tensor_copy(rows[n][:], turned[n][0:K, 0:P])
            dve.drain()
            nc.vector.tensor_tensor_scan(state[:, 1:P + 1], rows[1][:], rows[0][:], init, op0, op1)
            dve.drain().then_inc(scanned, 1)
            dve.wait_ge(back, 1)
            nc.vector.tensor_copy(cin[:], turned[2][:, 0:K])
    return cin


def node_targets(k, ctx, tag, start, count):
    nc = k.nc
    first = ctx.enter_context(nc.sbuf_tensor(f"{tag}_first_i", [P, NT], I32))
    last = ctx.enter_context(nc.sbuf_tensor(f"{tag}_last_i", [P, NT], I32))
    some = ctx.enter_context(nc.sbuf_tensor(f"{tag}_some", [P, NT], F32))
    with (nc.sbuf_tensor(f"{tag}_spare", [P, 1], F32) as spare,
          nc.sbuf_tensor(f"{tag}_a", [P, NT], F32) as a,
          nc.sbuf_tensor(f"{tag}_b", [P, NT], F32) as b,
          nc.Block() as block):
        @block.vector
        def _(dve):
            s, n = start[:, 0:NT], count[:, 0:NT]
            nc.vector.tensor_scalar(some[:], n, 0.0, None, ALU.is_gt)
            nc.vector.tensor_scalar(spare[:], k.lane[:], float(G), None, ALU.add)
            nc.vector.tensor_tensor(b[:], s, n, ALU.add)
            dve.drain()
            nc.vector.tensor_scalar(last[:], b[:], -1.0, 0.0, ALU.add, ALU.max)
            nc.vector.tensor_scalar(a[:], s, spare[:, 0:1], None, ALU.subtract)
            dve.drain()
            nc.vector.tensor_tensor(a[:], a[:], some[:], ALU.mult)
            dve.drain()
            nc.vector.tensor_scalar(first[:], a[:], spare[:, 0:1], None, ALU.add)
    return first, last, some


def spread_to_starts(k, tag, node_h, first_i, adst_d):
    nc = k.nc
    with ExitStack() as c:
        zero = c.enter_context(nc.sbuf_tensor(f"{tag}_zero", [P, J * 4], F32))
        rows = c.enter_context(nc.sbuf_tensor(f"{tag}_rows", [P, NT, 4], F32))
        made, cleared, done = [c.enter_context(k.semaphore(f"{tag}_{n}")) for n in ("made", "cleared", "done")]
        block = c.enter_context(nc.Block())

        @block.vector
        def _(dve):
            nc.vector.memset(zero[:], 0.0)
            nc.vector.tensor_copy(rows[:], node_h[:, :, ROW:ROW + 4])
            dve.drain().then_inc(made, 1)

        @block.sync
        def _(sp):
            sp.wait_ge(made, 1)
            sp.dma_start(adst_d[0:G, :].rearrange("(p j) h -> p (j h)", p=P), zero[:]).then_inc(cleared, 16)

        @block.gpsimd
        def _(pool):
            pool.wait_ge(cleared, 16)
            for t in range(NT):
                nc.gpsimd.indirect_dma_start(adst_d, bass.IndirectOffsetOnAxis(ap=first_i[:, t:t + 1], axis=0),
                                             rows[:, t, :], None).then_inc(done, 16)
            pool.wait_ge(done, 16 * NT)


def sorted_lists(k, tag, sorted_d, idx_all, same):
    nc = k.nc
    with (nc.sbuf_tensor(f"{tag}_cur", [P, J, 2], F32) as cur,
          nc.sbuf_tensor(f"{tag}_prev", [P, J, 2], F32) as prev,
          k.semaphore(f"{tag}_lists_in") as lists_in, nc.Block() as block):
        @block.sync
        def _(sp):
            for tile, at in ((cur, 1), (prev, 0)):
                sp.dma_start(tile[:], sorted_d[at:at + G, :].rearrange("(p j) w -> p j w", p=P)
                             ).then_inc(lists_in, 16)

        @block.vector
        def _(dve):
            dve.wait_ge(lists_in, 32)
            nc.vector.tensor_copy(idx_all[:], cur[:, :, 0])
            nc.vector.tensor_tensor(same[:], cur[:, :, 1], prev[:, :, 1], ALU.is_equal)


def gather_beside(k, c, tag, table, idx_all, edge):
    nc = k.nc
    R = 16
    pairs = J // (2 * R)
    idx = [c.enter_context(nc.sbuf_tensor(f"{tag}_idx{h}", [P, R], I32)) for h in (0, 1)]
    got = [c.enter_context(nc.sbuf_tensor(f"{tag}_got{h}", [P, R, ROW], F32)) for h in (0, 1)]
    gathered = [c.enter_context(k.semaphore(f"{tag}_gathered{h}")) for h in (0, 1)]
    moved, idx_ready = (c.enter_context(k.semaphore(f"{tag}_{n}")) for n in ("moved", "idx_ready"))

    def program(pool):
        def ask(n, h):
            nc.gpsimd.tensor_copy(idx[h][:], idx_all[:, ds(n * R, R)]).then_inc(idx_ready, 1)
            pool.wait_ge(idx_ready, n + 1)
            pool.sem_inc(k.turn, 1)
            for b in range(R):
                nc.gpsimd.indirect_dma_start(got[h][:, b, :], None, table, bass.IndirectOffsetOnAxis(
                    ap=idx[h][:, b:b + 1], axis=0)).then_inc(gathered[h], 16)

        def move(n, h, nth):
            pool.wait_ge(gathered[h], nth * (16 * R))
            pool.sem_inc(k.turn, 1)
            nc.gpsimd.tensor_copy(edge[:, ds(n * R, R), :], got[h][:]).then_inc(moved, 1)
            pool.wait_ge(moved, n + 1)
            pool.sem_inc(k.turn, 1)

        ask(0, 0)
        ask(1, 1)
        with pool.Fori(1, pairs) as i:
            for h in (0, 1):
                move(2 * i + h - 2, h, i)
                ask(2 * i + h, h)
        for h in (0, 1):
            move(2 * pairs - 2 + h, h, pairs)
    return program


def leaky(nc, out, x):
    nc.vector.scalar_tensor_tensor(out, x, 0.2, x, ALU.mult, ALU.max)


def edge_softmax(k, tag, edge, same, adst_d, seg_d, segm_d):
    nc = k.nc
    with ExitStack() as c:
        def sb(name, shape, dt=F32):
            return c.enter_context(nc.sbuf_tensor(f"{tag}_{name}", shape, dt))

        a_dst, top = sb("a_dst", [P, J, 4]), sb("top", [P, J, 4])
        pen, junk = sb("pen", [P, J]), sb("junk", [P, J])
        all_same, all_pen = sb("all_same", [P, 4]), sb("all_pen", [P, 4])
        last4, last20 = sb("last4", [P, 4]), sb("last20", [P, ROW])
        a_src = edge[:, :, HG:ROW]
        same4 = same[:].unsqueeze(2).broadcast_to([P, J, 4])

        with k.semaphore(f"{tag}_a_in") as a_in, nc.Block() as block:
            @block.sync
            def _(sp):
                sp.dma_start(a_dst[:], adst_d[0:G, :].rearrange("(p j) h -> p j h", p=P)).then_inc(a_in, 16)

            @block.vector
            def _(dve):
                nc.vector.tensor_reduce(all_same[:, 0:1], same[:], AX_X, ALU.min)
                nc.vector.tensor_scalar(pen[:], same[:], -1.0, -LOW, ALU.add, ALU.mult)
                dve.drain()
                for h in (1, 2, 3):
                    nc.vector.tensor_copy(all_same[:, h:h + 1], all_same[:, 0:1])
                dve.drain()
                nc.vector.tensor_scalar(all_pen[:], all_same[:], -1.0, -LOW, ALU.add, ALU.mult)
                dve.wait_ge(a_in, 16)
                for h in range(4):
                    nc.vector.tensor_tensor_scan(junk[:], same[:], a_dst[:, :, h], 0.0, ALU.mult, ALU.add)
                    dve.drain()
                    nc.vector.tensor_copy(last4[:, h:h + 1], junk[:, J - 1:J])
                    dve.drain()
        fill_in = carry_in(k, c, f"{tag}_c1", last4, all_same, 4, ALU.mult, ALU.add, 0.0)

        with nc.Block() as block:
            @block.vector
            def _(dve):
                for h in range(4):
                    nc.vector.tensor_tensor_scan(a_dst[:, :, h], same[:], a_dst[:, :, h],
                                                 fill_in[:, h:h + 1], ALU.mult, ALU.add)
                    nc.vector.tensor_tensor_scan(junk[:], pen[:], a_src[:, :, h], LOW, ALU.add, ALU.max)
                    dve.drain()
                    nc.vector.tensor_copy(last4[:, h:h + 1], junk[:, J - 1:J])
                    dve.drain()
        top_in = carry_in(k, c, f"{tag}_c2", last4, all_pen, 4, ALU.add, ALU.max, LOW)

        decay = a_dst
        before0, factor = sb("before0", [P, 4]), sb("factor", [P, ROW])
        with k.semaphore(f"{tag}_asked") as asked, k.semaphore(f"{tag}_answered") as answered, \
                nc.Block() as block:
            @block.vector
            def _(dve):
                for h in range(4):
                    nc.vector.tensor_tensor_scan(top[:, :, h], pen[:], a_src[:, :, h], top_in[:, h:h + 1],
                                                 ALU.add, ALU.max)
                dve.drain()
                nc.vector.tensor_tensor(top[:], top[:], a_dst[:], ALU.add)
                nc.vector.tensor_tensor(a_src, a_src, a_dst[:], ALU.add)
                nc.vector.tensor_tensor(before0[:], top_in[:], a_dst[:, 0, :], ALU.add)
                dve.drain()
                leaky(nc, top[:], top[:])
                leaky(nc, a_src, a_src)
                leaky(nc, before0[:], before0[:])
                dve.drain()
                nc.vector.tensor_tensor(a_src, a_src, top[:], ALU.subtract).then_inc(asked, 1)
                nc.vector.tensor_tensor(decay[:, 1:J, :], top[:, 0:J - 1, :], top[:, 1:J, :], ALU.subtract)
                nc.vector.tensor_tensor(decay[:, 0, :], before0[:], top[:, 0, :], ALU.subtract)
                nc.vector.tensor_tensor(factor[:, 0:4], before0[:], top[:, J - 1, :], ALU.subtract)
                dve.drain()
                nc.vector.tensor_scalar(decay[:], decay[:], 0.0, None, ALU.min).then_inc(asked, 1)
                nc.vector.tensor_scalar(factor[:, 0:4], factor[:, 0:4], 0.0, None, ALU.min).then_inc(asked, 1)
                dve.wait_ge(answered, 3)
                nc.vector.tensor_tensor(decay[:], decay[:], same4, ALU.mult)
                nc.vector.tensor_tensor(factor[:, HG:ROW], factor[:, 0:4], all_same[:], ALU.mult)
                h16 = edge[:, :, 0:HG].rearrange("p j (h e) -> p j h e", e=4)
                for h in range(4):
                    nc.vector.tensor_tensor(h16[:, :, h, :], h16[:, :, h, :],
                                            a_src[:, :, h].unsqueeze(2).broadcast_to([P, J, 4]), ALU.mult)
                dve.drain()
                for h in range(4):
                    nc.vector.tensor_scalar(factor[:, 4 * h:4 * h + 4], k.ones[:, 0:4],
                                            factor[:, HG + h:HG + h + 1], None, ALU.mult)
                for f in range(ROW):
                    h = f // 4 if f < HG else f - HG
                    nc.vector.tensor_tensor_scan(junk[:], decay[:, :, h], edge[:, :, f], 0.0, ALU.mult, ALU.add)
                    dve.drain()
                    nc.vector.tensor_copy(last20[:, f:f + 1], junk[:, J - 1:J])
                    dve.drain()

            @block.scalar
            def _(act):
                for n, x in enumerate((a_src, decay[:], factor[:, 0:4])):
                    act.wait_ge(asked, n + 1)
                    nc.scalar.activation(x, x, ACT.Exp).then_inc(answered, 1)
        sum_in = carry_in(k, c, f"{tag}_c3", last20, factor, ROW, ALU.mult, ALU.add, 0.0)

        with k.semaphore(f"{tag}_ran") as ran, k.semaphore(f"{tag}_stored") as stored, nc.Block() as block:
            @block.vector
            def _(dve):
                for f in range(ROW):
                    h = f // 4 if f < HG else f - HG
                    nc.vector.tensor_tensor_scan(edge[:, :, f], decay[:, :, h], edge[:, :, f],
                                                 sum_in[:, f:f + 1], ALU.mult, ALU.add)
                dve.drain().then_inc(ran, 1)

            @block.sync
            def _(sp):
                sp.dma_start(segm_d.rearrange("(p j) w -> p j w", p=P), top[:]).then_inc(stored, 16)
                sp.wait_ge(ran, 1)
                sp.dma_start(seg_d.rearrange("(p j) w -> p j w", p=P), edge[:]).then_inc(stored, 16)
                sp.wait_ge(stored, 32)


def node_gates(k, tag, node_h, last_i, some, seg_d, segm_d, gates):
    nc, I = k.nc, k.ins
    with ExitStack() as c:
        def sb(name, shape, dt=F32):
            return c.enter_context(nc.sbuf_tensor(f"{tag}_{name}", shape, dt))

        b_gat, gamma, beta = load_params(k, c, tag, [
            ("bg", [P, HG], row_on_all(I["L1_ffn_b_gat"])), ("gamma", [P, HG], row_on_all(I["L1_ffn_ln_gamma"])),
            ("beta", [P, HG], row_on_all(I["L1_ffn_ln_beta"]))])
        sums, top = sb("sums", [P, NT, ROW]), sb("top", [P, NT, 4])
        loop, best, c1, c2 = (sb(n, [P, NT, 4]) for n in ("loop", "best", "c1", "c2"))
        agg, tmp = sb("agg", [P, NT, HG]), sb("tmp", [P, NT, HG])
        den, mean, var, gone = sb("den", [P, NT, 4]), sb("mean", [P, NT]), sb("var", [P, NT]), sb("gone", [P, NT])
        score = sb("score", [P, NT, 4])
        bufs = gate_buffers(k, c, tag, 4)
        got = c.enter_context(k.semaphore(f"{tag}_got"))
        asked = c.enter_context(k.semaphore(f"{tag}_asked"))
        answered = c.enter_context(k.semaphore(f"{tag}_answered"))
        block = c.enter_context(nc.Block())

        def wide(a, n):
            return a.unsqueeze(2).broadcast_to([P, NT, n])

        def by_head(a):
            return a.unsqueeze(3).broadcast_to([P, NT, 4, 4])

        def h4(a):
            return a.rearrange("p t (h e) -> p t h e", e=4)

        def param(v):
            return v[:].unsqueeze(1).broadcast_to([P, NT, HG])

        @block.gpsimd
        def _(pool):
            for t in range(NT):
                at = bass.IndirectOffsetOnAxis(ap=last_i[:, t:t + 1], axis=0)
                nc.gpsimd.indirect_dma_start(sums[:, t, :], None, seg_d, at).then_inc(got, 16)
                at = bass.IndirectOffsetOnAxis(ap=last_i[:, t:t + 1], axis=0)
                nc.gpsimd.indirect_dma_start(top[:, t, :], None, segm_d, at).then_inc(got, 16)

        @block.scalar
        def _(act):
            act.wait_ge(asked, 1)
            nc.scalar.activation(c1[:], c1[:], ACT.Exp)
            nc.scalar.activation(c2[:], c2[:], ACT.Exp)
            act.drain().then_inc(answered, 1)
            act.wait_ge(asked, 2)
            nc.scalar.activation(var[:], var[:], ACT.Sqrt, bias=k.eps[:, 0:1], scale=1.0 / HG).then_inc(answered, 1)
            act.wait_ge(asked, 3)
            nc.scalar.activation(bufs[5][:], bufs[5][:], ACT.Exp).then_inc(answered, 1)

        @block.vector
        def _(dve):
            def then(ins):
                dve.drain()

            h = node_h[:, :, 0:HG]
            then(nc.vector.tensor_tensor(loop[:], node_h[:, :, HG:ROW], node_h[:, :, ROW:ROW + 4], ALU.add))
            then(leaky(nc, loop[:], loop[:]))
            then(nc.vector.tensor_scalar(gone[:], some[:], -1.0, -LOW, ALU.add, ALU.mult))
            dve.wait_ge(got, 32 * NT)
            then(nc.vector.tensor_tensor(top[:], top[:], wide(some[:], 4), ALU.mult))
            then(nc.vector.tensor_tensor(top[:], top[:], wide(gone[:], 4), ALU.add))
            then(nc.vector.tensor_tensor(best[:], top[:], loop[:], ALU.max))
            nc.vector.tensor_tensor(c1[:], top[:], best[:], ALU.subtract)
            nc.vector.tensor_tensor(c2[:], loop[:], best[:], ALU.subtract)
            dve.drain().then_inc(asked, 1)
            dve.wait_ge(answered, 1)
            then(nc.vector.tensor_tensor(den[:], sums[:, :, HG:ROW], c1[:], ALU.mult))
            then(nc.vector.tensor_tensor(den[:], den[:], c2[:], ALU.add))
            then(nc.vector.tensor_scalar(den[:], den[:], 1e-16, None, ALU.add))
            then(nc.vector.reciprocal(best[:], den[:]))
            nc.vector.tensor_tensor(c1[:], c1[:], best[:], ALU.mult)
            then(nc.vector.tensor_tensor(c2[:], c2[:], best[:], ALU.mult))
            nc.vector.tensor_tensor(h4(agg[:]), h4(sums[:, :, 0:HG]), by_head(c1[:]), ALU.mult)
            then(nc.vector.tensor_tensor(h4(tmp[:]), h4(h), by_head(c2[:]), ALU.mult))
            then(nc.vector.tensor_tensor(agg[:], agg[:], tmp[:], ALU.add))
            then(nc.vector.tensor_tensor(agg[:], agg[:], param(b_gat), ALU.add))
            then(nc.vector.tensor_reduce(mean[:], agg[:], AX_X, ALU.add))
            then(nc.vector.tensor_scalar(mean[:], mean[:], 1.0 / HG, None, ALU.mult))
            then(nc.vector.tensor_tensor(agg[:], agg[:], wide(mean[:], HG), ALU.subtract))
            then(nc.vector.tensor_tensor(tmp[:], agg[:], agg[:], ALU.mult))
            nc.vector.tensor_reduce(var[:], tmp[:], AX_X, ALU.add).then_inc(asked, 1)
            dve.wait_ge(answered, 2)
            then(nc.vector.reciprocal(mean[:], var[:]))
            then(nc.vector.tensor_tensor(agg[:], agg[:], wide(mean[:], HG), ALU.mult))
            then(nc.vector.tensor_tensor(agg[:], agg[:], param(gamma), ALU.mult))
            then(nc.vector.tensor_tensor(agg[:], agg[:], param(beta), ALU.add))
            then(nc.vector.tensor_reduce(score[:], agg[:].rearrange("p t (h e) -> p t e h", e=4), AX_X, ALU.add))
            then(nc.vector.tensor_scalar(score[:], score[:], 0.25, None, ALU.mult))
            top_two(k, dve, score, gates, 4, asked, answered, 3, bufs)


NAMES = ['x', 'src', 'dst', 'edge_attr_128', 'edge_weight', 'node_vec1', 'node_vec1_n2', 'L0_gnn_c1_w1',
         'L0_gnn_c1_b1', 'L0_gnn_c1_w2', 'L0_gnn_c1_b2', 'L0_gnn_c1_g', 'L0_gnn_c1_b', 'L0_gnn_bn1_g',
         'L0_gnn_bn1_b', 'L0_gnn_c2_w1', 'L0_gnn_c2_b1', 'L0_gnn_c2_w2', 'L0_gnn_c2_b2', 'L0_gnn_c2_g',
         'L0_gnn_c2_b', 'L0_gnn_bn2_g', 'L0_gnn_bn2_b', 'L0_mix_kln_weight', 'L0_mix_kln_bias',
         'L0_mix_vln_weight', 'L0_mix_vln_bias', 'L0_ffn_gamma', 'L0_ffn_beta', 'L0_ffn_Wr', 'L0_ffn_br',
         'L0_ffn_W1', 'L0_ffn_b1', 'L0_ffn_W2', 'L0_ffn_b2', 'L1_gnn_z_in', 'L1_gnn_z_out', 'L1_gnn_W_cent',
         'L1_gnn_b_cent', 'L1_gnn_W_vor', 'L1_gnn_b_vor', 'L1_gnn_W_sum', 'L1_gnn_b_sum', 'L1_mix_W_qkv',
         'L1_mix_W_out', 'L1_mix_b_out', 'L1_ffn_W_gat', 'L1_ffn_att_src', 'L1_ffn_att_dst', 'L1_ffn_b_gat',
         'L1_ffn_ln_gamma', 'L1_ffn_ln_beta', 'L1_ffn_W1', 'L1_ffn_b1', 'L1_ffn_W2', 'L1_ffn_b2',
         'L1_ffn_edge_index']


def load_attributes(k, rest_in):
    attr = k.ins["edge_attr_128"]
    Q = 8

    def fill(sp, pay, n, last, sem, turn):
        full, rest = Q, 0
        if last:
            full, rest = divmod(E - n * Q * P, P)
            if full >= Q:
                full, rest = Q, 0
            if rest:
                sp.dma_start(pay[0:rest, full, 0:P], attr[E - rest:E, :]).then_inc(rest_in, 16)
                sp.wait_ge(rest_in, 16)
        sp.dma_start(pay[:, 0:full, 0:P], attr[ds(n * Q * P, full * P), :].rearrange("(b p) f -> p b f", p=P)
                     ).then_inc(sem, 16)
    return fill


def first_node_columns(k, tag, tile_row_d, out):
    nc = k.nc
    with (nc.sbuf_tensor(f"{tag}_fi", [P, NSB * P], I32) as raw,
          k.semaphore(f"{tag}_fin") as landed, nc.Block() as block):
        @block.sync
        def _(sp):
            sp.dma_start(raw[:], row_on_all(tile_row_d)).then_inc(landed, 16)

        @block.vector
        def _(dve):
            dve.wait_ge(landed, 16)
            nc.vector.tensor_scalar(out[:], raw[:], float(P), None, ALU.mult)


def build(nc, ins, out):
    k = Kernel(nc, ins, out)
    I = ins
    h_d = k.dram("h_d", (N, C))
    x1_d, x2_d, x3_d, xn_d = (k.dram(n, (N, C)) for n in ("x1_d", "x2_d", "x3_d", "xn_d"))
    yT_d, y2T_d = k.dram("yT_d", (P, 2, NP)), k.dram("y2T_d", (P, 2, NP))
    zin_d, zout_d = k.dram("zin_d", (NP, C)), k.dram("zout_d", (NP, C))
    attr_sorted_d = k.dram("attr_sorted_d", (EP, P + 1))
    gat_sorted_d = k.dram("gat_sorted_d", (G + 1, 2))
    gat_rows_d = k.dram("gat_rows_d", (N, ROW))
    experts_d = k.dram("experts_d", (N, 4, C))
    adst_d, seg_d, segm_d = k.dram("adst_d", (G + P, 4)), k.dram("seg_d", (G, ROW)), k.dram("segm_d", (G, 4))

    with ExitStack() as top:
        def keep(name, shape, dt=F32):
            return top.enter_context(nc.sbuf_tensor(name, shape, dt))

        k.turn = top.enter_context(k.semaphore("turn"))
        rest_in = top.enter_context(k.semaphore("rest_in"))
        constants(k, top)
        in_deg, in_start, in_tiles = (keep(f"dst_{n}", [P, NHI]) for n in ("count", "start", "tiles"))
        out_deg, out_start, out_tiles = (keep(f"src_{n}", [P, NHI]) for n in ("count", "start", "tiles"))
        gat_count, gat_start, gat_tiles = (keep(f"gat_{n}", [P, NHI]) for n in ("count", "start", "tiles"))
        gates8, gates4 = keep("gates8", [P, NT, 8]), keep("gates4", [P, NT, 4])

        node_h = keep("node_h", [P, NT, ROW + 4])

        with ExitStack() as c:
            edge_sum = c.enter_context(nc.sbuf_tensor("edge_sum", [P, NP], F32))
            sum_tile_row = c.enter_context(nc.sbuf_tensor("sum_tile_row", [1, NSB * P], I32))
            sum_chunk_row = c.enter_context(nc.sbuf_tensor("sum_chunk_row", [1, NSB * P], I32))
            with ExitStack() as c1:
                gat_pos = c1.enter_context(nc.sbuf_tensor("gat_pos", [P, CG], I32))
                rows, low, (gsrc, gdst) = edge_keys(k, c1, "g", CG, G, [
                    ("src", I["L1_ffn_edge_index"][0]), ("dst", I["L1_ffn_edge_index"][1])],
                    [N - 1, N], [0, 0], 1)
                with ExitStack() as c2:
                    lo, hi = digits(k, c2, "gd", gdst, CG)
                    histogram(k, "gd", lo, hi, CG, gat_count)
                    prefix(k, "gd", gat_count, gat_start, gat_tiles)
                    shifted = c2.enter_context(nc.sbuf_tensor("gat_shifted", [P, NHI], F32))
                    first = c2.enter_context(nc.sbuf_tensor("gat_first_row", [1, 2], F32))
                    with k.semaphore("gat_minus") as made, k.semaphore("gat_zeroth") as stored, nc.Block() as block:
                        @block.vector
                        def _(dve):
                            nc.vector.tensor_scalar(shifted[:], gat_start[:], 1.0, None, ALU.add)
                            nc.vector.memset(first[:], -1.0).then_inc(made, 1)

                        @block.sync
                        def _(sp):
                            sp.wait_ge(made, 1)
                            sp.dma_start(gat_sorted_d[0:1, :], first[:]).then_inc(stored, 16)
                            sp.wait_ge(stored, 16)
                    sort_edges(k, c2, "gs", CG, gdst, lo, hi, shifted, rows[:, 1, :], low, [], 2, None, None,
                               gat_pos)

                conv_tile_row = c1.enter_context(nc.sbuf_tensor("conv_tile_row", [1, NSB * P], I32))
                src_i = c1.enter_context(nc.sbuf_tensor("conv_src", [P, NSB * P], I32))
                rel = c1.enter_context(nc.sbuf_tensor("conv_rel", [P, NSB * P], F32))
                weight = c1.enter_context(nc.sbuf_tensor("conv_weight", [P, NSB * P], F32))
                with ExitStack() as c2:
                    rows, low, (esrc, edst, _) = edge_keys(k, c2, "e", CE, E, [
                        ("src", I["src"]), ("dst", I["dst"]), ("weight", I["edge_weight"])],
                        [None] * 3, [PAD_KEY, PAD_KEY, 0.0], 0)
                    dlo, dhi = digits(k, c2, "ed", edst, CE)
                    histogram(k, "ed", dlo, dhi, CE, in_deg)
                    slo, shi = digits(k, c2, "es", esrc, CE)
                    histogram(k, "es", slo, shi, CE, out_deg)
                    prefix(k, "ed", in_deg, in_start, in_tiles)
                    prefix(k, "es", out_deg, out_start, out_tiles)
                    tile, chunk = schedule(k, c2, "ed", in_tiles)
                    step_columns(k, "ed", rows, tile, chunk, src_i, rel, weight)
                    step_registers(k, "ed_tile", tile, conv_tile_row)
                    tile, chunk = schedule(k, c2, "es", out_tiles)
                    step_registers(k, "es_tile", tile, sum_tile_row)
                    step_registers(k, "es_chunk", chunk, sum_chunk_row)
                    sort_edges(k, c2, "ss", CE, esrc, slo, shi, out_start, rows[:, 0, :], low, [(P, esrc)],
                               P + 1, load_attributes(k, rest_in), attr_sorted_d)

                with ExitStack() as c2:
                    kv = c2.enter_context(nc.sbuf_tensor("kv", [P, 2, P], F32))
                    acc = c2.enter_context(nc.sbuf_tensor("acc", [P, 2, NP], F32))
                    input_stage(k, c2, "in", h_d, kv)
                    aggregate(k, "a1", h_d, src_i, rel, weight, conv_tile_row, acc)
                    dense_and_norms(k, c2, "n1", acc, "L0_gnn_c1_w2", "L0_gnn_c1_b2", [
                        ("L0_gnn_c1_g", "L0_gnn_c1_b", True), ("L0_gnn_bn1_g", "L0_gnn_bn1_b", True)])
                    rows_from_channels(k, c2, "rc", acc, h_d, "L0_gnn_c2_w1", "L0_gnn_c2_b1")
                    aggregate(k, "a2", h_d, src_i, rel, weight, conv_tile_row, acc)
                    dense_and_norms(k, c2, "n2", acc, "L0_gnn_c2_w2", "L0_gnn_c2_b2", [
                        ("L0_gnn_c2_g", "L0_gnn_c2_b", True), ("L0_gnn_bn2_g", "L0_gnn_bn2_b", False)])
                    mix_and_gate_stage(k, c2, "mg", acc, kv, x1_d, yT_d, gates8)
                with ExitStack() as c2:
                    scatter = scatter_beside(k, c2, "gw", CG, gat_pos, (gsrc, gdst), gat_sorted_d)
                    expert_stage(k, c2, "e0", 8, yT_d, x1_d, x2_d, gates8, "L0_ffn_W1", "L0_ffn_b1",
                                 "L0_ffn_W2", "L0_ffn_b2", scatter)

            with ExitStack() as c2:
                first_all = c2.enter_context(nc.sbuf_tensor("first_all", [P, NSB * P], F32))
                first_node_columns(k, "fa", k.buffers["es_tile_row_d"], first_all)
                segment_sum(k, "sm", attr_sorted_d, P, sum_chunk_row, first_all, sum_tile_row, edge_sum)
            degree_rows(k, "di", I["L1_gnn_z_in"], in_deg, zin_d)
            degree_rows(k, "do", I["L1_gnn_z_out"], out_deg, zout_d)
            with ExitStack() as c2:
                xT = c2.enter_context(nc.sbuf_tensor("xT", [P, 2, NP], F32))
                kmax = c2.enter_context(nc.sbuf_tensor("kmax", [P, 1], F32))
                cw = c2.enter_context(nc.sbuf_tensor("cw", [P, C], F32))
                channels_stage(k, c2, "cs", x2_d, xn_d, xT, kmax)
                context_stage(k, c2, "cx", xT, kmax, cw)
                graph_and_mix_stage(k, c2, "gm", x2_d, xn_d, xT, cw, edge_sum, out_deg, zin_d, zout_d,
                                    x3_d, y2T_d, gat_rows_d, node_h)

        with ExitStack() as c:
            first_i, last_i, some = node_targets(k, c, "nt", gat_start, gat_count)
            spread_to_starts(k, "sp", node_h, first_i, adst_d)
            with ExitStack() as c2:
                edge = c2.enter_context(nc.sbuf_tensor("edge", [P, J, ROW], F32))
                same = c2.enter_context(nc.sbuf_tensor("same", [P, J], F32))
                with ExitStack() as c3:
                    idx_all = c3.enter_context(nc.sbuf_tensor("gat_idx", [P, J], I32))
                    sorted_lists(k, "sl", gat_sorted_d, idx_all, same)
                    gather = gather_beside(k, c3, "ge", gat_rows_d, idx_all, edge)
                    expert_outputs(k, c3, "e1", 4, y2T_d, experts_d, "L1_ffn_W1", "L1_ffn_b1", "L1_ffn_W2",
                                   "L1_ffn_b2", gather)
                edge_softmax(k, "ex", edge, same, adst_d, seg_d, segm_d)
            node_gates(k, "ng", node_h, last_i, some, seg_d, segm_d, gates4)
            combine_stage(k, c, "cb", 4, experts_d, x3_d, out, gates4)


def kernel(**inputs):
    import concourse.bacc as bacc
    from concourse.bass_utils import run_bass_kernel_spmd

    nc = bacc.Bacc("TRN2", target_bir_lowering=False, num_devices=1)
    arrays, ins = {}, {}
    for name in NAMES:
        a = np.ascontiguousarray(inputs[name])
        arrays[f"in_{name}"] = a
        ins[name] = nc.dram_tensor(f"in_{name}", a.shape, mybir.dt.from_np(a.dtype), kind="ExternalInput").ap()
    out = nc.dram_tensor("out_0", (N, C), F32, kind="ExternalOutput").ap()
    build(nc, ins, out)
    r = run_bass_kernel_spmd(nc, [arrays], core_ids=[0])
    return r.results[0]["out_0"]
```

```python
from contextlib import ExitStack, contextmanager

import numpy as np
import concourse.bass as bass
from concourse import mybir

F32 = mybir.dt.float32
BF16 = mybir.dt.bfloat16
I32 = mybir.dt.int32
ALU = mybir.AluOpType
ACT = mybir.ActivationFunctionType
AX_X = mybir.AxisListType.X

P = 128
N = 6250
C = 256
NT = 49
NP = NT * P
REAL_T = -(-N // P)
LAST = N - (REAL_T - 1) * P
E = 100000
CE = 784
EP = CE * P
G = 131072
CG = G // P
NHI = 64
PAD_KEY = NHI * P - 1
NS = 832
NSB = 7
NEG = -3.0e38
EPS = 1e-5


def ds(start, n):
    return bass.ds(start, n)


class Kernel:

    def __init__(self, nc, ins, out):
        self.nc, self.ins, self.out = nc, ins, out
        self.buffers = {}
        self.retired = []

    @contextmanager
    def semaphore(self, name):
        if len(self.retired) > 64:
            self.nc.clear_and_free_semaphores(self.retired)
            self.nc.all_engine_barrier()
            self.retired = []
        sem = self.nc.alloc_semaphore(name)
        yield sem
        self.retired.append(sem)

    @staticmethod
    def nth(t, b):
        return t // 2 + 1 if isinstance(t, int) else (t - b) // 2 + 1

    def dram(self, name, shape, dt=F32):
        t = self.nc.dram_tensor(name, shape, dt, kind="Internal").ap()
        self.buffers[name] = t
        return t


def constants(k, ctx):
    nc = k.nc

    def sb(name, shape, dt=F32):
        return ctx.enter_context(nc.sbuf_tensor(name, shape, dt))

    ident = sb("ident", [P, P])
    ones = sb("ones", [P, P])
    before = sb("before", [P, P])
    block_diag = sb("block_diag", [P, P])
    ramp = sb("ramp", [P, P])
    ramp_bf = sb("ramp_bf", [P, P], BF16)
    lane = sb("lane", [P, 1])
    eps = sb("eps", [P, 1])
    minus_lane = sb("minus_lane", [P, 1])
    ramp_16 = sb("ramp_16", [P, P, 16], BF16)
    lane_i = sb("lane_i", [P, 1], I32)
    ramp_i = sb("ramp_i", [P, P], I32)
    k.ident, k.ones, k.before, k.block_diag, k.ramp, k.ramp_bf, k.lane, k.eps = (
        ident, ones, before, block_diag, ramp, ramp_bf, lane, eps)
    k.minus_lane, k.ramp_16 = minus_lane, ramp_16
    with k.semaphore("const_made") as made, nc.Block() as block:
        @block.gpsimd
        def _(pool):
            nc.gpsimd.memset(ones[:], 1.0).then_inc(made, 1)
            nc.gpsimd.iota(ramp_i[:], [[1, P]], base=0, channel_multiplier=0).then_inc(made, 1)
            nc.gpsimd.iota(lane_i[:], [[1, 1]], base=0, channel_multiplier=1).then_inc(made, 1)
            pool.wait_ge(made, 3)
            nc.gpsimd.affine_select(out=ident[:], in_=ones[:], pattern=[[-1, P]], compare_op=ALU.is_equal,
                                    fill=0.0, base=0, channel_multiplier=1)
            nc.gpsimd.affine_select(out=before[:], in_=ones[:], pattern=[[1, P]], compare_op=ALU.is_gt,
                                    fill=0.0, base=0, channel_multiplier=-1)
            for q in range(4):
                cols = slice(32 * q, 32 * q + 32)
                nc.gpsimd.affine_select(out=block_diag[:, cols], in_=ones[:, cols], pattern=[[0, 32]],
                                        compare_op=ALU.is_ge, fill=0.0, base=-32 * q,
                                        channel_multiplier=1)
            pool.drain()
            for q in range(4):
                cols = slice(32 * q, 32 * q + 32)
                nc.gpsimd.affine_select(out=block_diag[:, cols], in_=block_diag[:, cols],
                                        pattern=[[0, 32]], compare_op=ALU.is_gt, fill=0.0,
                                        base=32 * q + 32, channel_multiplier=-1)

        @block.vector
        def _(dve):
            nc.vector.memset(eps[:], EPS)
            dve.wait_ge(made, 3)
            nc.vector.tensor_copy(ramp[:], ramp_i[:])
            nc.vector.tensor_copy(ramp_bf[:], ramp_i[:])
            nc.vector.tensor_copy(lane[:], lane_i[:])
            nc.vector.tensor_scalar(minus_lane[:], lane_i[:], -1.0, None, ALU.mult)
            nc.vector.tensor_copy(ramp_16[:], ramp_i[:].unsqueeze(2).broadcast_to([P, P, 16]))


def edge_keys(k, ctx, tag, chunks, real, inputs, clamp, pad, sort_by):
    nc = k.nc
    per = 7 if chunks == CE else chunks // P
    parts = chunks // per
    width = per * P
    rows_d = k.dram(f"{tag}_rows", (chunks, len(inputs), P))
    low_d = k.dram(f"{tag}_low", (chunks * P,), BF16)
    cols = [ctx.enter_context(nc.sbuf_tensor(f"{tag}_{n}_cols", [P, chunks], F32)) for n, _ in inputs]
    with ExitStack() as c:
        raw = [c.enter_context(nc.sbuf_tensor(f"{tag}_{n}_raw", [P, width], a.dtype)) for n, a in inputs]
        rows = [c.enter_context(nc.sbuf_tensor(f"{tag}_{n}_f", [P, width], F32)) for n, _ in inputs]
        key_i = c.enter_context(nc.sbuf_tensor(f"{tag}_key_i", [P, width], I32))
        low_i = c.enter_context(nc.sbuf_tensor(f"{tag}_low_i", [P, width], I32))
        low = c.enter_context(nc.sbuf_tensor(f"{tag}_low_bf", [P, width], BF16))
        turned = c.enter_context(nc.psum_tensor(f"{tag}_turned", [P, 2, 512], F32))
        low_made = c.enter_context(k.semaphore(f"{tag}_low_made"))
        padded = c.enter_context(k.semaphore(f"{tag}_padded"))
        loaded = c.enter_context(k.semaphore(f"{tag}_loaded"))
        made = c.enter_context(k.semaphore(f"{tag}_made"))
        transposed = c.enter_context(k.semaphore(f"{tag}_transposed"))
        copied = c.enter_context(k.semaphore(f"{tag}_copied"))
        stored = c.enter_context(k.semaphore(f"{tag}_stored"))
        block = c.enter_context(nc.Block())
        full, rest = divmod(real, width)
        n_in = len(inputs)

        @block.sync
        def _(sp):
            n = 0
            sp.wait_ge(padded, n_in)
            for t, (_, a) in zip(raw, inputs):
                sp.dma_start(t[0:full, :], a[0:full * width].rearrange("(p w) -> p w", w=width)
                             ).then_inc(loaded, 16)
                n += 1
                if rest:
                    sp.dma_start(t[full:full + 1, 0:rest],
                                 a[full * width:real].rearrange("(p w) -> p w", p=1)).then_inc(loaded, 16)
                    n += 1
            sp.wait_ge(made, n_in)
            for j in range(n_in):
                sp.dma_start(rows_d[:, j, :].rearrange("(p b) e -> p b e", b=per),
                             rows[j][0:parts].rearrange("p (b e) -> p b e", e=P)).then_inc(stored, 16)
            sp.wait_ge(low_made, 1)
            sp.dma_start(low_d.rearrange("(p w) -> p w", w=width), low[0:parts, :]).then_inc(stored, 16)
            sp.wait_ge(stored, 16 * (n_in + 1))

        @block.vector
        def _(dve):
            for t, v in zip(raw, pad):
                nc.vector.memset(t[:], v).then_inc(padded, 1)
            dve.wait_ge(loaded, 16 * n_in * (2 if rest else 1))
            for j in range(n_in):
                if clamp[j] is None:
                    nc.vector.tensor_copy(rows[j][:], raw[j][:]).then_inc(made, 1)
                else:
                    nc.vector.tensor_scalar(rows[j][:], raw[j][:], float(clamp[j]), None,
                                            ALU.min).then_inc(made, 1)
            dve.drain()
            nc.vector.tensor_copy(key_i[:], rows[sort_by][:])
            dve.drain()
            nc.vector.tensor_scalar(low_i[:], key_i[:], 127, None, ALU.bitwise_and)
            dve.drain()
            nc.vector.tensor_copy(low[:], low_i[:]).then_inc(low_made, 1)
            for n in range(n_in * per):
                j, b = divmod(n, per)
                dve.wait_ge(transposed, n + 1)
                nc.vector.tensor_copy(cols[j][:].rearrange("e (p b) -> e b p", b=per)[:, b, :],
                                      turned[:, n % 2, 0:parts]).then_inc(copied, 1)

        @block.tensor
        def _(pe):
            pe.wait_ge(made, n_in)
            for n in range(n_in * per):
                j, b = divmod(n, per)
                if n >= 2:
                    pe.wait_ge(copied, n - 1)
                nc.tensor.transpose(turned[:, n % 2, 0:parts], rows[j][0:parts, b * P:(b + 1) * P],
                                    k.ident[0:parts, 0:parts]).then_inc(transposed, 1)
    return rows_d, low_d, cols


def digits(k, ctx, tag, key, chunks):
    nc = k.nc
    lo = ctx.enter_context(nc.sbuf_tensor(f"{tag}_lo", [P, chunks], BF16))
    hi = ctx.enter_context(nc.sbuf_tensor(f"{tag}_hi", [P, chunks], BF16))
    with (nc.sbuf_tensor(f"{tag}_ki", [P, chunks], I32) as ki,
          nc.sbuf_tensor(f"{tag}_di", [P, chunks], I32) as di,
          nc.Block() as block):
        @block.vector
        def _(dve):
            nc.vector.tensor_copy(ki[:], key[:])
            dve.drain()
            nc.vector.tensor_scalar(di[:], ki[:], 7, None, ALU.logical_shift_right)
            dve.drain()
            nc.vector.tensor_copy(hi[:], di[:])
            dve.drain()
            nc.vector.tensor_scalar(di[:], ki[:], 127, None, ALU.bitwise_and)
            dve.drain()
            nc.vector.tensor_copy(lo[:], di[:])
    return lo, hi


def histogram(k, tag, lo, hi, chunks, count):
    nc = k.nc
    B = 16
    batches = chunks // B

    def over_batches(eng, body):
        with eng.Fori(0, batches // 2) as i:
            for b in (0, 1):
                body(2 * i + b, b)
        if batches % 2:
            body(batches - 1, 0)

    with ExitStack() as c:
        one_lo = [c.enter_context(nc.sbuf_tensor(f"{tag}_one_lo{b}", [P, P, B], BF16)) for b in (0, 1)]
        one_hi = [c.enter_context(nc.sbuf_tensor(f"{tag}_one_hi{b}", [P, NHI, B], BF16)) for b in (0, 1)]
        zero = c.enter_context(nc.sbuf_tensor(f"{tag}_zero", [P, P], BF16))
        total = c.enter_context(nc.psum_tensor(f"{tag}_total", [P, NHI], F32))
        made = c.enter_context(k.semaphore(f"{tag}_h_made"))
        used = c.enter_context(k.semaphore(f"{tag}_h_used"))
        summed = c.enter_context(k.semaphore(f"{tag}_h_summed"))
        zeroed = c.enter_context(k.semaphore(f"{tag}_h_zeroed"))
        block = c.enter_context(nc.Block())

        @block.vector
        def _(dve):
            nc.vector.memset(zero[:], 0.0).then_inc(zeroed, 1)
            dve.sem_inc(used, 2)

            def one_hots(n, b):
                dve.wait_ge(used, n + 1)
                at = ds(n * B, B)
                nc.vector.tensor_tensor(one_lo[b][:], k.ramp_16[:], lo[:, at].unsqueeze(1).broadcast_to(
                    [P, P, B]), ALU.is_equal)
                nc.vector.tensor_tensor(one_hi[b][:], k.ramp_16[:, 0:NHI, :], hi[:, at].unsqueeze(1).broadcast_to(
                    [P, NHI, B]), ALU.is_equal)
                dve.drain().then_inc(made, 1)
            over_batches(dve, one_hots)
            dve.wait_ge(summed, 1)
            nc.vector.tensor_copy(count[:], total[:])

        @block.tensor
        def _(pe):
            pe.wait_ge(zeroed, 1)
            nc.tensor.matmul(total[:], zero[:], zero[:, 0:NHI], start=True, stop=False,
                             skip_group_check=True)

            def count_up(n, b):
                pe.wait_ge(made, n + 1)
                for j in range(B):
                    mm = nc.tensor.matmul(total[:], one_lo[b][:, :, j], one_hi[b][:, :, j],
                                          start=False, stop=False, skip_group_check=True)
                mm.then_inc(used, 1)
            over_batches(pe, count_up)
            nc.tensor.matmul(total[:], zero[:], zero[:, 0:NHI], start=False, stop=True,
                             skip_group_check=True).then_inc(summed, 1)


def prefix(k, tag, count, start, tile_start):
    nc = k.nc
    with ExitStack() as c:
        per_hi = c.enter_context(nc.psum_tensor(f"{tag}_per_hi", [P, NHI], F32))
        within = c.enter_context(nc.psum_tensor(f"{tag}_within", [P, NHI], F32))
        total = c.enter_context(nc.sbuf_tensor(f"{tag}_total_sb", [P, NHI], F32))
        upto = c.enter_context(nc.sbuf_tensor(f"{tag}_upto", [P, NHI], F32))
        summed = c.enter_context(k.semaphore(f"{tag}_p_summed"))
        block = c.enter_context(nc.Block())

        @block.tensor
        def _(pe):
            nc.tensor.matmul(per_hi[:], k.ones[:], count[:], start=True, stop=True)
            nc.tensor.matmul(within[:], k.before[:], count[:], start=True, stop=True).then_inc(summed, 1)

        @block.vector
        def _(dve):
            dve.wait_ge(summed, 1)
            nc.vector.tensor_copy(total[:], per_hi[:])
            dve.drain()
            nc.vector.tensor_tensor_scan(upto[:], k.ones[:, 0:NHI], total[:], 0.0, ALU.mult, ALU.add)
            dve.drain()
            nc.vector.tensor_tensor(tile_start[:], upto[:], total[:], ALU.subtract)
            dve.drain()
            nc.vector.tensor_tensor(start[:], tile_start[:], within[:], ALU.add)


def schedule(k, ctx, tag, tile_start):
    nc = k.nc
    step_tile = ctx.enter_context(nc.sbuf_tensor(f"{tag}_step_tile", [P, NSB], F32))
    step_chunk = ctx.enter_context(nc.sbuf_tensor(f"{tag}_step_chunk", [P, NSB], F32))
    T1 = REAL_T - 1
    with (nc.sbuf_tensor(f"{tag}_qi", [P, NHI], I32) as qi,
          nc.sbuf_tensor(f"{tag}_enter", [P, NHI], F32) as enter,
          nc.sbuf_tensor(f"{tag}_cmp", [P, NHI], F32) as cmp,
          nc.sbuf_tensor(f"{tag}_s", [P, NSB], F32) as s,
          nc.Block() as block):
        @block.vector
        def _(dve):
            nc.vector.tensor_copy(qi[:], tile_start[:])
            for b in range(NSB):
                nc.vector.tensor_scalar(s[:, b:b + 1], k.lane[:], float(b * P), None, ALU.add)
            dve.drain()
            nc.vector.tensor_scalar(qi[:], qi[:], 7, None, ALU.logical_shift_right)
            dve.drain()
            nc.vector.tensor_tensor(enter[:], qi[:], k.ramp[:, 0:NHI], ALU.add)
            dve.drain()
            for b in range(NSB):
                nc.vector.tensor_scalar(cmp[:, 0:T1], enter[:, 1:1 + T1], s[:, b:b + 1], 0.0, ALU.is_le,
                                        ALU.add, accum_out=step_tile[:, b:b + 1])
                dve.drain()
            nc.vector.tensor_tensor(step_chunk[:], s[:], step_tile[:], ALU.subtract)
            dve.drain()
            nc.vector.tensor_scalar(step_chunk[:], step_chunk[:], float(CE - 1), None, ALU.min)
    return step_tile, step_chunk


def step_columns(k, tag, rows_d, step_tile, step_chunk, src_i, rel, weight):
    nc = k.nc
    table = rows_d.rearrange("c j e -> c (j e)")
    with ExitStack() as c:
        got = [c.enter_context(nc.sbuf_tensor(f"{tag}_got{b}", [P, 3 * P], F32)) for b in range(NSB)]
        chunk_i = c.enter_context(nc.sbuf_tensor(f"{tag}_chunk_i", [P, NSB], I32))
        first = c.enter_context(nc.sbuf_tensor(f"{tag}_first", [P, NSB], F32))
        turned = c.enter_context(nc.psum_tensor(f"{tag}_turned2", [P, 2, 4, P], F32))
        index_made = c.enter_context(k.semaphore(f"{tag}_index_made"))
        gathered = [c.enter_context(k.semaphore(f"{tag}_gathered{b}")) for b in range(NSB)]
        made = c.enter_context(k.semaphore(f"{tag}_rel_made"))
        transposed = c.enter_context(k.semaphore(f"{tag}_transposed2"))
        copied = c.enter_context(k.semaphore(f"{tag}_copied2"))
        block = c.enter_context(nc.Block())

        @block.gpsimd
        def _(pool):
            pool.wait_ge(index_made, 1)
            for b in range(NSB):
                nc.gpsimd.indirect_dma_start(got[b][:], None, table, bass.IndirectOffsetOnAxis(
                    ap=chunk_i[:, b:b + 1], axis=0)).then_inc(gathered[b], 16)

        @block.vector
        def _(dve):
            nc.vector.tensor_copy(chunk_i[:], step_chunk[:]).then_inc(index_made, 1)
            nc.vector.tensor_scalar(first[:], step_tile[:], float(P), None, ALU.mult)
            dve.drain()
            for b in range(NSB):
                dve.wait_ge(gathered[b], 16)
                nc.vector.tensor_scalar(got[b][:, P:2 * P], got[b][:, P:2 * P], first[:, b:b + 1], None,
                                        ALU.subtract)
                nc.vector.tensor_scalar(got[b][:, 0:P], got[b][:, 0:P], float(N - 1), None, ALU.min)
                dve.drain().then_inc(made, 1)
            for b in range(NSB):
                dve.wait_ge(transposed, b + 1)
                at = slice(b * P, (b + 1) * P)
                nc.vector.tensor_copy(src_i[:, at], turned[:, b % 2, 0, :])
                nc.vector.tensor_copy(rel[:, at], turned[:, b % 2, 1, :])
                nc.vector.tensor_copy(weight[:, at], turned[:, b % 2, 2, :])
                dve.drain().then_inc(copied, 1)

        @block.tensor
        def _(pe):
            for b in range(NSB):
                pe.wait_ge(made, b + 1)
                if b >= 2:
                    pe.wait_ge(copied, b - 1)
                for j in range(3):
                    mm = nc.tensor.transpose(turned[:, b % 2, j, :], got[b][:, j * P:(j + 1) * P], k.ident[:])
                mm.then_inc(transposed, 1)


def step_registers(k, tag, values, row, factor=1):
    nc = k.nc
    row_d = k.dram(f"{tag}_row_d", (NSB * P,), I32)
    with ExitStack() as c:
        as_int = c.enter_context(nc.sbuf_tensor(f"{tag}_as_int", [P, NSB], I32))
        made = c.enter_context(k.semaphore(f"{tag}_made"))
        moved = c.enter_context(k.semaphore(f"{tag}_moved"))
        block = c.enter_context(nc.Block())

        @block.vector
        def _(dve):
            nc.vector.tensor_scalar(as_int[:], values[:], float(factor), None, ALU.mult).then_inc(made, 1)

        @block.sync
        def _(sp):
            sp.wait_ge(made, 1)
            for b in range(NSB):
                sp.dma_start(row_d[b * P:(b + 1) * P].rearrange("(p b) -> p b", b=1),
                             as_int[:, b:b + 1]).then_inc(moved, 16)
            sp.wait_ge(moved, 16 * NSB)
            sp.dma_start(row[:], row_d.rearrange("(a s) -> a s", a=1)).then_inc(moved, 16)
            sp.wait_ge(moved, 16 * (NSB + 1))


def aggregate(k, tag, table, src_i, rel, weight, tile_row, acc):
    nc = k.nc
    R = 8
    with ExitStack() as c:
        def sb(name, shape, dt=F32):
            return c.enter_context(nc.sbuf_tensor(f"{tag}_{name}", shape, dt))

        def sem(name):
            return c.enter_context(k.semaphore(f"{tag}_{name}"))

        idx = [sb(f"idx{h}", [P, R], I32) for h in (0, 1)]
        msg = [sb(f"msg{b}", [P, C]) for b in range(2 * R)]
        pick = [sb(f"pick{b}", [P, P]) for b in range(R)]
        part = [c.enter_context(nc.psum_tensor(f"{tag}_part{b}", [P, 4, P], F32)) for b in range(R)]
        idx_ready, pick_ready = sem("idx_ready"), sem("pick_ready")
        zeroed = sem("zeroed")
        gathered = [sem(f"gathered{b}") for b in range(2 * R)]
        turn = sem("turn")
        summed, added = sem("summed"), sem("added")
        block = c.enter_context(nc.Block())

        @block.gpsimd
        def _(pool):
            pool.sem_inc(summed, 2 * R)
            with pool.Fori(0, NS // (2 * R)) as i:
                for h in (0, 1):
                    half = 2 * i + h
                    pool.wait_ge(summed, (half + 1) * R)
                    pool.sem_inc(turn, 1)
                    nc.gpsimd.tensor_copy(idx[h][:], src_i[:, ds(half * R, R)]).then_inc(idx_ready, 1)
                    pool.wait_ge(idx_ready, half + 1)
                    pool.sem_inc(turn, 1)
                    for b in range(R):
                        nc.gpsimd.indirect_dma_start(msg[h * R + b][:], None, table, bass.IndirectOffsetOnAxis(
                            ap=idx[h][:, b:b + 1], axis=0)).then_inc(gathered[h * R + b], 16)

        @block.vector
        def _(dve):
            nc.vector.memset(acc[:], 0.0)
            dve.drain()
            regs = [dve.alloc_register(f"{tag}_tile{b}") for b in range(R)]

            def picks(first, slot):
                for b in range(4):
                    s = first + b
                    nc.vector.tensor_scalar(pick[slot + b][:], k.ramp[:], rel[:, ds(s, 1)],
                                            weight[:, ds(s, 1)], ALU.is_equal, ALU.mult
                                            ).then_inc(pick_ready, 1)

            picks(0, 0)
            with dve.Fori(0, NS // R) as i:
                dve.reg_load(regs, tile_row[0:1, ds(i * R, R)])
                tiles = [dve.snap(r, min_val=0, max_val=REAL_T - 1) for r in regs]
                for g in (0, 1):
                    picks(i * R + 4 * g + 4, 4 - 4 * g)
                    for b in range(4 * g, 4 * g + 4):
                        dve.wait_ge(summed, i * R + b + 1 + 2 * R)
                        at = ds(tiles[b] * P, P)
                        nc.vector.tensor_tensor(acc[:, :, at], acc[:, :, at], part[b][:, 0:2, :], ALU.add)
                        dve.drain().then_inc(added, 1)

        @block.tensor
        def _(pe):
            pe.sem_inc(added, R)
            with pe.Fori(0, NS // (2 * R)) as i:
                for h in (0, 1):
                    for b in range(R):
                        s = (2 * i + h) * R + b
                        pe.wait_ge(gathered[h * R + b], i * 16 + 16)
                        pe.wait_ge(pick_ready, s + 1)
                        pe.wait_ge(added, s + 1)
                        for half in (0, 1):
                            mm = nc.tensor.matmul(part[b][:, half, :], msg[h * R + b][:, half * P:(half + 1) * P],
                                                  pick[b][:], start=True, stop=True)
                        mm.then_inc(summed, 1)


def sort_edges(k, ctx, tag, chunks, key, lo, hi, start, key_rows, low_d, payload, width, fill, out_d):
    nc = k.nc
    Q = 8
    S = 4
    quads = chunks // Q
    with ExitStack() as c:
        def sb(name, shape, dt=F32):
            return c.enter_context(nc.sbuf_tensor(f"{tag}_{name}", shape, dt))

        def sem(name):
            return c.enter_context(k.semaphore(f"{tag}_{name}"))

        key_row = [sb(f"key_row{s}", [P, Q * P]) for s in range(S)]
        low_row = [sb(f"low_row{s}", [P, Q * P], BF16) for s in range(S)]
        pay = [sb(f"pay{q}", [P, Q, width]) for q in (0, 1)]
        pos = [sb(f"pos{q}", [P, Q], I32) for q in (0, 1)]
        base = [sb(f"base{q}", [P, Q]) for q in (0, 1)]
        same = [sb(f"same{q}", [P, Q]) for q in (0, 1)]
        hi_f = sb("hi_f", [P, chunks])
        lowT = [sb(f"lowT{q}", [P, Q * P]) for q in (0, 1)]
        one_lo = [sb(f"s_one_lo{q}", [P, P, Q], BF16) for q in (0, 1)]
        one_hi = [sb(f"s_one_hi{q}", [P, NHI, Q], BF16) for q in (0, 1)]
        junk_hi = [sb(f"junk_hi{j}", [P, NHI]) for j in (0, 1)]
        junk_row = [sb(f"junk_row{j}", [P, 2 * P]) for j in (0, 1)]
        earlier = sb("earlier", [P, 2, 2 * P])
        counts_sb = [sb(f"counts_sb{b}", [P, NHI]) for b in (0, 1)]
        counts = c.enter_context(nc.psum_tensor(f"{tag}_counts", [P, 512], F32))
        found = [c.enter_context(nc.psum_tensor(f"{tag}_found{g}", [P, 8, NHI], F32)) for g in range(4)]
        key_in = [sem(f"key_in{s}") for s in range(S)]
        low_in = [sem(f"low_in{s}") for s in range(S)]
        pay_in = [sem(f"pay_in{q}") for q in (0, 1)]
        hot_ready, quad_used, lowT_ready = sem("hot_ready"), sem("quad_used"), sem("lowT_ready")
        count_ready, count_copied, found_ready = sem("count_ready"), sem("count_copied"), sem("found_ready")
        found_read, pos_ready, key_used = sem("found_read"), sem("pos_ready"), sem("key_used")
        turn, pay_free = sem("turn"), sem("pay_free")
        scattered = [sem(f"scattered{q}") for q in (0, 1)]
        mask_made = sem("mask_made")
        block = c.enter_context(nc.Block())

        def over_quads(eng, first, count, body):
            whole = count // S
            with eng.Fori(0, whole) as i:
                for s in range(S):
                    body(i * S + (first + s), (first + s) % S, i + ((first + s) // S + 1))
            for n in range(first + whole * S, first + count):
                body(n, n % S, n // S + 1)

        @block.sync
        def _(sp):
            def rows(n, s):
                sp.dma_start(key_row[s][:].rearrange("p (b e) -> p b e", e=P),
                             key_rows[ds(n * Q, Q), :].unsqueeze(0).broadcast_to([P, Q, P])
                             ).then_inc(key_in[s], 16)
                sp.dma_start(low_row[s][:], low_d[ds(n * Q * P, Q * P)].unsqueeze(0)
                             .broadcast_to([P, Q * P])).then_inc(low_in[s], 16)

            for s in range(S - 1):
                rows(s, s)
            if fill:
                fill(sp, pay[0], 0, False, pay_in[0], turn)
                fill(sp, pay[1], 1, False, pay_in[1], turn)
            rows(S - 1, S - 1)

            def step(n, s, nth):
                if fill:
                    sp.wait_ge(scattered[s % 2], nth_two(n, s) * (16 * Q))
                    sp.sem_inc(pay_free, 1)
                    fill(sp, pay[s % 2], n + 2, isinstance(n, int) and n + 2 == quads - 1, pay_in[s % 2], turn)
                sp.wait_ge(key_used, n + 1)
                sp.wait_ge(lowT_ready, n + 1)
                if not isinstance(n, int) or n + S < quads:
                    rows(n + S, s)

            def nth_two(n, s):
                return n // 2 + 1 if isinstance(n, int) else (n - s % 2) // 2 + 1
            over_quads(sp, 0, quads - S, step)
            for n in range(quads - S, quads - 2):
                step(n, n % S, None)
            for q in (0, 1):
                sp.wait_ge(scattered[q], 8 * Q * quads)

        @block.gpsimd
        def _(pool):
            nc.gpsimd.memset(earlier[:], 1.0).then_inc(mask_made, 1)
            pool.wait_ge(mask_made, 1)
            nc.gpsimd.affine_select(out=earlier[:], in_=earlier[:], pattern=[[P, 2], [-1, 2 * P]],
                                    compare_op=ALU.is_gt, fill=0.0, base=0,
                                    channel_multiplier=1).then_inc(mask_made, 1)
            with pool.Fori(0, quads // 2) as i:
                for q in (0, 1):
                    pool.wait_ge(pos_ready, 2 * i + q + 1)
                    pool.sem_inc(turn, 1)
                    if fill:
                        pool.wait_ge(pay_in[q], 16 * i + 16)
                        pool.sem_inc(turn, 1)
                    for b in range(Q):
                        nc.gpsimd.indirect_dma_start(out_d, bass.IndirectOffsetOnAxis(
                            ap=pos[q][:, b:b + 1], axis=0), pay[q][:, b, :], None).then_inc(scattered[q], 16)

        @block.vector
        def _(dve):
            nc.vector.tensor_copy(hi_f[:], hi[:])
            dve.wait_ge(mask_made, 2)
            dve.drain()
            dve.sem_inc(quad_used, 2)
            dve.sem_inc(pay_free, 2)

            def one_hots(n, s, nth):
                q = s % 2
                at = ds(n * Q, Q)
                dve.wait_ge(quad_used, n + 1)
                nc.vector.tensor_tensor(one_lo[q][:], k.ramp_16[:, :, 0:Q], lo[:, at].unsqueeze(1).broadcast_to(
                    [P, P, Q]), ALU.is_equal)
                nc.vector.tensor_tensor(one_hi[q][:], k.ramp_16[:, 0:NHI, 0:Q], hi[:, at].unsqueeze(1).broadcast_to(
                    [P, NHI, Q]), ALU.is_equal)
                dve.drain().then_inc(hot_ready, 1)

            def ranks(n, s, nth):
                q = s % 2
                dve.wait_ge(key_in[s], nth * 16)
                for g in range(4):
                    dve.wait_ge(found_ready, n * 4 + g + 1)
                    for j in (0, 1):
                        ch = n * Q + 2 * g + j
                        col = 2 * g + j
                        w = (j + 1) * P
                        nc.vector.scalar_tensor_tensor(junk_hi[j][:], k.ramp[:, 0:NHI], hi_f[:, ds(ch, 1)],
                                                       found[g][:, j, :], ALU.is_equal, ALU.mult,
                                                       accum_out=base[q][:, col:col + 1])
                        nc.vector.scalar_tensor_tensor(junk_row[j][:, 0:w],
                                                       key_row[s][:, g * 2 * P:g * 2 * P + w],
                                                       key[:, ds(ch, 1)], earlier[:, j, 0:w],
                                                       ALU.is_equal, ALU.mult,
                                                       accum_out=same[q][:, col:col + 1])
                    dve.drain().then_inc(found_read, 1)
                dve.sem_inc(key_used, 1)
                dve.wait_ge(pay_free, n + 1)
                nc.vector.tensor_tensor(pos[q][:], base[q][:], same[q][:], ALU.add)
                for cols, tile in payload:
                    nc.vector.tensor_copy(pay[q][:, :, cols], tile[:, ds(n * Q, Q)])
                dve.drain().then_inc(pos_ready, 1)

            def quad(n, s, nth):
                one_hots(n + 1, (s + 1) % S, None)
                ranks(n, s, nth)
            one_hots(0, 0, None)
            over_quads(dve, 0, quads - 1, quad)
            ranks(quads - 1, (quads - 1) % S, (quads - 1) // S + 1)

        @block.scalar
        def _(act):
            def low_hots(n, s, nth, g):
                q = s % 2
                if g == 0:
                    act.wait_ge(low_in[s], nth * 16)
                    act.wait_ge(quad_used, n + 1)
                at = slice(2 * g * P, 2 * (g + 1) * P)
                nc.scalar.activation(lowT[q][:, at], low_row[s][:, at], ACT.Square, bias=k.minus_lane[:, 0:1])
                act.drain()
                nc.scalar.activation(lowT[q][:, at], lowT[q][:, at], ACT.Relu, bias=k.ones[:, 0:1], scale=-1.0)
                if g == 3:
                    act.drain().then_inc(lowT_ready, 1)

            def copy(n, g):
                act.wait_ge(count_ready, n * 4 + g + 1)
                nc.scalar.copy(counts_sb[g % 2][:], counts[:, 0:NHI]).then_inc(count_copied, 1)

            def quad(n, s, nth):
                for g in range(4):
                    copy(n - 1, g)
                    low_hots(n, s, nth, g)
            for g in range(4):
                low_hots(0, 0, 1, g)
            over_quads(act, 1, quads - 1, quad)
            for g in range(4):
                copy(quads - 1, g)

        @block.tensor
        def _(pe):
            pe.sem_inc(found_read, 4)
            nc.tensor.matmul(counts[:, 0:NHI], k.ident[:], start[:], start=True, stop=False,
                             skip_group_check=True).then_inc(count_ready, 1)
            with pe.Fori(0, quads // 2) as i:
                for q in (0, 1):
                    n = 2 * i + q
                    pe.wait_ge(hot_ready, n + 1)
                    pe.wait_ge(lowT_ready, n + 1)
                    for g in range(4):
                        pe.wait_ge(count_copied, n * 4 + g + 1)
                        for j in (0, 1):
                            mm = nc.tensor.matmul(counts[:, 0:NHI], one_lo[q][:, :, 2 * g + j],
                                                  one_hi[q][:, :, 2 * g + j],
                                                  start=False, stop=False, skip_group_check=True)
                        mm.then_inc(count_ready, 1)
                        pe.wait_ge(found_read, n * 4 + g + 1)
                        for j in (0, 1):
                            at = slice((2 * g + j) * P, (2 * g + j + 1) * P)
                            mm = nc.tensor.matmul(found[g][:, j, :], lowT[q][:, at], counts_sb[g % 2][:],
                                                  start=True, stop=True)
                        mm.then_inc(found_ready, 1)
                    pe.drain().then_inc(quad_used, 1)
            nc.tensor.matmul(counts[:, 0:NHI], one_lo[0][:, :, 0], one_hi[0][:, :, 0], start=False,
                             stop=True, skip_group_check=True)
    return out_d


class RanksBeside:
    Q, S = 8, 5
    TURN = 10

    def __init__(self, k, c, tag, chunks, key, lo, hi, start, key_rows, low_d, payload, out_d):
        nc = k.nc
        Q, S = self.Q, self.S

        def sb(name, shape, dt=F32):
            return c.enter_context(nc.sbuf_tensor(f"{tag}_{name}", shape, dt))

        def sem(name):
            return c.enter_context(k.semaphore(f"{tag}_{name}"))

        self.k, self.nc, self.quads = k, nc, chunks // Q
        self.key, self.lo, self.hi, self.start = key, lo, hi, start
        self.key_rows, self.low_d, self.payload, self.out_d = key_rows, low_d, payload, out_d
        self.key_row = [sb(f"key_row{s}", [P, Q * P]) for s in range(S)]
        self.low_row = [sb(f"low_row{s}", [P, Q * P], BF16) for s in range(S)]
        self.pos = sb("pos", [P, chunks], I32)
        self.base = [sb(f"base{q}", [P, Q]) for q in (0, 1)]
        self.same = [sb(f"same{q}", [P, Q]) for q in (0, 1)]
        self.hi_f = sb("hi_f", [P, chunks])
        self.lowT = [sb(f"lowT{q}", [P, Q * P]) for q in (0, 1)]
        self.one_lo = [sb(f"one_lo{q}", [P, P, Q], BF16) for q in (0, 1)]
        self.one_hi = [sb(f"one_hi{q}", [P, NHI, Q], BF16) for q in (0, 1)]
        self.junk_hi = [sb(f"junk_hi{j}", [P, NHI]) for j in (0, 1)]
        self.junk_row = [sb(f"junk_row{j}", [P, 2 * P]) for j in (0, 1)]
        self.earlier = sb("earlier", [P, 2, 2 * P])
        self.counts_sb = [sb(f"counts_sb{b}", [P, NHI]) for b in (0, 1)]
        self.pos_slot = [sb(f"pos_slot{h}", [P, 2 * Q], I32) for h in (0, 1)]
        self.pay_slot = [sb(f"pay_slot{h}", [P, 2 * Q, 2]) for h in (0, 1)]
        self.counts = c.enter_context(nc.psum_tensor(f"{tag}_counts", [P, 512], F32))
        self.found = c.enter_context(nc.psum_tensor(f"{tag}_found", [P, 8, NHI], F32))
        self.key_in = [sem(f"key_in{s}") for s in range(S)]
        self.low_in = [sem(f"low_in{s}") for s in range(S)]
        self.scattered = [sem(f"scattered{h}") for h in (0, 1)]
        (self.hot_ready, self.quad_used, self.lowT_ready, self.count_ready, self.count_copied,
         self.found_ready, self.found_read, self.pos_ready, self.key_used, self.mask_made, self.copied) = map(
            sem, ("hot_ready", "quad_used", "lowT_ready", "count_ready", "count_copied", "found_ready",
                  "found_read", "pos_ready", "key_used", "mask_made", "copied"))

    def turn(self, eng, i):
        values = (i * self.TURN, i * (self.TURN // self.S), i * (self.TURN * 4))
        return values if isinstance(i, int) else tuple(eng.snap(v) for v in values)

    def place(self, turn, quad):
        return turn[0] + quad, quad % self.S, turn[1] + (quad // self.S + 1), quad % 2

    def load_rows(self, sp, n, s):
        Q = self.Q
        sp.dma_start(self.key_row[s][:].rearrange("p (b e) -> p b e", e=P),
                     self.key_rows[ds(n * Q, Q), :].unsqueeze(0).broadcast_to([P, Q, P])
                     ).then_inc(self.key_in[s], 16)
        sp.dma_start(self.low_row[s][:], self.low_d[ds(n * Q * P, Q * P)].unsqueeze(0)
                     .broadcast_to([P, Q * P])).then_inc(self.low_in[s], 16)

    def sync_start(self, sp):
        for s in range(self.S):
            self.load_rows(sp, s, s)

    def sync_quad(self, sp, turn, quad):
        n, s, _, _ = self.place(turn, quad)
        if isinstance(n, int) and n + self.S >= self.quads:
            return
        sp.wait_ge(self.key_used, n + 1)
        sp.wait_ge(self.lowT_ready, n + 1)
        self.load_rows(sp, n + self.S, s)

    def pool_start(self, pool):
        nc = self.nc
        nc.gpsimd.memset(self.earlier[:], 1.0).then_inc(self.mask_made, 1)
        pool.wait_ge(self.mask_made, 1)
        nc.gpsimd.affine_select(out=self.earlier[:], in_=self.earlier[:], pattern=[[P, 2], [-1, 2 * P]],
                                compare_op=ALU.is_gt, fill=0.0, base=0,
                                channel_multiplier=1).then_inc(self.mask_made, 1)

    def pool_rest(self, pool):
        nc, R = self.nc, 2 * self.Q

        def slot(n, h, before):
            pos, pay = self.pos_slot[h], self.pay_slot[h]
            pool.wait_ge(self.pos_ready, n * 2 + 2)
            pool.sem_inc(self.k.turn, 1)
            if before is not None:
                pool.wait_ge(self.scattered[h], before)
                pool.sem_inc(self.k.turn, 1)
            nc.gpsimd.tensor_copy(pos[:], self.pos[:, ds(n * R, R)]).then_inc(self.copied, 1)
            for f in (0, 1):
                nc.gpsimd.tensor_copy(pay[:, :, f], self.payload[f][:, ds(n * R, R)]).then_inc(self.copied, 1)
            pool.wait_ge(self.copied, n * 3 + 3)
            pool.sem_inc(self.k.turn, 1)
            for b in range(R):
                nc.gpsimd.indirect_dma_start(self.out_d, bass.IndirectOffsetOnAxis(ap=pos[:, b:b + 1], axis=0),
                                             pay[:, b, :], None).then_inc(self.scattered[h], 16)
        for h in (0, 1):
            slot(h, h, None)
        with pool.Fori(1, self.quads // 4) as i:
            for h in (0, 1):
                slot(2 * i + h, h, i * (16 * R))
        for h in (0, 1):
            pool.wait_ge(self.scattered[h], self.quads // 4 * R * 16)

    def one_hots(self, dve, n, q):
        nc, Q = self.nc, self.Q
        at = ds(n * Q, Q)
        dve.wait_ge(self.quad_used, n + 1)
        nc.vector.tensor_tensor(self.one_lo[q][:], self.k.ramp_16[:, :, 0:Q],
                                self.lo[:, at].unsqueeze(1).broadcast_to([P, P, Q]), ALU.is_equal)
        nc.vector.tensor_tensor(self.one_hi[q][:], self.k.ramp_16[:, 0:NHI, 0:Q],
                                self.hi[:, at].unsqueeze(1).broadcast_to([P, NHI, Q]), ALU.is_equal)
        dve.drain().then_inc(self.hot_ready, 1)

    def vector_start(self, dve):
        self.nc.vector.tensor_copy(self.hi_f[:], self.hi[:])
        dve.wait_ge(self.mask_made, 2)
        dve.drain()
        dve.sem_inc(self.quad_used, 2)
        self.one_hots(dve, 0, 0)

    def vector_step(self, dve, turn, step):
        nc, Q, g = self.nc, self.Q, step % 4
        n, s, nth, q = self.place(turn, step // 4)
        if g == 0:
            dve.wait_ge(self.key_in[s], nth * 16)
        dve.wait_ge(self.found_ready, turn[2] + (step + 1))
        for j in (0, 1):
            ch = n * Q + 2 * g + j
            col = 2 * g + j
            w = (j + 1) * P
            nc.vector.scalar_tensor_tensor(self.junk_hi[j][:], self.k.ramp[:, 0:NHI], self.hi_f[:, ds(ch, 1)],
                                           self.found[:, j, :], ALU.is_equal, ALU.mult,
                                           accum_out=self.base[q][:, col:col + 1])
            nc.vector.scalar_tensor_tensor(self.junk_row[j][:, 0:w],
                                           self.key_row[s][:, g * 2 * P:g * 2 * P + w],
                                           self.key[:, ds(ch, 1)], self.earlier[:, j, 0:w],
                                           ALU.is_equal, ALU.mult,
                                           accum_out=self.same[q][:, col:col + 1])
        dve.drain().then_inc(self.found_read, 1)
        if g == 0 and not (isinstance(n, int) and n + 1 == self.quads):
            self.one_hots(dve, n + 1, 1 - q)
        if g == 3:
            dve.sem_inc(self.key_used, 1)
            nc.vector.tensor_tensor(self.pos[:, ds(n * Q, Q)], self.base[q][:], self.same[q][:],
                                    ALU.add).then_inc(self.pos_ready, 1)

    def low_hots(self, act, n, s, nth, q, g):
        nc = self.nc
        if g == 0:
            act.wait_ge(self.low_in[s], nth * 16)
            act.wait_ge(self.quad_used, n + 1)
        at = slice(2 * g * P, 2 * (g + 1) * P)
        nc.scalar.activation(self.lowT[q][:, at], self.low_row[s][:, at], ACT.Square,
                             bias=self.k.minus_lane[:, 0:1])
        act.drain()
        nc.scalar.activation(self.lowT[q][:, at], self.lowT[q][:, at], ACT.Relu, bias=self.k.ones[:, 0:1],
                             scale=-1.0)
        if g == 3:
            act.drain().then_inc(self.lowT_ready, 1)

    def scalar_start(self, act):
        for g in range(4):
            self.low_hots(act, 0, 0, 1, 0, g)
        self.scalar_step(act, (0, 0, 0), 0)

    def scalar_step(self, act, turn, step):
        g = step % 4
        n, _, _, _ = self.place(turn, step // 4)
        if isinstance(n, int) and n == self.quads:
            return
        act.wait_ge(self.count_ready, turn[2] + (step + 1))
        self.nc.scalar.copy(self.counts_sb[g % 2][:], self.counts[:, 0:NHI]).then_inc(self.count_copied, 1)
        if not (isinstance(n, int) and n + 1 == self.quads):
            n, s, nth, q = self.place(turn, step // 4 + 1)
            self.low_hots(act, n, s, nth, q, g)

    def tensor_start(self, pe):
        pe.sem_inc(self.found_read, 1)
        self.nc.tensor.matmul(self.counts[:, 0:NHI], self.k.ident[:], self.start[:], start=True, stop=False,
                              skip_group_check=True).then_inc(self.count_ready, 1)

    def tensor_step(self, pe, turn, step):
        nc, g = self.nc, step % 4
        n, _, _, q = self.place(turn, step // 4)
        if g == 0:
            pe.wait_ge(self.hot_ready, n + 1)
            pe.wait_ge(self.lowT_ready, n + 1)
        pe.wait_ge(self.count_copied, turn[2] + (step + 1))
        for j in (0, 1):
            mm = nc.tensor.matmul(self.counts[:, 0:NHI], self.one_lo[q][:, :, 2 * g + j],
                                  self.one_hi[q][:, :, 2 * g + j], start=False, stop=False,
                                  skip_group_check=True)
        mm.then_inc(self.count_ready, 1)
        pe.wait_ge(self.found_read, turn[2] + (step + 1))
        for j in (0, 1):
            at = slice((2 * g + j) * P, (2 * g + j + 1) * P)
            mm = nc.tensor.matmul(self.found[:, j, :], self.lowT[q][:, at], self.counts_sb[g % 2][:],
                                  start=True, stop=True)
        mm.then_inc(self.found_ready, 1)
        if g == 3:
            pe.drain().then_inc(self.quad_used, 1)

    def tensor_end(self, pe):
        self.nc.tensor.matmul(self.counts[:, 0:NHI], self.one_lo[0][:, :, 0], self.one_hi[0][:, :, 0],
                              start=False, stop=True, skip_group_check=True)


def segment_sum(k, tag, sorted_d, width, chunk_row, first_all, first_row, acc):
    nc = k.nc
    R = 8
    S = 16
    with ExitStack() as c:
        def sb(name, shape, dt=F32):
            return c.enter_context(nc.sbuf_tensor(f"{tag}_{name}", shape, dt))

        def sem(name):
            return c.enter_context(k.semaphore(f"{tag}_{name}"))

        rows = sb("rows", [P, S, width + 1])
        pick = sb("pick", [P, R, P])
        own = sb("own", [P, R])
        part = [c.enter_context(nc.psum_tensor(f"{tag}_part{b}", [P, 512], F32)) for b in range(R)]
        GS = S // 4
        loaded = [sem(f"loaded{q}") for q in range(GS)]
        pick_ready, summed, added = sem("pick_ready"), sem("summed"), sem("added")
        block = c.enter_context(nc.Block())

        @block.gpsimd
        def _(pool):
            pool.sem_inc(summed, GS)
            with pool.Fori(0, NS // S) as i:
                for q in range(GS):
                    at = slice(4 * q % R, 4 * q % R + 4)
                    pool.wait_ge(loaded[q], i * 64 + 64)
                    pool.sem_inc(k.turn, 1)
                    pool.wait_ge(summed, i * GS + q + 1 + GS - R // 4)
                    pool.sem_inc(k.turn, 1)
                    nc.gpsimd.tensor_tensor(own[:, at], rows[:, 4 * q:4 * q + 4, width],
                                            first_all[:, ds(i * S + 4 * q, 4)], ALU.subtract)
                    pool.drain()
                    for b in range(4 * q % R, 4 * q % R + 4):
                        made = nc.gpsimd.tensor_scalar(pick[:, b, :], k.ramp[:], own[:, b:b + 1], None,
                                                       ALU.is_equal)
                    made.then_inc(pick_ready, 1)

        def loads(eng, groups):
            regs = [eng.alloc_register(f"{tag}_chunk{groups[0]}_{b}") for b in range(4)]
            with eng.Fori(0, NS // S) as i:
                for q in groups:
                    eng.reg_load(regs, chunk_row[0:1, ds(i * S + 4 * q, 4)])
                    chunks = [eng.snap(r, min_val=0, max_val=CE - 1) for r in regs]
                    eng.wait_ge(summed, i * GS + q + 1)
                    for b in range(4):
                        eng.dma_start(rows[:, 4 * q + b, :], sorted_d[ds(chunks[b] * P, P), :]
                                      ).then_inc(loaded[q], 16)

        @block.sync
        def _(sp):
            loads(sp, (0, 2))

        @block.scalar
        def _(act):
            loads(act, (1, 3))

        @block.vector
        def _(dve):
            nc.vector.memset(acc[:], 0.0)
            dve.drain()
            regs = [dve.alloc_register(f"{tag}_tile{b}") for b in range(8)]

            with dve.Fori(0, NS // S) as i:
                for q in range(GS):
                    if q % 2 == 0:
                        dve.reg_load(regs, first_row[0:1, ds(i * S + 4 * q, 8)])
                        first = [dve.snap(r, min_val=0, max_val=(REAL_T - 1) * P) for r in regs]
                    dve.wait_ge(summed, i * GS + q + 1 + GS)
                    for b in range(4):
                        at = ds(first[4 * (q % 2) + b], P)
                        nc.vector.tensor_tensor(acc[:, at], acc[:, at], part[(4 * q + b) % R][:, 0:P], ALU.add)
                        dve.drain()
                    dve.sem_inc(added, 1)

        @block.tensor
        def _(pe):
            pe.sem_inc(added, R // 4)
            with pe.Fori(0, NS // S) as i:
                for q in range(GS):
                    pe.wait_ge(loaded[q], i * 64 + 64)
                    pe.wait_ge(pick_ready, i * GS + q + 1)
                    pe.wait_ge(added, i * GS + q + 1)
                    for b in range(4 * q, 4 * q + 4):
                        mm = nc.tensor.matmul(part[b % R][:, 0:P], rows[:, b, 0:width], pick[:, b % R, :],
                                              start=True, stop=True)
                    mm.then_inc(summed, 1)


def over_tiles(eng, body):
    with eng.Fori(0, (REAL_T - 1) // 2) as i:
        for b in (0, 1):
            body(2 * i + b, b, P)
    body(REAL_T - 1, 0, LAST)


def root(k, act, st, rows, asked, answered, nth):
    act.wait_ge(asked, nth)
    k.nc.scalar.activation(st[0:rows, 8:9], st[0:rows, 7:8], ACT.Sqrt,
                           bias=k.eps[0:rows, 0:1]).then_inc(answered, 1)


S4 = 4


def over_fours(eng, *phases):
    with eng.Fori(0, REAL_T // S4) as i:
        for phase in phases:
            for b in range(S4):
                phase(i * S4 + b, b, P)
    for phase in phases:
        phase(REAL_T - 1, 0, LAST)


def over_fours_io(sp, load, *stores):
    for b in range(S4):
        load(b, b, P)
    with sp.Fori(0, REAL_T // S4 - 1) as i:
        for b in range(S4):
            load(i * S4 + b + S4, b, P)
        for store in stores:
            for b in range(S4):
                store(i * S4 + b, b, P)
    load(REAL_T - 1, 0, LAST)
    for store in stores:
        for b in range(S4):
            store(REAL_T - 1 - S4 + b, b, P)
    for store in stores:
        store(REAL_T - 1, 0, LAST)


def times(t, b):
    return (t - b) // S4 + 1


def all_stored(sp, sems):
    for b, sem in enumerate(sems):
        sp.wait_ge(sem, 16 * (times(REAL_T - 1 if b == 0 else REAL_T - 1 - S4 + b, b) + 1))


def request(t, b, part, parts):
    if isinstance(t, int):
        return parts * t + part + 1
    return (t - b) * parts + (part * S4 + b + 1)


def over_fours_at_once(eng, *phases):
    with eng.Fori(0, REAL_T // S4) as i:
        for phase in phases:
            phase([(i * S4 + b, b) for b in range(S4)], P)
    for phase in phases:
        phase([(REAL_T - 1, 0)], LAST)


def norm_stats(k, dve, x, st, tiles, rows, asked):
    for _, b in tiles:
        k.nc.vector.bn_stats(st[b][0:rows, 0:6], x[b][0:rows, :])
    dve.drain()
    for _, b in tiles:
        k.nc.vector.bn_aggr(st[b][0:rows, 6:8], st[b][0:rows, 0:6]).then_inc(asked, 1)


def norm_apply(k, dve, x, out, st, tiles, rows, answered, part, parts, ready=None):
    for t, b in tiles:
        dve.wait_ge(answered, request(t, b, part, parts))
        k.nc.vector.reciprocal(st[b][0:rows, 9:10], st[b][0:rows, 8:9])
    dve.drain()
    for _, b in tiles:
        done = k.nc.vector.tensor_scalar(out[b][0:rows, :], x[b][0:rows, :], st[b][0:rows, 6:7],
                                         st[b][0:rows, 9:10], ALU.subtract, ALU.mult)
        if ready is not None:
            done.then_inc(ready, 1)
    dve.drain()


def load_params(k, ctx, tag, loads):
    nc = k.nc
    tiles = [ctx.enter_context(nc.sbuf_tensor(f"{tag}_{name}", shape, F32)) for name, shape, _ in loads]
    with k.semaphore(f"{tag}_params_in") as loaded, nc.Block() as block:
        @block.sync
        def _(sp):
            for t, (_, _, source) in zip(tiles, loads):
                sp.dma_start(t[:], source, allow_slow_non_contiguous=True).then_inc(loaded, 16)
            sp.wait_ge(loaded, 16 * len(loads))
    return tiles


def row_on_all(v):
    return v.unsqueeze(0).broadcast_to([P, v.shape[0]])


def halves(w):
    return w.rearrange("(h p) m -> p h m", p=P)


def halves_col(v):
    return v.rearrange("(h p) -> p h", p=P)


def input_stage(k, ctx, tag, h_d, kv):
    nc, I = k.nc, k.ins
    with ExitStack() as c:
        def sb(name, shape, dt=F32):
            return c.enter_context(nc.sbuf_tensor(f"{tag}_{name}", shape, dt))

        def sem(name):
            return c.enter_context(k.semaphore(f"{tag}_{name}"))

        def flat(w):
            return row_on_all(w.rearrange("h a d -> (h a d)"))

        w1, b1, kw, kb, vw, vb = load_params(k, c, tag, [
            ("w1", [P, 2, C], halves(I["L0_gnn_c1_w1"])), ("b1", [1, C], I["L0_gnn_c1_b1"].unsqueeze(0)),
            ("kw", [P, C], flat(I["L0_mix_kln_weight"])), ("kb", [P, C], flat(I["L0_mix_kln_bias"])),
            ("vw", [P, C], flat(I["L0_mix_vln_weight"])), ("vb", [P, C], flat(I["L0_mix_vln_bias"]))])
        def slots(name, shape):
            return [sb(f"{name}{b}", shape) for b in range(S4)]

        x, xn, h, z, kk, vv, sq = (slots(n, [P, C]) for n in ("x", "xn", "h", "z", "kk", "vv", "sq"))
        xnT, st, hs = slots("xnT", [P, 2, P]), slots("st", [P, 16]), slots("hs", [P, 4, 8])
        zero = sb("zero", [P, P])
        turned = [c.enter_context(nc.psum_tensor(f"{tag}_turned{b}", [P, 4, P], F32)) for b in range(S4)]
        hp = [c.enter_context(nc.psum_tensor(f"{tag}_hp{b}", [P, 512], F32)) for b in (0, 1)]
        kvp = c.enter_context(nc.psum_tensor(f"{tag}_kvp", [P, 4, P], F32))
        x_in, h_out = [sem(f"x_in{b}") for b in range(S4)], [sem(f"h_out{b}") for b in range(S4)]
        x_used, xn_ready, xn_used, z_ready, kv_ready, kv_used = map(
            sem, ("x_used", "xn_ready", "xn_used", "z_ready", "kv_ready", "kv_used"))
        turned_ready, xnT_ready, hp_ready, h_ready, pool_step, zeroed, kv_summed = map(
            sem, ("turned_ready", "xnT_ready", "hp_ready", "h_ready", "pool_step", "zeroed", "kv_summed"))
        asked, answered, bank_free = sem("asked"), sem("answered"), sem("bank_free")
        block = c.enter_context(nc.Block())

        @block.sync
        def _(sp):
            sp.sem_inc(x_used, S4)
            for b in range(S4):
                sp.sem_inc(h_out[b], 16)

            def load(t, b, rows):
                sp.wait_ge(x_used, t + 1)
                sp.dma_start(x[b][0:rows, :], I["x"][ds(t * P, rows), :]).then_inc(x_in[b], 16)

            def store(t, b, r):
                sp.wait_ge(h_ready, t + 1)
                sp.dma_start(h_d[ds(t * P, r), :], h[b][0:r, :]).then_inc(h_out[b], 16)
            over_fours_io(sp, load, store)
            all_stored(sp, h_out)

        @block.vector
        def _(dve):
            nc.vector.memset(zero[:], 0.0).then_inc(zeroed, 1)
            dve.sem_inc(xn_used, S4)
            dve.sem_inc(kv_ready, S4)

            def by_head(a, r):
                return a[0:r].rearrange("p (h d) -> p h d", d=32)

            def wide(a, r):
                return a.unsqueeze(2).broadcast_to([r, 8, 32])

            def stats(tiles, r):
                for t, b in tiles:
                    dve.wait_ge(x_in[b], times(t, b) * 16)
                norm_stats(k, dve, x, st, tiles, r, asked)

            def apply(tiles, r):
                for t, _ in tiles:
                    dve.wait_ge(xn_used, t + 1)
                norm_apply(k, dve, x, xn, st, tiles, r, answered, 0, 2, xn_ready)
                dve.sem_inc(x_used, len(tiles))

            def head_stats(tiles, r):
                for _, b in tiles:
                    nc.vector.tensor_reduce(hs[b][0:r, 0, :], by_head(xn[b], r), AX_X, ALU.add)
                dve.drain()
                for _, b in tiles:
                    nc.vector.tensor_scalar(hs[b][0:r, 0, :], hs[b][0:r, 0, :], 1.0 / 32, None, ALU.mult)
                dve.drain()
                for t, b in tiles:
                    dve.wait_ge(kv_ready, t + 1)
                    nc.vector.tensor_tensor(by_head(z[b], r), by_head(xn[b], r), wide(hs[b][0:r, 0, :], r),
                                            ALU.subtract)
                dve.drain()
                for _, b in tiles:
                    nc.vector.tensor_tensor(sq[b][0:r], z[b][0:r], z[b][0:r], ALU.mult)
                dve.drain()
                for _, b in tiles:
                    nc.vector.tensor_reduce(hs[b][0:r, 1, :], by_head(sq[b], r), AX_X, ALU.add
                                            ).then_inc(asked, 1)

            def head_apply(tiles, r):
                for t, b in tiles:
                    dve.wait_ge(answered, request(t, b, 1, 2))
                    nc.vector.tensor_scalar(hs[b][0:r, 2, :], hs[b][0:r, 2, :], EPS, None, ALU.add)
                dve.drain()
                for _, b in tiles:
                    nc.vector.reciprocal(hs[b][0:r, 3, :], hs[b][0:r, 2, :])
                dve.drain()
                for _, b in tiles:
                    nc.vector.tensor_tensor(by_head(z[b], r), by_head(z[b], r), wide(hs[b][0:r, 3, :], r),
                                            ALU.mult).then_inc(z_ready, 1)
                dve.drain()
            over_fours_at_once(dve, stats, apply, head_stats, head_apply)
            dve.wait_ge(kv_summed, 1)
            for half in (0, 1):
                nc.vector.scalar_tensor_tensor(kv[:, half, :], kvp[:, half, :], 1.0 / N, k.block_diag[:],
                                               ALU.mult, ALU.mult)

        @block.gpsimd
        def _(pool):
            pool.sem_inc(kv_used, S4)

            def tile(t, b, r):
                pool.wait_ge(z_ready, t + 1)
                pool.sem_inc(pool_step, 1)
                pool.wait_ge(kv_used, t + 1)
                pool.sem_inc(pool_step, 1)
                nc.gpsimd.tensor_tensor(kk[b][0:r], z[b][0:r], kw[0:r], ALU.mult)
                nc.gpsimd.tensor_tensor(vv[b][0:r], z[b][0:r], vw[0:r], ALU.mult)
                pool.drain()
                nc.gpsimd.tensor_tensor(kk[b][0:r], kk[b][0:r], kb[0:r], ALU.add)
                nc.gpsimd.tensor_tensor(vv[b][0:r], vv[b][0:r], vb[0:r], ALU.add)
                pool.drain().then_inc(kv_ready, 1)
            over_fours(pool, tile)

        @block.tensor
        def _(pe):
            pe.wait_ge(zeroed, 1)
            pe.sem_inc(bank_free, 2)
            for half in (0, 1):
                nc.tensor.matmul(kvp[:, half, :], zero[:], zero[:], start=half == 0, stop=False, skip_group_check=True)

            def turn(t, b, r):
                pe.wait_ge(xn_ready, t + 1)
                for half in (0, 1):
                    mm = nc.tensor.transpose(turned[b][:, half, 0:r], xn[b][0:r, half * P:(half + 1) * P],
                                             k.ident[0:r, 0:r])
                mm.then_inc(turned_ready, 1)

            def dense(t, b, r):
                bank = hp[b % 2]
                pe.wait_ge(xnT_ready, t + 1)
                pe.sem_inc(xn_used, 1)
                pe.wait_ge(bank_free, t + 1)
                nc.tensor.matmul(bank[0:r, 0:C], k.ones[0:1, 0:r], b1[:], start=True, stop=False)
                for half in (0, 1):
                    mm = nc.tensor.matmul(bank[0:r, 0:C], xnT[b][:, half, 0:r], w1[:, half, :],
                                          start=False, stop=half == 1)
                mm.then_inc(hp_ready, 1)

            def outer(t, b, r):
                pe.wait_ge(kv_ready, t + 1 + S4)
                for half in (0, 1):
                    at = slice(half * P, (half + 1) * P)
                    mm = nc.tensor.matmul(kvp[:, half, :], kk[b][0:r, at], vv[b][0:r, at], start=False,
                                          stop=False, skip_group_check=True)
                mm.then_inc(kv_used, 1)
            over_fours(pe, turn, dense, outer)
            nc.tensor.matmul(kvp[:, 0, :], zero[:], zero[:], start=False, stop=True,
                             skip_group_check=True).then_inc(kv_summed, 1)

        @block.scalar
        def _(act):
            def first_root(t, b, r):
                root(k, act, st[b], r, asked, answered, request(t, b, 0, 2))

            def copy(t, b, r):
                act.wait_ge(turned_ready, t + 1)
                nc.scalar.copy(xnT[b][:, :, 0:r], turned[b][:, 0:2, 0:r]).then_inc(xnT_ready, 1)

            def head_root(t, b, r):
                act.wait_ge(asked, request(t, b, 1, 2))
                nc.scalar.activation(hs[b][0:r, 2, :], hs[b][0:r, 1, :], ACT.Sqrt,
                                     scale=1.0 / 31).then_inc(answered, 1)

            def relu(t, b, r):
                act.wait_ge(hp_ready, t + 1)
                act.wait_ge(h_out[b], times(t, b) * 16)
                nc.scalar.activation(h[b][0:r, :], hp[b % 2][0:r, 0:C], ACT.Relu).then_inc(h_ready, 1)
                act.wait_ge(h_ready, t + 1)
                act.sem_inc(bank_free, 1)
            over_fours(act, first_root, copy, head_root, relu)


W = 448


def dense_and_norms(k, ctx, tag, acc, w_name, b_name, norms):
    nc, I = k.nc, k.ins
    blocks = NP // W
    NCK, CK = 25, N // 25
    with ExitStack() as c:
        def sb(name, shape, dt=F32):
            return c.enter_context(nc.sbuf_tensor(f"{tag}_{name}", shape, dt))

        def sem(name):
            return c.enter_context(k.semaphore(f"{tag}_{name}"))

        loads = [("w", [P, 2, C], halves(I[w_name])), ("b", [P, 2], halves_col(I[b_name]))]
        for n, (g, b, _) in enumerate(norms):
            loads += [(f"g{n}", [P, 2], halves_col(I[g])), (f"b{n}", [P, 2], halves_col(I[b]))]
        w, b, *gb = load_params(k, c, tag, loads)
        stats = sb("stats", [P, 2, NCK, 6])
        mv, sc = sb("mv", [P, 2, 2]), sb("sc", [P, 4, 2])
        out = [[c.enter_context(nc.psum_tensor(f"{tag}_out{s}{h}", [P, 512], F32)) for h in (0, 1)]
               for s in (0, 1)]
        made, moved = sem("made"), sem("moved")
        asked, answered, scaled, applied = sem("asked"), sem("answered"), sem("scaled"), sem("applied")
        block = c.enter_context(nc.Block())

        @block.tensor
        def _(pe):
            pe.sem_inc(moved, 2)
            with pe.Fori(0, blocks // 2) as i:
                for s in (0, 1):
                    n = 2 * i + s
                    pe.wait_ge(moved, n + 1)
                    for co in (0, 1):
                        for ci in (0, 1):
                            mm = nc.tensor.matmul(out[s][co][:, 0:W], w[:, ci, co * P:(co + 1) * P],
                                                  acc[:, ci, ds(n * W, W)], start=ci == 0, stop=ci == 1)
                    mm.then_inc(made, 1)

        @block.scalar
        def _(act):
            with act.Fori(0, blocks // 2) as i:
                for s in (0, 1):
                    n = 2 * i + s
                    act.wait_ge(made, n + 1)
                    for co in (0, 1):
                        nc.scalar.activation(acc[:, co, ds(n * W, W)], out[s][co][:, 0:W], ACT.Identity,
                                             bias=b[:, co:co + 1])
                    act.drain().then_inc(moved, 1)
            for n, (_, _, relu) in enumerate(norms):
                act.wait_ge(asked, n + 1)
                nc.scalar.activation(sc[:, 0, :], mv[:, :, 1], ACT.Sqrt, bias=k.eps[:, 0:1]
                                     ).then_inc(answered, 1)
                act.wait_ge(scaled, n + 1)
                for half in (0, 1):
                    nc.scalar.activation(acc[:, half, :], acc[:, half, :], ACT.Relu if relu else ACT.Identity,
                                         bias=sc[:, 3, half:half + 1], scale=sc[:, 2, half:half + 1])
                act.drain().then_inc(applied, 1)

        @block.vector
        def _(dve):
            dve.wait_ge(moved, 2 + blocks)
            for n in range(len(norms)):
                if n:
                    dve.wait_ge(applied, n)
                with dve.Fori(0, NCK) as i:
                    for half in (0, 1):
                        nc.vector.bn_stats(stats[:, half, ds(i, 1), :], acc[:, half, ds(i * CK, CK)])
                dve.drain()
                for half in (0, 1):
                    nc.vector.bn_aggr(mv[:, half, :], stats[:, half].rearrange("p a b -> p (a b)"))
                dve.drain().then_inc(asked, 1)
                dve.wait_ge(answered, n + 1)
                nc.vector.reciprocal(sc[:, 1, :], sc[:, 0, :])
                dve.drain()
                nc.vector.tensor_tensor(sc[:, 2, :], sc[:, 1, :], gb[2 * n][:], ALU.mult)
                dve.drain()
                nc.vector.tensor_tensor(sc[:, 1, :], mv[:, :, 0], sc[:, 2, :], ALU.mult)
                dve.drain()
                nc.vector.tensor_tensor(sc[:, 3, :], gb[2 * n + 1][:], sc[:, 1, :], ALU.subtract)
                dve.drain().then_inc(scaled, 1)
            dve.wait_ge(applied, len(norms))


def rows_from_channels(k, ctx, tag, acc, h_d, w_name, b_name):
    nc, I = k.nc, k.ins
    with ExitStack() as c:
        def sb(name, shape, dt=F32):
            return c.enter_context(nc.sbuf_tensor(f"{tag}_{name}", shape, dt))

        def sem(name):
            return c.enter_context(k.semaphore(f"{tag}_{name}"))

        w, b1 = load_params(k, c, tag, [("w", [P, 2, C], halves(I[w_name])),
                                        ("b", [1, C], I[b_name].unsqueeze(0))])
        aT = [sb(f"aT{b}", [P, 2, P]) for b in (0, 1)]
        h = [sb(f"h{b}", [P, C]) for b in (0, 1)]
        hp = [c.enter_context(nc.psum_tensor(f"{tag}_hp{b}", [P, 512], F32)) for b in (0, 1)]
        a_ready, hp_ready, h_ready, h_free = sem("a_ready"), sem("hp_ready"), sem("h_ready"), sem("h_free")
        h_out = [sem("h_out0"), sem("h_out1")]
        block = c.enter_context(nc.Block())

        @block.vector
        def _(dve):
            dve.sem_inc(hp_ready, 2)

            def tile(t, b, r):
                dve.wait_ge(hp_ready, t + 1)
                nc.vector.tensor_copy(aT[b][:, :, 0:r], acc[:, :, ds(t * P, r)]).then_inc(a_ready, 1)
            over_tiles(dve, tile)

        @block.tensor
        def _(pe):
            pe.sem_inc(h_ready, 2)

            def tile(t, b, r):
                pe.wait_ge(a_ready, t + 1)
                pe.wait_ge(h_ready, t + 1)
                nc.tensor.matmul(hp[b][0:r, 0:C], k.ones[0:1, 0:r], b1[:], start=True, stop=False)
                for half in (0, 1):
                    mm = nc.tensor.matmul(hp[b][0:r, 0:C], aT[b][:, half, 0:r], w[:, half, :],
                                          start=False, stop=half == 1)
                mm.then_inc(hp_ready, 1)
            over_tiles(pe, tile)

        @block.scalar
        def _(act):
            act.sem_inc(h_free, 2)

            def tile(t, b, r):
                act.wait_ge(hp_ready, t + 3)
                act.wait_ge(h_free, t + 1)
                nc.scalar.activation(h[b][0:r, :], hp[b][0:r, 0:C], ACT.Relu).then_inc(h_ready, 1)
            over_tiles(act, tile)

        @block.sync
        def _(sp):
            def tile(t, b, r):
                sp.wait_ge(h_ready, t + 3)
                sp.dma_start(h_d[ds(t * P, r), :], h[b][0:r, :]).then_inc(h_out[b], 16)
                sp.wait_ge(h_out[b], k.nth(t, b) * 16)
                sp.sem_inc(h_free, 1)
            over_tiles(sp, tile)


def mix_and_gate_stage(k, ctx, tag, z, kv, x1_d, yT_d, gates):
    nc, I = k.nc, k.ins
    NE = 8
    with ExitStack() as c:
        def sb(name, shape, dt=F32):
            return c.enter_context(nc.sbuf_tensor(f"{tag}_{name}", shape, dt))

        def sem(name):
            return c.enter_context(k.semaphore(f"{tag}_{name}"))

        gamma, beta, wr, br = load_params(k, c, tag, [
            ("gamma", [P, C], row_on_all(I["L0_ffn_gamma"])), ("beta", [P, C], row_on_all(I["L0_ffn_beta"])),
            ("wr", [P, 2, NE], halves(I["L0_ffn_Wr"])), ("br", [P, NE], row_on_all(I["L0_ffn_br"]))])

        def slots(name, shape):
            return [sb(f"{name}{b}", shape) for b in range(S4)]

        x, xn, x1, y, t1 = (slots(n, [P, C]) for n in ("x", "xn", "x1", "y", "t1"))
        xnT, zc, yT = (slots(n, [P, 2, P]) for n in ("xnT", "zc", "yT"))
        st = slots("st", [P, 16])
        masks = gate_buffers(k, c, tag, NE)
        logits = sb("logits", [P, NT, NE])
        turned = [c.enter_context(nc.psum_tensor(f"{tag}_turned{b}", [P, 4, P], F32)) for b in range(S4)]
        mixed = [c.enter_context(nc.psum_tensor(f"{tag}_mixed{b}", [P, 4, P], F32)) for b in range(S4)]
        x_in, x1_out, y_out = ([sem(f"{n}{b}") for b in range(S4)] for n in ("x_in", "x1_out", "y_out"))
        x_used, asked, answered, xn_ready, z_ready, turned_ready, xnT_ready, mixed_ready = map(sem, (
            "x_used", "asked", "answered", "xn_ready", "z_ready", "turned_ready", "xnT_ready", "mixed_ready"))
        x1_ready, y_ready, yturn_ready, yT_ready, lg_ready, tile_done = map(sem, (
            "x1_ready", "y_ready", "yturn_ready", "yT_ready", "lg_ready", "tile_done"))
        block = c.enter_context(nc.Block())

        @block.sync
        def _(sp):
            sp.sem_inc(x_used, S4)
            for b in range(S4):
                sp.sem_inc(x1_out[b], 16)
                sp.sem_inc(y_out[b], 16)

            def load(t, b, rows):
                sp.wait_ge(x_used, t + 1)
                sp.dma_start(x[b][0:rows, :], I["x"][ds(t * P, rows), :]).then_inc(x_in[b], 16)

            def store_x1(t, b, r):
                sp.wait_ge(x1_ready, t + 1)
                sp.dma_start(x1_d[ds(t * P, r), :], x1[b][0:r, :]).then_inc(x1_out[b], 16)

            def store_y(t, b, r):
                sp.wait_ge(yT_ready, t + 1)
                sp.sem_inc(k.turn, 1)
                sp.dma_start(yT_d[:, :, ds(t * P, r)], yT[b][:, :, 0:r]).then_inc(y_out[b], 16)
            over_fours_io(sp, load, store_x1, store_y)
            all_stored(sp, x1_out)
            all_stored(sp, y_out)

        @block.gpsimd
        def _(pool):
            def copy(t, b, r):
                pool.wait_ge(tile_done, t + 1)
                pool.sem_inc(k.turn, 1)
                nc.gpsimd.tensor_copy(zc[b][:, :, 0:r], z[:, :, ds(t * P, r)]).then_inc(z_ready, 1)
            over_fours(pool, copy)

        @block.vector
        def _(dve):
            dve.sem_inc(tile_done, S4)
            nc.vector.memset(logits[:], 0.0)
            nc.vector.memset(gates[:], 0.0)
            dve.drain()

            def stats(tiles, r):
                for t, b in tiles:
                    dve.wait_ge(x_in[b], times(t, b) * 16)
                norm_stats(k, dve, x, st, tiles, r, asked)

            def apply(tiles, r):
                norm_apply(k, dve, x, xn, st, tiles, r, answered, 0, 3, xn_ready)

            def mix(tiles, r):
                for t, b in tiles:
                    dve.wait_ge(mixed_ready, t + 1)
                    zt = turned[b][0:r, 2:4, :].rearrange("p h d -> p (h d)")
                    nc.vector.tensor_tensor(t1[b][0:r], zt, xn[b][0:r], ALU.add)
                dve.drain()
                for _, b in tiles:
                    nc.vector.scalar_tensor_tensor(t1[b][0:r], t1[b][0:r], 0.0, xn[b][0:r], ALU.max, ALU.add)
                dve.drain()
                for _, b in tiles:
                    nc.vector.tensor_tensor(t1[b][0:r], t1[b][0:r], mixed[b][0:r, 0:2, :].rearrange(
                        "p h d -> p (h d)"), ALU.add)
                dve.drain()
                for t, b in tiles:
                    dve.wait_ge(x1_out[b], times(t, b) * 16)
                    nc.vector.tensor_tensor(x1[b][0:r], t1[b][0:r], x[b][0:r], ALU.add).then_inc(x1_ready, 1)
                dve.drain()
                dve.sem_inc(x_used, len(tiles))
                norm_stats(k, dve, x1, st, tiles, r, asked)

            def second_norm(tiles, r):
                norm_apply(k, dve, x1, t1, st, tiles, r, answered, 1, 3)
                norm_stats(k, dve, t1, st, tiles, r, asked)

            def third_norm(tiles, r):
                norm_apply(k, dve, t1, y, st, tiles, r, answered, 2, 3)
                for _, b in tiles:
                    nc.vector.tensor_tensor(y[b][0:r], y[b][0:r], gamma[0:r], ALU.mult)
                dve.drain()
                for _, b in tiles:
                    nc.vector.tensor_tensor(y[b][0:r], y[b][0:r], beta[0:r], ALU.add).then_inc(y_ready, 1)
                dve.drain()

            def take_logits(tiles, r):
                for t, b in tiles:
                    dve.wait_ge(lg_ready, t + 1)
                    nc.vector.tensor_tensor(logits[0:r, ds(t, 1), :], turned[b][0:r, 0, 0:NE], br[0:r, :],
                                            ALU.add)
                dve.drain().then_inc(tile_done, len(tiles))
            over_fours_at_once(dve, stats, apply, mix, second_norm, third_norm, take_logits)
            top_two(k, dve, logits, gates, NE, asked, answered, 3 * REAL_T + 1, masks)

        @block.scalar
        def _(act):
            def root_of(part):
                return lambda t, b, r: root(k, act, st[b], r, asked, answered, request(t, b, part, 3))

            def copy_xn(t, b, r):
                act.wait_ge(turned_ready, t + 1)
                nc.scalar.copy(xnT[b][:, :, 0:r], turned[b][:, 0:2, 0:r]).then_inc(xnT_ready, 1)

            def copy_y(t, b, r):
                act.wait_ge(yturn_ready, t + 1)
                act.wait_ge(y_out[b], times(t, b) * 16)
                nc.scalar.copy(yT[b][:, :, 0:r], mixed[b][:, 2:4, 0:r]).then_inc(yT_ready, 1)
            over_fours(act, root_of(0), copy_xn, root_of(1), root_of(2), copy_y)
            act.wait_ge(asked, 3 * REAL_T + 1)
            nc.scalar.activation(masks[5][:], masks[5][:], ACT.Exp).then_inc(answered, 1)

        @block.tensor
        def _(pe):
            def turn_xn(t, b, r):
                pe.wait_ge(xn_ready, t + 1)
                pe.wait_ge(tile_done, t + 1)
                for half in (0, 1):
                    mm = nc.tensor.transpose(turned[b][:, half, 0:r], xn[b][0:r, half * P:(half + 1) * P],
                                             k.ident[0:r, 0:r])
                mm.then_inc(turned_ready, 1)

            def mix(t, b, r):
                pe.wait_ge(z_ready, t + 1)
                pe.wait_ge(xnT_ready, t + 1)
                for half in (0, 1):
                    nc.tensor.transpose(turned[b][0:r, 2 + half, :], zc[b][:, half, 0:r], k.ident[:])
                for half in (0, 1):
                    mm = nc.tensor.matmul(mixed[b][0:r, half, :], xnT[b][:, half, 0:r], kv[:, half, :],
                                          start=True, stop=True)
                mm.then_inc(mixed_ready, 1)

            def turn_y(t, b, r):
                pe.wait_ge(y_ready, t + 1)
                for half in (0, 1):
                    mm = nc.tensor.transpose(mixed[b][:, 2 + half, 0:r], y[b][0:r, half * P:(half + 1) * P],
                                             k.ident[0:r, 0:r])
                mm.then_inc(yturn_ready, 1)

            def score(t, b, r):
                pe.wait_ge(yT_ready, t + 1)
                for half in (0, 1):
                    mm = nc.tensor.matmul(turned[b][0:r, 0, 0:NE], yT[b][:, half, 0:r], wr[:, half, :],
                                          start=half == 0, stop=half == 1)
                mm.then_inc(lg_ready, 1)
            over_fours(pe, turn_xn, mix, turn_y, score)


def gate_buffers(k, c, tag, NE):
    nc = k.nc
    big = [c.enter_context(nc.sbuf_tensor(f"{tag}_gm{n}", [P, NT, NE], F32)) for n in range(4)]
    small = [c.enter_context(nc.sbuf_tensor(f"{tag}_gs{n}", [P, NT], F32)) for n in range(4)]
    return big + small


def top_two(k, dve, score, gates, NE, asked, answered, nth, bufs):
    nc = k.nc
    masked, number, hot1, hot2, best, gap, w1, w2 = bufs
    shape = [P, NT, NE]

    def wide(a):
        return a[:].unsqueeze(2).broadcast_to(shape)

    ramp = k.ramp[:, 0:NE].unsqueeze(1).broadcast_to(shape)
    nc.vector.tensor_copy(masked[:], score[:])
    dve.drain()
    for hot, value in ((hot1, best), (hot2, gap)):
        nc.vector.tensor_reduce(value[:], masked[:], AX_X, ALU.max)
        dve.drain()
        nc.vector.tensor_tensor(number[:], masked[:], wide(value), ALU.is_lt)
        dve.drain()
        nc.vector.scalar_tensor_tensor(number[:], number[:], float(NE), ramp, ALU.mult, ALU.add)
        dve.drain()
        nc.vector.tensor_reduce(w1[:], number[:], AX_X, ALU.min)
        dve.drain()
        nc.vector.tensor_tensor(hot[:], ramp, wide(w1), ALU.is_equal)
        dve.drain()
        nc.vector.scalar_tensor_tensor(masked[:], hot[:], NEG, masked[:], ALU.mult, ALU.add)
        dve.drain()
    nc.vector.tensor_tensor(gap[:], gap[:], best[:], ALU.subtract).then_inc(asked, 1)
    dve.wait_ge(answered, nth)
    nc.vector.tensor_scalar(w1[:], gap[:], 1.0, None, ALU.add)
    dve.drain()
    nc.vector.reciprocal(w2[:], w1[:])
    dve.drain()
    nc.vector.tensor_tensor(w1[:], gap[:], w2[:], ALU.mult)
    nc.vector.tensor_tensor(hot1[:], hot1[:], wide(w2), ALU.mult)
    dve.drain()
    nc.vector.tensor_tensor(hot2[:], hot2[:], wide(w1), ALU.mult)
    dve.drain()
    nc.vector.tensor_tensor(gates[:], hot1[:], hot2[:], ALU.add)
    dve.drain()


def expert_stage(k, ctx, tag, NE, xT_d, x_d, out_d, gates, w1_name, b1_name, w2_name, b2_name, ranks, beside):
    nc, I = k.nc, k.ins
    GN = 2 * P
    H = 4
    with ExitStack() as c:
        def sb(name, shape, dt=F32):
            return c.enter_context(nc.sbuf_tensor(f"{tag}_{name}", shape, dt))

        def sem(name):
            return c.enter_context(k.semaphore(f"{tag}_{name}"))

        w1, w2, b2, b1_rows = load_params(k, c, tag, [
            ("w1", [P, NE, 2, H * P], I[w1_name].rearrange("e (h p) m -> p e h m", p=P)),
            ("w2", [P, NE, H, C], I[w2_name].rearrange("e (h p) m -> p e h m", p=P)),
            ("b2", [NE, C], I[b2_name]),
            ("b1", [NE * H, P], I[b1_name].rearrange("e (h p) -> (e h) p", p=P))])
        b1 = sb("b1c", [P, NE * H])
        xT = [sb(f"xT{u}", [P, 2, GN]) for u in (0, 1)]
        x = [sb(f"x{u}", [P, 2, C]) for u in (0, 1)]
        gs = [sb(f"gs{u}", [P, 2, NE]) for u in (0, 1)]
        gT = [sb(f"gT{u}", [NE, 2, P]) for u in (0, 1)]
        hid = [sb(f"hid{v}", [P, H, GN]) for v in (0, 1)]
        hp = [c.enter_context(nc.psum_tensor(f"{tag}_hp{v}", [P, H, GN], F32)) for v in (0, 1)]
        yp = [c.enter_context(nc.psum_tensor(f"{tag}_yp{v}", [P, 2, C], F32)) for v in (0, 1)]
        gp, bp = yp[0].rearrange("p a (b q) -> p (a b) q", q=P), yp[1]
        xT_in, x_in = [sem("xT_in0"), sem("xT_in1")], [sem("x_in0"), sem("x_in1")]
        x_out = [sem("x_out0"), sem("x_out1")]
        xT_used, g_ready, gp_ready, gT_ready, bp_ready = map(
            sem, ("xT_used", "g_ready", "gp_ready", "gT_ready", "bp_ready"))
        hp_ready, hid_ready, yp_ready, yp_read, x_ready = map(
            sem, ("hp_ready", "hid_ready", "yp_ready", "yp_read", "x_ready"))
        b1_turned, b1_ready, hid_used, bp_read = map(sem, ("b1_turned", "b1_ready", "hid_used", "bp_read"))
        block = c.enter_context(nc.Block())

        pairs = N // GN // 2

        def over_groups(eng, body):
            with eng.Fori(0, pairs) as i:
                turn = ranks.turn(eng, i)
                for u in (0, 1):
                    body(turn, 2 * i + u, u, (P, P))
            body(ranks.turn(eng, pairs), N // GN, 0, (LAST,))

        order = [("up", 0), ("up", 1)]
        for e in range(NE):
            order += [("down", e)] + ([("up", e + 2)] if e + 2 < NE else [])

        def placed(u, tiles):
            at = {}
            if len(tiles) == 1:
                for n, (what, e) in enumerate(order):
                    at[what, e, 0] = [2 * n, 2 * n + 1]
                return at
            places = [(8 * n + m * 8 // parts, (what, e, m)) for n, (what, e) in enumerate(order)
                      for parts in ((4,) if what == "up" else (2,)) for m in range(parts)]
            for step in range(20):
                _, where = min((abs(position - step * 8 * len(order) / 20), where)
                               for position, where in places)
                at.setdefault(where, []).append(20 * u + step)
            return at

        def steps_of(at, what, e):
            return [step for m in range(4) for step in at.get((what, e, m), ())]

        @block.sync
        def _(sp):
            sp.sem_inc(xT_used, 2)
            for u in (0, 1):
                sp.sem_inc(x_out[u], 16)

            def load(n, u, tiles):
                w = sum(tiles)
                sp.wait_ge(xT_used, n + 1)
                sp.dma_start(xT[u][:, :, 0:w], xT_d[:, :, ds(n * GN, w)]).then_inc(xT_in[u], 16)
                sp.wait_ge(x_out[u], k.nth(n, u) * 16)
                r = tiles[0]
                sp.dma_start(x[u][0:r, 0:len(tiles), :], x_d[ds(n * GN, w), :].rearrange(
                    "(a p) m -> p a m", p=r)).then_inc(x_in[u], 16)

            def store(n, u, tiles):
                w, r = sum(tiles), tiles[0]
                sp.wait_ge(x_ready, n + 1)
                sp.dma_start(out_d[ds(n * GN, w), :].rearrange("(a p) m -> p a m", p=r),
                             x[u][0:r, 0:len(tiles), :]).then_inc(x_out[u], 16)

            def keys(i, quads):
                turn = ranks.turn(sp, i)
                for quad in quads:
                    ranks.sync_quad(sp, turn, quad)

            both = (P, P)
            load(0, 0, both)
            ranks.sync_start(sp)
            with sp.Fori(0, pairs - 1) as i:
                for u in (0, 1):
                    load(2 * i + u + 1, 1 - u, both)
                    keys(i, range(5 * u, 5 * u + 5))
                    store(2 * i + u, u, both)
            last = 2 * pairs
            load(last - 1, 1, both)
            keys(pairs - 1, range(5))
            store(last - 2, 0, both)
            load(last, 0, (LAST,))
            keys(pairs - 1, range(5, 10))
            store(last - 1, 1, both)
            keys(pairs, range(8))
            store(last, 0, (LAST,))
            for u in (0, 1):
                sp.wait_ge(x_out[u], 16 * (pairs + 2 - u))

        @block.gpsimd
        def _(pool):
            ranks.pool_start(pool)
            beside(pool)
            ranks.pool_rest(pool)

        @block.vector
        def _(dve):
            ranks.vector_start(dve)

            def group(turn, n, u, tiles):
                r, nt = tiles[0], len(tiles)
                nc.vector.tensor_copy(gs[u][:, 0:nt, :], gates[:, ds(n * 2, nt), :]).then_inc(g_ready, 1)
                for step in steps_of(placed(u, tiles), "up", 0):
                    ranks.vector_step(dve, turn, step)
                dve.wait_ge(gp_ready, n + 1)
                nc.vector.tensor_copy(gT[u][:, 0:nt, :], gp[0:NE, 0:nt, :]).then_inc(gT_ready, 1)
                for step in steps_of(placed(u, tiles), "up", 1):
                    ranks.vector_step(dve, turn, step)
                dve.wait_ge(x_in[u], k.nth(n, u) * 16)
                dve.wait_ge(bp_ready, n + 1)
                nc.vector.tensor_tensor(x[u][0:r, 0:nt, :], x[u][0:r, 0:nt, :], bp[0:r, 0:nt, :], ALU.add)
                dve.drain()
                dve.sem_inc(bp_read, 1)
                at = placed(u, tiles)
                for what, e in order[2:]:
                    for step in steps_of(at, what, e):
                        ranks.vector_step(dve, turn, step)
                    if what == "up":
                        continue
                    dve.wait_ge(yp_ready, n * NE + e + 1)
                    for a in range(nt):
                        nc.vector.scalar_tensor_tensor(x[u][0:r, a, :], yp[e % 2][0:r, a, :],
                                                       gs[u][0:r, a, e:e + 1], x[u][0:r, a, :],
                                                       ALU.mult, ALU.add)
                    dve.drain().then_inc(yp_read, 1)
                dve.sem_inc(x_ready, 1)
            over_groups(dve, group)

        @block.scalar
        def _(act):
            act.wait_ge(b1_turned, 1)
            nc.scalar.copy(b1[:], gp[:, 0, 0:NE * H]).then_inc(b1_ready, 1)
            act.wait_ge(b1_ready, 1)

            ranks.scalar_start(act)

            def group(turn, n, u, tiles):
                w = sum(tiles)
                first = n * NE if isinstance(n, int) else act.snap(n * NE)

                def gelu(e):
                    m = first + e
                    act.wait_ge(hp_ready, m + 1)
                    act.wait_ge(hid_used, m + 1)
                    for j in range(H):
                        nc.scalar.activation(hid[e % 2][:, j, 0:w], hp[e % 2][:, j, 0:w], ACT.Gelu,
                                             bias=b1[:, e * H + j:e * H + j + 1])
                    act.drain().then_inc(hid_ready, 1)

                at = placed(u, tiles)
                for what, e in order:
                    for step in steps_of(at, what, e):
                        ranks.scalar_step(act, turn, step + 1)
                    if what == "up":
                        gelu(e)
            over_groups(act, group)

        @block.tensor
        def _(pe):
            nc.tensor.transpose(gp[:, 0, 0:NE * H], b1_rows[:], k.ident[0:NE * H, 0:NE * H]
                                ).then_inc(b1_turned, 1)
            pe.wait_ge(b1_ready, 1)
            pe.sem_inc(hid_used, 2)
            pe.sem_inc(yp_read, 2)
            ranks.tensor_start(pe)

            def group(turn, n, u, tiles):
                w, r, nt = sum(tiles), tiles[0], len(tiles)

                at = placed(u, tiles)
                first = n * NE if isinstance(n, int) else pe.snap(n * NE)

                def take(what, e, part):
                    for step in at.get((what, e, part), ()):
                        ranks.tensor_step(pe, turn, step)

                def up(e):
                    m = first + e
                    if e >= 2:
                        pe.wait_ge(hid_ready, m - 1)
                    for j in range(H):
                        take("up", e, j)
                        for ci in (0, 1):
                            mm = nc.tensor.matmul(hp[e % 2][:, j, 0:w], w1[:, e, ci, j * P:(j + 1) * P],
                                                  xT[u][:, ci, 0:w], start=ci == 0, stop=ci == 1)
                    mm.then_inc(hp_ready, 1)

                def down(e):
                    m = first + e
                    take("down", e, 0)
                    pe.wait_ge(hid_ready, m + 1)
                    pe.wait_ge(yp_read, m + 1)
                    if e == 1:
                        pe.wait_ge(bp_read, n + 1)
                    for a in range(nt):
                        if a == 1:
                            take("down", e, 1)
                        for j in range(H):
                            mm = nc.tensor.matmul(yp[e % 2][0:r, a, :], hid[e % 2][:, j, a * P:a * P + r],
                                                  w2[:, e, j, :], start=j == 0, stop=j == H - 1)
                    mm.then_inc(yp_ready, 1)
                    pe.sem_inc(hid_used, 1)

                pe.wait_ge(xT_in[u], k.nth(n, u) * 16)
                up(0)
                pe.wait_ge(g_ready, n + 1)
                pe.wait_ge(yp_read, first + 2)
                for a in range(nt):
                    mm = nc.tensor.transpose(gp[0:NE, a, :], gs[u][:, a, :], k.ident[:])
                mm.then_inc(gp_ready, 1)
                up(1)
                pe.wait_ge(gT_ready, n + 1)
                for a in range(nt):
                    mm = nc.tensor.matmul(bp[0:r, a, :], gT[u][:, a, 0:r], b2[:], start=True, stop=True)
                mm.then_inc(bp_ready, 1)
                for what, e in order[2:]:
                    if what == "up":
                        up(e)
                    else:
                        down(e)
                pe.sem_inc(xT_used, 1)
            over_groups(pe, group)
            ranks.tensor_end(pe)


def expert_outputs(k, ctx, tag, NE, xT_d, y_d, w1_name, b1_name, w2_name, b2_name, beside):
    nc, I = k.nc, k.ins
    GN = 2 * P
    H = 4
    with ExitStack() as c:
        def sb(name, shape, dt=F32):
            return c.enter_context(nc.sbuf_tensor(f"{tag}_{name}", shape, dt))

        def sem(name):
            return c.enter_context(k.semaphore(f"{tag}_{name}"))

        w1, w2, b2, b1_rows = load_params(k, c, tag, [
            ("w1", [P, NE, 2, H * P], I[w1_name].rearrange("e (h p) m -> p e h m", p=P)),
            ("w2", [P, NE, H, C], I[w2_name].rearrange("e (h p) m -> p e h m", p=P)),
            ("b2", [P, NE * C], row_on_all(I[b2_name].rearrange("e m -> (e m)"))),
            ("b1", [NE * H, P], I[b1_name].rearrange("e (h p) -> (e h) p", p=P))])
        b1 = sb("b1c", [P, NE * H])
        xT = [sb(f"xT{u}", [P, 2, GN]) for u in (0, 1)]
        y = [sb(f"y{e}", [P, 2, C]) for e in range(NE)]
        hid = [sb(f"hid{v}", [P, H, GN]) for v in (0, 1)]
        hp = [c.enter_context(nc.psum_tensor(f"{tag}_hp{v}", [P, H, GN], F32)) for v in (0, 1)]
        yp = [c.enter_context(nc.psum_tensor(f"{tag}_yp{v}", [P, 2, C], F32)) for v in (0, 1)]
        gp = c.enter_context(nc.psum_tensor(f"{tag}_gp", [P, 4, P], F32))
        xT_in = [sem("xT_in0"), sem("xT_in1")]
        y_out = [sem(f"y_out{e}") for e in range(NE)]
        xT_used, b1_turned, b1_ready, hid_used = map(sem, ("xT_used", "b1_turned", "b1_ready", "hid_used"))
        hp_ready, hid_ready, yp_ready, y_ready, yp_read = map(
            sem, ("hp_ready", "hid_ready", "yp_ready", "y_ready", "yp_read"))
        block = c.enter_context(nc.Block())

        pairs = N // GN // 2

        def over_groups(eng, body):
            with eng.Fori(0, pairs) as i:
                for u in (0, 1):
                    body(2 * i + u, u, (P, P))
            body(N // GN, 0, (LAST,))

        @block.sync
        def _(sp):
            sp.sem_inc(xT_used, 2)

            def load(n, u, w):
                sp.wait_ge(xT_used, n + 1)
                sp.dma_start(xT[u][:, :, 0:w], xT_d[:, :, ds(n * GN, w)]).then_inc(xT_in[u], 16)

            def store(n, tiles):
                w, r = sum(tiles), tiles[0]
                for e in range(NE):
                    sp.wait_ge(y_ready, n * NE + e + 1)
                    sp.dma_start(y_d[ds(n * GN, w), e, :].rearrange("(a p) m -> p a m", p=r),
                                 y[e][0:r, 0:len(tiles), :]).then_inc(y_out[e], 16)

            load(0, 0, GN)
            with sp.Fori(0, pairs - 1) as i:
                for u in (0, 1):
                    load(2 * i + u + 1, 1 - u, GN)
                    store(2 * i + u, (P, P))
            last = 2 * pairs
            load(last - 1, 1, GN)
            store(last - 2, (P, P))
            load(last, 0, LAST)
            store(last - 1, (P, P))
            store(last, (LAST,))
            for e in range(NE):
                sp.wait_ge(y_out[e], 16 * (last + 2))

        @block.gpsimd
        def _(pool):
            beside(pool)

        @block.vector
        def _(dve):
            for e in range(NE):
                dve.sem_inc(y_out[e], 16)

            def group(n, u, tiles):
                r, nt = tiles[0], len(tiles)
                for e in range(NE):
                    m = n * NE + e
                    dve.wait_ge(y_out[e], n * 16 + 16)
                    dve.wait_ge(yp_ready, m + 1)
                    nc.vector.tensor_tensor(y[e][0:r, 0:nt, :], yp[e % 2][0:r, 0:nt, :],
                                            b2[0:r, e * C:(e + 1) * C].unsqueeze(1).broadcast_to([r, nt, C]),
                                            ALU.add)
                    dve.drain().then_inc(y_ready, 1)
                    dve.sem_inc(yp_read, 1)
            over_groups(dve, group)

        @block.scalar
        def _(act):
            act.wait_ge(b1_turned, 1)
            nc.scalar.copy(b1[:], gp[:, 0, 0:NE * H]).then_inc(b1_ready, 1)
            act.wait_ge(b1_ready, 1)

            def group(n, u, tiles):
                w = sum(tiles)
                for e in range(NE):
                    m = n * NE + e
                    act.wait_ge(hp_ready, m + 1)
                    act.wait_ge(hid_used, m + 1)
                    for j in range(H):
                        nc.scalar.activation(hid[e % 2][:, j, 0:w], hp[e % 2][:, j, 0:w], ACT.Gelu,
                                             bias=b1[:, e * H + j:e * H + j + 1])
                    act.drain().then_inc(hid_ready, 1)
            over_groups(act, group)

        @block.tensor
        def _(pe):
            nc.tensor.transpose(gp[:, 0, 0:NE * H], b1_rows[:], k.ident[0:NE * H, 0:NE * H]
                                ).then_inc(b1_turned, 1)
            pe.wait_ge(b1_ready, 1)
            pe.sem_inc(hid_used, 2)
            pe.sem_inc(yp_read, 2)

            def group(n, u, tiles):
                w, r, nt = sum(tiles), tiles[0], len(tiles)

                def up(e):
                    m = n * NE + e
                    if e >= 2:
                        pe.wait_ge(hid_ready, m - 1)
                    for j in range(H):
                        for ci in (0, 1):
                            mm = nc.tensor.matmul(hp[e % 2][:, j, 0:w], w1[:, e, ci, j * P:(j + 1) * P],
                                                  xT[u][:, ci, 0:w], start=ci == 0, stop=ci == 1)
                    mm.then_inc(hp_ready, 1)

                def down(e):
                    m = n * NE + e
                    pe.wait_ge(hid_ready, m + 1)
                    pe.wait_ge(yp_read, m + 1)
                    for a in range(nt):
                        for j in range(H):
                            mm = nc.tensor.matmul(yp[e % 2][0:r, a, :], hid[e % 2][:, j, a * P:a * P + r],
                                                  w2[:, e, j, :], start=j == 0, stop=j == H - 1)
                    mm.then_inc(yp_ready, 1)
                    pe.sem_inc(hid_used, 1)

                pe.wait_ge(xT_in[u], k.nth(n, u) * 16)
                up(0)
                up(1)
                for e in range(NE):
                    down(e)
                    if e + 2 < NE:
                        up(e + 2)
                pe.sem_inc(xT_used, 1)
            over_groups(pe, group)


def combine_stage(k, ctx, tag, NE, y_d, x_d, out_d, gates):
    nc = k.nc
    S = 4
    with ExitStack() as c:
        x = [c.enter_context(nc.sbuf_tensor(f"{tag}_x{b}", [P, C], F32)) for b in range(S)]
        y = [c.enter_context(nc.sbuf_tensor(f"{tag}_y{b}", [P, NE, C], F32)) for b in range(S)]
        landed = [c.enter_context(k.semaphore(f"{tag}_landed{b}")) for b in range(S)]
        out = [c.enter_context(k.semaphore(f"{tag}_out{b}")) for b in range(S)]
        done = c.enter_context(k.semaphore(f"{tag}_done"))
        block = c.enter_context(nc.Block())

        def over(eng, body):
            with eng.Fori(0, REAL_T // S) as i:
                for b in range(S):
                    body(i * S + b, b, i * 16 + 16, P)
            body(REAL_T - 1, 0, REAL_T // S * 16 + 16, LAST)

        @block.sync
        def _(sp):
            def load(t, b, nth, r):
                sp.wait_ge(out[b], nth)
                sp.dma_start(y[b][0:r], y_d[ds(t * P, r), :, :]).then_inc(landed[b], 16)
                sp.dma_start(x[b][0:r, :], x_d[ds(t * P, r), :]).then_inc(landed[b], 16)
            over(sp, load)

        @block.vector
        def _(dve):
            def tile(t, b, nth, r):
                dve.wait_ge(landed[b], 2 * nth)
                for e in range(NE):
                    nc.vector.scalar_tensor_tensor(x[b][0:r, :], y[b][0:r, e, :], gates[0:r, ds(t, 1), e],
                                                   x[b][0:r, :], ALU.mult, ALU.add)
                    dve.drain()
                dve.sem_inc(done, 1)
            over(dve, tile)

        @block.scalar
        def _(act):
            for b in range(S):
                act.sem_inc(out[b], 16)

            def store(t, b, nth, r):
                act.wait_ge(done, t + 1)
                act.dma_start(out_d[ds(t * P, r), :], x[b][0:r, :]).then_inc(out[b], 16)
            over(act, store)
            for b in range(S):
                act.wait_ge(out[b], 16 * (REAL_T // S + 1 + (b == 0)))


SCALE = 32 ** -0.5
HG = 16
ROW = HG + 4


def channels_stage(k, ctx, tag, x2_d, xn_d, xT, kmax):
    nc, I = k.nc, k.ins
    blocks = NP // W
    with ExitStack() as c:
        def sb(name, shape, dt=F32):
            return c.enter_context(nc.sbuf_tensor(f"{tag}_{name}", shape, dt))

        def sem(name):
            return c.enter_context(k.semaphore(f"{tag}_{name}"))

        wk, = load_params(k, c, tag, [("wk", [P, 2, P], halves(I["L1_mix_W_qkv"])[:, :, P:2 * P])])
        x, xn = ([sb(f"{n}{b}", [P, C]) for b in range(S4)] for n in ("x", "xn"))
        st, kpart = [sb(f"st{b}", [P, 16]) for b in range(S4)], sb("kpart", [P, blocks])
        turned = [c.enter_context(nc.psum_tensor(f"{tag}_turned{b}", [P, 4, P], F32)) for b in range(S4)]
        kp = [c.enter_context(nc.psum_tensor(f"{tag}_kp{b}", [P, 512], F32)) for b in (0, 1)]
        x_in, xn_out = ([sem(f"{n}{b}") for b in range(S4)] for n in ("x_in", "xn_out"))
        x_used, xn_ready, turned_ready, turned_read, asked, answered, kp_ready, kp_read = map(sem, (
            "x_used", "xn_ready", "turned_ready", "turned_read", "asked", "answered", "kp_ready",
            "kp_read"))
        block = c.enter_context(nc.Block())

        @block.sync
        def _(sp):
            sp.sem_inc(x_used, S4)
            for b in range(S4):
                sp.sem_inc(xn_out[b], 16)

            def load(t, b, r):
                sp.wait_ge(x_used, t + 1)
                sp.dma_start(x[b][0:r, :], x2_d[ds(t * P, r), :]).then_inc(x_in[b], 16)

            def store(t, b, r):
                sp.wait_ge(xn_ready, t + 1)
                sp.dma_start(xn_d[ds(t * P, r), :], xn[b][0:r, :]).then_inc(xn_out[b], 16)
            over_fours_io(sp, load, store)
            all_stored(sp, xn_out)

        @block.vector
        def _(dve):
            def stats(tiles, r):
                for t, b in tiles:
                    dve.wait_ge(x_in[b], times(t, b) * 16)
                norm_stats(k, dve, x, st, tiles, r, asked)

            def apply(tiles, r):
                for t, b in tiles:
                    dve.wait_ge(xn_out[b], times(t, b) * 16)
                    dve.wait_ge(turned_ready, t + 1)
                norm_apply(k, dve, x, xn, st, tiles, r, answered, 0, 1, xn_ready)
                dve.sem_inc(x_used, len(tiles))
            dve.sem_inc(turned_ready, S4)
            over_fours(dve, lambda t, b, r: stats([(t, b)], r), lambda t, b, r: apply([(t, b)], r))
            with dve.Fori(0, blocks // 2 - 1) as i:
                for s in (0, 1):
                    dve.wait_ge(kp_ready, 2 * i + s + 1)
                    nc.vector.tensor_reduce(kpart[:, ds(2 * i + s, 1)], kp[s][:, 0:W], AX_X, ALU.max
                                            ).then_inc(kp_read, 1)
            for n in (blocks - 2, blocks - 1):
                dve.wait_ge(kp_ready, n + 1)
                w = min(W, N - n * W)
                nc.vector.tensor_reduce(kpart[:, n:n + 1], kp[n % 2][:, 0:w], AX_X, ALU.max).then_inc(kp_read, 1)
            dve.drain()
            nc.vector.tensor_reduce(kmax[:], kpart[:], AX_X, ALU.max)

        @block.scalar
        def _(act):
            nc.scalar.activation(xT[:, :, N:NP], k.ones[:, 0:2 * (NP - N)].rearrange("p (a b) -> p a b", a=2),
                                 ACT.Copy, scale=0.0)

            def roots(t, b, r):
                root(k, act, st[b], r, asked, answered, t + 1)

            def copy(t, b, r):
                act.wait_ge(turned_ready, t + 1 + S4)
                nc.scalar.copy(xT[:, :, ds(t * P, r)], turned[b][:, 0:2, 0:r]).then_inc(turned_read, 1)
            over_fours(act, roots, copy)

        @block.tensor
        def _(pe):
            pe.sem_inc(turned_read, S4)
            pe.sem_inc(kp_read, 2)

            def tile(t, b, r):
                pe.wait_ge(xn_ready, t + 1)
                pe.wait_ge(turned_read, t + 1)
                for half in (0, 1):
                    mm = nc.tensor.transpose(turned[b][:, half, 0:r], xn[b][0:r, half * P:(half + 1) * P],
                                             k.ident[0:r, 0:r])
                mm.then_inc(turned_ready, 1)
            over_fours(pe, tile)
            pe.wait_ge(turned_read, S4 + REAL_T)
            with pe.Fori(0, blocks // 2) as i:
                for s in (0, 1):
                    pe.wait_ge(kp_read, 2 * i + s + 1)
                    for ci in (0, 1):
                        mm = nc.tensor.matmul(kp[s][:, 0:W], wk[:, ci, :], xT[:, ci, ds((2 * i + s) * W, W)],
                                              start=ci == 0, stop=ci == 1)
                    mm.then_inc(kp_ready, 1)


def context_stage(k, ctx, tag, xT, kmax, ctx_out):
    nc, I = k.nc, k.ins
    with ExitStack() as c:
        def sb(name, shape, dt=F32):
            return c.enter_context(nc.sbuf_tensor(f"{tag}_{name}", shape, dt))

        def sem(name):
            return c.enter_context(k.semaphore(f"{tag}_{name}"))

        wkv, wo = load_params(k, c, tag, [("wkv", [P, 2, 2 * P], halves(I["L1_mix_W_qkv"])[:, :, P:3 * P]),
                                          ("wo", [P, C], I["L1_mix_W_out"])])
        xs = [sb(f"xs{b}", [P, 2, P]) for b in range(S4)]
        ek = [sb(f"ek{b}", [P, P]) for b in range(S4)]
        v1 = [sb(f"v1{b}", [P, P + 1]) for b in range(S4)]
        maxrow, kmax_wide = sb("maxrow", [P, P]), sb("kmax_wide", [P, P])
        zero = sb("zero", [P, P + 1])
        cs, csT, inv = sb("cs", [P, P]), sb("csT", [P, P]), sb("inv", [P, 1])
        kvp = [c.enter_context(nc.psum_tensor(f"{tag}_kvp{b}", [P, 512], F32)) for b in range(S4)]
        cp = c.enter_context(nc.psum_tensor(f"{tag}_cp", [P, 512], F32))
        mp = c.enter_context(nc.psum_tensor(f"{tag}_mp", [P, 512], F32))
        xs_ready, kvp_ready, shifted, v_ready, ek_ready, summed = map(
            sem, ("xs_ready", "kvp_ready", "shifted", "v_ready", "ek_ready", "summed"))
        begun, row_ready, one, turned, copied, outed = map(
            sem, ("begun", "row_ready", "one", "turned", "copied", "outed"))
        block = c.enter_context(nc.Block())

        @block.gpsimd
        def _(pool):
            pool.sem_inc(kvp_ready, S4)

            def tile(t, b, r):
                pool.wait_ge(kvp_ready, t + 1)
                pool.sem_inc(k.turn, 1)
                nc.gpsimd.tensor_copy(xs[b][:, :, 0:r], xT[:, :, ds(t * P, r)]).then_inc(xs_ready, 1)
            over_fours(pool, tile)

        @block.vector
        def _(dve):
            nc.vector.memset(zero[:], 0.0)
            for b in range(S4):
                nc.vector.memset(v1[b][:, P:P + 1], 1.0)
            nc.vector.tensor_scalar(kmax_wide[:], k.ones[:], kmax[:, 0:1], None, ALU.mult)
            dve.drain().then_inc(begun, 1)
            dve.wait_ge(row_ready, 1)
            nc.vector.tensor_copy(maxrow[:], mp[:, 0:P])
            dve.drain()
            dve.sem_inc(summed, S4)

            def tile(t, b, r):
                dve.wait_ge(kvp_ready, t + 1 + S4)
                dve.wait_ge(summed, t + 1)
                nc.vector.tensor_tensor(ek[b][0:r], kvp[b][0:r, 0:P], maxrow[0:r], ALU.subtract
                                        ).then_inc(shifted, 1)
                nc.vector.tensor_copy(v1[b][0:r, 0:P], kvp[b][0:r, P:2 * P]).then_inc(v_ready, 1)
            over_fours(dve, tile)
            dve.wait_ge(summed, 1 + S4 + REAL_T)
            nc.vector.reciprocal(inv[:], cp[:, P:P + 1])
            dve.drain()
            nc.vector.tensor_scalar(cs[:], cp[:, 0:P], inv[:, 0:1], SCALE, ALU.mult, ALU.mult)
            dve.drain()
            nc.vector.tensor_tensor(cs[:], cs[:], k.block_diag[:], ALU.mult)
            dve.drain().then_inc(one, 1)
            dve.wait_ge(turned, 1)
            nc.vector.tensor_copy(csT[:], mp[:, 0:P]).then_inc(copied, 1)
            dve.wait_ge(outed, 1)
            nc.vector.tensor_copy(ctx_out[:], kvp[0][:, 0:C])

        @block.scalar
        def _(act):
            def tile(t, b, r):
                act.wait_ge(shifted, t + 1)
                nc.scalar.activation(ek[b][0:r], ek[b][0:r], ACT.Exp).then_inc(ek_ready, 1)
            over_fours(act, tile)

        @block.tensor
        def _(pe):
            pe.wait_ge(begun, 1)
            nc.tensor.matmul(mp[:, 0:P], kmax_wide[:], k.ident[:], start=True, stop=True).then_inc(row_ready, 1)
            nc.tensor.matmul(cp[:, 0:P + 1], zero[:, 0:P], zero[:], start=True, stop=False,
                             skip_group_check=True)

            def dense(t, b, r):
                pe.wait_ge(xs_ready, t + 1)
                for half in (0, 1):
                    mm = nc.tensor.matmul(kvp[b][0:r, 0:2 * P], xs[b][:, half, 0:r], wkv[:, half, :],
                                          start=half == 0, stop=half == 1)
                mm.then_inc(kvp_ready, 1)

            def outer(t, b, r):
                pe.wait_ge(v_ready, t + 1)
                pe.wait_ge(ek_ready, t + 1)
                nc.tensor.matmul(cp[:, 0:P + 1], ek[b][0:r, :], v1[b][0:r, :], start=False, stop=False,
                                 skip_group_check=True).then_inc(summed, 1)
            over_fours(pe, dense, outer)
            nc.tensor.matmul(cp[:, 0:P + 1], zero[:, 0:P], zero[:], start=False, stop=True,
                             skip_group_check=True).then_inc(summed, 1)
            pe.wait_ge(one, 1)
            nc.tensor.transpose(mp[:, 0:P], cs[:], k.ident[:]).then_inc(turned, 1)
            pe.wait_ge(copied, 1)
            nc.tensor.matmul(kvp[0][:, 0:C], csT[:], wo[:], start=True, stop=True).then_inc(outed, 1)


def degree_index(k, tables):
    nc = k.nc
    with nc.Block() as block:
        @block.vector
        def _(dve):
            for z_d, count, idx in tables:
                nc.vector.tensor_scalar(idx[:], count[:, 0:NT], float(z_d.shape[0] - 1), None, ALU.min)


def degree_rows_beside(k, c, tag, tables):
    nc = k.nc
    R = 8
    rows = [c.enter_context(nc.sbuf_tensor(f"{tag}_rows{b}", [P, C], F32)) for b in range(R)]
    got = [c.enter_context(k.semaphore(f"{tag}_got{b}")) for b in range(R)]
    out = [c.enter_context(k.semaphore(f"{tag}_out{b}")) for b in range(R)]
    todo = [(z_d, idx, out_d, t) for z_d, idx, out_d in tables for t in range(NT)]

    def program(pool):
        def store(n):
            b = n % R
            _, _, out_d, t = todo[n]
            pool.wait_ge(got[b], 16 * (n // R + 1))
            pool.dma_start(out_d[t * P:(t + 1) * P, :], rows[b][:]).then_inc(out[b], 16)

        for n, (z_d, idx, _, t) in enumerate(todo):
            b = n % R
            if n >= R:
                pool.wait_ge(out[b], 16 * (n // R))
            nc.gpsimd.indirect_dma_start(rows[b][:], None, z_d, bass.IndirectOffsetOnAxis(
                ap=idx[:, t:t + 1], axis=0)).then_inc(got[b], 16)
            if n >= R // 2:
                store(n - R // 2)
        for n in range(len(todo) - R // 2, len(todo)):
            store(n)
        for b in range(R):
            pool.wait_ge(out[b], 16 * len(range(b, len(todo), R)))
    return program


def graph_and_mix_stage(k, ctx, tag, x2_d, xn_d, xT, cw, edge_sum, out_deg, zin_d, zout_d, x3_d, yT_d,
                        h_d, node_h):
    nc, I = k.nc, k.ins
    with ExitStack() as c:
        def sb(name, shape, dt=F32):
            return c.enter_context(nc.sbuf_tensor(f"{tag}_{name}", shape, dt))

        def sem(name):
            return c.enter_context(k.semaphore(f"{tag}_{name}"))

        def col(v):
            return v.rearrange("n a -> (n a)")

        wq, ws, wc, bc, wv, bv, bs, bo, wg, a_src, a_dst = load_params(k, c, tag, [
            ("wq", [P, 2, P], halves(I["L1_mix_W_qkv"])[:, :, 0:P]),
            ("ws", [P, C], I["L1_gnn_W_sum"]),
            ("wc", [P, C], row_on_all(I["L1_gnn_W_cent"].rearrange("a c -> (a c)"))),
            ("bc", [P, C], row_on_all(I["L1_gnn_b_cent"])),
            ("wv", [P, C], row_on_all(I["L1_gnn_W_vor"].rearrange("a c -> (a c)"))),
            ("bv", [P, C], row_on_all(I["L1_gnn_b_vor"])),
            ("bs", [P, C], row_on_all(I["L1_gnn_b_sum"])),
            ("bo", [1, C], I["L1_mix_b_out"].unsqueeze(0)),
            ("wg", [P, 2, HG], halves(I["L1_ffn_W_gat"])),
            ("as", [P, HG], row_on_all(I["L1_ffn_att_src"].rearrange("a b -> (a b)"))),
            ("ad", [P, HG], row_on_all(I["L1_ffn_att_dst"].rearrange("a b -> (a b)")))])

        def slots(name, shape):
            return [sb(f"{name}{b}", shape) for b in range(S4)]

        x2, xn, zi, zo, x3, y, t1 = (slots(n, [P, C]) for n in ("x2", "xn", "zi", "zo", "x3", "y", "t1"))
        cv, cent, prod = slots("cv", [P, 2]), slots("cent", [P, 2, C]), slots("prod", [P, 2, HG])
        es, qT, yT = slots("es", [P, P]), slots("qT", [P, P]), slots("yT", [P, 2, P])
        hrow, st = slots("hrow", [P, ROW + 4]), slots("st", [P, 16])
        qp = [c.enter_context(nc.psum_tensor(f"{tag}_qp{b}", [P, 4, P], F32)) for b in range(S4)]
        sp_ = [c.enter_context(nc.psum_tensor(f"{tag}_sp{b}", [P, 512], F32)) for b in range(S4)]
        loaded, out = ([sem(f"{n}{b}") for b in range(S4)] for n in ("loaded", "out"))
        used, asked, answered, es_ready, qp_ready, qT_ready, sum_ready, cent_ready, sig_ready = map(sem, (
            "used", "asked", "answered", "es_ready", "qp_ready", "qT_ready", "sum_ready", "cent_ready",
            "sig_ready"))
        y_ready, yp_ready, yT_ready, hp_ready, hrow_ready, hrow_used = map(sem, (
            "y_ready", "yp_ready", "yT_ready", "hp_ready", "hrow_ready", "hrow_used"))
        block = c.enter_context(nc.Block())

        @block.sync
        def _(sp):
            sp.sem_inc(used, S4)
            for b in range(S4):
                sp.sem_inc(out[b], 48)

            def load(t, b, r):
                at = ds(t * P, r)
                sp.wait_ge(used, t + 1)
                for dst, src in ((x2, x2_d), (xn, xn_d), (zi, zin_d), (zo, zout_d)):
                    sp.dma_start(dst[b][0:r, :], src[at, :]).then_inc(loaded[b], 16)
                sp.dma_start(cv[b][0:r, 0:1], I["node_vec1_n2"][at, :]).then_inc(loaded[b], 16)
                sp.dma_start(cv[b][0:r, 1:2], I["node_vec1"][at, :]).then_inc(loaded[b], 16)

            def store(t, b, r):
                at = ds(t * P, r)
                sp.wait_ge(hrow_ready, t + 1)
                sp.dma_start(x3_d[at, :], x3[b][0:r, :]).then_inc(out[b], 16)
                sp.dma_start(yT_d[:, :, at], yT[b][:, :, 0:r]).then_inc(out[b], 16)
                sp.dma_start(h_d[at, :], hrow[b][0:r, 0:ROW]).then_inc(out[b], 16)
            over_fours_io(sp, load, store)
            for b in range(S4):
                sp.wait_ge(out[b], 48 * (REAL_T // S4 + 1 + (b == 0)))

        @block.gpsimd
        def _(pool):
            pool.sem_inc(hp_ready, S4)

            def copy(t, b, r):
                pool.wait_ge(hp_ready, t + 1)
                pool.sem_inc(k.turn, 1)
                nc.gpsimd.tensor_copy(es[b][:, 0:r], edge_sum[:, ds(t * P, r)]).then_inc(es_ready, 1)
            over_fours(pool, copy)

        @block.vector
        def _(dve):
            dve.sem_inc(sig_ready, S4)
            nc.vector.memset(node_h[:], 0.0)
            dve.drain()

            def parts(tiles, r):
                for t, b in tiles:
                    dve.wait_ge(loaded[b], times(t, b) * 96)
                    for j, (w_, b_) in enumerate(((wc, bc), (wv, bv))):
                        done = nc.vector.scalar_tensor_tensor(cent[b][0:r, j, :], w_[0:r], cv[b][0:r, j:j + 1],
                                                              b_[0:r], ALU.mult, ALU.add)
                    done.then_inc(cent_ready, 1)
                for _, b in tiles:
                    nc.vector.tensor_tensor(t1[b][0:r], x2[b][0:r], xn[b][0:r], ALU.add)
                dve.drain()
                for z in (zi, zo):
                    for _, b in tiles:
                        nc.vector.tensor_tensor(t1[b][0:r], t1[b][0:r], z[b][0:r], ALU.add)
                    dve.drain()
                for t, b in tiles:
                    nc.vector.scalar_tensor_tensor(t1[b][0:r], bs[0:r], out_deg[0:r, ds(t, 1)], t1[b][0:r],
                                                   ALU.mult, ALU.add)
                dve.drain().then_inc(used, len(tiles))

            def whole(tiles, r):
                for t, b in tiles:
                    dve.wait_ge(sig_ready, t + 1 + S4)
                    nc.vector.tensor_tensor(t1[b][0:r], t1[b][0:r], cent[b][0:r, 0, :], ALU.add)
                dve.drain()
                for _, b in tiles:
                    nc.vector.tensor_tensor(t1[b][0:r], t1[b][0:r], cent[b][0:r, 1, :], ALU.add)
                dve.drain()
                for t, b in tiles:
                    dve.wait_ge(sum_ready, t + 1)
                    dve.wait_ge(out[b], times(t, b) * 48)
                    nc.vector.tensor_tensor(x3[b][0:r], t1[b][0:r], sp_[b][0:r, 0:C], ALU.add)
                dve.drain()
                norm_stats(k, dve, x3, st, tiles, r, asked)

            def norm(tiles, r):
                norm_apply(k, dve, x3, y, st, tiles, r, answered, 0, 1, y_ready)

            def attention(tiles, r):
                for t, b in tiles:
                    dve.wait_ge(hp_ready, t + 1 + S4)
                    h = sp_[b][0:r, 0:HG]
                    nc.vector.tensor_copy(hrow[b][0:r, 0:HG], h)
                    nc.vector.tensor_tensor(prod[b][0:r, 0, :], h, a_src[0:r], ALU.mult)
                    nc.vector.tensor_tensor(prod[b][0:r, 1, :], h, a_dst[0:r], ALU.mult)
                dve.drain()
                for _, b in tiles:
                    nc.vector.tensor_reduce(hrow[b][0:r, HG:HG + 8].rearrange("p (a h) -> p a h", a=2),
                                            prod[b][0:r].rearrange("p a (h e) -> p a h e", e=4), AX_X, ALU.add)
                dve.drain()
                for t, b in tiles:
                    nc.vector.tensor_copy(node_h[0:r, ds(t, 1), :], hrow[b][0:r, :])
                dve.drain().then_inc(hrow_ready, len(tiles))
                dve.sem_inc(hrow_used, len(tiles))
            over_fours_at_once(dve, parts, whole, norm, attention)

        @block.scalar
        def _(act):
            def sigmoid(t, b, r):
                act.wait_ge(cent_ready, t + 1)
                nc.scalar.activation(cent[b][0:r], cent[b][0:r], ACT.Sigmoid).then_inc(sig_ready, 1)

            def copy_q(t, b, r):
                act.wait_ge(qp_ready, t + 1)
                nc.scalar.copy(qT[b][:, 0:r], qp[b][:, 0, 0:r]).then_inc(qT_ready, 1)

            def roots(t, b, r):
                root(k, act, st[b], r, asked, answered, t + 1)

            def copy_y(t, b, r):
                act.wait_ge(yp_ready, t + 1)
                nc.scalar.copy(yT[b][:, :, 0:r], qp[b][:, 2:4, 0:r]).then_inc(yT_ready, 1)
            over_fours(act, copy_q, sigmoid, roots, copy_y)

        @block.tensor
        def _(pe):
            pe.sem_inc(hrow_used, S4)

            def query(t, b, r):
                for half in (0, 1):
                    mm = nc.tensor.matmul(qp[b][:, 0, 0:r], wq[:, half, :], xT[:, half, ds(t * P, r)],
                                          start=half == 0, stop=half == 1)
                mm.then_inc(qp_ready, 1)

            def total(t, b, r):
                pe.wait_ge(es_ready, t + 1)
                pe.wait_ge(qT_ready, t + 1)
                pe.wait_ge(hrow_used, t + 1)
                nc.tensor.matmul(sp_[b][0:r, 0:C], k.ones[0:1, 0:r], bo[:], start=True, stop=False)
                nc.tensor.matmul(sp_[b][0:r, 0:C], es[b][:, 0:r], ws[:], start=False, stop=False)
                nc.tensor.matmul(sp_[b][0:r, 0:C], qT[b][:, 0:r], cw[:], start=False, stop=True
                                 ).then_inc(sum_ready, 1)

            def turn(t, b, r):
                pe.wait_ge(y_ready, t + 1)
                for half in (0, 1):
                    mm = nc.tensor.transpose(qp[b][:, 2 + half, 0:r], y[b][0:r, half * P:(half + 1) * P],
                                             k.ident[0:r, 0:r])
                mm.then_inc(yp_ready, 1)

            def project(t, b, r):
                pe.wait_ge(yT_ready, t + 1)
                for half in (0, 1):
                    mm = nc.tensor.matmul(sp_[b][0:r, 0:HG], yT[b][:, half, 0:r], wg[:, half, :],
                                          start=half == 0, stop=half == 1)
                mm.then_inc(hp_ready, 1)
            over_fours(pe, query, total, turn, project)


J = G // P
LOW = -1.0e38


def carry_in(k, ctx, tag, last, factor, K, op0, op1, init):
    nc = k.nc
    cin = ctx.enter_context(nc.sbuf_tensor(f"{tag}_cin", [P, K], F32))
    with ExitStack() as c:
        rows = [c.enter_context(nc.sbuf_tensor(f"{tag}_row{n}", [K, P], F32)) for n in (0, 1)]
        state = c.enter_context(nc.sbuf_tensor(f"{tag}_state", [K, P + 1], F32))
        turned = [c.enter_context(nc.psum_tensor(f"{tag}_turn{n}", [P, 512], F32)) for n in range(3)]
        there, scanned, back = [c.enter_context(k.semaphore(f"{tag}_{n}")) for n in ("there", "scanned", "back")]
        block = c.enter_context(nc.Block())

        @block.tensor
        def _(pe):
            nc.tensor.transpose(turned[0][0:K, 0:P], last[:], k.ident[:])
            nc.tensor.transpose(turned[1][0:K, 0:P], factor[:], k.ident[:]).then_inc(there, 1)
            pe.wait_ge(scanned, 1)
            nc.tensor.transpose(turned[2][:, 0:K], state[:, 0:P], k.ident[0:K, 0:K]).then_inc(back, 1)

        @block.vector
        def _(dve):
            nc.vector.memset(state[:, 0:1], init)
            dve.wait_ge(there, 1)
            for n in (0, 1):
                nc.vector.tensor_copy(rows[n][:], turned[n][0:K, 0:P])
            dve.drain()
            nc.vector.tensor_tensor_scan(state[:, 1:P + 1], rows[1][:], rows[0][:], init, op0, op1)
            dve.drain().then_inc(scanned, 1)
            dve.wait_ge(back, 1)
            nc.vector.tensor_copy(cin[:], turned[2][:, 0:K])
    return cin


def node_targets(k, ctx, tag, start, count):
    nc = k.nc
    first = ctx.enter_context(nc.sbuf_tensor(f"{tag}_first_i", [P, NT], I32))
    last = ctx.enter_context(nc.sbuf_tensor(f"{tag}_last_i", [P, NT], I32))
    some = ctx.enter_context(nc.sbuf_tensor(f"{tag}_some", [P, NT], F32))
    with (nc.sbuf_tensor(f"{tag}_spare", [P, 1], F32) as spare,
          nc.sbuf_tensor(f"{tag}_a", [P, NT], F32) as a,
          nc.sbuf_tensor(f"{tag}_b", [P, NT], F32) as b,
          nc.Block() as block):
        @block.vector
        def _(dve):
            s, n = start[:, 0:NT], count[:, 0:NT]
            nc.vector.tensor_scalar(some[:], n, 0.0, None, ALU.is_gt)
            nc.vector.tensor_scalar(spare[:], k.lane[:], float(G), None, ALU.add)
            nc.vector.tensor_tensor(b[:], s, n, ALU.add)
            dve.drain()
            nc.vector.tensor_scalar(last[:], b[:], -1.0, 0.0, ALU.add, ALU.max)
            nc.vector.tensor_scalar(a[:], s, spare[:, 0:1], None, ALU.subtract)
            dve.drain()
            nc.vector.tensor_tensor(a[:], a[:], some[:], ALU.mult)
            dve.drain()
            nc.vector.tensor_scalar(first[:], a[:], spare[:, 0:1], None, ALU.add)
    return first, last, some


def spread_to_starts(k, tag, node_h, first_i, adst_d):
    nc = k.nc
    with ExitStack() as c:
        zero = c.enter_context(nc.sbuf_tensor(f"{tag}_zero", [P, J * 4], F32))
        rows = c.enter_context(nc.sbuf_tensor(f"{tag}_rows", [P, NT, 4], F32))
        made, cleared, done = [c.enter_context(k.semaphore(f"{tag}_{n}")) for n in ("made", "cleared", "done")]
        block = c.enter_context(nc.Block())

        @block.vector
        def _(dve):
            nc.vector.memset(zero[:], 0.0)
            nc.vector.tensor_copy(rows[:], node_h[:, :, ROW:ROW + 4])
            dve.drain().then_inc(made, 1)

        @block.sync
        def _(sp):
            sp.wait_ge(made, 1)
            sp.dma_start(adst_d[0:G, :].rearrange("(p j) h -> p (j h)", p=P), zero[:]).then_inc(cleared, 16)

        @block.gpsimd
        def _(pool):
            pool.wait_ge(cleared, 16)
            for t in range(NT):
                nc.gpsimd.indirect_dma_start(adst_d, bass.IndirectOffsetOnAxis(ap=first_i[:, t:t + 1], axis=0),
                                             rows[:, t, :], None).then_inc(done, 16)
            pool.wait_ge(done, 16 * NT)


def sorted_lists(k, tag, sorted_d, idx_all, same):
    nc = k.nc
    with (nc.sbuf_tensor(f"{tag}_cur", [P, J, 2], F32) as cur,
          nc.sbuf_tensor(f"{tag}_prev", [P, J, 2], F32) as prev,
          k.semaphore(f"{tag}_lists_in") as lists_in, nc.Block() as block):
        @block.sync
        def _(sp):
            for tile, at in ((cur, 1), (prev, 0)):
                sp.dma_start(tile[:], sorted_d[at:at + G, :].rearrange("(p j) w -> p j w", p=P)
                             ).then_inc(lists_in, 16)

        @block.vector
        def _(dve):
            dve.wait_ge(lists_in, 32)
            nc.vector.tensor_copy(idx_all[:], cur[:, :, 0])
            nc.vector.tensor_tensor(same[:], cur[:, :, 1], prev[:, :, 1], ALU.is_equal)


def gather_beside(k, c, tag, table, idx_all, edge):
    nc = k.nc
    R = 16
    pairs = J // (2 * R)
    idx = [c.enter_context(nc.sbuf_tensor(f"{tag}_idx{h}", [P, R], I32)) for h in (0, 1)]
    got = [c.enter_context(nc.sbuf_tensor(f"{tag}_got{h}", [P, R, ROW], F32)) for h in (0, 1)]
    gathered = [c.enter_context(k.semaphore(f"{tag}_gathered{h}")) for h in (0, 1)]
    moved, idx_ready = (c.enter_context(k.semaphore(f"{tag}_{n}")) for n in ("moved", "idx_ready"))

    def program(pool):
        def ask(n, h):
            nc.gpsimd.tensor_copy(idx[h][:], idx_all[:, ds(n * R, R)]).then_inc(idx_ready, 1)
            pool.wait_ge(idx_ready, n + 1)
            pool.sem_inc(k.turn, 1)
            for b in range(R):
                nc.gpsimd.indirect_dma_start(got[h][:, b, :], None, table, bass.IndirectOffsetOnAxis(
                    ap=idx[h][:, b:b + 1], axis=0)).then_inc(gathered[h], 16)

        def move(n, h, nth):
            pool.wait_ge(gathered[h], nth * (16 * R))
            pool.sem_inc(k.turn, 1)
            nc.gpsimd.tensor_copy(edge[:, ds(n * R, R), :], got[h][:]).then_inc(moved, 1)
            pool.wait_ge(moved, n + 1)
            pool.sem_inc(k.turn, 1)

        ask(0, 0)
        ask(1, 1)
        with pool.Fori(1, pairs) as i:
            for h in (0, 1):
                move(2 * i + h - 2, h, i)
                ask(2 * i + h, h)
        for h in (0, 1):
            move(2 * pairs - 2 + h, h, pairs)
    return program


def leaky(nc, out, x):
    nc.vector.scalar_tensor_tensor(out, x, 0.2, x, ALU.mult, ALU.max)


def edge_softmax(k, tag, edge, same, adst_d, seg_d, segm_d):
    nc = k.nc
    with ExitStack() as c:
        def sb(name, shape, dt=F32):
            return c.enter_context(nc.sbuf_tensor(f"{tag}_{name}", shape, dt))

        a_dst, top = sb("a_dst", [P, J, 4]), sb("top", [P, J, 4])
        pen, junk = sb("pen", [P, J]), sb("junk", [P, J])
        all_same, all_pen = sb("all_same", [P, 4]), sb("all_pen", [P, 4])
        last4, last20 = sb("last4", [P, 4]), sb("last20", [P, ROW])
        a_src = edge[:, :, HG:ROW]
        same4 = same[:].unsqueeze(2).broadcast_to([P, J, 4])

        with k.semaphore(f"{tag}_a_in") as a_in, nc.Block() as block:
            @block.sync
            def _(sp):
                sp.dma_start(a_dst[:], adst_d[0:G, :].rearrange("(p j) h -> p j h", p=P)).then_inc(a_in, 16)

            @block.vector
            def _(dve):
                nc.vector.tensor_reduce(all_same[:, 0:1], same[:], AX_X, ALU.min)
                nc.vector.tensor_scalar(pen[:], same[:], -1.0, -LOW, ALU.add, ALU.mult)
                dve.drain()
                for h in (1, 2, 3):
                    nc.vector.tensor_copy(all_same[:, h:h + 1], all_same[:, 0:1])
                dve.drain()
                nc.vector.tensor_scalar(all_pen[:], all_same[:], -1.0, -LOW, ALU.add, ALU.mult)
                dve.wait_ge(a_in, 16)
                for h in range(4):
                    nc.vector.tensor_tensor_scan(junk[:], same[:], a_dst[:, :, h], 0.0, ALU.mult, ALU.add)
                    dve.drain()
                    nc.vector.tensor_copy(last4[:, h:h + 1], junk[:, J - 1:J])
                    dve.drain()
        fill_in = carry_in(k, c, f"{tag}_c1", last4, all_same, 4, ALU.mult, ALU.add, 0.0)

        with nc.Block() as block:
            @block.vector
            def _(dve):
                for h in range(4):
                    nc.vector.tensor_tensor_scan(a_dst[:, :, h], same[:], a_dst[:, :, h],
                                                 fill_in[:, h:h + 1], ALU.mult, ALU.add)
                    nc.vector.tensor_tensor_scan(junk[:], pen[:], a_src[:, :, h], LOW, ALU.add, ALU.max)
                    dve.drain()
                    nc.vector.tensor_copy(last4[:, h:h + 1], junk[:, J - 1:J])
                    dve.drain()
        top_in = carry_in(k, c, f"{tag}_c2", last4, all_pen, 4, ALU.add, ALU.max, LOW)

        decay = a_dst
        before0, factor = sb("before0", [P, 4]), sb("factor", [P, ROW])
        with k.semaphore(f"{tag}_asked") as asked, k.semaphore(f"{tag}_answered") as answered, \
                nc.Block() as block:
            @block.vector
            def _(dve):
                for h in range(4):
                    nc.vector.tensor_tensor_scan(top[:, :, h], pen[:], a_src[:, :, h], top_in[:, h:h + 1],
                                                 ALU.add, ALU.max)
                dve.drain()
                nc.vector.tensor_tensor(top[:], top[:], a_dst[:], ALU.add)
                nc.vector.tensor_tensor(a_src, a_src, a_dst[:], ALU.add)
                nc.vector.tensor_tensor(before0[:], top_in[:], a_dst[:, 0, :], ALU.add)
                dve.drain()
                leaky(nc, top[:], top[:])
                leaky(nc, a_src, a_src)
                leaky(nc, before0[:], before0[:])
                dve.drain()
                nc.vector.tensor_tensor(a_src, a_src, top[:], ALU.subtract).then_inc(asked, 1)
                nc.vector.tensor_tensor(decay[:, 1:J, :], top[:, 0:J - 1, :], top[:, 1:J, :], ALU.subtract)
                nc.vector.tensor_tensor(decay[:, 0, :], before0[:], top[:, 0, :], ALU.subtract)
                nc.vector.tensor_tensor(factor[:, 0:4], before0[:], top[:, J - 1, :], ALU.subtract)
                dve.drain()
                nc.vector.tensor_scalar(decay[:], decay[:], 0.0, None, ALU.min).then_inc(asked, 1)
                nc.vector.tensor_scalar(factor[:, 0:4], factor[:, 0:4], 0.0, None, ALU.min).then_inc(asked, 1)
                dve.wait_ge(answered, 3)
                nc.vector.tensor_tensor(decay[:], decay[:], same4, ALU.mult)
                nc.vector.tensor_tensor(factor[:, HG:ROW], factor[:, 0:4], all_same[:], ALU.mult)
                h16 = edge[:, :, 0:HG].rearrange("p j (h e) -> p j h e", e=4)
                for h in range(4):
                    nc.vector.tensor_tensor(h16[:, :, h, :], h16[:, :, h, :],
                                            a_src[:, :, h].unsqueeze(2).broadcast_to([P, J, 4]), ALU.mult)
                dve.drain()
                for h in range(4):
                    nc.vector.tensor_scalar(factor[:, 4 * h:4 * h + 4], k.ones[:, 0:4],
                                            factor[:, HG + h:HG + h + 1], None, ALU.mult)
                for f in range(ROW):
                    h = f // 4 if f < HG else f - HG
                    nc.vector.tensor_tensor_scan(junk[:], decay[:, :, h], edge[:, :, f], 0.0, ALU.mult, ALU.add)
                    dve.drain()
                    nc.vector.tensor_copy(last20[:, f:f + 1], junk[:, J - 1:J])
                    dve.drain()

            @block.scalar
            def _(act):
                for n, x in enumerate((a_src, decay[:], factor[:, 0:4])):
                    act.wait_ge(asked, n + 1)
                    nc.scalar.activation(x, x, ACT.Exp).then_inc(answered, 1)
        sum_in = carry_in(k, c, f"{tag}_c3", last20, factor, ROW, ALU.mult, ALU.add, 0.0)

        with k.semaphore(f"{tag}_ran") as ran, k.semaphore(f"{tag}_stored") as stored, nc.Block() as block:
            @block.vector
            def _(dve):
                for f in range(ROW):
                    h = f // 4 if f < HG else f - HG
                    nc.vector.tensor_tensor_scan(edge[:, :, f], decay[:, :, h], edge[:, :, f],
                                                 sum_in[:, f:f + 1], ALU.mult, ALU.add)
                dve.drain().then_inc(ran, 1)

            @block.sync
            def _(sp):
                sp.dma_start(segm_d.rearrange("(p j) w -> p j w", p=P), top[:]).then_inc(stored, 16)
                sp.wait_ge(ran, 1)
                sp.dma_start(seg_d.rearrange("(p j) w -> p j w", p=P), edge[:]).then_inc(stored, 16)
                sp.wait_ge(stored, 32)


def node_gates(k, tag, node_h, last_i, some, seg_d, segm_d, gates):
    nc, I = k.nc, k.ins
    with ExitStack() as c:
        def sb(name, shape, dt=F32):
            return c.enter_context(nc.sbuf_tensor(f"{tag}_{name}", shape, dt))

        b_gat, gamma, beta = load_params(k, c, tag, [
            ("bg", [P, HG], row_on_all(I["L1_ffn_b_gat"])), ("gamma", [P, HG], row_on_all(I["L1_ffn_ln_gamma"])),
            ("beta", [P, HG], row_on_all(I["L1_ffn_ln_beta"]))])
        sums, top = sb("sums", [P, NT, ROW]), sb("top", [P, NT, 4])
        loop, best, c1, c2 = (sb(n, [P, NT, 4]) for n in ("loop", "best", "c1", "c2"))
        agg, tmp = sb("agg", [P, NT, HG]), sb("tmp", [P, NT, HG])
        den, mean, var, gone = sb("den", [P, NT, 4]), sb("mean", [P, NT]), sb("var", [P, NT]), sb("gone", [P, NT])
        score = sb("score", [P, NT, 4])
        bufs = gate_buffers(k, c, tag, 4)
        got = c.enter_context(k.semaphore(f"{tag}_got"))
        asked = c.enter_context(k.semaphore(f"{tag}_asked"))
        answered = c.enter_context(k.semaphore(f"{tag}_answered"))
        block = c.enter_context(nc.Block())

        def wide(a, n):
            return a.unsqueeze(2).broadcast_to([P, NT, n])

        def by_head(a):
            return a.unsqueeze(3).broadcast_to([P, NT, 4, 4])

        def h4(a):
            return a.rearrange("p t (h e) -> p t h e", e=4)

        def param(v):
            return v[:].unsqueeze(1).broadcast_to([P, NT, HG])

        @block.gpsimd
        def _(pool):
            for t in range(NT):
                at = bass.IndirectOffsetOnAxis(ap=last_i[:, t:t + 1], axis=0)
                nc.gpsimd.indirect_dma_start(sums[:, t, :], None, seg_d, at).then_inc(got, 16)
                at = bass.IndirectOffsetOnAxis(ap=last_i[:, t:t + 1], axis=0)
                nc.gpsimd.indirect_dma_start(top[:, t, :], None, segm_d, at).then_inc(got, 16)

        @block.scalar
        def _(act):
            act.wait_ge(asked, 1)
            nc.scalar.activation(c1[:], c1[:], ACT.Exp)
            nc.scalar.activation(c2[:], c2[:], ACT.Exp)
            act.drain().then_inc(answered, 1)
            act.wait_ge(asked, 2)
            nc.scalar.activation(var[:], var[:], ACT.Sqrt, bias=k.eps[:, 0:1], scale=1.0 / HG).then_inc(answered, 1)
            act.wait_ge(asked, 3)
            nc.scalar.activation(bufs[5][:], bufs[5][:], ACT.Exp).then_inc(answered, 1)

        @block.vector
        def _(dve):
            def then(ins):
                dve.drain()

            h = node_h[:, :, 0:HG]
            then(nc.vector.tensor_tensor(loop[:], node_h[:, :, HG:ROW], node_h[:, :, ROW:ROW + 4], ALU.add))
            then(leaky(nc, loop[:], loop[:]))
            then(nc.vector.tensor_scalar(gone[:], some[:], -1.0, -LOW, ALU.add, ALU.mult))
            dve.wait_ge(got, 32 * NT)
            then(nc.vector.tensor_tensor(top[:], top[:], wide(some[:], 4), ALU.mult))
            then(nc.vector.tensor_tensor(top[:], top[:], wide(gone[:], 4), ALU.add))
            then(nc.vector.tensor_tensor(best[:], top[:], loop[:], ALU.max))
            nc.vector.tensor_tensor(c1[:], top[:], best[:], ALU.subtract)
            nc.vector.tensor_tensor(c2[:], loop[:], best[:], ALU.subtract)
            dve.drain().then_inc(asked, 1)
            dve.wait_ge(answered, 1)
            then(nc.vector.tensor_tensor(den[:], sums[:, :, HG:ROW], c1[:], ALU.mult))
            then(nc.vector.tensor_tensor(den[:], den[:], c2[:], ALU.add))
            then(nc.vector.tensor_scalar(den[:], den[:], 1e-16, None, ALU.add))
            then(nc.vector.reciprocal(best[:], den[:]))
            nc.vector.tensor_tensor(c1[:], c1[:], best[:], ALU.mult)
            then(nc.vector.tensor_tensor(c2[:], c2[:], best[:], ALU.mult))
            nc.vector.tensor_tensor(h4(agg[:]), h4(sums[:, :, 0:HG]), by_head(c1[:]), ALU.mult)
            then(nc.vector.tensor_tensor(h4(tmp[:]), h4(h), by_head(c2[:]), ALU.mult))
            then(nc.vector.tensor_tensor(agg[:], agg[:], tmp[:], ALU.add))
            then(nc.vector.tensor_tensor(agg[:], agg[:], param(b_gat), ALU.add))
            then(nc.vector.tensor_reduce(mean[:], agg[:], AX_X, ALU.add))
            then(nc.vector.tensor_scalar(mean[:], mean[:], 1.0 / HG, None, ALU.mult))
            then(nc.vector.tensor_tensor(agg[:], agg[:], wide(mean[:], HG), ALU.subtract))
            then(nc.vector.tensor_tensor(tmp[:], agg[:], agg[:], ALU.mult))
            nc.vector.tensor_reduce(var[:], tmp[:], AX_X, ALU.add).then_inc(asked, 1)
            dve.wait_ge(answered, 2)
            then(nc.vector.reciprocal(mean[:], var[:]))
            then(nc.vector.tensor_tensor(agg[:], agg[:], wide(mean[:], HG), ALU.mult))
            then(nc.vector.tensor_tensor(agg[:], agg[:], param(gamma), ALU.mult))
            then(nc.vector.tensor_tensor(agg[:], agg[:], param(beta), ALU.add))
            then(nc.vector.tensor_reduce(score[:], agg[:].rearrange("p t (h e) -> p t e h", e=4), AX_X, ALU.add))
            then(nc.vector.tensor_scalar(score[:], score[:], 0.25, None, ALU.mult))
            top_two(k, dve, score, gates, 4, asked, answered, 3, bufs)


NAMES = ['x', 'src', 'dst', 'edge_attr_128', 'edge_weight', 'node_vec1', 'node_vec1_n2', 'L0_gnn_c1_w1',
         'L0_gnn_c1_b1', 'L0_gnn_c1_w2', 'L0_gnn_c1_b2', 'L0_gnn_c1_g', 'L0_gnn_c1_b', 'L0_gnn_bn1_g',
         'L0_gnn_bn1_b', 'L0_gnn_c2_w1', 'L0_gnn_c2_b1', 'L0_gnn_c2_w2', 'L0_gnn_c2_b2', 'L0_gnn_c2_g',
         'L0_gnn_c2_b', 'L0_gnn_bn2_g', 'L0_gnn_bn2_b', 'L0_mix_kln_weight', 'L0_mix_kln_bias',
         'L0_mix_vln_weight', 'L0_mix_vln_bias', 'L0_ffn_gamma', 'L0_ffn_beta', 'L0_ffn_Wr', 'L0_ffn_br',
         'L0_ffn_W1', 'L0_ffn_b1', 'L0_ffn_W2', 'L0_ffn_b2', 'L1_gnn_z_in', 'L1_gnn_z_out', 'L1_gnn_W_cent',
         'L1_gnn_b_cent', 'L1_gnn_W_vor', 'L1_gnn_b_vor', 'L1_gnn_W_sum', 'L1_gnn_b_sum', 'L1_mix_W_qkv',
         'L1_mix_W_out', 'L1_mix_b_out', 'L1_ffn_W_gat', 'L1_ffn_att_src', 'L1_ffn_att_dst', 'L1_ffn_b_gat',
         'L1_ffn_ln_gamma', 'L1_ffn_ln_beta', 'L1_ffn_W1', 'L1_ffn_b1', 'L1_ffn_W2', 'L1_ffn_b2',
         'L1_ffn_edge_index']


def load_attributes(k, rest_in):
    attr = k.ins["edge_attr_128"]
    Q = 8

    def fill(sp, pay, n, last, sem, turn):
        full, rest = Q, 0
        if last:
            full, rest = divmod(E - n * Q * P, P)
            if full >= Q:
                full, rest = Q, 0
            if rest:
                sp.dma_start(pay[0:rest, full, 0:P], attr[E - rest:E, :]).then_inc(rest_in, 16)
                sp.wait_ge(rest_in, 16)
        sp.dma_start(pay[:, 0:full, 0:P], attr[ds(n * Q * P, full * P), :].rearrange("(b p) f -> p b f", p=P)
                     ).then_inc(sem, 16)
    return fill


def first_node_columns(k, tag, first_row_d, out):
    nc = k.nc
    with (nc.sbuf_tensor(f"{tag}_fi", [P, NSB * P], I32) as raw,
          k.semaphore(f"{tag}_fin") as landed, nc.Block() as block):
        @block.sync
        def _(sp):
            sp.dma_start(raw[:], row_on_all(first_row_d)).then_inc(landed, 16)

        @block.vector
        def _(dve):
            dve.wait_ge(landed, 16)
            nc.vector.tensor_copy(out[:], raw[:])


def build(nc, ins, out):
    k = Kernel(nc, ins, out)
    I = ins
    h_d = k.dram("h_d", (N, C))
    x1_d, x2_d, x3_d, xn_d = (k.dram(n, (N, C)) for n in ("x1_d", "x2_d", "x3_d", "xn_d"))
    yT_d, y2T_d = k.dram("yT_d", (P, 2, NP)), k.dram("y2T_d", (P, 2, NP))
    zin_d, zout_d = k.dram("zin_d", (NP, C)), k.dram("zout_d", (NP, C))
    attr_sorted_d = k.dram("attr_sorted_d", (EP, P + 1))
    gat_sorted_d = k.dram("gat_sorted_d", (G + 1, 2))
    gat_rows_d = k.dram("gat_rows_d", (N, ROW))
    experts_d = k.dram("experts_d", (N, 4, C))
    adst_d, seg_d, segm_d = k.dram("adst_d", (G + P, 4)), k.dram("seg_d", (G, ROW)), k.dram("segm_d", (G, 4))

    with ExitStack() as top:
        def keep(name, shape, dt=F32):
            return top.enter_context(nc.sbuf_tensor(name, shape, dt))

        k.turn = top.enter_context(k.semaphore("turn"))
        rest_in = top.enter_context(k.semaphore("rest_in"))
        constants(k, top)
        in_deg, in_start, in_tiles = (keep(f"dst_{n}", [P, NHI]) for n in ("count", "start", "tiles"))
        out_deg, out_start, out_tiles = (keep(f"src_{n}", [P, NHI]) for n in ("count", "start", "tiles"))
        gat_count, gat_start, gat_tiles = (keep(f"gat_{n}", [P, NHI]) for n in ("count", "start", "tiles"))
        gates8, gates4 = keep("gates8", [P, NT, 8]), keep("gates4", [P, NT, 4])

        node_h = keep("node_h", [P, NT, ROW + 4])

        with ExitStack() as c:
            sum_first_row = c.enter_context(nc.sbuf_tensor("sum_first_row", [1, NSB * P], I32))
            sum_chunk_row = c.enter_context(nc.sbuf_tensor("sum_chunk_row", [1, NSB * P], I32))
            with ExitStack() as c1:
                g_rows, g_low, (gsrc, gdst) = edge_keys(k, c1, "g", CG, G, [
                    ("src", I["L1_ffn_edge_index"][0]), ("dst", I["L1_ffn_edge_index"][1])],
                    [N - 1, N], [0, 0], 1)
                g_lo, g_hi = digits(k, c1, "gd", gdst, CG)
                histogram(k, "gd", g_lo, g_hi, CG, gat_count)
                prefix(k, "gd", gat_count, gat_start, gat_tiles)
                shifted = c1.enter_context(nc.sbuf_tensor("gat_shifted", [P, NHI], F32))
                with ExitStack() as c2:
                    first = c2.enter_context(nc.sbuf_tensor("gat_first_row", [1, 2], F32))
                    with k.semaphore("gat_minus") as made, k.semaphore("gat_zeroth") as stored, nc.Block() as block:
                        @block.vector
                        def _(dve):
                            nc.vector.tensor_scalar(shifted[:], gat_start[:], 1.0, None, ALU.add)
                            nc.vector.memset(first[:], -1.0).then_inc(made, 1)

                        @block.sync
                        def _(sp):
                            sp.wait_ge(made, 1)
                            sp.dma_start(gat_sorted_d[0:1, :], first[:]).then_inc(stored, 16)
                            sp.wait_ge(stored, 16)

                with ExitStack() as c1e:
                    conv_tile_row = c1e.enter_context(nc.sbuf_tensor("conv_tile_row", [1, NSB * P], I32))
                    src_i = c1e.enter_context(nc.sbuf_tensor("conv_src", [P, NSB * P], I32))
                    rel = c1e.enter_context(nc.sbuf_tensor("conv_rel", [P, NSB * P], F32))
                    weight = c1e.enter_context(nc.sbuf_tensor("conv_weight", [P, NSB * P], F32))
                    with ExitStack() as c2:
                        rows, low, (esrc, edst, _) = edge_keys(k, c2, "e", CE, E, [
                            ("src", I["src"]), ("dst", I["dst"]), ("weight", I["edge_weight"])],
                            [None] * 3, [PAD_KEY, PAD_KEY, 0.0], 0)
                        dlo, dhi = digits(k, c2, "ed", edst, CE)
                        histogram(k, "ed", dlo, dhi, CE, in_deg)
                        slo, shi = digits(k, c2, "es", esrc, CE)
                        histogram(k, "es", slo, shi, CE, out_deg)
                        prefix(k, "ed", in_deg, in_start, in_tiles)
                        prefix(k, "es", out_deg, out_start, out_tiles)
                        tile, chunk = schedule(k, c2, "ed", in_tiles)
                        step_columns(k, "ed", rows, tile, chunk, src_i, rel, weight)
                        step_registers(k, "ed_tile", tile, conv_tile_row)
                        tile, chunk = schedule(k, c2, "es", out_tiles)
                        step_registers(k, "es_first", tile, sum_first_row, P)
                        step_registers(k, "es_chunk", chunk, sum_chunk_row)
                        sort_edges(k, c2, "ss", CE, esrc, slo, shi, out_start, rows[:, 0, :], low, [(P, esrc)],
                                   P + 1, load_attributes(k, rest_in), attr_sorted_d)

                    with ExitStack() as c2:
                        kv = c2.enter_context(nc.sbuf_tensor("kv", [P, 2, P], F32))
                        acc = c2.enter_context(nc.sbuf_tensor("acc", [P, 2, NP], F32))
                        input_stage(k, c2, "in", h_d, kv)
                        aggregate(k, "a1", h_d, src_i, rel, weight, conv_tile_row, acc)
                        dense_and_norms(k, c2, "n1", acc, "L0_gnn_c1_w2", "L0_gnn_c1_b2", [
                            ("L0_gnn_c1_g", "L0_gnn_c1_b", True), ("L0_gnn_bn1_g", "L0_gnn_bn1_b", True)])
                        rows_from_channels(k, c2, "rc", acc, h_d, "L0_gnn_c2_w1", "L0_gnn_c2_b1")
                        aggregate(k, "a2", h_d, src_i, rel, weight, conv_tile_row, acc)
                        dense_and_norms(k, c2, "n2", acc, "L0_gnn_c2_w2", "L0_gnn_c2_b2", [
                            ("L0_gnn_c2_g", "L0_gnn_c2_b", True), ("L0_gnn_bn2_g", "L0_gnn_bn2_b", False)])
                        mix_and_gate_stage(k, c2, "mg", acc, kv, x1_d, yT_d, gates8)
                with ExitStack() as c2:
                    in_i, out_i = (c2.enter_context(nc.sbuf_tensor(n, [P, NT], I32)) for n in ("in_row", "out_row"))
                    z_in, z_out = I["L1_gnn_z_in"], I["L1_gnn_z_out"]
                    degree_index(k, [(z_in, in_deg, in_i), (z_out, out_deg, out_i)])
                    degrees = degree_rows_beside(k, c2, "dr", [(z_in, in_i, zin_d), (z_out, out_i, zout_d)])
                    ranks = RanksBeside(k, c2, "gs", CG, gdst, g_lo, g_hi, shifted, g_rows[:, 1, :], g_low,
                                        (gsrc, gdst), gat_sorted_d)
                    expert_stage(k, c2, "e0", 8, yT_d, x1_d, x2_d, gates8, "L0_ffn_W1", "L0_ffn_b1",
                                 "L0_ffn_W2", "L0_ffn_b2", ranks, degrees)

            edge_sum = c.enter_context(nc.sbuf_tensor("edge_sum", [P, NP], F32))
            with ExitStack() as c2:
                first_all = c2.enter_context(nc.sbuf_tensor("first_all", [P, NSB * P], F32))
                first_node_columns(k, "fa", k.buffers["es_first_row_d"], first_all)
                segment_sum(k, "sm", attr_sorted_d, P, sum_chunk_row, first_all, sum_first_row, edge_sum)
            with ExitStack() as c2:
                xT = c2.enter_context(nc.sbuf_tensor("xT", [P, 2, NP], F32))
                kmax = c2.enter_context(nc.sbuf_tensor("kmax", [P, 1], F32))
                cw = c2.enter_context(nc.sbuf_tensor("cw", [P, C], F32))
                channels_stage(k, c2, "cs", x2_d, xn_d, xT, kmax)
                context_stage(k, c2, "cx", xT, kmax, cw)
                graph_and_mix_stage(k, c2, "gm", x2_d, xn_d, xT, cw, edge_sum, out_deg, zin_d, zout_d,
                                    x3_d, y2T_d, gat_rows_d, node_h)

        with ExitStack() as c:
            first_i, last_i, some = node_targets(k, c, "nt", gat_start, gat_count)
            spread_to_starts(k, "sp", node_h, first_i, adst_d)
            with ExitStack() as c2:
                edge = c2.enter_context(nc.sbuf_tensor("edge", [P, J, ROW], F32))
                same = c2.enter_context(nc.sbuf_tensor("same", [P, J], F32))
                with ExitStack() as c3:
                    idx_all = c3.enter_context(nc.sbuf_tensor("gat_idx", [P, J], I32))
                    sorted_lists(k, "sl", gat_sorted_d, idx_all, same)
                    gather = gather_beside(k, c3, "ge", gat_rows_d, idx_all, edge)
                    expert_outputs(k, c3, "e1", 4, y2T_d, experts_d, "L1_ffn_W1", "L1_ffn_b1", "L1_ffn_W2",
                                   "L1_ffn_b2", gather)
                edge_softmax(k, "ex", edge, same, adst_d, seg_d, segm_d)
            node_gates(k, "ng", node_h, last_i, some, seg_d, segm_d, gates4)
            combine_stage(k, c, "cb", 4, experts_d, x3_d, out, gates4)


def kernel(**inputs):
    import concourse.bacc as bacc
    from concourse.bass_utils import run_bass_kernel_spmd

    nc = bacc.Bacc("TRN2", target_bir_lowering=False, num_devices=1)
    arrays, ins = {}, {}
    for name in NAMES:
        a = np.ascontiguousarray(inputs[name])
        arrays[f"in_{name}"] = a
        ins[name] = nc.dram_tensor(f"in_{name}", a.shape, mybir.dt.from_np(a.dtype), kind="ExternalInput").ap()
    out = nc.dram_tensor("out_0", (N, C), F32, kind="ExternalOutput").ap()
    build(nc, ins, out)
    r = run_bass_kernel_spmd(nc, [arrays], core_ids=[0])
    return r.results[0]["out_0"]
```
